# Optimizing a Trainium2 kernel written in Bass

```python
import numpy as np
import jax
import jax.numpy as jnp

def _softmax(x, axis=-1):
    return jax.nn.softmax(x, axis=axis)

def _gelu(x):
    return jax.nn.gelu(x, approximate=True)

def _silu(x):
    return jax.nn.silu(x)

def _sigmoid(x):
    return jax.nn.sigmoid(x)

def _layernorm(x, axis=-1, eps=1e-05):
    m = jnp.mean(x, axis=axis, keepdims=True)
    v = jnp.var(x, axis=axis, keepdims=True)
    return (x - m) / jnp.sqrt(v + eps)

def _scatter_add(tgt, idx, src, axis=0):
    return tgt.at[idx].add(src)

def _segment_sum(src, seg, n):
    return jax.ops.segment_sum(src, seg, n)
kernel_name = 'mk_xattn_ffn_d4_seqx_r4_5b1764'

def setup_inputs(seed: int=0):
    np.random.seed(seed)
    _w = jnp.asarray

    def _rec_inputs():
        import jax
        import jax.numpy as jnp
        _rk = jax.random.key(seed)
        x = -0.0002928 + 1 * jax.random.normal(jax.random.fold_in(_rk, 1), (2, 1024, 256), jnp.float32)
        _lenS = 1024 - jax.random.randint(jax.random.fold_in(_rk, 7), (2,), 0, max(1, 1024 // 4) + 1, jnp.int32)
        _lenS2 = 77 - jax.random.randint(jax.random.fold_in(_rk, 8), (2,), 0, max(1, 77 // 4) + 1, jnp.int32)
        _ctx_1024P = jax.random.normal(jax.random.fold_in(_rk, 11), (2, 16, 256), jnp.float32)
        _ctx_1024c = jax.random.dirichlet(jax.random.fold_in(_rk, 511), 0.3 * jnp.ones((16,), jnp.float32), (2, 77))
        _ctx_1024t = jnp.einsum('bsk,bkd->bsd', _ctx_1024c, _ctx_1024P)
        _ctx_1024t = _ctx_1024t * jax.lax.rsqrt(jnp.mean(jnp.square(_ctx_1024t)) + 1e-12) * 0.953939
        ctx_1024 = 0.000227908 + 0.99994 * (_ctx_1024t + 0.3 * jax.random.normal(jax.random.fold_in(_rk, 611), (2, 77, 256), jnp.float32))
        fside_Bx16xSxS2_0 = -3.27644e-05 + 1.00007 * jax.random.normal(jax.random.fold_in(_rk, 16), (2, 16, 1024, 77), jnp.float32)
        _validS = jnp.arange(1024)[None, :] < _lenS[:, None]
        _validS2 = jnp.arange(77)[None, :] < _lenS2[:, None]
        _causal = jnp.tril(jnp.ones((1024, 1024), dtype=bool))
        mask_SxS_bc0 = jnp.logical_not(jnp.broadcast_to(_causal[:, :], (1024, 1024)))
        mask_BxS2_bf1 = jnp.ones((2, 77), dtype=bool)
        mask_Bx1xSxS2_bk1 = jnp.broadcast_to(_validS2[:, None, None, :], (2, 1, 1024, 77))
        mask_Bx1xSxS2_ik1 = jnp.where(jnp.broadcast_to(_validS2[:, None, None, :], (2, 1, 1024, 77)), 1, 0).astype(jnp.int32)
        return (x, ctx_1024, fside_Bx16xSxS2_0, mask_SxS_bc0, mask_BxS2_bf1, mask_Bx1xSxS2_bk1, mask_Bx1xSxS2_ik1)
    x, ctx_1024, fside_Bx16xSxS2_0, mask_SxS_bc0, mask_BxS2_bf1, mask_Bx1xSxS2_bk1, mask_Bx1xSxS2_ik1 = _rec_inputs()

    def _L0_xattn_setup():
        import jax, jax.numpy as jnp
        import numpy as np
        from jax import lax
        H = 16
        K1, K2 = (3, 3)
        LN_EPS = 1e-05

        def _ln(x, g, b):
            m = jnp.mean(x, axis=-1, keepdims=True)
            v = jnp.mean(jnp.square(x - m), axis=-1, keepdims=True)
            return (x - m) * lax.rsqrt(v + LN_EPS) * g + b

        def _gelu(x):
            return jax.nn.gelu(x, approximate=False)
        key = jax.random.key(seed)
        B, T, D, Th = (4, 256, 256, 64)
        C = 2 * D
        ks = jax.random.split(key, 16)

        def w(k, shape):
            fan_in = shape[0]
            return (jax.random.normal(k, shape, jnp.float32) / np.sqrt(fan_in)).astype(jnp.float32)
        inp = {'x': jax.random.normal(ks[0], (B, T, D), jnp.float32), 'historical_data': jax.random.normal(ks[1], (B, Th, D), jnp.float32), 'Wq': w(ks[2], (D, D)), 'Wk': w(ks[3], (D, D)), 'Wv': w(ks[4], (D, D)), 'hist_W': w(ks[5], (D, C)), 'hist_b': jnp.zeros((C,), jnp.float32), 'hist_ln_g': jnp.ones((C,), jnp.float32), 'hist_ln_b': jnp.zeros((C,), jnp.float32), 'ctx_W1': w(ks[6], (C, C // 4)), 'ctx_b1': jnp.zeros((C // 4,), jnp.float32), 'ctx_W2': w(ks[7], (C // 4, 1)), 'ctx_b2': jnp.zeros((1,), jnp.float32), 'kg_W1': w(ks[8], (C, D)), 'kg_b1': jnp.zeros((D,), jnp.float32), 'kg_ln_g': jnp.ones((D,), jnp.float32), 'kg_ln_b': jnp.zeros((D,), jnp.float32), 'kg_W2': w(ks[9], (D, H * K1 * K2)), 'kg_b2': jnp.zeros((H * K1 * K2,), jnp.float32), 'proj_W': w(ks[10], (D, D)), 'proj_b': jnp.zeros((D,), jnp.float32), 'causal_mask': jnp.triu(jnp.ones((T, T), bool), k=1)}
        return inp
    _L0_xattn_all = _L0_xattn_setup()
    _L0_xattn_in = {k: v for k, v in _L0_xattn_all.items() if k in ('Wq', 'Wk', 'Wv', 'hist_W', 'hist_b', 'hist_ln_g', 'hist_ln_b', 'ctx_W1', 'ctx_b1', 'ctx_W2', 'ctx_b2', 'kg_W1', 'kg_b1', 'kg_ln_g', 'kg_ln_b', 'kg_W2', 'kg_b2', 'proj_W', 'proj_b')}
    del _L0_xattn_all

    def _L0_ffn_setup():
        import jax, jax.numpy as jnp
        import numpy as np
        BLOCK = 32
        W_BITS = 4
        ACT_BITS = 16

        def act_qdq(x):
            qmax = 2.0 ** (ACT_BITS - 1) - 1.0
            scale = jnp.maximum(jnp.max(jnp.abs(x)) / qmax, 1e-12)
            return jnp.clip(jnp.round(x / scale), -qmax - 1.0, qmax) * scale

        def fixed_qdq_u16(x):
            scale = 1.0 / 65536.0
            return jnp.clip(jnp.round(x / scale), 0.0, 65535.0) * scale

        def lpbq_dequant(w):
            O, I = w.shape
            qmax = 2.0 ** (W_BITS - 1) - 1.0
            wb = w.reshape(O, I // BLOCK, BLOCK)
            s = jnp.maximum(jnp.max(jnp.abs(wb), axis=-1, keepdims=True) / qmax, 1e-12)
            wq = jnp.clip(jnp.round(wb / s), -qmax - 1.0, qmax) * s
            return wq.reshape(O, I)
        key = jax.random.key(seed)
        k1, k2, k3, k4 = jax.random.split(key, 4)
        B, S, H, I = (2, 1024, 256, 768)
        x = jax.random.normal(k1, (B, S, H), jnp.float32)
        w_gate = jax.random.normal(k2, (I, H), jnp.float32) * 0.02
        w_up = jax.random.normal(k3, (I, H), jnp.float32) * 0.02
        w_down = jax.random.normal(k4, (H, I), jnp.float32) * 0.02
        return {'x': x, 'w_gate': w_gate, 'w_up': w_up, 'w_down': w_down}
    _L0_ffn_all = _L0_ffn_setup()
    _L0_ffn_in = {k: v for k, v in _L0_ffn_all.items() if k in ('w_gate', 'w_up', 'w_down')}
    del _L0_ffn_all

    def _L1_xattn_setup():
        import jax, jax.numpy as jnp
        import numpy as np
        DIM = 256
        DIM_LATENT = 256
        DIM_HEAD = 64
        HEADS = 16
        INNER = HEADS * DIM_HEAD

        def layernorm(x, g, b, eps=1e-05):
            m = jnp.mean(x, axis=-1, keepdims=True)
            v = jnp.mean((x - m) ** 2, axis=-1, keepdims=True)
            return (x - m) / jnp.sqrt(v + eps) * g + b

        def rmsnorm(x, gamma, eps=1e-08):
            n = jnp.linalg.norm(x, axis=-1, keepdims=True) * x.shape[-1] ** (-0.5)
            return x / jnp.maximum(n, eps) * gamma
        key = jax.random.key(seed)
        ks = jax.random.split(key, 8)
        b, n, m = (4, 1024, 128)
        x = jax.random.normal(ks[0], (b, n, DIM), dtype=jnp.float32)
        latents = jax.random.normal(ks[1], (b, m, DIM_LATENT), dtype=jnp.float32)
        mask = jnp.ones((b, n), dtype=bool)
        s = 0.02
        return {'x': x, 'latents': latents, 'mask': mask, 'ln_x_g': jnp.ones((DIM,), jnp.float32), 'ln_x_b': jnp.zeros((DIM,), jnp.float32), 'ln_l_g': jnp.ones((DIM_LATENT,), jnp.float32), 'ln_l_b': jnp.zeros((DIM_LATENT,), jnp.float32), 'qn_g': jnp.ones((DIM_HEAD,), jnp.float32), 'kn_g': jnp.ones((DIM_HEAD,), jnp.float32), 'Wq': jax.random.normal(ks[2], (DIM_LATENT, INNER), jnp.float32) * s, 'Wkv': jax.random.normal(ks[3], (DIM, 2 * INNER), jnp.float32) * s, 'Wout': jax.random.normal(ks[4], (INNER, DIM_LATENT), jnp.float32) * s, 'bout': jnp.zeros((DIM_LATENT,), jnp.float32)}
    _L1_xattn_all = _L1_xattn_setup()
    _L1_xattn_in = {k: v for k, v in _L1_xattn_all.items() if k in ('ln_x_g', 'ln_x_b', 'ln_l_g', 'ln_l_b', 'qn_g', 'kn_g', 'Wq', 'Wkv', 'Wout', 'bout')}
    del _L1_xattn_all

    def _L1_ffn_setup():
        import jax, jax.numpy as jnp
        import numpy as np
        B, S, D = (4, 512, 256)
        E = 8
        F = 1024
        T = B * S
        CAP = 320
        key = jax.random.key(seed)
        k1, k2, k3, k4 = jax.random.split(key, 4)
        inputs = jax.random.normal(k1, (B, S, D), dtype=jnp.float32)
        gate_w = jax.random.normal(k2, (D, E), dtype=jnp.float32) / np.sqrt(D)
        w1 = jax.random.normal(k3, (E, D, F), dtype=jnp.float32) / np.sqrt(D)
        w2 = jax.random.normal(k4, (E, F, D), dtype=jnp.float32) / np.sqrt(F)
        return {'inputs': inputs, 'gate_w': gate_w, 'w1': w1, 'w2': w2}
    _L1_ffn_all = _L1_ffn_setup()
    _L1_ffn_in = {k: v for k, v in _L1_ffn_all.items() if k in ('gate_w', 'w1', 'w2')}
    del _L1_ffn_all

    def _L2_xattn_setup():
        import jax, jax.numpy as jnp
        import numpy as np
        B, S, D, H = (4, 512, 256, 16)
        HD = D // H
        key = jax.random.key(seed)
        ks = jax.random.split(key, 12)
        scale = 1.0 / np.sqrt(D)
        inp = {'queries': jax.random.normal(ks[0], (B, S, D), jnp.float32), 'keys': jax.random.normal(ks[1], (B, S, D), jnp.float32), 'values': jax.random.normal(ks[2], (B, S, D), jnp.float32), 'mask': jax.random.randint(ks[3], (B, 1, S, S), 0, 2).astype(bool), 'Wq': jax.random.normal(ks[4], (D, D), jnp.float32) * scale, 'bq': jnp.zeros((D,), jnp.float32), 'Wk': jax.random.normal(ks[5], (D, D), jnp.float32) * scale, 'bk': jnp.zeros((D,), jnp.float32), 'Wv': jax.random.normal(ks[6], (D, D), jnp.float32) * scale, 'bv': jnp.zeros((D,), jnp.float32), 'Wo': jax.random.normal(ks[7], (D, D), jnp.float32) * scale, 'bo': jnp.zeros((D,), jnp.float32)}
        return inp
    _L2_xattn_all = _L2_xattn_setup()
    _L2_xattn_in = {k: v for k, v in _L2_xattn_all.items() if k in ('Wq', 'bq', 'Wk', 'bk', 'Wv', 'bv', 'Wo', 'bo')}
    del _L2_xattn_all

    def _L2_ffn_setup():
        import jax, jax.numpy as jnp
        import numpy as np
        TOP_P = 0.8
        B, T, H, F, E = (2, 512, 256, 1024, 8)
        key = jax.random.key(seed)
        k0, k1, k2, k3 = jax.random.split(key, 4)
        x = jax.random.normal(k0, (B, T, H), jnp.float32)
        Wr = jax.random.normal(k1, (H, E), jnp.float32) * 0.02
        br = jnp.zeros((E,), jnp.float32)
        W1 = jax.random.normal(k2, (E, H, F), jnp.float32) * 0.02
        b1 = jnp.zeros((E, F), jnp.float32)
        W2 = jax.random.normal(k3, (E, F, H), jnp.float32) * 0.02
        b2 = jnp.zeros((E, H), jnp.float32)
        return {'x': x, 'Wr': Wr, 'br': br, 'W1': W1, 'b1': b1, 'W2': W2, 'b2': b2}
    _L2_ffn_all = _L2_ffn_setup()
    _L2_ffn_in = {k: v for k, v in _L2_ffn_all.items() if k in ('Wr', 'br', 'W1', 'b1', 'W2', 'b2')}
    del _L2_ffn_all

    def _L3_xattn_setup():
        import jax, jax.numpy as jnp
        import numpy as np
        DIM = 256
        NUM_HEADS = 16
        HEAD_DIM = DIM // NUM_HEADS
        SCALE = HEAD_DIM ** (-0.5)
        key = jax.random.key(seed)
        ks = jax.random.split(key, 13)
        B, L, S = (2, 512, 512)
        inp = {'query': jax.random.normal(ks[0], (B, L, DIM), jnp.float32), 'key': jax.random.normal(ks[1], (B, S, DIM), jnp.float32), 'value': jax.random.normal(ks[2], (B, S, DIM), jnp.float32), 'mask': jax.random.randint(ks[3], (B, 1, L, S), 0, 2, jnp.int32), 'attn_bias': jax.random.normal(ks[4], (B, NUM_HEADS, L, S), jnp.float32), 'Wq': jax.random.normal(ks[5], (DIM, DIM), jnp.float32) * DIM ** (-0.5), 'bq': jax.random.normal(ks[6], (DIM,), jnp.float32) * 0.02, 'Wk': jax.random.normal(ks[7], (DIM, DIM), jnp.float32) * DIM ** (-0.5), 'bk': jax.random.normal(ks[8], (DIM,), jnp.float32) * 0.02, 'Wv': jax.random.normal(ks[9], (DIM, DIM), jnp.float32) * DIM ** (-0.5), 'bv': jax.random.normal(ks[10], (DIM,), jnp.float32) * 0.02, 'Wo': jax.random.normal(ks[11], (DIM, DIM), jnp.float32) * DIM ** (-0.5), 'bo': jax.random.normal(ks[12], (DIM,), jnp.float32) * 0.02}
        return inp
    _L3_xattn_all = _L3_xattn_setup()
    _L3_xattn_in = {k: v for k, v in _L3_xattn_all.items() if k in ('Wq', 'bq', 'Wk', 'bk', 'Wv', 'bv', 'Wo', 'bo')}
    del _L3_xattn_all

    def _L3_ffn_setup():
        import jax, jax.numpy as jnp
        import numpy as np
        NUM_EXPERTS = 8
        N_EMBD = 256
        D_FF = 4 * N_EMBD
        B, S = (4, 512)
        key = jax.random.key(seed)
        ks = jax.random.split(key, 6)
        x = jax.random.normal(ks[0], (B, S, N_EMBD), dtype=jnp.float32)
        gate_w = jax.random.normal(ks[1], (N_EMBD, NUM_EXPERTS), dtype=jnp.float32) * 0.02
        w1 = jax.random.normal(ks[2], (NUM_EXPERTS, N_EMBD, D_FF), dtype=jnp.float32) * 0.02
        b1 = jnp.zeros((NUM_EXPERTS, D_FF), dtype=jnp.float32)
        w2 = jax.random.normal(ks[3], (NUM_EXPERTS, D_FF, N_EMBD), dtype=jnp.float32) * 0.02
        b2 = jnp.zeros((NUM_EXPERTS, N_EMBD), dtype=jnp.float32)
        return {'x': x, 'gate_w': gate_w, 'w1': w1, 'b1': b1, 'w2': w2, 'b2': b2}
    _L3_ffn_all = _L3_ffn_setup()
    _L3_ffn_in = {k: v for k, v in _L3_ffn_all.items() if k in ('gate_w', 'w1', 'b1', 'w2', 'b2')}
    del _L3_ffn_all
    return {'x': x, 'ctx_1024': ctx_1024, 'fside_Bx16xSxS2_0': fside_Bx16xSxS2_0, 'mask_SxS_bc0': mask_SxS_bc0, 'mask_BxS2_bf1': mask_BxS2_bf1, 'mask_Bx1xSxS2_bk1': mask_Bx1xSxS2_bk1, 'mask_Bx1xSxS2_ik1': mask_Bx1xSxS2_ik1, 'L0_xattn_Wq': _L0_xattn_in['Wq'], 'L0_xattn_Wk': _L0_xattn_in['Wk'], 'L0_xattn_Wv': _L0_xattn_in['Wv'], 'L0_xattn_hist_W': _L0_xattn_in['hist_W'], 'L0_xattn_hist_b': _L0_xattn_in['hist_b'], 'L0_xattn_hist_ln_g': _L0_xattn_in['hist_ln_g'], 'L0_xattn_hist_ln_b': _L0_xattn_in['hist_ln_b'], 'L0_xattn_ctx_W1': _L0_xattn_in['ctx_W1'], 'L0_xattn_ctx_b1': _L0_xattn_in['ctx_b1'], 'L0_xattn_ctx_W2': _L0_xattn_in['ctx_W2'], 'L0_xattn_ctx_b2': _L0_xattn_in['ctx_b2'], 'L0_xattn_kg_W1': _L0_xattn_in['kg_W1'], 'L0_xattn_kg_b1': _L0_xattn_in['kg_b1'], 'L0_xattn_kg_ln_g': _L0_xattn_in['kg_ln_g'], 'L0_xattn_kg_ln_b': _L0_xattn_in['kg_ln_b'], 'L0_xattn_kg_W2': _L0_xattn_in['kg_W2'], 'L0_xattn_kg_b2': _L0_xattn_in['kg_b2'], 'L0_xattn_proj_W': _L0_xattn_in['proj_W'], 'L0_xattn_proj_b': _L0_xattn_in['proj_b'], 'L0_ffn_w_gate': _L0_ffn_in['w_gate'], 'L0_ffn_w_up': _L0_ffn_in['w_up'], 'L0_ffn_w_down': _L0_ffn_in['w_down'], 'L1_xattn_ln_x_g': _L1_xattn_in['ln_x_g'], 'L1_xattn_ln_x_b': _L1_xattn_in['ln_x_b'], 'L1_xattn_ln_l_g': _L1_xattn_in['ln_l_g'], 'L1_xattn_ln_l_b': _L1_xattn_in['ln_l_b'], 'L1_xattn_qn_g': _L1_xattn_in['qn_g'], 'L1_xattn_kn_g': _L1_xattn_in['kn_g'], 'L1_xattn_Wq': _L1_xattn_in['Wq'], 'L1_xattn_Wkv': _L1_xattn_in['Wkv'], 'L1_xattn_Wout': _L1_xattn_in['Wout'], 'L1_xattn_bout': _L1_xattn_in['bout'], 'L1_ffn_gate_w': _L1_ffn_in['gate_w'], 'L1_ffn_w1': _L1_ffn_in['w1'], 'L1_ffn_w2': _L1_ffn_in['w2'], 'L2_xattn_Wq': _L2_xattn_in['Wq'], 'L2_xattn_bq': _L2_xattn_in['bq'], 'L2_xattn_Wk': _L2_xattn_in['Wk'], 'L2_xattn_bk': _L2_xattn_in['bk'], 'L2_xattn_Wv': _L2_xattn_in['Wv'], 'L2_xattn_bv': _L2_xattn_in['bv'], 'L2_xattn_Wo': _L2_xattn_in['Wo'], 'L2_xattn_bo': _L2_xattn_in['bo'], 'L2_ffn_Wr': _L2_ffn_in['Wr'], 'L2_ffn_br': _L2_ffn_in['br'], 'L2_ffn_W1': _L2_ffn_in['W1'], 'L2_ffn_b1': _L2_ffn_in['b1'], 'L2_ffn_W2': _L2_ffn_in['W2'], 'L2_ffn_b2': _L2_ffn_in['b2'], 'L3_xattn_Wq': _L3_xattn_in['Wq'], 'L3_xattn_bq': _L3_xattn_in['bq'], 'L3_xattn_Wk': _L3_xattn_in['Wk'], 'L3_xattn_bk': _L3_xattn_in['bk'], 'L3_xattn_Wv': _L3_xattn_in['Wv'], 'L3_xattn_bv': _L3_xattn_in['bv'], 'L3_xattn_Wo': _L3_xattn_in['Wo'], 'L3_xattn_bo': _L3_xattn_in['bo'], 'L3_ffn_gate_w': _L3_ffn_in['gate_w'], 'L3_ffn_w1': _L3_ffn_in['w1'], 'L3_ffn_b1': _L3_ffn_in['b1'], 'L3_ffn_w2': _L3_ffn_in['w2'], 'L3_ffn_b2': _L3_ffn_in['b2']}

def reference(x, ctx_1024, fside_Bx16xSxS2_0, mask_SxS_bc0, mask_BxS2_bf1, mask_Bx1xSxS2_bk1, mask_Bx1xSxS2_ik1, L0_xattn_Wq, L0_xattn_Wk, L0_xattn_Wv, L0_xattn_hist_W, L0_xattn_hist_b, L0_xattn_hist_ln_g, L0_xattn_hist_ln_b, L0_xattn_ctx_W1, L0_xattn_ctx_b1, L0_xattn_ctx_W2, L0_xattn_ctx_b2, L0_xattn_kg_W1, L0_xattn_kg_b1, L0_xattn_kg_ln_g, L0_xattn_kg_ln_b, L0_xattn_kg_W2, L0_xattn_kg_b2, L0_xattn_proj_W, L0_xattn_proj_b, L0_ffn_w_gate, L0_ffn_w_up, L0_ffn_w_down, L1_xattn_ln_x_g, L1_xattn_ln_x_b, L1_xattn_ln_l_g, L1_xattn_ln_l_b, L1_xattn_qn_g, L1_xattn_kn_g, L1_xattn_Wq, L1_xattn_Wkv, L1_xattn_Wout, L1_xattn_bout, L1_ffn_gate_w, L1_ffn_w1, L1_ffn_w2, L2_xattn_Wq, L2_xattn_bq, L2_xattn_Wk, L2_xattn_bk, L2_xattn_Wv, L2_xattn_bv, L2_xattn_Wo, L2_xattn_bo, L2_ffn_Wr, L2_ffn_br, L2_ffn_W1, L2_ffn_b1, L2_ffn_W2, L2_ffn_b2, L3_xattn_Wq, L3_xattn_bq, L3_xattn_Wk, L3_xattn_bk, L3_xattn_Wv, L3_xattn_bv, L3_xattn_Wo, L3_xattn_bo, L3_ffn_gate_w, L3_ffn_w1, L3_ffn_b1, L3_ffn_w2, L3_ffn_b2):
    import jax
    import jax.numpy as jnp

    def _L0_xattn_ref(x, historical_data, Wq, Wk, Wv, hist_W, hist_b, hist_ln_g, hist_ln_b, ctx_W1, ctx_b1, ctx_W2, ctx_b2, kg_W1, kg_b1, kg_ln_g, kg_ln_b, kg_W2, kg_b2, proj_W, proj_b, causal_mask):
        import jax, jax.numpy as jnp
        import numpy as np
        from jax import lax
        H = 16
        K1, K2 = (3, 3)
        LN_EPS = 1e-05

        def _ln(x, g, b):
            m = jnp.mean(x, axis=-1, keepdims=True)
            v = jnp.mean(jnp.square(x - m), axis=-1, keepdims=True)
            return (x - m) * lax.rsqrt(v + LN_EPS) * g + b

        def _gelu(x):
            return jax.nn.gelu(x, approximate=False)
        B, T, D = x.shape
        hd = D // H
        scale = hd ** (-0.5)
        q = (x @ Wq).reshape(B, T, H, hd).transpose(0, 2, 1, 3)
        k = (x @ Wk).reshape(B, T, H, hd).transpose(0, 2, 1, 3)
        v = (x @ Wv).reshape(B, T, H, hd).transpose(0, 2, 1, 3)
        attn = jnp.einsum('bhqd,bhkd->bhqk', q, k) * scale
        eh = _gelu(_ln(historical_data @ hist_W + hist_b, hist_ln_g, hist_ln_b))
        aw = _gelu(eh @ ctx_W1 + ctx_b1) @ ctx_W2 + ctx_b2
        aw = jax.nn.softmax(aw, axis=1)
        cc = jnp.sum(eh * aw, axis=1)
        kp = _gelu(_ln(cc @ kg_W1 + kg_b1, kg_ln_g, kg_ln_b)) @ kg_W2 + kg_b2
        kernels = jax.nn.softmax(kp.reshape(B, H, K1 * K2), axis=-1)
        kernels = kernels.reshape(B * H, 1, K1, K2)
        mask = causal_mask[None, None]
        attn0 = jnp.where(mask, 0.0, attn).reshape(1, B * H, T, T)
        attn = lax.conv_general_dilated(attn0, kernels, window_strides=(1, 1), padding=((K1 // 2, K1 // 2), (K2 // 2, K2 // 2)), feature_group_count=B * H, dimension_numbers=('NCHW', 'OIHW', 'NCHW')).reshape(B, H, T, T)
        attn = jnp.where(mask, -jnp.inf, attn)
        p = jax.nn.softmax(attn, axis=-1)
        out = jnp.einsum('bhqk,bhkd->bhqd', p, v)
        out = out.transpose(0, 2, 1, 3).reshape(B, T, D)
        return out @ proj_W + proj_b

    def _L0_ffn_ref(x, w_gate, w_up, w_down):
        import jax, jax.numpy as jnp
        import numpy as np
        BLOCK = 32
        W_BITS = 4
        ACT_BITS = 16

        def act_qdq(x):
            qmax = 2.0 ** (ACT_BITS - 1) - 1.0
            scale = jnp.maximum(jnp.max(jnp.abs(x)) / qmax, 1e-12)
            return jnp.clip(jnp.round(x / scale), -qmax - 1.0, qmax) * scale

        def fixed_qdq_u16(x):
            scale = 1.0 / 65536.0
            return jnp.clip(jnp.round(x / scale), 0.0, 65535.0) * scale

        def lpbq_dequant(w):
            O, I = w.shape
            qmax = 2.0 ** (W_BITS - 1) - 1.0
            wb = w.reshape(O, I // BLOCK, BLOCK)
            s = jnp.maximum(jnp.max(jnp.abs(wb), axis=-1, keepdims=True) / qmax, 1e-12)
            wq = jnp.clip(jnp.round(wb / s), -qmax - 1.0, qmax) * s
            return wq.reshape(O, I)
        x = act_qdq(x)
        up = act_qdq(x @ lpbq_dequant(w_up).T)
        gate = act_qdq(x @ lpbq_dequant(w_gate).T)
        sig = fixed_qdq_u16(jax.nn.sigmoid(gate))
        gate = act_qdq(gate * sig)
        o = act_qdq(gate * up)
        return o @ lpbq_dequant(w_down).T

    def _L1_xattn_ref(x, latents, mask, ln_x_g, ln_x_b, ln_l_g, ln_l_b, qn_g, kn_g, Wq, Wkv, Wout, bout):
        import jax, jax.numpy as jnp
        import numpy as np
        DIM = 256
        DIM_LATENT = 256
        DIM_HEAD = 64
        HEADS = 16
        INNER = HEADS * DIM_HEAD

        def layernorm(x, g, b, eps=1e-05):
            m = jnp.mean(x, axis=-1, keepdims=True)
            v = jnp.mean((x - m) ** 2, axis=-1, keepdims=True)
            return (x - m) / jnp.sqrt(v + eps) * g + b

        def rmsnorm(x, gamma, eps=1e-08):
            n = jnp.linalg.norm(x, axis=-1, keepdims=True) * x.shape[-1] ** (-0.5)
            return x / jnp.maximum(n, eps) * gamma
        b, n, _ = x.shape
        m = latents.shape[1]
        h, d = (HEADS, DIM_HEAD)
        scale = d ** (-0.5)
        xn = layernorm(x, ln_x_g, ln_x_b)
        ln = layernorm(latents, ln_l_g, ln_l_b)
        q = (ln @ Wq).reshape(b, m, h, d).transpose(0, 2, 1, 3)
        kv = jnp.concatenate([xn @ Wkv, ln @ Wkv], axis=1)
        kv = kv.reshape(b, n + m, 2, h, d)
        k = kv[:, :, 0].transpose(0, 2, 1, 3)
        v = kv[:, :, 1].transpose(0, 2, 1, 3)
        qn = rmsnorm(q, qn_g) * scale
        kn = rmsnorm(k, kn_g)
        sim = jnp.einsum('bhid,bhjd->bhij', qn, kn)
        max_neg = -jnp.finfo(sim.dtype).max
        padded_mask = jnp.concatenate([mask, jnp.ones((b, m), bool)], axis=1)
        sim = jnp.where(padded_mask[:, None, None, :], sim, max_neg)
        attn = jax.nn.softmax(sim.astype(jnp.float32), axis=-1).astype(sim.dtype)
        out = jnp.einsum('bhij,bhjd->bhid', attn, v)
        out = out.transpose(0, 2, 1, 3).reshape(b, m, h * d)
        return out @ Wout + bout

    def _L1_ffn_ref(inputs, gate_w, w1, w2):
        import jax, jax.numpy as jnp
        import numpy as np
        B, S, D = (4, 512, 256)
        E = 8
        F = 1024
        T = B * S
        CAP = 320
        tokens = inputs.reshape(-1, D)
        logits = tokens @ gate_w
        probs = jax.nn.softmax(logits, axis=-1)
        expert_idx = jnp.argmax(probs, axis=-1)
        mask1 = jax.nn.one_hot(expert_idx, E, dtype=tokens.dtype)
        pos = (jnp.cumsum(mask1, axis=0) - 1.0).astype(jnp.int32)
        sec_mask = mask1[:, :, None] * jax.nn.one_hot(pos, CAP, dtype=tokens.dtype)
        combine_weights = probs[:, :, None] * sec_mask
        expert_input = jnp.einsum('tec,td->ecd', sec_mask, tokens)
        h = jax.nn.relu(jnp.einsum('ecd,edf->ecf', expert_input, w1))
        expert_output = jnp.einsum('ecf,efd->ecd', h, w2)
        out = jnp.einsum('tec,ecd->td', combine_weights, expert_output)
        return out.reshape(inputs.shape)

    def _L2_xattn_ref(queries, keys, values, mask, Wq, bq, Wk, bk, Wv, bv, Wo, bo):
        import jax, jax.numpy as jnp
        import numpy as np
        B, S, D, H = (4, 512, 256, 16)
        HD = D // H
        b, sq, d = queries.shape

        def split_heads(x):
            return x.reshape(b, x.shape[1], H, HD).transpose(0, 2, 1, 3)
        q = split_heads(queries @ Wq + bq)
        k = split_heads(keys @ Wk + bk)
        v = split_heads(values @ Wv + bv)
        scores = jnp.einsum('bhqd,bhkd->bhqk', q, k) / jnp.sqrt(jnp.float32(HD))
        scores = jnp.where(mask, jnp.float32(-1000000000000000.0), scores)
        attn = jax.nn.softmax(scores, axis=-1)
        ctx = jnp.einsum('bhqk,bhkd->bhqd', attn, v)
        ctx = ctx.transpose(0, 2, 1, 3).reshape(b, sq, d)
        return ctx @ Wo + bo

    def _L2_ffn_ref(x, Wr, br, W1, b1, W2, b2):
        import jax, jax.numpy as jnp
        import numpy as np
        TOP_P = 0.8
        B, T, H, F, E = (2, 512, 256, 1024, 8)
        probs = jax.nn.softmax(x @ Wr + br, axis=-1)
        sorted_idx = jnp.argsort(-probs, axis=-1)
        sorted_probs = jnp.take_along_axis(probs, sorted_idx, axis=-1)
        cum = jnp.cumsum(sorted_probs, axis=-1)
        mask = cum < TOP_P
        mask = mask.at[..., 0].set(True)
        inv = jnp.argsort(sorted_idx, axis=-1)
        keep = jnp.take_along_axis(mask, inv, axis=-1)
        gate = probs * keep
        h = jax.nn.relu(jnp.einsum('bth,ehf->betf', x, W1) + b1[None, :, None, :])
        y = jnp.einsum('betf,efh->beth', h, W2) + b2[None, :, None, :]
        return jnp.einsum('bte,beth->bth', gate, y)

    def _L3_xattn_ref(query, key, value, mask, attn_bias, Wq, bq, Wk, bk, Wv, bv, Wo, bo):
        import jax, jax.numpy as jnp
        import numpy as np
        DIM = 256
        NUM_HEADS = 16
        HEAD_DIM = DIM // NUM_HEADS
        SCALE = HEAD_DIM ** (-0.5)
        B, L, _ = query.shape
        S = key.shape[1]
        H, D = (NUM_HEADS, HEAD_DIM)
        q = (query @ Wq + bq).reshape(B, L, H, D).transpose(0, 2, 1, 3)
        k = (key @ Wk + bk).reshape(B, S, H, D).transpose(0, 2, 1, 3)
        v = (value @ Wv + bv).reshape(B, S, H, D).transpose(0, 2, 1, 3)
        scores = jnp.einsum('bhld,bhsd->bhls', q, k) * SCALE + attn_bias
        scores = jnp.where(mask == 0, -jnp.inf, scores)
        probs = jax.nn.softmax(scores, axis=-1)
        out = jnp.einsum('bhls,bhsd->bhld', probs, v)
        out = out.transpose(0, 2, 1, 3).reshape(B, L, DIM)
        return out @ Wo + bo

    def _L3_ffn_ref(x, gate_w, w1, b1, w2, b2):
        import jax, jax.numpy as jnp
        import numpy as np
        NUM_EXPERTS = 8
        N_EMBD = 256
        D_FF = 4 * N_EMBD
        B, S = (4, 512)
        Bb, Ss, D = x.shape
        x_flat = x.reshape(-1, D)
        router_logits = x_flat @ gate_w
        router_probs = jax.nn.softmax(router_logits, axis=-1)
        expert_idx = jnp.argmax(router_probs, axis=-1)
        expert_w = jnp.take_along_axis(router_probs, expert_idx[:, None], axis=1)[:, 0]
        out = jnp.zeros_like(x_flat)
        for e in range(NUM_EXPERTS):
            h = jax.nn.gelu(x_flat @ w1[e] + b1[e], approximate=False)
            y = h @ w2[e] + b2[e]
            sel = expert_idx == e
            out = out + jnp.where(sel, expert_w, 0.0)[:, None] * y
        return out.reshape(Bb, Ss, D)
    x = x + _L0_xattn_ref(_layernorm(x, axis=-1), ctx_1024, L0_xattn_Wq, L0_xattn_Wk, L0_xattn_Wv, L0_xattn_hist_W, L0_xattn_hist_b, L0_xattn_hist_ln_g, L0_xattn_hist_ln_b, L0_xattn_ctx_W1, L0_xattn_ctx_b1, L0_xattn_ctx_W2, L0_xattn_ctx_b2, L0_xattn_kg_W1, L0_xattn_kg_b1, L0_xattn_kg_ln_g, L0_xattn_kg_ln_b, L0_xattn_kg_W2, L0_xattn_kg_b2, L0_xattn_proj_W, L0_xattn_proj_b, mask_SxS_bc0)
    x = x + _L0_ffn_ref(_layernorm(x, axis=-1), L0_ffn_w_gate, L0_ffn_w_up, L0_ffn_w_down)
    x = x + _L1_xattn_ref(ctx_1024, _layernorm(x, axis=-1), mask_BxS2_bf1, L1_xattn_ln_x_g, L1_xattn_ln_x_b, L1_xattn_ln_l_g, L1_xattn_ln_l_b, L1_xattn_qn_g, L1_xattn_kn_g, L1_xattn_Wq, L1_xattn_Wkv, L1_xattn_Wout, L1_xattn_bout)
    x = x + _L1_ffn_ref(_layernorm(x, axis=-1), L1_ffn_gate_w, L1_ffn_w1, L1_ffn_w2)
    x = x + _L2_xattn_ref(_layernorm(x, axis=-1), ctx_1024, ctx_1024, mask_Bx1xSxS2_bk1, L2_xattn_Wq, L2_xattn_bq, L2_xattn_Wk, L2_xattn_bk, L2_xattn_Wv, L2_xattn_bv, L2_xattn_Wo, L2_xattn_bo)
    x = x + _L2_ffn_ref(_layernorm(x, axis=-1), L2_ffn_Wr, L2_ffn_br, L2_ffn_W1, L2_ffn_b1, L2_ffn_W2, L2_ffn_b2)
    x = x + _L3_xattn_ref(_layernorm(x, axis=-1), ctx_1024, ctx_1024, mask_Bx1xSxS2_ik1, fside_Bx16xSxS2_0, L3_xattn_Wq, L3_xattn_bq, L3_xattn_Wk, L3_xattn_bk, L3_xattn_Wv, L3_xattn_bv, L3_xattn_Wo, L3_xattn_bo)
    x = x + _L3_ffn_ref(_layernorm(x, axis=-1), L3_ffn_gate_w, L3_ffn_w1, L3_ffn_b1, L3_ffn_w2, L3_ffn_b2)
    return x

_drawn_inputs = setup_inputs


def setup_inputs(seed=0):
    import zlib

    import numpy as np

    out = dict(_drawn_inputs(seed))
    spreads = {'L0_xattn_hist_b': (0.0, 0.674),
     'L0_xattn_hist_ln_g': (1.0, 0.6),
     'L0_xattn_hist_ln_b': (0.0, 0.8),
     'L0_xattn_ctx_b1': (0.0, 2.0),
     'L0_xattn_kg_b1': (0.0, 0.483),
     'L0_xattn_kg_ln_g': (1.0, 0.6),
     'L0_xattn_kg_ln_b': (0.0, 0.8),
     'L0_xattn_kg_b2': (0.0, 0.737),
     'L0_xattn_proj_b': (0.0, 0.1),
     'L1_xattn_ln_x_g': (1.0, 0.6),
     'L1_xattn_ln_x_b': (0.0, 0.8),
     'L1_xattn_ln_l_g': (1.0, 0.6),
     'L1_xattn_ln_l_b': (0.0, 0.269),
     'L1_xattn_qn_g': (1.0, 0.6),
     'L1_xattn_kn_g': (1.0, 0.6),
     'L1_xattn_bout': (0.0, 0.1),
     'L2_xattn_bq': (0.0, 0.1),
     'L2_xattn_bk': (0.0, 2.0),
     'L2_xattn_bv': (0.0, 0.1),
     'L2_xattn_bo': (0.0, 0.1),
     'L2_ffn_br': (0.0, 0.547),
     'L2_ffn_b1': (0.0, 0.747),
     'L2_ffn_b2': (0.0, 0.314),
     'L3_ffn_b1': (0.0, 0.8),
     'L3_ffn_b2': (0.0, 0.61)}
    factors = {'L0_xattn_ctx_W1': 6.797,
     'L0_xattn_ctx_W2': 6.402,
     'L3_xattn_bq': 8.0,
     'L3_xattn_bk': 64.0,
     'L3_xattn_bv': 3.725,
     'L3_xattn_bo': 4.146,
     'L3_ffn_gate_w': 2.993,
     'L3_ffn_w1': 3.852,
     'L3_ffn_w2': 3.566}
    for name, (base, spread) in spreads.items():
        noise = np.random.default_rng([zlib.crc32(name.encode()), seed]).standard_normal(out[name].shape)
        drawn = base * np.exp(spread * noise) if base else spread * noise
        out[name] = jnp.asarray(drawn.astype(out[name].dtype))
    for name, factor in factors.items():
        out[name] = (out[name] * factor).astype(out[name].dtype)
    return out
```

```python
from contextlib import ExitStack

import concourse.bass as bass
from concourse import mybir

ALU = mybir.AluOpType
ACT = mybir.ActivationFunctionType
F32 = mybir.dt.float32
BF16 = mybir.dt.bfloat16
U8 = mybir.dt.uint8
I32 = mybir.dt.int32
U32 = mybir.dt.uint32
AX_X = mybir.AxisListType.X
RMAX = bass.bass_isa.ReduceOp.max

P = 128
B, S, D = 2, 1024, 256
NCTX = 77
H = 16
HD = D // H
T = B * S
TILES = T // P
TPB = S // P
DC = D // P
LN_EPS = 1e-5
NEG = -1e30


def chain(eng, sem, base=0):
    done = [0]

    def step(ins):
        done[0] += 1
        ins.then_inc(sem, 1)
        eng.wait_ge(sem, base + done[0])
        return ins

    step.done = done
    return step


class Stage:

    def __init__(self, nc, ctx, tag):
        self.nc, self.ctx, self.tag, self.sems = nc, ctx, tag, []
        ctx.callback(self.clear)

    def sb(self, name, shape, dt=F32):
        return self.ctx.enter_context(self.nc.sbuf_tensor(f"{self.tag}_{name}", shape, dt))

    def ps(self, name, shape, dt=F32):
        return self.ctx.enter_context(self.nc.psum_tensor(f"{self.tag}_{name}", shape, dt))

    def sem(self, name):
        made = self.ctx.enter_context(self.nc.semaphore(f"{self.tag}_{name}"))
        self.sems.append(made)
        return made

    def clear(self):
        with self.nc.Block() as block:
            @block.gpsimd
            def _(pool):
                runs = []
                for num in sorted(s.num for s in self.sems):
                    if runs and runs[-1].stop == num:
                        runs[-1] = range(runs[-1].start, num + 1)
                    else:
                        runs.append(range(num, num + 1))
                for run in runs:
                    pool.sem_clear(run)


def tile_of(buf, t):
    return buf[:, bass.ds(t, 1), :].rearrange("p a n -> p (a n)")


def setup_stage(nc, env, args):
    with ExitStack() as ctx:
        st = Stage(nc, ctx, "set")
        x_loaded, ctx_loaded = st.sem("x_loaded"), st.sem("ctx_loaded")
        zeroed, made = st.sem("zeroed"), st.sem("made")
        block = ctx.enter_context(nc.Block())

        @block.sync
        def _(sp):
            sp.dma_start(env.x[:], args["x"].rearrange("b (t p) d -> p (b t) d", p=P)).then_inc(x_loaded, 16)
            sp.dma_start(env.ctx_tok[0:NCTX], args["ctx_1024"].rearrange("b t d -> t b d")).then_inc(ctx_loaded, 16)
            sp.wait_ge(x_loaded, 16)
            sp.wait_ge(ctx_loaded, 16)

        @block.gpsimd
        def _(pool):
            nc.gpsimd.memset(env.ident[:], 0.0).then_inc(zeroed, 1)
            nc.gpsimd.memset(env.ones[:], 1.0).then_inc(made, 1)
            nc.gpsimd.memset(env.eps[:], LN_EPS).then_inc(made, 1)
            pool.wait_ge(zeroed, 1)
            nc.gpsimd.affine_select(out=env.ident[:], in_=env.ident[:], compare_op=ALU.not_equal, fill=1.0, base=0,
                                    pattern=[[-1, P]], channel_multiplier=1).then_inc(made, 1)


def row_stats(nc, dve, st, step, src, n, mean, var, stats):
    counted = st.sem("counted")
    with dve.Fori(0, n) as t:
        nc.vector.bn_stats(stats[:, bass.ds(t, 1), :].rearrange("p a n -> p (a n)"), tile_of(src, t)).then_inc(counted, 1)
    dve.wait_ge(counted, n)
    merge_stats(nc, step, mean, var, stats, D)


def merge_stats(nc, step, mean, var, stats, width):
    even, odd = stats[:, :, 1], stats[:, :, 4]
    step(nc.vector.tensor_tensor(mean, even, odd, ALU.add))
    step(nc.vector.tensor_tensor(var, even, odd, ALU.subtract))
    step(nc.vector.tensor_scalar(mean, mean, 0.5, None, ALU.mult))
    step(nc.vector.scalar_tensor_tensor(var, var, 0.25, var, ALU.mult, ALU.mult))
    step(nc.vector.scalar_tensor_tensor(var, stats[:, :, 2], 1.0 / width, var, ALU.mult, ALU.add))
    step(nc.vector.scalar_tensor_tensor(var, stats[:, :, 5], 1.0 / width, var, ALU.mult, ALU.add))


def layernorm_stage(nc, env, tag, src, dst_tok=None, dst_T=None):
    with ExitStack() as ctx:
        st = Stage(nc, ctx, tag)
        stats = st.sb("stats", [P, TILES, 6])
        mean, var, rstd = (st.sb(n, [P, TILES]) for n in ("mean", "var", "rstd"))
        turn = st.sb("turn", [P, 2, D])
        turned = st.ps("turned", [P, 2, 512])
        linked, var_ready, std_ready = st.sem("linked"), st.sem("var_ready"), st.sem("std_ready")
        normed, transposed, evacuated = st.sem("normed"), st.sem("transposed"), st.sem("evacuated")
        kept = st.sem("kept")
        both = dst_tok is not None and dst_T is not None
        block = ctx.enter_context(nc.Block())

        @block.vector
        def _(dve):
            step = chain(dve, linked)
            row_stats(nc, dve, st, step, src, TILES, mean[:], var[:], stats)
            nc.vector.tensor_scalar(var[:], var[:], LN_EPS, None, ALU.add).then_inc(var_ready, 1)
            dve.wait_ge(std_ready, 1)
            step(nc.vector.reciprocal(rstd[:], rstd[:]))

            def tile(t, u, reuse):
                if dst_T is not None and reuse:
                    dve.wait_ge(transposed, t - 1)
                if both and reuse:
                    dve.wait_ge(kept, t - 1)
                out = tile_of(dst_tok, t) if dst_T is None else turn[:, u, :]
                nc.vector.tensor_scalar(out, tile_of(src, t), mean[:, bass.ds(t, 1)], rstd[:, bass.ds(t, 1)],
                                        ALU.subtract, ALU.mult).then_inc(normed, 1)

            for u in range(2):
                tile(u, u, False)
            with dve.Fori(1, TILES // 2) as i:
                for u in range(2):
                    tile(2 * i + u, u, True)
            dve.wait_ge(normed, TILES)

        if both:
            @block.gpsimd
            def _(pool):
                with pool.Fori(0, TILES // 2) as i:
                    for u in range(2):
                        pool.wait_ge(normed, 2 * i + (u + 1))
                        nc.gpsimd.tensor_copy(tile_of(dst_tok, 2 * i + u), turn[:, u, :]).then_inc(kept, 1)
                pool.wait_ge(kept, TILES)

        @block.scalar
        def _(act):
            act.wait_ge(var_ready, 1)
            nc.scalar.activation(rstd[:], var[:], ACT.Sqrt).then_inc(std_ready, 1)
            if dst_T is not None:
                with act.Fori(0, TILES // 2) as i:
                    for u in range(2):
                        t = 2 * i + u
                        act.wait_ge(transposed, t + 1)
                        nc.scalar.copy(dst_T[:, :, bass.ds(t * P, P)],
                                       turned[:, u, 0:D].rearrange("p (c t) -> p c t", c=DC)).then_inc(evacuated, 1)
                act.wait_ge(evacuated, TILES)

        if dst_T is not None:
            @block.tensor
            def _(pe):
                def tile(t, u, reuse):
                    pe.wait_ge(normed, t + 1)
                    if reuse:
                        pe.wait_ge(evacuated, t - 1)
                    for c in range(DC):
                        last = nc.tensor.transpose(turned[:, u, c * P:(c + 1) * P], turn[:, u, c * P:(c + 1) * P],
                                                   env.ident[:])
                    last.then_inc(transposed, 1)

                for u in range(2):
                    tile(u, u, False)
                with pe.Fori(1, TILES // 2) as i:
                    for u in range(2):
                        tile(2 * i + u, u, True)


def store_stage(nc, env, out):
    with ExitStack() as ctx:
        st = Stage(nc, ctx, "fin")
        stored = st.sem("stored")
        block = ctx.enter_context(nc.Block())

        @block.sync
        def _(sp):
            sp.dma_start(out.rearrange("b (t p) d -> p (b t) d", p=P), env.x[:]).then_inc(stored, 16)
            sp.wait_ge(stored, 16)


class Env:

    def __init__(self, nc, ctx):
        sb = lambda name, shape, dt=F32: ctx.enter_context(nc.sbuf_tensor(name, shape, dt))
        self.x = sb("x_res", [P, TILES, D])
        self.ctx_tok = sb("ctx_tok", [P, B, D])
        self.ident = sb("ident", [P, P])
        self.ones = sb("ones", [P, P])
        self.eps = sb("eps", [P, 1])
        sems = lambda name, n: [[ctx.enter_context(nc.semaphore(f"{name}{k}_{i}")) for i in range(n)] for k in range(2)]
        self.scattered = sems("rows_scattered", 1)
        self.stored = sems("expert_rows_stored", 2)
        self.gathered = sems("expert_rows_gathered", TILES)



C = 2 * D
CC = C // P
CQ = C // 4
TAPS = 9
KW = H * TAPS


def conv_kernels_stage(nc, env, tag, args, name, kern_dram):
    w = lambda n: args[f"{name}_{n}"]
    with ExitStack() as ctx:
        st = Stage(nc, ctx, tag)
        sb, ps, sem = st.sb, st.ps, st.sem
        hw, w1, w2 = sb("hw", [P, DC, C]), sb("w1", [P, CC, CQ]), sb("w2", [P, 1])
        kw1, kw2 = sb("kw1", [P, CC, D]), sb("kw2", [P, DC, KW])
        hb, hg, hs = (sb(n, [P, C]) for n in ("hb", "hg", "hs"))
        b1, b2 = sb("b1", [P, 1]), sb("b2", [1, 1])
        kb, kg, ks, kb2 = sb("kb", [B, D]), sb("kg", [B, D]), sb("ks", [B, D]), sb("kb2", [B, KW])
        ctxT = sb("ctxT", [P, DC, B * NCTX])
        eh = sb("eh", [P, B, C])
        ehT = sb("ehT", [P, CC, B * NCTX])
        stats, mean, var, rstd = sb("stats", [P, B, 6]), sb("mean", [P, B]), sb("var", [P, B]), sb("rstd", [P, B])
        kstats, kmean, kvar, krstd = (sb(n, s) for n, s in (("kstats", [B, 1, 6]), ("kmean", [B, 1]), ("kvar", [B, 1]), ("krstd", [B, 1])))
        a1 = sb("a1", [P, B * NCTX])
        aw, one = sb("aw", [1, B, NCTX]), sb("one", [1, B])
        awc = sb("awc", [P, B])
        ccT = sb("ccT", [P, CC, B])
        kh = sb("kh", [B, D])
        khT = sb("khT", [P, DC, B])
        kern, kcol = sb("kern", [B, KW]), sb("kcol", [B, H])
        ps_a, ps_b = ps("ps_a", [P, 512]), ps("ps_b", [P, B, 512])
        loaded, on_pe, on_act, linked, ready, stored = (sem(n) for n in ("loaded", "on_pe", "on_act", "linked", "ready", "stored"))
        block = ctx.enter_context(nc.Block())
        tokens = slice(0, NCTX)
        LOADED, HIST, NORMED, SHIFTED, WEIGHTS, WCOL, POOLED, KHID, KNORMED, KVEC, KSHIFTED, KERNELS = range(1, 13)

        @block.sync
        def _(sp):
            mat = lambda n: w(n).rearrange("(c p) n -> p c n", p=P)
            wide = lambda n, rows: w(n).partition_broadcast(rows)
            loads = [(hw, mat("hist_W")), (w1, mat("ctx_W1")), (w2, w("ctx_W2")), (kw1, mat("kg_W1")), (kw2, mat("kg_W2")),
                     (hb, wide("hist_b", P)), (hg, wide("hist_ln_g", P)), (hs, wide("hist_ln_b", P)),
                     (b1, w("ctx_b1").rearrange("(p a) -> p a", a=1)), (b2, w("ctx_b2").rearrange("(p a) -> p a", a=1)),
                     (kb, wide("kg_b1", B)), (kg, wide("kg_ln_g", B)), (ks, wide("kg_ln_b", B)), (kb2, wide("kg_b2", B))]
            for dst, src in loads:
                sp.dma_start(dst[:], src).then_inc(loaded, 16)
            sp.wait_ge(loaded, 16 * len(loads))
            sp.sem_inc(ready, 1)
            sp.wait_ge(ready, KERNELS)
            sp.dma_start(kern_dram, kern[:]).then_inc(stored, 16)
            sp.wait_ge(stored, 16)

        @block.tensor
        def _(pe):
            for b in range(B):
                for c in range(DC):
                    last = nc.tensor.transpose(ps_a[:, (c * B + b) * NCTX:(c * B + b + 1) * NCTX],
                                               env.ctx_tok[tokens, b, c * P:(c + 1) * P], env.ident[tokens, tokens])
            last.then_inc(on_pe, 1)
            pe.wait_ge(on_act, 1)
            pe.wait_ge(ready, LOADED)
            for b in range(B):
                for c in range(DC):
                    last = nc.tensor.matmul(ps_b[tokens, b, :], ctxT[:, c, b * NCTX:(b + 1) * NCTX], hw[:, c, :], start=c == 0,
                                            stop=c == DC - 1)
            last.then_inc(on_pe, 1)
            pe.wait_ge(on_act, 3)
            for b in range(B):
                for c in range(CC):
                    last = nc.tensor.transpose(ps_b[:, b, c * NCTX:(c + 1) * NCTX], eh[tokens, b, c * P:(c + 1) * P],
                                               env.ident[tokens, tokens])
            last.then_inc(on_pe, 1)
            pe.wait_ge(on_act, 5)
            for c in range(CC):
                last = nc.tensor.matmul(ps_a[:, 0:B * NCTX], w1[:, c, :], ehT[:, c, :], start=c == 0, stop=c == CC - 1)
            last.then_inc(on_pe, 1)
            pe.wait_ge(on_act, 6)
            nc.tensor.matmul(ps_a[0:1, 0:B * NCTX], w2[:], a1[:], start=True, stop=True).then_inc(on_pe, 1)
            pe.wait_ge(ready, WEIGHTS)
            for b in range(B):
                last = nc.tensor.matmul(ps_a[tokens, b:b + 1], aw[0:1, b, :], env.ones[0:1, 0:1], start=True, stop=True)
            last.then_inc(on_pe, 1)
            pe.wait_ge(ready, WCOL)
            for c in range(CC):
                for b in range(B):
                    last = nc.tensor.matmul(ps_a[:, c * B + b:c * B + b + 1], eh[tokens, b, c * P:(c + 1) * P], awc[tokens, b:b + 1],
                                            start=True, stop=True)
            last.then_inc(on_pe, 1)
            pe.wait_ge(ready, POOLED)
            for c in range(CC):
                last = nc.tensor.matmul(ps_a[0:B, 0:D], ccT[:, c, :], kw1[:, c, :], start=c == 0, stop=c == CC - 1)
            last.then_inc(on_pe, 1)
            pe.wait_ge(on_act, 9)
            for c in range(DC):
                last = nc.tensor.transpose(ps_a[:, c * B:(c + 1) * B], kh[:, c * P:(c + 1) * P], env.ident[0:B, 0:B])
            last.then_inc(on_pe, 1)
            pe.wait_ge(ready, KVEC)
            for c in range(DC):
                last = nc.tensor.matmul(ps_a[0:B, 0:KW], khT[:, c, :], kw2[:, c, :], start=c == 0, stop=c == DC - 1)
            last.then_inc(on_pe, 1)

        @block.scalar
        def _(act):
            act.wait_ge(on_pe, 1)
            nc.scalar.copy(ctxT[:], ps_a[:, 0:DC * B * NCTX].rearrange("p (c t) -> p c t", c=DC)).then_inc(on_act, 1)
            act.wait_ge(ready, HIST)
            nc.scalar.activation(rstd[tokens], var[tokens], ACT.Sqrt).then_inc(on_act, 1)
            act.wait_ge(ready, NORMED)
            nc.scalar.activation(eh[tokens], eh[tokens], ACT.Gelu).then_inc(on_act, 1)
            act.wait_ge(on_pe, 3)
            for b in range(B):
                nc.scalar.copy(ehT[:, :, b * NCTX:(b + 1) * NCTX],
                               ps_b[:, b, 0:CC * NCTX].rearrange("p (c t) -> p c t", c=CC)).then_inc(on_act, 1)
            act.wait_ge(on_pe, 4)
            nc.scalar.activation(a1[:], ps_a[:, 0:B * NCTX], ACT.Gelu, bias=b1[:, 0:1]).then_inc(on_act, 1)
            act.wait_ge(ready, SHIFTED)
            nc.scalar.activation(aw[:], aw[:], ACT.Exp).then_inc(on_act, 1)
            act.wait_ge(ready, KHID)
            nc.scalar.activation(krstd[:], kvar[:], ACT.Sqrt).then_inc(on_act, 1)
            act.wait_ge(ready, KNORMED)
            nc.scalar.activation(kh[:], kh[:], ACT.Gelu).then_inc(on_act, 1)
            act.wait_ge(ready, KSHIFTED)
            nc.scalar.activation(kern[:], kern[:], ACT.Exp).then_inc(on_act, 1)

        @block.vector
        def _(dve):
            step = chain(dve, linked)
            tt = lambda o, a, b_, op: step(nc.vector.tensor_tensor(o, a, b_, op))

            def finish(ins):
                ins.then_inc(ready, 1)

            dve.wait_ge(ready, LOADED)
            dve.wait_ge(on_pe, 2)
            for b in range(B):
                tt(eh[tokens, b, :], ps_b[tokens, b, :], hb[tokens, :], ALU.add)
            for b in range(B):
                step(nc.vector.bn_stats(stats[tokens, b, :], eh[tokens, b, :]))
            merge_stats(nc, step, mean[tokens], var[tokens], stats[tokens], C)
            finish(nc.vector.tensor_scalar(var[tokens], var[tokens], LN_EPS, None, ALU.add))
            dve.wait_ge(on_act, 2)
            step(nc.vector.reciprocal(rstd[tokens], rstd[tokens]))
            for b in range(B):
                e = eh[tokens, b, :]
                step(nc.vector.tensor_scalar(e, e, mean[tokens, b:b + 1], rstd[tokens, b:b + 1], ALU.subtract, ALU.mult))
                tt(e, e, hg[tokens, :], ALU.mult)
                if b == 0:
                    tt(e, e, hs[tokens, :], ALU.add)
                else:
                    finish(nc.vector.tensor_tensor(e, e, hs[tokens, :], ALU.add))
            dve.wait_ge(on_pe, 5)
            step(nc.vector.tensor_scalar(aw[:].rearrange("p b t -> p (b t)"), ps_a[0:1, 0:B * NCTX], b2[:, 0:1], None, ALU.add))
            step(nc.vector.tensor_reduce(one[:], aw[:], AX_X, ALU.max))
            finish(nc.vector.tensor_tensor(aw[:], aw[:], one[:].unsqueeze(2).to_broadcast([1, B, NCTX]), ALU.subtract))
            dve.wait_ge(on_act, 7)
            step(nc.vector.tensor_reduce(one[:], aw[:], AX_X, ALU.add))
            step(nc.vector.reciprocal(one[:], one[:]))
            finish(nc.vector.tensor_tensor(aw[:], aw[:], one[:].unsqueeze(2).to_broadcast([1, B, NCTX]), ALU.mult))
            dve.wait_ge(on_pe, 6)
            finish(nc.vector.tensor_copy(awc[tokens], ps_a[tokens, 0:B]))
            dve.wait_ge(on_pe, 7)
            finish(nc.vector.tensor_copy(ccT[:].rearrange("p c b -> p (c b)"), ps_a[:, 0:CC * B]))
            dve.wait_ge(on_pe, 8)
            tt(kh[:], ps_a[0:B, 0:D], kb[:], ALU.add)
            step(nc.vector.bn_stats(kstats[:, 0, :], kh[:]))
            merge_stats(nc, step, kmean[:], kvar[:], kstats[:], D)
            finish(nc.vector.tensor_scalar(kvar[:], kvar[:], LN_EPS, None, ALU.add))
            dve.wait_ge(on_act, 8)
            step(nc.vector.reciprocal(krstd[:], krstd[:]))
            step(nc.vector.tensor_scalar(kh[:], kh[:], kmean[:, 0:1], krstd[:, 0:1], ALU.subtract, ALU.mult))
            tt(kh[:], kh[:], kg[:], ALU.mult)
            finish(nc.vector.tensor_tensor(kh[:], kh[:], ks[:], ALU.add))
            dve.wait_ge(on_pe, 9)
            finish(nc.vector.tensor_copy(khT[:].rearrange("p c b -> p (c b)"), ps_a[:, 0:DC * B]))
            dve.wait_ge(on_pe, 10)
            taps = kern[:].rearrange("p (h k) -> p h k", k=TAPS)
            over = kcol[:].unsqueeze(2).to_broadcast([B, H, TAPS])
            tt(kern[:], ps_a[0:B, 0:KW], kb2[:], ALU.add)
            step(nc.vector.tensor_reduce(kcol[:], taps, AX_X, ALU.max))
            finish(nc.vector.tensor_tensor(taps, taps, over, ALU.subtract))
            dve.wait_ge(on_act, 10)
            step(nc.vector.tensor_reduce(kcol[:], taps, AX_X, ALU.add))
            step(nc.vector.reciprocal(kcol[:], kcol[:]))
            finish(nc.vector.tensor_tensor(taps, taps, over, ALU.mult))



TAP = 3
ROWS = P - TAP + 1
WINDOWS = -(-S // ROWS)
PAD = ROWS * WINDOWS + TAP - 1
HEADS = B * H


def conv_attention_stage(nc, env, tag, args, name, kern_dram, mask):
    w = lambda n: args[f"{name}_{n}"]
    dram = lambda n, shape: nc.dram_tensor(f"{tag}_{n}", shape, F32).ap()
    q_dram, k_dram = dram("q", [B, D, PAD]), dram("k", [B, D, PAD])
    mixed_dram = dram("mixed", [B, TAP, D, S])
    with ExitStack() as outer:
        sto = Stage(nc, outer, tag)
        v = sto.sb("v", [P, HEADS, TPB, HD])
        spill = sto.sb("spill", [P, 2, HEADS, TPB])
        other = sto.sb("other", [1, 1], I32)
        with ExitStack() as ctx:
            project_qkv(nc, env, Stage(nc, ctx, tag + "p"), ctx, w, kern_dram, q_dram, k_dram, mixed_dram, v, spill)
        with ExitStack() as ctx:
            compare_mask(nc, env, Stage(nc, ctx, tag + "f"), ctx, mask, other)
        o_tok = sto.sb("o_tok", [P, HEADS, TPB, HD])
        with ExitStack() as ctx:
            st = Stage(nc, ctx, tag + "a")
            banks = st.ps("banks", [P, 8, 512])
            causal = causal_mask(nc, env, st, banks, q_dram, mixed_dram, v, spill, o_tok)
            general = any_mask(nc, env, st, tag, banks, kern_dram, mask, q_dram, k_dram, v, o_tok)
            block = ctx.enter_context(nc.Block())

            def choose(eng, way):
                is_other = eng.value_load(other[0:1, 0:1], min_val=0, max_val=1)
                with eng.If(is_other < 1):
                    causal[way](eng)
                with eng.Else():
                    general[way](eng)

            @block.sync
            def _(sp):
                choose(sp, "sync")

            @block.gpsimd
            def _(pool):
                choose(pool, "gpsimd")

            @block.tensor
            def _(pe):
                choose(pe, "tensor")

            @block.vector
            def _(dve):
                choose(dve, "vector")

            @block.scalar
            def _(act):
                choose(act, "scalar")
        with ExitStack() as ctx:
            project_out(nc, env, Stage(nc, ctx, tag + "o"), ctx, w, o_tok)


def compare_mask(nc, env, st, ctx, mask, other):
    given = st.sb("given", [P, TPB, S], U8)
    after = st.sb("after", [P, TPB, S])
    worst = st.sb("worst", [P, 1])
    sum_ps = st.ps("sum_ps", [P, 512])
    loaded, ones_set, after_made, differs, found, summed, told = (
        st.sem(n) for n in ("loaded", "ones_set", "after_made", "differs", "found", "summed", "told"))
    block = ctx.enter_context(nc.Block())

    @block.sync
    def _(sp):
        sp.dma_start(given[:], mask.rearrange("(t p) j -> p t j", p=P)).then_inc(loaded, 16)
        sp.wait_ge(loaded, 16)

    @block.gpsimd
    def _(pool):
        nc.gpsimd.memset(after[:], 1.0).then_inc(ones_set, 1)
        pool.wait_ge(ones_set, 1)
        nc.gpsimd.affine_select(out=after[:], in_=after[:], compare_op=ALU.is_gt, fill=0.0, base=0,
                                pattern=[[-P, TPB], [1, S]], channel_multiplier=-1).then_inc(after_made, 1)

    @block.vector
    def _(dve):
        dve.wait_ge(loaded, 16)
        dve.wait_ge(after_made, 1)
        nc.vector.tensor_tensor(after[:], given[:], after[:], ALU.not_equal).then_inc(differs, 1)
        dve.wait_ge(differs, 1)
        nc.vector.tensor_reduce(worst[:], after[:].rearrange("p t j -> p (t j)"), AX_X, ALU.max).then_inc(found, 1)
        dve.wait_ge(summed, 1)
        nc.vector.tensor_scalar(other[:], sum_ps[0:1, 0:1], 1.0, None, ALU.min).then_inc(told, 1)
        dve.wait_ge(told, 1)

    @block.tensor
    def _(pe):
        pe.wait_ge(found, 1)
        nc.tensor.matmul(sum_ps[0:1, 0:1], worst[:], env.ones[:, 0:1], start=True, stop=True).then_inc(summed, 1)


def project_qkv(nc, env, st, ctx, w, kern_dram, q_dram, k_dram, mixed_dram, v, spill):
    xT = st.sb("xT", [P, DC, T])
    layernorm_stage(nc, env, st.tag + "l", env.x, dst_T=xT)
    wq, wk, wv = (st.sb(n, [P, DC, D]) for n in ("wq", "wk", "wv"))
    qk = st.sb("qk", [P, 2, B, DC, PAD])
    half = H // DC
    coef = st.sb("coef", [P, B, DC, TAP * TAP])
    ind = st.sb("ind", [P, half])
    mix = st.sb("mix", [P, 2, S])
    near, diag, before = (st.sb(n, [P, S]) for n in ("near", "diag", "before"))
    y_ps, v_ps, d_ps = st.ps("y_ps", [P, 4, 512]), st.ps("v_ps", [P, 2, 512]), st.ps("d_ps", [P, 512])
    loaded, zeroed, y_done, y_evac, v_done, v_evac, stored, coef_loaded, ones_set, ind_lower, ind_made = (
        st.sem(n) for n in ("loaded", "zeroed", "y_done", "y_evac", "v_done", "v_evac", "stored", "coef_loaded", "ones_set",
                            "ind_lower", "ind_made"))
    begun, mixed, mix_parts, crossed, spills, spill_done, spill_evac = (
        st.sem(n) for n in ("begun", "mixed", "mix_parts", "crossed", "spills", "spill_done", "spill_evac"))
    mix_stored = [st.sem(f"mix_stored{u}") for u in range(2)]
    parts = [(b, c) for b in range(B) for c in range(DC)]
    mixes = [(b, c, a) for b, c in parts for a in range(TAP)]
    block = ctx.enter_context(nc.Block())
    HALF = S // 512
    jobs = [(k, b, c, n) for k in range(2) for b in range(B) for c in range(DC) for n in range(HALF)]

    @block.sync
    def _(sp):
        for dst, src in ((wq, "Wq"), (wk, "Wk"), (wv, "Wv")):
            sp.dma_start(dst[:], w(src).rearrange("(c p) n -> p c n", p=P)).then_inc(loaded, 16)
        kern = kern_dram.rearrange("b (c h k) -> h b c k", c=DC, h=half)
        for h in range(half):
            for b in range(B):
                sp.dma_start(coef[h * HD:(h + 1) * HD, b], kern[h, b].partition_broadcast(HD)).then_inc(coef_loaded, 16)
        sp.wait_ge(zeroed, 2)
        for k, dram in enumerate((q_dram, k_dram)):
            sp.wait_ge(y_evac, (k + 1) * len(jobs) // 2)
            sp.dma_start(dram.rearrange("b (c p) t -> p b c t", p=P), qk[:, k]).then_inc(stored, 16)
        for i, (b, c, a) in enumerate(mixes):
            sp.wait_ge(mixed, i + 1)
            sp.dma_start(mixed_dram[b, a, c * P:(c + 1) * P, :], mix[:, i % 2, :]).then_inc(mix_stored[i % 2], 16)
        for u in range(2):
            sp.wait_ge(mix_stored[u], 8 * len(mixes))
        sp.wait_ge(stored, 32)

    @block.gpsimd
    def _(pool):
        nc.gpsimd.memset(qk[:, :, :, :, 0:1], 0.0).then_inc(zeroed, 1)
        nc.gpsimd.memset(qk[:, :, :, :, S + 1:PAD], 0.0).then_inc(zeroed, 1)
        nc.gpsimd.memset(ind[:], 1.0).then_inc(ones_set, 1)
        pool.wait_ge(ones_set, 1)
        nc.gpsimd.affine_select(out=ind[:], in_=ind[:], compare_op=ALU.is_ge, fill=0.0, base=0,
                                pattern=[[-HD, half]], channel_multiplier=1).then_inc(ind_lower, 1)
        pool.wait_ge(ind_lower, 1)
        nc.gpsimd.affine_select(out=ind[:], in_=ind[:], compare_op=ALU.is_ge, fill=0.0, base=HD - 1,
                                pattern=[[HD, half]], channel_multiplier=-1).then_inc(ind_made, 1)

    @block.tensor
    def _(pe):
        pe.wait_ge(loaded, 48)
        for i, (k, b, c, n) in enumerate(jobs):
            if i >= 4:
                pe.wait_ge(y_evac, i - 3)
            for d in range(DC):
                last = nc.tensor.matmul(y_ps[:, i % 4, :], (wq, wk)[k][:, d, c * P:(c + 1) * P],
                                        xT[:, d, b * S + n * 512:b * S + (n + 1) * 512], start=d == 0, stop=d == DC - 1)
            last.then_inc(y_done, 1)
        for t in range(TILES):
            if t >= 2:
                pe.wait_ge(v_evac, t - 1)
            for d in range(DC):
                last = nc.tensor.matmul(v_ps[:, t % 2, 0:D], xT[:, d, t * P:(t + 1) * P], wv[:, d, :], start=d == 0,
                                        stop=d == DC - 1)
            last.then_inc(v_done, 1)
        pe.wait_ge(ind_made, 1)
        for i, (b, c) in enumerate(parts):
            pe.wait_ge(spills, 2 * i + 2)
            for k, feats in enumerate((diag, before)):
                for n in range(TPB):
                    at = ((k * B * DC + i) * TPB + n) * half
                    last = nc.tensor.matmul(d_ps[:, at:at + half], feats[:, n * P:(n + 1) * P], ind[:], start=True, stop=True)
            last.then_inc(spill_done, 1)

    @block.scalar
    def _(act):
        for i, (k, b, c, n) in enumerate(jobs):
            act.wait_ge(y_done, i + 1)
            nc.scalar.mul(qk[:, k, b, c, 1 + n * 512:1 + (n + 1) * 512], y_ps[:, i % 4, :],
                          HD ** -0.5 if k == 0 else 1.0).then_inc(y_evac, 1)
        act.wait_ge(y_evac, len(jobs))
        act.wait_ge(coef_loaded, 16 * half * B)
        act.wait_ge(zeroed, 2)
        for i, (b, c, a) in enumerate(mixes):
            if i >= 2:
                act.wait_ge(mix_stored[i % 2], 16 * (i // 2))
            nc.scalar.activation(mix[:, i % 2, :], qk[:, 1, b, c, 0:S], ACT.Identity,
                                 scale=coef[:, b, c, a * TAP:a * TAP + 1]).then_inc(begun, 1)

    @block.vector
    def _(dve):
        for t in range(TILES):
            dve.wait_ge(v_done, t + 1)
            b, n = divmod(t, TPB)
            nc.vector.tensor_copy(v[:, b * H:(b + 1) * H, n, :],
                                  v_ps[:, t % 2, 0:D].rearrange("p (h d) -> p h d", h=H)).then_inc(v_evac, 1)
        dve.wait_ge(y_evac, len(jobs))
        dve.wait_ge(coef_loaded, 16 * half * B)
        dve.wait_ge(zeroed, 2)
        for i, (b, c, a) in enumerate(mixes):
            row, keys = mix[:, i % 2, :], qk[:, 1, b, c]
            dve.wait_ge(begun, i + 1)
            nc.vector.scalar_tensor_tensor(row, keys[:, 1:S + 1], coef[:, b, c, a * TAP + 1:a * TAP + 2], row, ALU.mult,
                                           ALU.add).then_inc(mix_parts, 1)
            dve.wait_ge(mix_parts, i + 1)
            nc.vector.scalar_tensor_tensor(row, keys[:, 2:S + 2], coef[:, b, c, a * TAP + 2:a * TAP + 3], row, ALU.mult,
                                           ALU.add).then_inc(mixed, 1)
        step = chain(dve, crossed)
        for i, (b, c) in enumerate(parts):
            q, k, tap = qk[:, 0, b, c], qk[:, 1, b, c], lambda n: coef[:, b, c, n:n + 1]
            if i:
                dve.wait_ge(spill_done, i)
            step(nc.vector.tensor_tensor(near[:], q[:, 0:S], k[:, 1:S + 1], ALU.mult))
            step(nc.vector.tensor_scalar(diag[:], q[:, 0:S], tap(2), None, ALU.mult))
            step(nc.vector.scalar_tensor_tensor(diag[:], q[:, 1:S + 1], tap(TAP + 2), diag[:], ALU.mult, ALU.add))
            step(nc.vector.tensor_tensor(diag[:], diag[:], k[:, 2:S + 2], ALU.mult))
            nc.vector.scalar_tensor_tensor(diag[:], near[:], tap(1), diag[:], ALU.mult, ALU.add).then_inc(spills, 1)
            nc.vector.tensor_scalar(before[:], near[:], tap(2), None, ALU.mult).then_inc(spills, 1)
        dve.wait_ge(spill_done, len(parts))
        for k in range(2):
            for i in range(len(parts)):
                at = (k * len(parts) + i) * TPB * half
                nc.vector.tensor_copy(spill[:, k, i * half:(i + 1) * half, :].rearrange("p h t -> p t h"),
                                      d_ps[:, at:at + TPB * half].rearrange("p (t h) -> p t h", t=TPB)).then_inc(spill_evac, 1)
        dve.wait_ge(spill_evac, 2 * len(parts))


def causal_mask(nc, env, st, banks, q_dram, mixed_dram, v, spill, o_tok):
    sb, sem = lambda n, *a: st.sb("tri_" + n, *a), lambda n: st.sem("tri_" + n)
    FEATS = TAP * HD
    PAIRS_IN = 2
    ROUNDS = HEADS // (2 * PAIRS_IN)
    order = [(2 * r + u, (TPB - 1 - m, m)[u]) for r in range(PAIRS_IN) for m in range(TPB) for u in range(2)]
    STEPS = len(order)
    groups = [[range(a, min(a + 4, n + 1)) for a in range(0, n + 1, 4)] for _, n in order]
    first = [sum(len(g) for g in groups[:k]) for k in range(STEPS + 1)]
    GROUPS = first[-1]
    AHEAD = 2
    WIN = P + 1
    qs, ks = sb("qs", [FEATS, 2 * PAIRS_IN, S]), sb("ks", [FEATS, 2 * PAIRS_IN, S])
    own, prev, later = sb("own", [P, WIN]), sb("prev", [P, WIN]), sb("later", [P, WIN])
    off = sb("off", [P, 2 * PAIRS_IN, 2, TPB])
    edge, part = sb("edge", [P, 2, WIN]), sb("part", [P, WIN])
    pr = sb("pr", [P, 2, S])
    pT = sb("pT", [P, 2, S])
    ntop, total, inv = (sb(n, [P, 2]) for n in ("ntop", "total", "inv"))
    s_ps = lambda k: banks[:, 2 * (k % 2):2 * (k % 2) + 2, :].rearrange("p a n -> p (a n)")
    t_ps = lambda g: banks[:, 4 + g % 2, :]
    o_ps = lambda k: banks[:, 6 + k % 2, 0:HD]
    staged = [sem(f"staged{r}") for r in range(PAIRS_IN)]
    t_evac = [sem(f"t_evac{u}") for u in range(2)]
    shapes_zero, shapes, off_ready, edge_part, edge_made, scored, edged, top_ready, exped = (
        sem(n) for n in ("shapes_zero", "shapes", "off_ready", "edge_part", "edge_made", "scored", "edged", "top_ready", "exped"))
    turned, inv_ready, o_done, o_evac, tables = (sem(n) for n in ("turned", "inv_ready", "o_done", "o_evac", "tables"))

    def rounds(eng, body):
        with eng.Fori(0, ROUNDS - 1) as i:
            body(i, False)
        body(ROUNDS - 1, True)

    def on_sync(sp):
        q = q_dram.rearrange("b (h f) t -> (b h) f t", h=H)
        m = mixed_dram.rearrange("b a (h f) t -> a b h f t", h=H)
        per_batch = ROUNDS // B

        def stage(b, i, r):
            for u in range(2 * r, 2 * r + 2):
                h = (i - b * per_batch) * (2 * PAIRS_IN) + u
                for a in range(TAP):
                    rows = slice(a * HD, (a + 1) * HD)
                    sp.dma_start(qs[rows, u, :], q[bass.ds(h + b * H, 1), :, a:a + S].rearrange("x f t -> (x f) t")).then_inc(staged[r], 16)
                    sp.dma_start(ks[rows, u, :], m[a, b, bass.ds(h, 1)].rearrange("x f t -> (x f) t")).then_inc(staged[r], 16)

        for r in range(PAIRS_IN):
            stage(0, 0, r)
        for b in range(B):
            with sp.Fori(max(1, b * per_batch), (b + 1) * per_batch) as i:
                for r in range(PAIRS_IN):
                    sp.wait_ge(scored, STEPS * i + (STEPS // PAIRS_IN * (r + 1) - STEPS))
                    stage(b, i, r)

    def on_gpsimd(pool):
        nc.gpsimd.memset(own[:], 0.0).then_inc(shapes_zero, 1)
        nc.gpsimd.memset(prev[:], 0.0).then_inc(shapes_zero, 1)
        nc.gpsimd.memset(later[:], 0.0).then_inc(shapes_zero, 1)
        pool.wait_ge(shapes_zero, 3)
        nc.gpsimd.affine_select(out=own[:], in_=own[:], compare_op=ALU.not_equal, fill=-1.0, base=1, pattern=[[-1, WIN]],
                                channel_multiplier=1).then_inc(shapes, 1)
        nc.gpsimd.affine_select(out=prev[:], in_=prev[:], compare_op=ALU.not_equal, fill=-1.0, base=0, pattern=[[-1, WIN]],
                                channel_multiplier=1).then_inc(shapes, 1)
        nc.gpsimd.affine_select(out=later[:], in_=later[:], compare_op=ALU.is_ge, fill=NEG, base=1, pattern=[[-1, WIN]],
                                channel_multiplier=1).then_inc(shapes, 1)
        pool.wait_ge(shapes, 3)

        def body(i, last):
            pool.wait_ge(edge_made, STEPS * i)
            for u in range(2 * PAIRS_IN):
                head = bass.ds(i * (2 * PAIRS_IN) + u, 1)
                nc.gpsimd.tensor_copy(off[:, u], spill[:, :, head, :].rearrange("p k a t -> p k (a t)")).then_inc(off_ready, 1)
            pool.wait_ge(off_ready, 2 * PAIRS_IN * i + 2 * PAIRS_IN)
            for k, (u, n) in enumerate(order):
                s = STEPS * i + k
                win = edge[:, k % 2, :]
                pool.wait_ge(edge_made, s)
                pool.wait_ge(edged, s + 1)
                nc.gpsimd.tensor_tensor(win, own[:], off[:, u, 0, n:n + 1].to_broadcast([P, WIN]), ALU.mult).then_inc(edge_part, 1)
                nc.gpsimd.tensor_tensor(part[:], prev[:], off[:, u, 1, n:n + 1].to_broadcast([P, WIN]), ALU.mult).then_inc(edge_part, 1)
                pool.wait_ge(edge_part, 3 * s + 2)
                nc.gpsimd.tensor_tensor(win, win, part[:], ALU.add).then_inc(edge_part, 1)
                pool.wait_ge(edge_part, 3 * s + 3)
                nc.gpsimd.tensor_tensor(win, win, later[:], ALU.add).then_inc(edge_made, 1)

        rounds(pool, body)

    def on_tensor(pe):
        def score(i, k):
            u, n = order[k % STEPS]
            if k % STEPS % (STEPS // PAIRS_IN) == 0:
                r = u // 2
                pe.wait_ge(staged[r], (i + k // STEPS) * (16 * 4 * TAP) + 16 * 4 * TAP)
            pe.wait_ge(exped, STEPS * i + (k + 1))
            keys = (n + 1) * P
            for a in range(0, keys, 512):
                z = min(a + 512, keys)
                last = nc.tensor.matmul(s_ps(k)[:, a:z], qs[:, u, n * P:(n + 1) * P], ks[:, u, a:z], start=True, stop=True)
            last.then_inc(scored, 1)

        def turn(i, k):
            pe.wait_ge(exped, STEPS * i + (k + 1 + AHEAD))
            for g, tiles in enumerate(groups[k]):
                at = first[k] + g
                pe.wait_ge(t_evac[at % 2], GROUPS // 2 * i + at // 2)
                for j in tiles:
                    last = nc.tensor.transpose(t_ps(at)[:, (j - tiles[0]) * P:(j - tiles[0] + 1) * P], pr[:, k % 2, j * P:(j + 1) * P],
                                               env.ident[:])
                last.then_inc(turned, 1)

        def weigh(i, k):
            u, n = order[k]
            for at in range(first[k], first[k + 1]):
                pe.wait_ge(t_evac[at % 2], GROUPS // 2 * i + (at // 2 + 1))
            pe.wait_ge(o_evac, STEPS * i + (k + 1))
            head = bass.ds(i * (2 * PAIRS_IN) + u, 1)
            for j in range(n + 1):
                last = nc.tensor.matmul(o_ps(k), pT[:, k % 2, j * P:(j + 1) * P], v[:, head, j, :].rearrange("p a d -> p (a d)"),
                                        start=j == 0, stop=j == n)
            last.then_inc(o_done, 1)

        pe.sem_inc(turned, AHEAD)
        pe.sem_inc(o_done, AHEAD)
        score(0, 0)

        def body(i, last):
            for k in range(STEPS):
                if k + 1 < STEPS or not last:
                    score(i, k + 1)
                turn(i, k)
                if k:
                    weigh(i, k - 1)
            weigh(i, STEPS - 1)

        rounds(pe, body)

    def copy_turned(eng, copy, i, k, which):
        for g, tiles in enumerate(groups[k]):
            at = first[k] + g
            if at % 2 == which:
                eng.wait_ge(turned, GROUPS * i + (at + 1 + AHEAD))
                eng.wait_ge(o_done, STEPS * i + (k + 1))
                n = len(tiles) * P
                copy(pT[:, k % 2, tiles[0] * P:tiles[0] * P + n], t_ps(at)[:, 0:n]).then_inc(t_evac[which], 1)

    def on_vector(dve):
        def top(i, k):
            u, n = order[k % STEPS]
            s = STEPS * i + k
            dve.wait_ge(scored, s + 1)
            dve.wait_ge(edge_made, s + 1)
            skip = 1 if n == 0 else 0
            win = s_ps(k)[:, n * P - 1 + skip:(n + 1) * P]
            nc.vector.tensor_tensor(win, win, edge[:, k % 2, skip:], ALU.add).then_inc(edged, 1)
            dve.wait_ge(edged, s + 1 + AHEAD)
            nc.vector.tensor_reduce(ntop[:, k % 2:k % 2 + 1], s_ps(k)[:, 0:(n + 1) * P], AX_X, ALU.max, negate=True).then_inc(top_ready, 1)

        def norm(i, k):
            u, n = order[k]
            s = STEPS * i + k
            dve.wait_ge(o_done, s + 1 + AHEAD)
            dve.wait_ge(inv_ready, s + 1 + AHEAD)
            head = bass.ds(i * (2 * PAIRS_IN) + u, 1)
            nc.vector.tensor_scalar(o_tok[:, head, n, :].rearrange("p a d -> p (a d)"), o_ps(k), inv[:, k % 2:k % 2 + 1], None,
                                    ALU.mult).then_inc(o_evac, 1)

        dve.sem_inc(edged, AHEAD)
        dve.sem_inc(o_evac, AHEAD)
        dve.sem_inc(inv_ready, AHEAD)
        top(0, 0)

        def body(i, last):
            for k in range(STEPS):
                if k + 1 < STEPS or not last:
                    top(i, k + 1)
                copy_turned(dve, nc.vector.tensor_copy, i, k, 1)
                dve.wait_ge(exped, STEPS * i + (k + 1 + AHEAD))
                dve.wait_ge(o_evac, STEPS * i + (k + 1))
                nc.vector.reciprocal(inv[:, k % 2:k % 2 + 1], total[:, k % 2:k % 2 + 1]).then_inc(inv_ready, 1)
                if k:
                    norm(i, k - 1)
            norm(i, STEPS - 1)

        rounds(dve, body)
        dve.wait_ge(o_evac, STEPS * ROUNDS + AHEAD)

    def on_scalar(act):
        nc.scalar.activation(total[:, 0:1], env.eps[:], ACT.Exp).then_inc(tables, 1)
        act.wait_ge(tables, 1)

        def soften(i, k):
            u, n = order[k % STEPS]
            s = STEPS * i + k
            act.wait_ge(top_ready, s + 1)
            act.wait_ge(turned, GROUPS * i + (first[k - 1] + AHEAD if k else AHEAD - len(groups[STEPS - 1])))
            act.wait_ge(inv_ready, s + 1)
            nc.scalar.activation(pr[:, k % 2, 0:(n + 1) * P], s_ps(k)[:, 0:(n + 1) * P], ACT.Exp, bias=ntop[:, k % 2:k % 2 + 1],
                                 accum_out=total[:, k % 2:k % 2 + 1]).then_inc(exped, 1)

        act.sem_inc(exped, AHEAD)
        soften(0, 0)

        def body(i, last):
            for k in range(STEPS):
                if k + 1 < STEPS or not last:
                    soften(i, k + 1)
                copy_turned(act, nc.scalar.copy, i, k, 0)

        rounds(act, body)

    return dict(sync=on_sync, gpsimd=on_gpsimd, tensor=on_tensor, vector=on_vector, scalar=on_scalar)


def any_mask(nc, env, st, tag, banks, kern_dram, mask, q_dram, k_dram, v, o_tok):
    o_dram = nc.dram_tensor(f"{tag}_o", [HEADS, ROWS * WINDOWS, HD], F32).ap()
    sb, sem = lambda n, *a: st.sb("any_" + n, *a), lambda n: st.sem("any_" + n)
    seen, gone = sb("seen", [P, WINDOWS, S], U8), sb("gone", [P, WINDOWS, S], U8)
    kern = sb("kern", [P, HEADS, TAP * TAP])
    tap = sb("tap", [P, TAP * TAP])
    down = sb("down", [P, TAP, P])
    band = sb("band", [P, TAP, P])
    qh, kh = sb("qh", [HD, PAD]), sb("kh", [HD, PAD])
    sm = sb("sm", [P, S + 2])
    z = sb("z", [P, S])
    pT = sb("pT", [P, TPB, P])
    ntop, total, inv = sb("ntop", [P, 1]), sb("total", [P, 1]), sb("inv", [P, 1])
    o = sb("o", [P, HD])
    s_ps, z_ps, t_ps = (banks[:, i:i + 2, :].rearrange("p a n -> p (a n)") for i in (0, 2, 4))
    o_ps = banks[:, 6, :]
    mask_zero, mask_loaded, kern_loaded, mask_ready, down_made, staged, stored, gathered = (
        sem(n) for n in ("mask_zero", "mask_loaded", "kern_loaded", "mask_ready", "down_made", "staged", "stored",
                         "gathered"))
    band_ready, scored, masked, summed, top_ready, exped, turned, t_evac, o_done, o_ready, padded, tables, taken, banded, band_parts, hidden, inv_ready = (
        sem(n) for n in ("band_ready", "scored", "masked", "summed", "top_ready", "exped", "turned", "t_evac", "o_done",
                         "o_ready", "padded", "tables", "taken", "banded", "band_parts", "hidden", "inv_ready"))

    def on_sync(sp):
        sp.wait_ge(mask_zero, 2)
        m = mask
        loads = []
        for i in range(WINDOWS):
            first, last = max(0, i * ROWS - 1), min(S, i * ROWS - 1 + P)
            loads.append((seen, first - (i * ROWS - 1), i, first, last))
            loads.append((gone, 0, i, i * ROWS, min(S, (i + 1) * ROWS)))
        for dst, at, i, first, last in loads:
            sp.dma_start(dst[at:at + last - first, i, :], m[first:last, :]).then_inc(mask_loaded, 16)
        sp.dma_start(kern[:], kern_dram.rearrange("b (h k) -> (b h) k", h=H).partition_broadcast(P)).then_inc(kern_loaded, 16)
        q_rows, k_rows = (d.rearrange("b (h f) t -> (b h) f t", h=H) for d in (q_dram, k_dram))

        def stage(g):
            sp.dma_start(qh[:], q_rows[bass.ds(g, 1)].rearrange("a f t -> (a f) t")).then_inc(staged, 16)
            sp.dma_start(kh[:], k_rows[bass.ds(g, 1)].rearrange("a f t -> (a f) t")).then_inc(staged, 16)

        with sp.Fori(0, HEADS) as g:
            sp.wait_ge(scored, WINDOWS * g)
            stage(g)
            for i in range(WINDOWS):
                sp.wait_ge(o_ready, WINDOWS * g + (i + 1))
                sp.dma_start(o_dram[bass.ds(g, 1), i * ROWS:(i + 1) * ROWS, :].rearrange("a t d -> (a t) d"),
                             o[0:ROWS]).then_inc(stored, 16)
        sp.wait_ge(stored, 16 * WINDOWS * HEADS)
        for n in range(TPB):
            sp.dma_start(o_tok[:, :, n, :], o_dram[:, n * P:(n + 1) * P, :].rearrange("g p d -> p g d")).then_inc(gathered, 16)
        sp.wait_ge(gathered, 16 * TPB)

    def on_gpsimd(pool):
        nc.gpsimd.memset(seen[:], 0.0).then_inc(mask_zero, 1)
        nc.gpsimd.memset(gone[:], 0.0).then_inc(mask_zero, 1)
        nc.gpsimd.memset(sm[:], 0.0).then_inc(padded, 1)
        nc.gpsimd.memset(down[:], 0.0).then_inc(padded, 1)
        pool.wait_ge(padded, 2)
        for a in range(TAP):
            nc.gpsimd.affine_select(out=down[:, a, :], in_=down[:, a, :], compare_op=ALU.not_equal, fill=1.0, base=-a,
                                    pattern=[[-1, P]], channel_multiplier=1).then_inc(down_made, 1)

    def on_tensor(pe):
        with pe.Fori(0, HEADS) as g:
            pe.wait_ge(staged, 32 * g + 32)
            for i in range(WINDOWS):
                s = WINDOWS * g + i
                pe.wait_ge(masked, s)
                for n in range(S // 512):
                    last = nc.tensor.matmul(s_ps[:, n * 512:(n + 1) * 512], qh[:, i * ROWS:i * ROWS + P],
                                            kh[:, 1 + n * 512:1 + (n + 1) * 512], start=True, stop=True)
                last.then_inc(scored, 1)
                if i == 0:
                    pe.wait_ge(band_ready, g + 1)
                pe.wait_ge(masked, s + 1)
                for n in range(S // 512):
                    for c in range(TAP):
                        last = nc.tensor.matmul(z_ps[:, n * 512:(n + 1) * 512], band[:, c, :], sm[:, c + n * 512:c + (n + 1) * 512],
                                                start=c == 0, stop=c == TAP - 1)
                last.then_inc(summed, 1)
                pe.wait_ge(exped, s + 1)
                for j in range(TPB):
                    last = nc.tensor.transpose(t_ps[:, j * P:(j + 1) * P], z[:, j * P:(j + 1) * P], env.ident[:])
                last.then_inc(turned, 1)
                pe.wait_ge(t_evac, s + 1)
                for j in range(TPB):
                    last = nc.tensor.matmul(o_ps[:, 0:HD], pT[:, j, :],
                                            v[:, bass.ds(g, 1), j, :].rearrange("p a d -> p (a d)"), start=j == 0, stop=j == TPB - 1)
                last.then_inc(o_done, 1)

    def on_vector(dve):
        dve.wait_ge(mask_loaded, 32 * WINDOWS)
        nc.vector.tensor_scalar(seen[:], seen[:], 0.0, None, ALU.is_equal).then_inc(mask_ready, 1)
        dve.wait_ge(mask_ready, 1)
        dve.wait_ge(kern_loaded, 16)
        dve.wait_ge(down_made, TAP)

        with dve.Fori(0, HEADS) as g:
            nc.vector.tensor_copy(tap[:], kern[:, bass.ds(g, 1), :].rearrange("p a k -> p (a k)")).then_inc(taken, 1)
            dve.wait_ge(taken, g + 1)
            dve.wait_ge(summed, WINDOWS * g)
            for c in range(TAP):
                for a in range(TAP):
                    weight = tap[:, a * TAP + c:a * TAP + c + 1]
                    if a == 0:
                        ins = nc.vector.tensor_scalar(band[:, c, :], down[:, a, :], weight, None, ALU.mult)
                    else:
                        dve.wait_ge(banded, 6 * g + (2 * c + a))
                        ins = nc.vector.scalar_tensor_tensor(band[:, c, :], down[:, a, :], weight, band[:, c, :], ALU.mult, ALU.add)
                    if a < TAP - 1:
                        ins.then_inc(banded, 1)
                    elif c < TAP - 1:
                        ins.then_inc(band_parts, 1)
                    else:
                        dve.wait_ge(band_parts, (TAP - 1) * (g + 1))
                        ins.then_inc(band_ready, 1)
            for i in range(WINDOWS):
                s = WINDOWS * g + i
                dve.wait_ge(scored, s + 1)
                dve.wait_ge(summed, s)
                nc.vector.tensor_tensor(sm[:, 1:S + 1], s_ps, seen[:, i, :], ALU.mult).then_inc(masked, 1)
                dve.wait_ge(summed, s + 1)
                dve.wait_ge(turned, s)
                nc.vector.scalar_tensor_tensor(z[:], gone[:, i, :], NEG, z_ps, ALU.mult, ALU.add).then_inc(hidden, 1)
                dve.wait_ge(hidden, s + 1)
                nc.vector.tensor_reduce(ntop[:], z[:], AX_X, ALU.max, negate=True).then_inc(top_ready, 1)
                dve.wait_ge(exped, s + 1)
                nc.vector.reciprocal(inv[:], total[:]).then_inc(inv_ready, 1)
                dve.wait_ge(inv_ready, s + 1)
                dve.wait_ge(o_done, s + 1)
                dve.wait_ge(stored, 16 * s)
                nc.vector.tensor_scalar(o[:], o_ps[:, 0:HD], inv[:, 0:1], None, ALU.mult).then_inc(o_ready, 1)

    def on_scalar(act):
        nc.scalar.activation(total[:], env.eps[:], ACT.Exp).then_inc(tables, 1)
        act.wait_ge(tables, 1)
        with act.Fori(0, HEADS) as g:
            for i in range(WINDOWS):
                s = WINDOWS * g + i
                act.wait_ge(top_ready, s + 1)
                nc.scalar.activation(z[:], z[:], ACT.Exp, bias=ntop[:, 0:1], accum_out=total[:]).then_inc(exped, 1)
                act.wait_ge(turned, s + 1)
                act.wait_ge(o_done, s)
                nc.scalar.copy(pT[:].rearrange("p j t -> p (j t)"), t_ps).then_inc(t_evac, 1)

    return dict(sync=on_sync, gpsimd=on_gpsimd, tensor=on_tensor, vector=on_vector, scalar=on_scalar)


def project_out(nc, env, st, ctx, w, o_tok):
    wo, bo = st.sb("wo", [P, DC, D]), st.sb("bo", [1, D])
    row = st.sb("row", [P, 2, D])
    oT = st.sb("oT", [P, 2, DC, P])
    t_ps, y_ps = st.ps("t_ps", [P, 2, 512]), st.ps("y_ps", [P, 2, 512])
    loaded, lined, turned, evacuated, y_done, added = (
        st.sem(n) for n in ("loaded", "lined", "turned", "evacuated", "y_done", "added"))
    block = ctx.enter_context(nc.Block())

    @block.sync
    def _(sp):
        sp.dma_start(wo[:], w("proj_W").rearrange("(c p) n -> p c n", p=P)).then_inc(loaded, 16)
        sp.dma_start(bo[:], w("proj_b").rearrange("(a n) -> a n", a=1)).then_inc(loaded, 16)

    @block.gpsimd
    def _(pool):
        for t in range(TILES):
            b, n = divmod(t, TPB)
            if t >= 2:
                pool.wait_ge(turned, t - 1)
            nc.gpsimd.tensor_copy(row[:, t % 2, :].rearrange("p (h d) -> p h d", h=H),
                                  o_tok[:, b * H:(b + 1) * H, n, :]).then_inc(lined, 1)

    @block.tensor
    def _(pe):
        def turn(t):
            pe.wait_ge(lined, t + 1)
            if t >= 2:
                pe.wait_ge(evacuated, t - 1)
            for c in range(DC):
                last = nc.tensor.transpose(t_ps[:, t % 2, c * P:(c + 1) * P], row[:, t % 2, c * P:(c + 1) * P], env.ident[:])
            last.then_inc(turned, 1)

        turn(0)
        pe.wait_ge(loaded, 32)
        for t in range(TILES):
            if t + 1 < TILES:
                turn(t + 1)
            pe.wait_ge(evacuated, t + 1)
            if t >= 2:
                pe.wait_ge(added, t - 1)
            nc.tensor.matmul(y_ps[:, t % 2, 0:D], env.ones[0:1, :], bo[:], start=True, stop=False)
            for c in range(DC):
                last = nc.tensor.matmul(y_ps[:, t % 2, 0:D], oT[:, t % 2, c, :], wo[:, c, :], start=False, stop=c == DC - 1)
            last.then_inc(y_done, 1)

    @block.scalar
    def _(act):
        for t in range(TILES):
            act.wait_ge(turned, t + 1)
            if t >= 2:
                act.wait_ge(y_done, t - 1)
            nc.scalar.copy(oT[:, t % 2], t_ps[:, t % 2, 0:D].rearrange("p (c t) -> p c t", c=DC)).then_inc(evacuated, 1)

    @block.vector
    def _(dve):
        for t in range(TILES):
            dve.wait_ge(y_done, t + 1)
            nc.vector.tensor_tensor(env.x[:, t, :], env.x[:, t, :], y_ps[:, t % 2, 0:D], ALU.add).then_inc(added, 1)



I = 768
IC = I // P
BLOCK = 32
QA = 32767.0
QW = 7.0
FLOOR = 1e-12
ROUND = 12582912.0
U16 = 65536.0
CHUNKS = T // 512


def quant_ffn_stage(nc, env, tag, args, name):
    w = lambda n: args[f"{name}_{n}"]
    with ExitStack() as ctx:
        st = Stage(nc, ctx, tag)
        xnT = st.sb("xnT", [P, DC, T])
        wT = st.sb("wT", [P, 2, DC, I])
        wdT = st.sb("wdT", [P, IC, D])
        layernorm_stage(nc, env, tag + "l", env.x, dst_T=xnT)
        with ExitStack() as inner:
            quant_weights(nc, env, Stage(nc, inner, tag + "w"), inner, w, wT, wdT)
        with ExitStack() as inner:
            quant_unit(nc, env, Stage(nc, inner, tag + "u"), inner, xnT, wT, wdT)


def quant_weights(nc, env, st, ctx, w, wT, wdT):
    NB = 3 * I * D // P // BLOCK
    raw = st.sb("raw", [P, 3 * I * D // P])
    scale, inv = st.sb("scale", [P, NB]), st.sb("inv", [P, NB])
    t_ps = st.ps("t_ps", [P, 2, 512])
    loaded, linked, ready, turned, evacuated = (st.sem(n) for n in ("loaded", "linked", "ready", "turned", "evacuated"))
    block = ctx.enter_context(nc.Block())
    part = lambda k: raw[:, k * IC * D:(k + 1) * IC * D]
    blocks = raw[:].rearrange("p (b i) -> p b i", i=BLOCK)
    over = lambda buf: buf[:].unsqueeze(2).to_broadcast([P, NB, BLOCK])
    pieces = []
    for k in range(2):
        rows = part(k).rearrange("p (o i) -> p o i", o=IC)
        for c in range(DC):
            for o in range(IC):
                pieces.append((rows[:, o, c * P:(c + 1) * P], (k, c, o)))
    rows = part(2).rearrange("p (o i) -> p o i", o=DC)
    for c in range(IC):
        for o in range(DC):
            pieces.append((rows[:, o, c * P:(c + 1) * P], (2, c, o)))
    flat = [wT[:, 0].rearrange("p c i -> p (c i)"), wT[:, 1].rearrange("p c i -> p (c i)"), wdT[:].rearrange("p c d -> p (c d)")]

    @block.sync
    def _(sp):
        for k, n in enumerate(("w_up", "w_gate")):
            sp.dma_start(part(k).rearrange("p (o i) -> p o i", o=IC), w(n).rearrange("(o p) i -> p o i", p=P)).then_inc(loaded, 16)
        sp.dma_start(part(2).rearrange("p (o i) -> p o i", o=DC), w("w_down").rearrange("(o p) i -> p o i", p=P)).then_inc(loaded, 16)

    @block.vector
    def _(dve):
        step = chain(dve, linked)
        dve.wait_ge(loaded, 48)
        step(nc.vector.tensor_reduce(scale[:], blocks, AX_X, ALU.max, apply_absolute_value=True))
        step(nc.vector.tensor_scalar(scale[:], scale[:], 1.0 / QW, FLOOR, ALU.mult, ALU.max))
        step(nc.vector.reciprocal(inv[:], scale[:]))
        step(nc.vector.tensor_tensor(blocks, blocks, over(inv), ALU.mult))
        step(nc.vector.tensor_scalar(raw[:], raw[:], ROUND, -ROUND, ALU.add, ALU.add))
        step(nc.vector.tensor_scalar(raw[:], raw[:], -QW - 1.0, QW, ALU.max, ALU.min))
        nc.vector.tensor_tensor(blocks, blocks, over(scale), ALU.mult).then_inc(ready, 1)

    @block.tensor
    def _(pe):
        pe.wait_ge(ready, 1)
        for n in range(len(pieces) // 4):
            if n >= 2:
                pe.wait_ge(evacuated, n - 1)
            for q in range(4):
                last = nc.tensor.transpose(t_ps[:, n % 2, q * P:(q + 1) * P], pieces[4 * n + q][0], env.ident[:])
            last.then_inc(turned, 1)

    @block.scalar
    def _(act):
        for n in range(len(pieces) // 4):
            act.wait_ge(turned, n + 1)
            k = pieces[4 * n][1][0]
            at0 = (4 * n - (0, 12, 24)[k]) * P
            nc.scalar.copy(flat[k][:, at0:at0 + 512], t_ps[:, n % 2, :]).then_inc(evacuated, 1)


def quant_unit(nc, env, st, ctx, xnT, wT, wdT):
    sb, ps, sem = st.sb, st.ps, st.sem
    act2 = [sb("up", [P, IC, T]), sb("gate", [P, IC, T])]
    up, gate = act2
    sig = sb("sig", [P, 2, T])
    tops = sb("tops", [P, 2, IC])
    top, amax, scale, inv = (sb(n, [P, 5]) for n in ("top", "amax", "scale", "inv"))
    both = sb("both", [P, 2])
    rnd = sb("rnd", [P, 1])
    h_ps = [ps("up_ps", [P, T]), ps("gate_ps", [P, T])]
    rnd_set, linked, top_ready, reduced, scale_ready, x_ready = (
        sem(n) for n in ("rnd_set", "linked", "top_ready", "reduced", "scale_ready", "x_ready"))
    h_done, up_evac, gate_evac, topped, g_lifted, g_whole, sig_ready, sig_lifted, sig_whole, gs_ready = (
        sem(n) for n in ("h_done", "up_evac", "gate_evac", "topped", "g_lifted", "g_whole", "sig_ready", "sig_lifted", "sig_whole",
                         "gs_ready"))
    u_lifted, u_whole, gs_lifted, gs_whole, o_ready, o_lifted, o_whole, y_done, added = (
        sem(n) for n in ("u_lifted", "u_whole", "gs_lifted", "gs_whole", "o_ready", "o_lifted", "o_whole", "y_done", "added"))
    gs_topped, o_topped = sem("gs_topped"), sem("o_topped")
    block = ctx.enter_context(nc.Block())
    col = lambda buf, k: buf[:, k:k + 1]
    X, UP, GATE, GS, O = range(5)

    @block.gpsimd
    def _(pool):
        nc.gpsimd.memset(rnd[:], ROUND).then_inc(rnd_set, 1)
        for n, ks in enumerate(((X,), (UP, GATE), (GS,), (O,))):
            if n == 3:
                for o in range(IC):
                    pool.wait_ge(u_lifted, o + 1)
                    nc.gpsimd.tensor_scalar(up[:, o, :], up[:, o, :], -ROUND, QA, ALU.add, ALU.min).then_inc(u_whole, 1)
            pool.wait_ge(top_ready, n + 1)
            nc.gpsimd.partition_all_reduce(amax[:, ks[0]:ks[-1] + 1], top[:, ks[0]:ks[-1] + 1], P, RMAX).then_inc(reduced, 1)

    @block.tensor
    def _(pe):
        pe.wait_ge(x_ready, 1)
        for o in range(IC):
            for k in range(2):
                if o:
                    pe.wait_ge((up_evac, gate_evac)[k], o)
                for n in range(CHUNKS):
                    for c in range(DC):
                        last = nc.tensor.matmul(h_ps[k][:, n * 512:(n + 1) * 512], wT[:, k, c, o * P:(o + 1) * P],
                                                xnT[:, c, n * 512:(n + 1) * 512], start=c == 0, stop=c == DC - 1)
                last.then_inc(h_done, 1)
        for t in range(TILES):
            if t % 4 == 0:
                pe.wait_ge(o_whole, t // 4 + 1)
            if t >= 4:
                pe.wait_ge(added, t - 3)
            y = h_ps[0][:, (t % 4) * 512:(t % 4) * 512 + D]
            for o in range(IC):
                last = nc.tensor.matmul(y, gate[:, o, t * P:(t + 1) * P], wdT[:, o, :], start=o == 0, stop=o == IC - 1)
            last.then_inc(y_done, 1)

    def sigmoid_times(dve, o):
        g, s = gate[:, o, :], sig[:, o % 2, :]
        dve.wait_ge(sig_ready, o + 1)
        nc.vector.tensor_scalar(s, s, U16, ROUND, ALU.mult, ALU.add).then_inc(sig_lifted, 1)
        dve.wait_ge(sig_lifted, o + 1)
        nc.vector.tensor_scalar(s, s, -ROUND, U16 - 1.0, ALU.add, ALU.min).then_inc(sig_whole, 1)
        dve.wait_ge(sig_whole, o + 1)
        nc.vector.scalar_tensor_tensor(g, g, col(both, 0), s, ALU.mult, ALU.mult).then_inc(gs_ready, 1)
        dve.wait_ge(gs_ready, o + 1)
        nc.vector.tensor_reduce(tops[:, 0, o:o + 1], g, AX_X, ALU.max, apply_absolute_value=True).then_inc(gs_topped, 1)

    def residual(dve, n):
        for t in range(4 * n, 4 * n + 4):
            xt = env.x[:, t, :]
            dve.wait_ge(y_done, t + 1)
            nc.vector.scalar_tensor_tensor(xt, h_ps[0][:, (t % 4) * 512:(t % 4) * 512 + D], col(scale, O), xt, ALU.mult,
                                           ALU.add).then_inc(added, 1)

    @block.vector
    def _(dve):
        step = chain(dve, linked)

        def scales(n, ks):
            dve.wait_ge(reduced, n + 1)
            cols = slice(ks[0], ks[-1] + 1)
            step(nc.vector.tensor_scalar(scale[:, cols], amax[:, cols], 1.0 / QA, FLOOR, ALU.mult, ALU.max))
            nc.vector.reciprocal(inv[:, cols], scale[:, cols]).then_inc(scale_ready, 1)
            dve.wait_ge(scale_ready, n + 1)

        flat = xnT[:].rearrange("p c t -> p (c t)")
        nc.vector.tensor_reduce(col(top, X), flat, AX_X, ALU.max, apply_absolute_value=True).then_inc(top_ready, 1)
        scales(0, (X,))
        step(nc.vector.tensor_scalar(flat, flat, col(inv, X), ROUND, ALU.mult, ALU.add))
        step(nc.vector.tensor_scalar(flat, flat, -ROUND, -QA - 1.0, ALU.add, ALU.max))
        nc.vector.tensor_scalar(flat, flat, QA, col(scale, X), ALU.min, ALU.mult).then_inc(x_ready, 1)
        for o in range(IC):
            dve.wait_ge(h_done, 2 * o + 2)
            nc.vector.tensor_copy(gate[:, o, :], h_ps[1][:]).then_inc(gate_evac, 1)
            dve.wait_ge(up_evac, o + 1)
            nc.vector.tensor_reduce(tops[:, 0, o:o + 1], up[:, o, :], AX_X, ALU.max, apply_absolute_value=True).then_inc(topped, 1)
            dve.wait_ge(gate_evac, o + 1)
            nc.vector.tensor_reduce(tops[:, 1, o:o + 1], gate[:, o, :], AX_X, ALU.max, apply_absolute_value=True).then_inc(topped, 1)
        dve.wait_ge(topped, 2 * IC)
        nc.vector.tensor_reduce(top[:, UP:GATE + 1], tops[:], AX_X, ALU.max).then_inc(top_ready, 1)
        scales(1, (UP, GATE))
        step(nc.vector.tensor_scalar(col(both, 0), col(scale, GATE), 1.0 / U16, None, ALU.mult))
        for o in range(IC):
            g, s = gate[:, o, :], sig[:, o % 2, :]
            dve.wait_ge(g_lifted, o + 1)
            nc.vector.tensor_scalar(g, g, -ROUND, QA, ALU.add, ALU.min).then_inc(g_whole, 1)
            if o:
                sigmoid_times(dve, o - 1)
        sigmoid_times(dve, IC - 1)
        dve.wait_ge(gs_topped, IC)
        nc.vector.tensor_reduce(col(top, GS), tops[:, 0, :], AX_X, ALU.max).then_inc(top_ready, 1)
        scales(2, (GS,))
        step(nc.vector.tensor_tensor(col(both, 1), col(scale, GS), col(scale, UP), ALU.mult))
        for o in range(IC):
            g = gate[:, o, :]
            dve.wait_ge(gs_lifted, o + 1)
            nc.vector.tensor_scalar(g, g, -ROUND, QA, ALU.add, ALU.min).then_inc(gs_whole, 1)
            dve.wait_ge(gs_whole, o + 1)
            dve.wait_ge(u_whole, o + 1)
            nc.vector.scalar_tensor_tensor(g, g, col(both, 1), up[:, o, :], ALU.mult, ALU.mult).then_inc(o_ready, 1)
            dve.wait_ge(o_ready, o + 1)
            nc.vector.tensor_reduce(tops[:, 1, o:o + 1], g, AX_X, ALU.max, apply_absolute_value=True).then_inc(o_topped, 1)
        dve.wait_ge(o_topped, IC)
        nc.vector.tensor_reduce(col(top, O), tops[:, 1, :], AX_X, ALU.max).then_inc(top_ready, 1)
        scales(3, (O,))
        for n in range(CHUNKS):
            part = gate[:, :, n * 512:(n + 1) * 512]
            dve.wait_ge(o_lifted, n + 1)
            nc.vector.tensor_scalar(part, part, -ROUND, QA, ALU.add, ALU.min).then_inc(o_whole, 1)
            if n:
                residual(dve, n - 1)
        residual(dve, CHUNKS - 1)

    def sigmoid(act, o):
        act.wait_ge(g_whole, o + 1)
        if o >= 2:
            act.wait_ge(gs_ready, o - 1)
        nc.scalar.activation(sig[:, o % 2, :], gate[:, o, :], ACT.Sigmoid, scale=col(scale, GATE)).then_inc(sig_ready, 1)

    @block.scalar
    def _(act):
        act.wait_ge(rnd_set, 1)

        def lift(buf, k, done):
            nc.scalar.activation(buf, buf, ACT.Identity, bias=rnd[:, 0:1], scale=col(inv, k)).then_inc(done, 1)

        for o in range(IC):
            act.wait_ge(h_done, 2 * o + 1)
            nc.scalar.copy(up[:, o, :], h_ps[0][:]).then_inc(up_evac, 1)
        act.wait_ge(scale_ready, 2)
        act.wait_ge(gate_evac, IC)
        for o in range(IC):
            lift(gate[:, o, :], GATE, g_lifted)
            if o:
                sigmoid(act, o - 1)
        sigmoid(act, IC - 1)
        for o in range(IC):
            lift(up[:, o, :], UP, u_lifted)
        act.wait_ge(scale_ready, 3)
        for o in range(IC):
            lift(gate[:, o, :], GS, gs_lifted)
        act.wait_ge(scale_ready, 4)
        for n in range(CHUNKS):
            lift(gate[:, :, n * 512:(n + 1) * 512], O, o_lifted)



DH = 64
INNER = H * DH
PAIRS = INNER // P
KT = TPB + 1
KEYS = S + NCTX
KPAD = KT * P
NEG_MAX = -3.4028234663852886e38


def latent_attention_stage(nc, env, tag, args, name):
    w = lambda n: args[f"{name}_{n}"]
    with ExitStack() as ctx:
        st = Stage(nc, ctx, tag)
        sb = st.sb
        xn = sb("xn", [P, TILES, D])
        layernorm_stage(nc, env, tag + "l", env.x, dst_tok=xn)
        p = {n: sb(n, s) for n, s in (("mean", [P, TILES + B]), ("rstd", [P, TILES + B]), ("gl", [P, DC]), ("bl", [P, DC]),
                                       ("gx", [P, DC]), ("bx", [P, DC]), ("gq", [P, 1]), ("gk", [P, 1]), ("hide", [P, B, NCTX]))}
        latent_norms(nc, env, st, tag, args, w, xn, p)
        for b in range(B):
            with ExitStack() as inner:
                sti = Stage(nc, inner, f"{tag}b{b}")
                qT, kT, v = sti.sb("qT", [P, PAIRS, S]), sti.sb("kT", [P, PAIRS, KPAD]), sti.sb("v", [P, KT, INNER])
                with ExitStack() as deep:
                    latent_project(nc, env, Stage(nc, deep, f"{tag}p{b}"), deep, w, b, xn, p, qT, kT, v)
                oT = qT
                with ExitStack() as deep:
                    latent_attend(nc, env, Stage(nc, deep, f"{tag}a{b}"), deep, b, p, qT, kT, v, oT)
                with ExitStack() as deep:
                    latent_emit(nc, env, Stage(nc, deep, f"{tag}o{b}"), deep, w, b, oT)


def latent_norms(nc, env, outer, tag, args, w, xn, p):
    with ExitStack() as ctx:
        st = Stage(nc, ctx, tag + "n")
        stats = st.sb("stats", [P, TILES + B, 6])
        var = st.sb("var", [P, TILES + B])
        mask_in = st.sb("mask_in", [P, B, NCTX], U8)
        loaded, counted, linked, var_ready, std_ready = (st.sem(n) for n in ("loaded", "counted", "linked", "var_ready", "std_ready"))
        stats_set = st.sem("stats_set")
        block = ctx.enter_context(nc.Block())

        @block.sync
        def _(sp):
            for n, k in (("ln_l_g", "gl"), ("ln_l_b", "bl"), ("ln_x_g", "gx"), ("ln_x_b", "bx")):
                sp.dma_start(p[k][:], w(n).rearrange("(c p) -> p c", p=P), allow_slow_non_contiguous=True).then_inc(loaded, 16)
            for n, k in (("qn_g", "gq"), ("kn_g", "gk")):
                for half in range(2):
                    sp.dma_start(p[k][half * DH:(half + 1) * DH, :], w(n).rearrange("(p a) -> p a", a=1)).then_inc(loaded, 16)
            sp.dma_start(mask_in[:], args["mask_BxS2_bf1"].partition_broadcast(P)).then_inc(loaded, 16)
            sp.wait_ge(loaded, 144)

        @block.vector
        def _(dve):
            step = chain(dve, linked)
            step(nc.vector.memset(stats[:, TILES:, :], 0.0))
            with dve.Fori(0, TILES) as t:
                nc.vector.bn_stats(tile_of(stats, t), tile_of(xn, t)).then_inc(counted, 1)
            for b in range(B):
                nc.vector.bn_stats(stats[0:NCTX, TILES + b, :], env.ctx_tok[0:NCTX, b, :]).then_inc(counted, 1)
            dve.wait_ge(counted, TILES + B)
            merge_stats(nc, step, p["mean"][:], var[:], stats, D)
            nc.vector.tensor_scalar(var[:], var[:], LN_EPS, None, ALU.add).then_inc(var_ready, 1)
            dve.wait_ge(loaded, 144)
            step(nc.vector.tensor_scalar(p["gq"][:], p["gq"][:], DH ** -0.5, None, ALU.mult))
            step(nc.vector.tensor_scalar(p["hide"][:], mask_in[:], 0.0, NEG_MAX, ALU.is_equal, ALU.mult))
            dve.wait_ge(std_ready, 1)
            step(nc.vector.reciprocal(p["rstd"][:], p["rstd"][:]))

        @block.scalar
        def _(act):
            act.wait_ge(var_ready, 1)
            nc.scalar.activation(p["rstd"][:], var[:], ACT.Sqrt).then_inc(std_ready, 1)


def latent_project(nc, env, st, ctx, w, b, xn, p, qT, kT, v):
    sb, ps, sem = st.sb, st.ps, st.sem
    wq, wkv = sb("wq", [P, DC, INNER]), sb("wkv", [P, DC, 2 * INNER])
    turn = sb("turn", [P, 2, D])
    lT = sb("lT", [P, 2, DC, P])
    sq = sb("sq", [P, 2, INNER])
    ss, rn = sb("ss", [P, 2, H]), sb("rn", [P, 2, H])
    qk = sb("qk", [P, 2, INNER])
    q_ps, k_ps, t_ps = ps("q_ps", [P, INNER]), ps("k_ps", [P, INNER]), ps("t_ps", [P, INNER])
    v_ps, x_ps = ps("v_ps", [P, 512]), ps("x_ps", [P, 512])
    loaded, normed, x_turned, x_evac, q_done, k_done, v_done, v_evac = (
        sem(n) for n in ("loaded", "normed", "x_turned", "x_evac", "q_done", "k_done", "v_done", "v_evac"))
    squared, summed, rooted, floored, inv_ready, scaled, turned, evacuated, table_loaded = (
        sem(n) for n in ("squared", "summed", "rooted", "floored", "inv_ready", "scaled", "turned", "evacuated", "table_loaded"))
    block = ctx.enter_context(nc.Block())
    g0 = b * TPB

    def tiles(eng, work):
        for n in range(2):
            work(n, n, P, n > 0, n > 1)
        with eng.Fori(1, TPB // 2) as i:
            for u in range(2):
                work(2 * i + u, u, P, True, True)
        work(TPB, 0, NCTX, True, True)

    @block.sync
    def _(sp):
        sp.dma_start(wq[:], w("Wq").rearrange("(c p) n -> p c n", p=P)).then_inc(loaded, 16)
        sp.dma_start(wkv[:], w("Wkv").rearrange("(c p) n -> p c n", p=P)).then_inc(loaded, 16)

    @block.vector
    def _(dve):
        def normalise(n, u, rows, again):
            if again:
                dve.wait_ge(x_turned, n - 1)
            if rows == P:
                src, col = tile_of(xn, n + g0), bass.ds(n + g0, 1)
            else:
                src, col = env.ctx_tok[0:rows, b, :], slice(TILES + b, TILES + b + 1)
            nc.vector.tensor_scalar(turn[0:rows, u, :], src, p["mean"][0:rows, col], p["rstd"][0:rows, col],
                                    ALU.subtract, ALU.mult).then_inc(normed, 1)

        def work(n, u, rows, once, again):
            normalise(n, u, rows, again)
            sides = (0, 1) if rows == P else (1,)
            for k in sides:
                dve.wait_ge(squared, 2 * n + (k + 1) if rows == P else 2 * n + 1)
                nc.vector.tensor_reduce(ss[0:rows, k, :], sq[0:rows, k, :].rearrange("p (h d) -> p h d", h=H), AX_X,
                                        ALU.add).then_inc(summed, 1)
            dve.wait_ge(rooted, n + 1)
            nc.vector.tensor_scalar(rn[0:rows], rn[0:rows], 1e-8, None, ALU.max).then_inc(floored, 1)
            dve.wait_ge(floored, n + 1)
            nc.vector.reciprocal(rn[0:rows], rn[0:rows]).then_inc(inv_ready, 1)
            dve.wait_ge(inv_ready, n + 1)
            for k in sides:
                if once:
                    dve.wait_ge(turned, 2 * n - 1 + k if rows == P else 2 * n)
                src = (q_ps, k_ps)[k]
                nc.vector.tensor_tensor(qk[0:rows, k, :].rearrange("p (h d) -> p h d", h=H),
                                        src[0:rows, :].rearrange("p (h d) -> p h d", h=H),
                                        rn[0:rows, k, :].unsqueeze(2).to_broadcast([rows, H, DH]), ALU.mult).then_inc(scaled, 1)
            for k in range(2):
                dve.wait_ge(v_done, 2 * n + (k + 1))
                nc.vector.tensor_copy(v[0:rows, bass.ds(n, 1), k * 512:(k + 1) * 512].rearrange("p a n -> p (a n)"),
                                      v_ps[0:rows, :]).then_inc(v_evac, 1)

        tiles(dve, work)

    @block.scalar
    def _(act):
        nc.scalar.activation(ss[:, 0, 0:1], env.eps[:], ACT.Sqrt).then_inc(table_loaded, 1)
        act.wait_ge(table_loaded, 1)

        def work(n, u, rows, once, again):
            g, o = (p["gl"], p["bl"]) if rows == P else (p["gx"], p["bx"])
            act.wait_ge(x_turned, n + 1)
            for c in range(DC):
                nc.scalar.activation(lT[:, u, c, 0:rows], x_ps[:, c * P:c * P + rows], ACT.Identity, bias=o[:, c:c + 1],
                                     scale=g[:, c:c + 1]).then_inc(x_evac, 1)
            sides = (0, 1) if rows == P else (1,)
            for k in sides:
                if rows == P:
                    act.wait_ge((q_done, k_done)[k], n + 1)
                    if once:
                        act.wait_ge(summed, 2 * n - 1 + k)
                else:
                    act.wait_ge(k_done, n + 1)
                    act.wait_ge(summed, 2 * n)
                nc.scalar.activation(sq[0:rows, k, :], (q_ps, k_ps)[k][0:rows, :], ACT.Square).then_inc(squared, 1)
            act.wait_ge(summed, 2 * n + len(sides))
            if once:
                act.wait_ge(scaled, 2 * n)
            src = ss[0:rows] if rows == P else ss[0:rows, 1, :]
            dst = rn[0:rows] if rows == P else rn[0:rows, 1, :]
            if rows != P:
                nc.scalar.activation(rn[0:rows, 0, :], ss[0:rows, 0, :], ACT.Sqrt, scale=1.0 / DH).then_inc(table_loaded, 1)
            nc.scalar.activation(dst, src, ACT.Sqrt, scale=1.0 / DH).then_inc(rooted, 1)
            for k in sides:
                m = 2 * n + k if rows == P else 2 * n
                act.wait_ge(turned, m + 1)
                for half in range(2):
                    dst = (qT, kT)[k][:, half * 4:(half + 1) * 4, bass.ds(n * P, rows)]
                    nc.scalar.activation(dst, t_ps[:, half * 512:(half + 1) * 512].rearrange("p (c t) -> p c t", c=4)[:, :, 0:rows],
                                         ACT.Identity, scale=p[("gq", "gk")[k]][:, 0:1]).then_inc(evacuated, 1)

        tiles(act, work)

    @block.tensor
    def _(pe):
        pe.wait_ge(loaded, 32)

        def front(n, u, rows, once, again):
            pe.wait_ge(normed, n + 1)
            if once:
                pe.wait_ge(x_evac, DC * n)
            for c in range(DC):
                last = nc.tensor.transpose(x_ps[:, c * P:c * P + rows], turn[0:rows, u, c * P:(c + 1) * P],
                                           env.ident[0:rows, 0:rows])
            last.then_inc(x_turned, 1)
            pe.wait_ge(x_evac, DC * (n + 1))
            if once:
                pe.wait_ge(scaled, 2 * n)
            sides = (0, 1) if rows == P else (1,)
            for k in sides:
                for half in range(2):
                    for c in range(DC):
                        wt = (wq, wkv)[k][:, c, half * 512:(half + 1) * 512]
                        last = nc.tensor.matmul((q_ps, k_ps)[k][0:rows, half * 512:(half + 1) * 512], lT[:, u, c, 0:rows], wt,
                                                start=c == 0, stop=c == DC - 1)
                last.then_inc((q_done, k_done)[k], 1)
            for half in range(2):
                if once or half:
                    pe.wait_ge(v_evac, 2 * n + half)
                for c in range(DC):
                    last = nc.tensor.matmul(v_ps[0:rows, :], lT[:, u, c, 0:rows],
                                            wkv[:, c, INNER + half * 512:INNER + (half + 1) * 512], start=c == 0, stop=c == DC - 1)
                last.then_inc(v_done, 1)

        def back(n, u, rows, once, again):
            sides = (0, 1) if rows == P else (1,)
            for k in sides:
                m = 2 * n + k if rows == P else 2 * n
                pe.wait_ge(scaled, m + 1)
                if once or k:
                    pe.wait_ge(evacuated, 2 * m)
                for c in range(PAIRS):
                    last = nc.tensor.transpose(t_ps[:, c * P:c * P + rows], qk[0:rows, k, c * P:(c + 1) * P],
                                               env.ident[0:rows, 0:rows])
                last.then_inc(turned, 1)

        def work(*a):
            front(*a)
            back(*a)

        tiles(pe, work)


def latent_attend(nc, env, st, ctx, b, p, qT, kT, v, oT):
    sb, ps, sem = st.sb, st.ps, st.sem
    qh, kh, vh = sb("qh", [P, S]), sb("kh", [P, KEYS]), sb("vh", [P, 2, KT, DH])
    pr = sb("pr", [P, 2, KEYS])
    pT = sb("pT", [P, KT, 512])
    ntop, total, inv = (sb(n, [P, 2]) for n in ("ntop", "total", "inv"))
    s_ps = ps("s_ps", [P, 2, 3 * 512])
    o_ps = ps("o_ps", [P, 2, 512])
    staged = [sem(f"staged{u}") for u in range(2)]
    scored, hidden, top_ready, exped, inv_ready, normed, turned, t_evac, o_done, o_evac, table_loaded = (
        sem(n) for n in ("scored", "hidden", "top_ready", "exped", "inv_ready", "normed", "turned", "t_evac", "o_done", "o_evac",
                         "table_loaded"))
    QT = TPB
    STEPS = 2 * QT
    ROUNDS = H // 2
    GROUPS = ((0, 4), (4, 8), (8, 9))
    block = ctx.enter_context(nc.Block())

    @block.sync
    def _(sp):
        def stage(i, u):
            half = slice(u * DH, (u + 1) * DH)
            pair = bass.ds(i, 1)
            sp.dma_start(qh[half, :], qT[half, pair, :].rearrange("p a n -> p (a n)")).then_inc(staged[u], 16)
            sp.dma_start(kh[half, :], kT[half, pair, 0:KEYS].rearrange("p a n -> p (a n)")).then_inc(staged[u], 16)
            sp.dma_start(vh[:, u, 0:TPB, :], v[:, 0:TPB, bass.ds(i * P + u * DH, DH)]).then_inc(staged[u], 16)
            sp.dma_start(vh[0:NCTX, u, TPB, :], v[0:NCTX, TPB, bass.ds(i * P + u * DH, DH)]).then_inc(staged[u], 16)

        for u in range(2):
            stage(0, u)
        with sp.Fori(1, ROUNDS) as i:
            for u in range(2):
                sp.wait_ge(o_done, 4 * i + (2 * u - 2))
                stage(i, u)

    @block.tensor
    def _(pe):
        def score(i, k):
            u, n, s = k // QT, k % QT, STEPS * i + k
            half = slice(u * DH, (u + 1) * DH)
            if n == 0:
                pe.wait_ge(staged[u], 64 * i + 64)
            if k < 2:
                pe.wait_ge(t_evac, 3 * s if k == 0 else 3 * s - 3)
            else:
                pe.wait_ge(t_evac, 3 * s - 3)
            for g in range(3):
                cols = slice(g * 512, min((g + 1) * 512, KEYS))
                last = nc.tensor.matmul(s_ps[:, k % 2, cols], qh[half, n * P:(n + 1) * P], kh[half, cols], start=True, stop=True)
            last.then_inc(scored, 1)

        def weigh(i, k):
            u, n, s = k // QT, k % QT, STEPS * i + k
            half = slice(u * DH, (u + 1) * DH)
            pe.wait_ge(normed, s + 1)
            for g, (a, z) in enumerate(GROUPS):
                for j in range(a, z):
                    rows = P if j < TPB else NCTX
                    last = nc.tensor.transpose(s_ps[0:rows, k % 2, g * 512 + (j - a) * P:g * 512 + (j - a + 1) * P],
                                               pr[:, k % 2, j * P:j * P + rows], env.ident[:])
                last.then_inc(turned, 1)
            if n % 4 == 3:
                q = k // 4
                pe.wait_ge(t_evac, 3 * s + 3)
                if k >= 8:
                    pe.wait_ge(o_evac, 4 * i + (q - 1))
                elif k < 4:
                    pe.wait_ge(o_evac, 4 * i)
                for j in range(KT):
                    rows = P if j < TPB else NCTX
                    last = nc.tensor.matmul(o_ps[half, q % 2, :], vh[0:rows, u, j, :], pT[0:rows, j, :], start=j == 0,
                                            stop=j == KT - 1)
                last.then_inc(o_done, 1)

        with pe.Fori(0, ROUNDS) as i:
            score(i, 0)
            for k in range(STEPS):
                if k + 1 < STEPS:
                    score(i, k + 1)
                weigh(i, k)

    def copy_turned(eng, i, k, g, act):
        n, s = k % QT, STEPS * i + k
        a, z = GROUPS[g]
        rows = P if a < TPB else NCTX
        eng.wait_ge(turned, 3 * s + (g + 1))
        if n % 4 == 0:
            eng.wait_ge(o_done, 4 * i + k // 4)
        src = s_ps[0:rows, k % 2, g * 512:g * 512 + (z - a) * P].rearrange("p (j t) -> p j t", j=z - a)
        dst = pT[0:rows, a:z, (n % 4) * P:(n % 4 + 1) * P]
        (nc.scalar.copy if act else nc.vector.tensor_copy)(dst, src).then_inc(t_evac, 1)

    @block.vector
    def _(dve):
        def top(i, k):
            s = STEPS * i + k
            dve.wait_ge(scored, s + 1)
            ctx_keys = s_ps[:, k % 2, S:KEYS]
            nc.vector.tensor_tensor(ctx_keys, ctx_keys, p["hide"][:, b, :], ALU.add).then_inc(hidden, 1)
            dve.wait_ge(hidden, s + 1)
            nc.vector.tensor_reduce(ntop[:, k % 2:k % 2 + 1], s_ps[:, k % 2, 0:KEYS], AX_X, ALU.max, negate=True).then_inc(top_ready, 1)

        def rest(i, k):
            u, n, s = k // QT, k % QT, STEPS * i + k
            dve.wait_ge(exped, s + 1)
            nc.vector.reciprocal(inv[:, k % 2:k % 2 + 1], total[:, k % 2:k % 2 + 1]).then_inc(inv_ready, 1)
            dve.wait_ge(inv_ready, s + 1)
            nc.vector.tensor_scalar(pr[:, k % 2, :], pr[:, k % 2, :], inv[:, k % 2:k % 2 + 1], None, ALU.mult).then_inc(normed, 1)
            copy_turned(dve, i, k, 1, False)

        def keep(i, q):
            u, part = q // 2, q % 2
            half = slice(u * DH, (u + 1) * DH)
            dve.wait_ge(o_done, 4 * i + (q + 1))
            nc.vector.tensor_copy(oT[half, bass.ds(i, 1), part * 512:(part + 1) * 512].rearrange("p a n -> p (a n)"),
                                  o_ps[half, q % 2, :]).then_inc(o_evac, 1)

        with dve.Fori(0, ROUNDS) as i:
            top(i, 0)
            for k in range(STEPS):
                if k + 1 < STEPS:
                    top(i, k + 1)
                rest(i, k)
                if k and k % 4 == 0:
                    keep(i, k // 4 - 1)
            keep(i, STEPS // 4 - 1)

    @block.scalar
    def _(act):
        nc.scalar.activation(total[:, 0:1], env.eps[:], ACT.Exp).then_inc(table_loaded, 1)
        act.wait_ge(table_loaded, 1)

        def soften(i, k):
            s = STEPS * i + k
            act.wait_ge(top_ready, s + 1)
            if k < 2:
                act.wait_ge(turned, 3 * s if k == 0 else 3 * s - 3)
            else:
                act.wait_ge(turned, 3 * s - 3)
            nc.scalar.activation(pr[:, k % 2, :], s_ps[:, k % 2, 0:KEYS], ACT.Exp, bias=ntop[:, k % 2:k % 2 + 1],
                                 accum_out=total[:, k % 2:k % 2 + 1]).then_inc(exped, 1)

        with act.Fori(0, ROUNDS) as i:
            soften(i, 0)
            for k in range(STEPS):
                if k + 1 < STEPS:
                    soften(i, k + 1)
                copy_turned(act, i, k, 0, True)
                copy_turned(act, i, k, 2, True)


def latent_emit(nc, env, st, ctx, w, b, oT):
    wout, bout = st.sb("wout", [P, PAIRS, D]), st.sb("bout", [1, D])
    y_ps = st.ps("y_ps", [P, 4, 512])
    loaded, y_done, added = st.sem("loaded"), st.sem("y_done"), st.sem("added")
    block = ctx.enter_context(nc.Block())

    @block.sync
    def _(sp):
        sp.dma_start(wout[:], w("Wout").rearrange("(c p) n -> p c n", p=P)).then_inc(loaded, 16)
        sp.dma_start(bout[:], w("bout").rearrange("(a n) -> a n", a=1)).then_inc(loaded, 16)

    @block.tensor
    def _(pe):
        pe.wait_ge(loaded, 32)
        for n in range(TPB):
            if n >= 4:
                pe.wait_ge(added, n - 3)
            nc.tensor.matmul(y_ps[:, n % 4, 0:D], env.ones[0:1, :], bout[:], start=True, stop=False)
            for c in range(PAIRS):
                last = nc.tensor.matmul(y_ps[:, n % 4, 0:D], oT[:, c, n * P:(n + 1) * P], wout[:, c, :], start=False,
                                        stop=c == PAIRS - 1)
            last.then_inc(y_done, 1)

    @block.vector
    def _(dve):
        for n in range(TPB):
            t = b * TPB + n
            dve.wait_ge(y_done, n + 1)
            nc.vector.tensor_tensor(env.x[:, t, :], env.x[:, t, :], y_ps[:, n % 4, 0:D], ALU.add).then_inc(added, 1)



E = 8
F = 1024
FC = F // P
NT = T // P + E - 1


def routed_ffn_stage(nc, env, tag, args, name, func, biased, capacity):
    w = lambda n: args[f"{name}_{n}"]
    sorted_x = nc.dram_tensor(f"{tag}_sorted_x", [NT * P, D], F32).ap()
    sorted_y = nc.dram_tensor(f"{tag}_sorted_y", [NT * P, D], F32).ap()
    with ExitStack() as ctx:
        st = Stage(nc, ctx, tag)
        w1 = st.sb("w1", [P, E, DC, F])
        w2 = st.sb("w2", [P, E, FC, D])
        b1 = st.sb("b1", [P, E, FC]) if biased else None
        b2 = st.sb("b2", [P, E, D]) if biased else None
        slot = st.sb("slot", [P, TILES], U32)
        weight = st.sb("weight", [P, TILES])
        expert_of = st.sb("expert_of", [P, NT], I32)
        weights_loaded = st.sem("weights_loaded")
        with ExitStack() as inner:
            route_tokens(nc, env, Stage(nc, inner, tag + "r"), inner, tag, w, capacity, sorted_x, slot, weight, expert_of,
                  w1, w2, b1, b2, weights_loaded)
        with ExitStack() as inner:
            routed_experts(nc, env, Stage(nc, inner, tag + "e"), inner, func, sorted_x, sorted_y, expert_of, w1, w2, b1, b2,
                    weights_loaded)
        with ExitStack() as inner:
            combine_experts(nc, env, Stage(nc, inner, tag + "c"), inner, sorted_y, slot, weight)


def route_tokens(nc, env, st, ctx, tag, w, capacity, sorted_x, slot, weight, expert_of, w1, w2, b1, b2, weights_loaded):
    xn = st.sb("xn", [P, TILES, D])
    xnT = st.sb("xnT", [P, DC, T])
    layernorm_stage(nc, env, tag + "l", env.x, dst_tok=xn, dst_T=xnT)
    gate = st.sb("gate", [P, DC, E])
    zero = st.sb("zero", [P, D])
    upto = st.sb("upto", [P, P])
    ids = st.sb("ids", [P, E])
    tile_ids = st.sb("tile_ids", [P, NT])
    lg, pr, hot, cand, place = (st.sb(n, [P, TILES, E]) for n in ("lg", "pr", "hot", "cand", "place"))
    off, count = st.sb("off", [P, TILES, E]), st.sb("count", [P, TILES, E])
    col = [st.sb(f"col{i}", [P, TILES]) for i in range(4)]
    per = [st.sb(f"per{i}", [P, E]) for i in range(5)]
    ends = st.sb("ends", [P, NT, E])
    tile_expert = st.sb("tile_expert", [P, NT])
    lg_ps, cum_ps, tot_ps = (st.ps(n, [P, 512]) for n in ("lg_ps", "cum_ps", "tot_ps"))
    gate_loaded, zero_made, zero_stored, upto_ones, consts = (
        st.sem(n) for n in ("gate_loaded", "zero_made", "zero_stored", "upto_ones", "consts"))
    lg_done, shifted, exped, hot_ready, counted, linked, slot_ready = (
        st.sem(n) for n in ("lg_done", "shifted", "exped", "hot_ready", "counted", "linked", "slot_ready"))
    scattered, = env.scattered.pop()
    block = ctx.enter_context(nc.Block())
    te = lambda buf: buf[:, 0:TILES * E].rearrange("p (t e) -> p t e", e=E)
    over_e = lambda buf: buf[:].unsqueeze(2).to_broadcast([P, TILES, E])
    over_t = lambda buf: buf[:].unsqueeze(1).to_broadcast([P, TILES, E])

    @block.sync
    def _(sp):
        sp.dma_start(gate[:], w("gate_w").rearrange("(c p) e -> p c e", p=P)).then_inc(gate_loaded, 16)
        sp.wait_ge(zero_made, 1)
        sp.dma_start(sorted_x.rearrange("(j p) d -> p j d", p=P),
                     zero[:].unsqueeze(1).to_broadcast([P, NT, D])).then_inc(zero_stored, 16)
        sp.dma_start(w1[:], w("w1").rearrange("e (c p) f -> p e c f", p=P)).then_inc(weights_loaded, 16)
        sp.dma_start(w2[:], w("w2").rearrange("e (c p) d -> p e c d", p=P)).then_inc(weights_loaded, 16)
        if b1 is not None:
            sp.dma_start(b1[:], w("b1").rearrange("e (c p) -> p e c", p=P), allow_slow_non_contiguous=True).then_inc(weights_loaded, 16)
            sp.dma_start(b2[:], w("b2").partition_broadcast(P)).then_inc(weights_loaded, 16)

    @block.gpsimd
    def _(pool):
        nc.gpsimd.memset(zero[:], 0.0).then_inc(zero_made, 1)
        nc.gpsimd.memset(upto[:], 1.0).then_inc(upto_ones, 1)
        nc.gpsimd.iota(ids[:], [[1, E]], base=0, channel_multiplier=0, allow_small_or_imprecise_dtypes=True).then_inc(consts, 1)
        nc.gpsimd.iota(tile_ids[:], [[1, NT]], base=0, channel_multiplier=0, allow_small_or_imprecise_dtypes=True).then_inc(consts, 1)
        pool.wait_ge(upto_ones, 1)
        nc.gpsimd.affine_select(out=upto[:], in_=upto[:], compare_op=ALU.is_ge, fill=0.0, base=0, pattern=[[1, P]],
                                channel_multiplier=-1).then_inc(consts, 1)
        pool.wait_ge(slot_ready, 1)
        pool.wait_ge(zero_stored, 16)
        for t in range(TILES):
            nc.gpsimd.indirect_dma_start(sorted_x, bass.IndirectOffsetOnAxis(ap=slot[:, t:t + 1], axis=0),
                                         xn[:, t, :], None).then_inc(scattered, 16)
        pool.wait_ge(scattered, 16 * TILES)

    @block.tensor
    def _(pe):
        pe.wait_ge(gate_loaded, 16)
        for t in range(TILES):
            for c in range(DC):
                last = nc.tensor.matmul(lg_ps[:, t * E:(t + 1) * E], xnT[:, c, t * P:(t + 1) * P], gate[:, c, :],
                                        start=c == 0, stop=c == DC - 1)
        last.then_inc(lg_done, 1)
        pe.wait_ge(hot_ready, 1)
        pe.wait_ge(consts, 3)
        hot2 = hot[:].rearrange("p t e -> p (t e)")
        nc.tensor.matmul(cum_ps[:, 0:TILES * E], upto[:], hot2, start=True, stop=True)
        nc.tensor.matmul(tot_ps[:, 0:TILES * E], env.ones[:], hot2, start=True, stop=True).then_inc(counted, 1)

    @block.scalar
    def _(act):
        act.wait_ge(shifted, 1)
        nc.scalar.activation(pr[:], lg[:], ACT.Exp).then_inc(exped, 1)

    @block.vector
    def _(dve):
        step = chain(dve, linked)
        tt = lambda o, a, b, op: step(nc.vector.tensor_tensor(o, a, b, op))
        ts = lambda o, a, s1, s2, op0, op1=None: step(
            nc.vector.tensor_scalar(o, a, s1, s2, op0) if op1 is None else nc.vector.tensor_scalar(o, a, s1, s2, op0, op1))
        dve.wait_ge(lg_done, 1)
        step(nc.vector.tensor_reduce(col[0][:], te(lg_ps), AX_X, ALU.max))
        nc.vector.tensor_tensor(lg[:], te(lg_ps), over_e(col[0]), ALU.subtract).then_inc(shifted, 1)
        dve.wait_ge(exped, 1)
        step(nc.vector.tensor_reduce(col[1][:], pr[:], AX_X, ALU.add))
        step(nc.vector.reciprocal(col[1][:], col[1][:]))
        tt(pr[:], pr[:], over_e(col[1]), ALU.mult)
        step(nc.vector.tensor_reduce(weight[:], pr[:], AX_X, ALU.max))
        tt(cand[:], pr[:], over_e(weight), ALU.is_lt)
        dve.wait_ge(consts, 3)
        step(nc.vector.scalar_tensor_tensor(cand[:], cand[:], float(E), over_t(ids), ALU.mult, ALU.add))
        step(nc.vector.tensor_reduce(col[2][:], cand[:], AX_X, ALU.min))
        nc.vector.tensor_tensor(hot[:], over_t(ids), over_e(col[2]), ALU.is_equal).then_inc(hot_ready, 1)
        dve.wait_ge(counted, 1)
        step(nc.vector.tensor_copy(count[:], te(tot_ps)))
        step(nc.vector.memset(off[:, 0, :], 0.0))
        for t in range(1, TILES):
            tt(off[:, t, :], off[:, t - 1, :], count[:, t - 1, :], ALU.add)
        tt(per[0][:], off[:, TILES - 1, :], count[:, TILES - 1, :], ALU.add)
        ts(per[1][:], per[0][:], 1.0 / P, (P - 1.0) / P - 0.5 + 0.5 / P, ALU.mult, ALU.add)
        ts(per[1][:], per[1][:], ROUND, -ROUND, ALU.add, ALU.add)
        step(nc.vector.tensor_copy(per[2][:, 0:1], per[1][:, 0:1]))
        for e in range(1, E):
            tt(per[2][:, e:e + 1], per[2][:, e - 1:e], per[1][:, e:e + 1], ALU.add)
        tt(per[3][:], per[2][:], per[1][:], ALU.subtract)
        ts(per[3][:], per[3][:], float(P), -1.0, ALU.mult, ALU.add)
        tt(place[:], off[:], te(cum_ps), ALU.add)
        tt(cand[:], place[:], over_t(per[3]), ALU.add)
        tt(cand[:], cand[:], hot[:], ALU.mult)
        step(nc.vector.tensor_reduce(col[3][:], cand[:], AX_X, ALU.add))
        nc.vector.tensor_copy(slot[:], col[3][:]).then_inc(slot_ready, 1)
        if capacity is not None:
            tt(place[:], place[:], hot[:], ALU.mult)
            step(nc.vector.tensor_reduce(col[0][:], place[:], AX_X, ALU.add))
            ts(col[0][:], col[0][:], float(capacity), None, ALU.is_le)
            tt(weight[:], weight[:], col[0][:], ALU.mult)
        tt(ends[:], per[2][:].unsqueeze(1).to_broadcast([P, NT, E]), tile_ids[:].unsqueeze(2).to_broadcast([P, NT, E]), ALU.is_le)
        step(nc.vector.tensor_reduce(tile_expert[:], ends[:], AX_X, ALU.add))
        ts(tile_expert[:], tile_expert[:], float(E - 1), None, ALU.min)
        step(nc.vector.tensor_copy(expert_of[:], tile_expert[:]))


def routed_experts(nc, env, st, ctx, func, sorted_x, sorted_y, expert_of, w1, w2, b1, b2, weights_loaded):
    xs, ys = st.sb("xs", [P, 2, D]), st.sb("ys", [P, 2, D])
    xT = st.sb("xT", [P, 2, DC, P])
    h = st.sb("h", [P, 2, F])
    hT = st.sb("hT", [P, FC, P])
    x_ps, y_ps = st.ps("x_ps", [P, 512]), st.ps("y_ps", [P, 512])
    h_ps = st.ps("h_ps", [P, 2, F])
    t_ps = st.ps("t_ps", [P, F])
    xs_loaded = [st.sem(f"xs_loaded{u}") for u in range(2)]
    ys_stored = env.stored.pop()
    x_turned, x_evac, h_done, h_evac, h_turned, hT_evac, y_done, y_evac = (
        st.sem(n) for n in ("x_turned", "x_evac", "h_done", "h_evac", "h_turned", "hT_evac", "y_done", "y_evac"))
    table_loaded = st.sem("table_loaded")
    HB = F // 512
    EV = FC if b1 is not None else HB
    block = ctx.enter_context(nc.Block())

    def of_buffer(j, u):
        return 8 * j + (16 - 8 * u)

    def pipeline(eng, front, back):
        front(0, 0)
        with eng.Fori(0, (NT - 1) // 2) as i:
            for v in range(2):
                front(2 * i + (1 + v), 1 - v)
                back(2 * i + v, v)
        back(NT - 1, (NT - 1) % 2)

    @block.sync
    def _(sp):
        def load(j, u):
            if not isinstance(j, int):
                sp.wait_ge(x_turned, j - 1)
            sp.dma_start(xs[:, u, :], sorted_x[bass.ds(j * P, P), :]).then_inc(xs_loaded[u], 16)

        load(0, 0)
        load(1, 1)
        with sp.Fori(1, (NT - 1) // 2) as i:
            for u in range(2):
                load(2 * i + u, u)
        sp.wait_ge(x_turned, NT - 2)
        load(NT - 1, (NT - 1) % 2)

    @block.gpsimd
    def _(pool):
        def store(j, u):
            pool.wait_ge(y_evac, j + 1)
            nc.gpsimd.dma_start(sorted_y[bass.ds(j * P, P), :], ys[:, u, :]).then_inc(ys_stored[u], 16)

        with pool.Fori(0, (NT - 1) // 2) as i:
            for u in range(2):
                store(2 * i + u, u)
        store(NT - 1, (NT - 1) % 2)
        pool.wait_ge(ys_stored[0], 16 * ((NT + 1) // 2))
        pool.wait_ge(ys_stored[1], 16 * (NT // 2))

    @block.tensor
    def _(pe):
        pe.wait_ge(weights_loaded, 32 if b1 is None else 64)

        def turn_x(j, u):
            pe.wait_ge(xs_loaded[u], of_buffer(j, u))
            if not isinstance(j, int):
                pe.wait_ge(x_evac, j)
            for c in range(DC):
                last = nc.tensor.transpose(x_ps[:, c * P:(c + 1) * P], xs[:, u, c * P:(c + 1) * P], env.ident[:])
            last.then_inc(x_turned, 1)

        def expand(j, u):
            e = pe.value_load(expert_of[0:1, bass.ds(j, 1)], min_val=0, max_val=E - 1)
            pe.wait_ge(x_evac, j + 1)
            for k in range(HB):
                for c in range(DC):
                    last = nc.tensor.matmul(h_ps[:, u, k * 512:(k + 1) * 512], xT[:, u, c, :],
                                            w1[:, bass.ds(e, 1), c, k * 512:(k + 1) * 512].rearrange("p a n -> p (a n)"),
                                            start=c == 0, stop=c == DC - 1)
            last.then_inc(h_done, 1)

        def turn_h(j, u, reuse):
            pe.wait_ge(h_evac, HB * (j + 1))
            if reuse:
                pe.wait_ge(hT_evac, EV * j)
            for f in range(FC):
                last = nc.tensor.transpose(t_ps[:, f * P:(f + 1) * P], h[:, u, f * P:(f + 1) * P], env.ident[:])
            last.then_inc(h_turned, 1)

        def reduce(j, u, reuse):
            e = pe.value_load(expert_of[0:1, bass.ds(j, 1)], min_val=0, max_val=E - 1)
            pe.wait_ge(hT_evac, EV * (j + 1))
            if reuse:
                pe.wait_ge(y_evac, j)
            for f in range(FC):
                last = nc.tensor.matmul(y_ps[:, 0:D], hT[:, f, :], w2[:, bass.ds(e, 1), f, :].rearrange("p a n -> p (a n)"),
                                        start=f == 0, stop=f == FC - 1)
            last.then_inc(y_done, 1)

        turn_x(0, 0)
        expand(0, 0)
        with pe.Fori(0, (NT - 1) // 2) as i:
            for v in range(2):
                j, u = 2 * i + v, v
                turn_x(j + 1, 1 - u)
                turn_h(j, u, True)
                expand(j + 1, 1 - u)
                reduce(j, u, True)
        turn_h(NT - 1, (NT - 1) % 2, True)
        reduce(NT - 1, (NT - 1) % 2, True)

    @block.scalar
    def _(act):
        def front(j, u):
            act.wait_ge(x_turned, j + 1)
            nc.scalar.copy(xT[:, u], x_ps[:, 0:D].rearrange("p (c t) -> p c t", c=DC)).then_inc(x_evac, 1)

        def back(j, u):
            e = act.value_load(expert_of[0:1, bass.ds(j, 1)], min_val=0, max_val=E - 1) if b1 is not None else None
            act.wait_ge(h_turned, j + 1)
            for k in range(EV):
                n = F // EV // P
                fs = slice(k * n, (k + 1) * n)
                bias = b1[:, bass.ds(e, 1), k] if b1 is not None else 0.0
                nc.scalar.activation(hT[:, fs, :], t_ps[:, k * n * P:(k + 1) * n * P].rearrange("p (f t) -> p f t", f=n),
                                     func, bias=bias).then_inc(hT_evac, 1)

        nc.scalar.activation(hT[:, 0, 0:1], env.eps[:], func).then_inc(table_loaded, 1)
        act.wait_ge(table_loaded, 1)
        pipeline(act, front, back)

    @block.vector
    def _(dve):
        def front(j, u):
            dve.wait_ge(h_done, j + 1)
            for k in range(HB):
                nc.vector.tensor_copy(h[:, u, k * 512:(k + 1) * 512], h_ps[:, u, k * 512:(k + 1) * 512]).then_inc(h_evac, 1)

        def back(j, u):
            e = dve.value_load(expert_of[0:1, bass.ds(j, 1)], min_val=0, max_val=E - 1) if b2 is not None else None
            dve.wait_ge(y_done, j + 1)
            if not isinstance(j, int):
                dve.wait_ge(ys_stored[u], of_buffer(j, u) - 16)
            elif j >= 2:
                dve.wait_ge(ys_stored[u], 16 * (j // 2))
            if b2 is None:
                nc.vector.tensor_copy(ys[:, u, :], y_ps[:, 0:D]).then_inc(y_evac, 1)
            else:
                nc.vector.tensor_tensor(ys[:, u, :], y_ps[:, 0:D], b2[:, bass.ds(e, 1), :].rearrange("p a n -> p (a n)"),
                                        ALU.add).then_inc(y_evac, 1)

        pipeline(dve, front, back)


def combine_experts(nc, env, st, ctx, sorted_y, slot, weight):
    yg = st.sb("yg", [P, TILES, D])
    gathered = env.gathered.pop()
    added = st.sem("added")
    block = ctx.enter_context(nc.Block())

    @block.gpsimd
    def _(pool):
        for t in range(TILES):
            nc.gpsimd.indirect_dma_start(yg[:, t, :], None, sorted_y, bass.IndirectOffsetOnAxis(ap=slot[:, t:t + 1], axis=0)
                                         ).then_inc(gathered[t], 16)

    @block.vector
    def _(dve):
        for t in range(TILES):
            dve.wait_ge(gathered[t], 16)
            nc.vector.scalar_tensor_tensor(env.x[:, t, :], yg[:, t, :], weight[:, t:t + 1], env.x[:, t, :], ALU.mult,
                                           ALU.add).then_inc(added, 1)
        dve.wait_ge(added, TILES)



WIDE = H * NCTX
BANK_HEADS = (range(0, 6), range(6, 12), range(12, 16))


def spread(ap, shape):
    return ap.to_broadcast(shape)


def cross_attention_stage(nc, env, tag, args, name, mask, side, hides):
    w = lambda n: args[f"{name}_{n}"]
    with ExitStack() as ctx:
        st = Stage(nc, ctx, tag)
        sb, ps, sem = st.sb, st.ps, st.sem
        stats = sb("stats", [P, TILES, 6])
        mean, var, rstd = (sb(n, [P, TILES]) for n in ("mean", "var", "rstd"))
        wq, wk, wv, wo = (sb(n, [P, DC, D]) for n in ("wq", "wk", "wv", "wo"))
        bq, bk = sb("bq", [P, DC]), sb("bk", [P, DC])
        bqs = sb("bqs", [P, DC])
        bv = sb("bv", [P, D])
        bo = sb("bo", [1, D])
        mask_in = sb("mask_in", [P, TILES, NCTX], mask.dtype)
        neg = sb("neg", [P, TILES, NCTX])
        half = H // DC
        ind = sb("ind", [P, half])
        ctxT = sb("ctxT", [P, DC, B * NCTX])
        kT = sb("kT", [P, DC, B * NCTX])
        kbd = sb("kbd", [P, DC, B, half * NCTX])
        v = sb("v", [P, B, D])
        turn = sb("turn", [P, 2, D])
        xT = sb("xT", [P, 2, DC, P])
        qT = sb("qT", [P, 2, DC, P])
        bias = sb("bias", [P, 2, WIDE]) if side is not None else None
        z = sb("z", [P, 2, WIDE])
        top, total, inv = (sb(n, [P, 2, H]) for n in ("top", "total", "inv"))
        pT = sb("pT", [P, H * P])
        at = sb("at", [P, D])
        aT = sb("aT", [P, DC, P])
        s_ps = ps("s_ps", [P, 3, 512])
        pt_ps = ps("pt_ps", [P, 2, 512])
        x_ps = ps("x_ps", [P, 512])
        o_ps = ps("o_ps", [P, 512])
        y_ps = ps("y_ps", [P, 512])

        kv_loaded, q_loaded, mask_loaded = (sem(n) for n in ("kv_loaded", "q_loaded", "mask_loaded"))
        side_loaded = [sem(f"side_loaded{u}") for u in range(2)]
        ones_set, ind_lower, ind_made = sem("ones_set"), sem("ind_lower"), sem("ind_made")
        linked, var_ready, std_ready, neg_ready = sem("linked"), sem("var_ready"), sem("std_ready"), sem("neg_ready")
        ctx_turned, ctx_evac, k_done, v_done, k_ready, kbd_ready = (
            sem(n) for n in ("ctx_turned", "ctx_evac", "k_done", "v_done", "k_ready", "kbd_ready"))
        normed, x_turned, x_evac, q_done, q_evac = (sem(n) for n in ("normed", "x_turned", "x_evac", "q_done", "q_evac"))
        scored, biased, z_added, top_ready, shifted, exped = (
            sem(n) for n in ("scored", "biased", "z_added", "top_ready", "shifted", "exped"))
        summed, inv_ready, p_turned, p_evac, pv_done, at_ready = (
            sem(n) for n in ("summed", "inv_ready", "p_turned", "p_evac", "pv_done", "at_ready"))
        a_turned, a_evac, y_done, added, bqs_ready = (sem(n) for n in ("a_turned", "a_evac", "y_done", "added", "bqs_ready"))
        block = ctx.enter_context(nc.Block())

        def body(eng, front, back):
            for b in range(B):
                g0 = b * TPB
                for n in range(2):
                    front(b, g0 + n, n, g0 + n >= 2, g0 + n >= 1)
                    if n:
                        back(b, g0, 0, g0 >= 1)
                with eng.Fori(1, TPB // 2) as i:
                    for u in range(2):
                        g = 2 * i + (g0 + u)
                        front(b, g, u, True, True)
                        back(b, g - 1, 1 - u, True)
                back(b, g0 + TPB - 1, 1, True)

        @block.sync
        def _(sp):
            sp.dma_start(wk[:], w("Wk").rearrange("(c p) n -> p c n", p=P)).then_inc(kv_loaded, 16)
            sp.dma_start(wv[:], w("Wv").rearrange("(c p) n -> p c n", p=P)).then_inc(kv_loaded, 16)
            sp.dma_start(bk[:], w("bk").rearrange("(c p) -> p c", p=P), allow_slow_non_contiguous=True).then_inc(kv_loaded, 16)
            sp.dma_start(bv[:], w("bv").partition_broadcast(P)).then_inc(kv_loaded, 16)
            sp.dma_start(mask_in[:], mask.rearrange("b (t p) j -> p (b t) j", p=P)).then_inc(mask_loaded, 16)
            sp.dma_start(wq[:], w("Wq").rearrange("(c p) n -> p c n", p=P)).then_inc(q_loaded, 16)
            sp.dma_start(bq[:], w("bq").rearrange("(c p) -> p c", p=P), allow_slow_non_contiguous=True).then_inc(q_loaded, 16)
            sp.dma_start(wo[:], w("Wo").rearrange("(c p) n -> p c n", p=P)).then_inc(q_loaded, 16)
            sp.dma_start(bo[:], w("bo").rearrange("(a n) -> a n", a=1)).then_inc(q_loaded, 16)
            if side is not None:
                def load(b, g, u, reuse):
                    if reuse:
                        sp.wait_ge(z_added, g - 1)
                    rows = bass.ds((g - b * TPB) * P, P)
                    sp.dma_start(bias[:, u, :].rearrange("p (h j) -> p h j", h=H),
                                 side[b, :, rows, :].rearrange("h p j -> p h j")).then_inc(side_loaded[u], 16)

                for b in range(B):
                    for u in range(2):
                        load(b, b * TPB + u, u, b > 0)
                    with sp.Fori(1, TPB // 2) as i:
                        for u in range(2):
                            load(b, 2 * i + (b * TPB + u), u, True)

        @block.gpsimd
        def _(pool):
            nc.gpsimd.memset(ind[:], 1.0).then_inc(ones_set, 1)
            pool.wait_ge(ones_set, 1)
            nc.gpsimd.affine_select(out=ind[:], in_=ind[:], compare_op=ALU.is_ge, fill=0.0, base=0,
                                    pattern=[[-HD, half]], channel_multiplier=1).then_inc(ind_lower, 1)
            pool.wait_ge(ind_lower, 1)
            nc.gpsimd.affine_select(out=ind[:], in_=ind[:], compare_op=ALU.is_ge, fill=0.0, base=HD - 1,
                                    pattern=[[HD, half]], channel_multiplier=-1).then_inc(ind_made, 1)
            pool.wait_ge(neg_ready, 1)

            def half_of(g, u):
                return 8 * g + (16 - 8 * u)

            def front(b, g, u, reuse2, reuse1):
                zt = z[:, u, :].rearrange("p (h j) -> p h j", h=H)
                if side is not None:
                    bt = bias[:, u, :].rearrange("p (h j) -> p h j", h=H)
                    pool.wait_ge(side_loaded[u], half_of(g, u))
                    nc.gpsimd.tensor_tensor(bt, bt, spread(neg[:, bass.ds(g, 1), :], [P, H, NCTX]), ALU.add).then_inc(biased, 1)
                pool.wait_ge(top_ready, g + 1)
                nc.gpsimd.tensor_tensor(zt, zt, spread(top[:, u, :].unsqueeze(2), [P, H, NCTX]),
                                        ALU.subtract).then_inc(shifted, 1)

            body(pool, front, lambda *a: None)

        @block.vector
        def _(dve):
            step = chain(dve, linked)
            row_stats(nc, dve, st, step, env.x, TILES, mean[:], var[:], stats)
            nc.vector.tensor_scalar(var[:], var[:], LN_EPS, None, ALU.add).then_inc(var_ready, 1)
            dve.wait_ge(mask_loaded, 16)
            if hides:
                nc.vector.tensor_scalar(neg[:], mask_in[:], -1e15, None, ALU.mult).then_inc(neg_ready, 1)
            else:
                nc.vector.tensor_scalar(neg[:], mask_in[:], 0.0, NEG, ALU.is_equal, ALU.mult).then_inc(neg_ready, 1)
            dve.wait_ge(q_loaded, 64)
            nc.vector.tensor_scalar(bqs[:], bq[:], HD ** -0.5, None, ALU.mult).then_inc(bqs_ready, 1)
            dve.wait_ge(kv_loaded, 64)
            dve.wait_ge(ind_made, 1)
            dve.wait_ge(k_done, 1)
            for c in range(DC):
                nc.vector.tensor_scalar(kT[:, c, :], x_ps[:, c * B * NCTX:(c + 1) * B * NCTX], bk[:, c:c + 1], None,
                                        ALU.add).then_inc(k_ready, 1)
            dve.wait_ge(k_ready, DC)
            for c in range(DC):
                for b in range(B):
                    nc.vector.tensor_tensor(kbd[:, c, b, :].rearrange("p (h j) -> p h j", h=half),
                                            spread(kT[:, c:c + 1, b * NCTX:(b + 1) * NCTX], [P, half, NCTX]),
                                            spread(ind[:, :].unsqueeze(2), [P, half, NCTX]),
                                            ALU.mult).then_inc(kbd_ready, 1)
            dve.wait_ge(v_done, 1)
            for b in range(B):
                nc.vector.tensor_tensor(v[0:NCTX, b, :], o_ps[0:NCTX, b * D:(b + 1) * D], bv[0:NCTX, :],
                                        ALU.add).then_inc(kbd_ready, 1)
            dve.wait_ge(std_ready, 1)
            step(nc.vector.reciprocal(rstd[:], rstd[:]))
            dve.wait_ge(neg_ready, 1)

            def front(b, g, u, reuse2, reuse1):
                if reuse2:
                    dve.wait_ge(x_turned, g - 1)
                nc.vector.tensor_scalar(turn[:, u, :], tile_of(env.x, g), mean[:, bass.ds(g, 1)], rstd[:, bass.ds(g, 1)],
                                        ALU.subtract, ALU.mult).then_inc(normed, 1)
                if not reuse1 or isinstance(g, int) and g % TPB == 0:
                    attend(b, g, u, reuse2)

            def attend(b, g, u, reuse2):
                dve.wait_ge(scored, g + 1)
                if reuse2:
                    dve.wait_ge(p_turned, 4 * (g - 1))
                if side is not None:
                    dve.wait_ge(biased, g + 1)
                for k, heads in enumerate(BANK_HEADS):
                    n, cols = len(heads), slice(heads[0] * NCTX, (heads[-1] + 1) * NCTX)
                    if side is not None:
                        add = bias[:, u, cols].rearrange("p (h j) -> p h j", h=n)
                    else:
                        add = spread(neg[:, bass.ds(g, 1), :], [P, n, NCTX])
                    nc.vector.tensor_tensor(z[:, u, cols].rearrange("p (h j) -> p h j", h=n),
                                            s_ps[:, k, 0:n * NCTX].rearrange("p (h j) -> p h j", h=n), add,
                                            ALU.add).then_inc(z_added if k == 2 else linked2, 1)
                dve.wait_ge(linked2, 2 * (g + 1))
                dve.wait_ge(z_added, g + 1)
                nc.vector.tensor_reduce(top[:, u, :], z[:, u, :].rearrange("p (h j) -> p h j", h=H), AX_X,
                                        ALU.max).then_inc(top_ready, 1)

            def back(b, g, u, reuse1):
                dve.wait_ge(exped, g + 1)
                nc.vector.tensor_reduce(total[:, u, :], z[:, u, :].rearrange("p (h j) -> p h j", h=H), AX_X,
                                        ALU.add).then_inc(summed, 1)
                dve.wait_ge(summed, g + 1)
                nc.vector.reciprocal(inv[:, u, :], total[:, u, :]).then_inc(inv_ready, 1)
                last = isinstance(g, int) and g % TPB == TPB - 1
                if not last:
                    attend(b, g + 1, 1 - u, not (isinstance(g, int) and g == 0))
                dve.wait_ge(pv_done, g + 1)
                dve.wait_ge(inv_ready, g + 1)
                if reuse1:
                    dve.wait_ge(a_turned, g)
                nc.vector.tensor_tensor(at[:].rearrange("p (h d) -> p h d", h=H),
                                        o_ps[:, 0:D].rearrange("p (h d) -> p h d", h=H),
                                        spread(inv[:, u, :].unsqueeze(2), [P, H, HD]), ALU.mult).then_inc(at_ready, 1)
                dve.wait_ge(y_done, g + 1)
                xt = tile_of(env.x, g)
                nc.vector.tensor_tensor(xt, xt, y_ps[:, 0:D], ALU.add).then_inc(added, 1)

            linked2 = sem("z_part")
            body(dve, front, back)

        @block.scalar
        def _(act):
            act.wait_ge(var_ready, 1)
            nc.scalar.activation(rstd[:], var[:], ACT.Sqrt).then_inc(std_ready, 1)
            act.wait_ge(ctx_turned, B)
            for b in range(B):
                nc.scalar.copy(ctxT[:, :, b * NCTX:(b + 1) * NCTX],
                               y_ps[:, b * D:b * D + DC * NCTX].rearrange("p (c t) -> p c t", c=DC)).then_inc(ctx_evac, 1)
            act.wait_ge(bqs_ready, 1)

            def front(b, g, u, reuse2, reuse1):
                act.wait_ge(x_turned, g + 1)
                nc.scalar.copy(xT[:, u], x_ps[:, 0:D].rearrange("p (c t) -> p c t", c=DC)).then_inc(x_evac, 1)
                act.wait_ge(q_done, g + 1)
                for c in range(DC):
                    nc.scalar.activation(qT[:, u, c, :], x_ps[:, D + c * P:D + (c + 1) * P], ACT.Identity,
                                         bias=bqs[:, c:c + 1], scale=HD ** -0.5).then_inc(q_evac, 1)
                if isinstance(g, int) and g % TPB == 0:
                    soften(g, u)

            def soften(g, u):
                act.wait_ge(shifted, g + 1)
                nc.scalar.activation(z[:, u, :], z[:, u, :], ACT.Exp).then_inc(exped, 1)

            def back(b, g, u, reuse1):
                for k in range(4):
                    act.wait_ge(p_turned, 4 * g + (k + 1))
                    nc.scalar.copy(pT[0:NCTX, k * 512:(k + 1) * 512], pt_ps[0:NCTX, k % 2, :]).then_inc(p_evac, 1)
                if not (isinstance(g, int) and g % TPB == TPB - 1):
                    soften(g + 1, 1 - u)
                act.wait_ge(a_turned, g + 1)
                nc.scalar.copy(aT[:], o_ps[:, D:2 * D].rearrange("p (c t) -> p c t", c=DC)).then_inc(a_evac, 1)

            body(act, front, back)

        @block.tensor
        def _(pe):
            for b in range(B):
                for c in range(DC):
                    last = nc.tensor.transpose(y_ps[:, b * D + c * NCTX:b * D + (c + 1) * NCTX],
                                               env.ctx_tok[0:NCTX, b, c * P:(c + 1) * P], env.ident[0:NCTX, 0:NCTX])
                last.then_inc(ctx_turned, 1)
            pe.wait_ge(ctx_evac, B)
            pe.wait_ge(kv_loaded, 64)
            for f in range(DC):
                for c in range(DC):
                    last = nc.tensor.matmul(x_ps[:, f * B * NCTX:(f + 1) * B * NCTX], wk[:, c, f * P:(f + 1) * P],
                                            ctxT[:, c, :], start=c == 0, stop=c == DC - 1)
            last.then_inc(k_done, 1)
            for b in range(B):
                for c in range(DC):
                    last = nc.tensor.matmul(o_ps[0:NCTX, b * D:(b + 1) * D], ctxT[:, c, b * NCTX:(b + 1) * NCTX],
                                            wv[:, c, :], start=c == 0, stop=c == DC - 1)
            last.then_inc(v_done, 1)
            pe.wait_ge(q_loaded, 64)
            pe.wait_ge(kbd_ready, DC * B + B)

            def front(b, g, u, reuse2, reuse1):
                pe.wait_ge(normed, g + 1)
                if reuse1:
                    pe.wait_ge(q_evac, DC * g)
                for c in range(DC):
                    last = nc.tensor.transpose(x_ps[:, c * P:(c + 1) * P], turn[:, u, c * P:(c + 1) * P], env.ident[:])
                last.then_inc(x_turned, 1)
                pe.wait_ge(x_evac, g + 1)
                for f in range(DC):
                    for c in range(DC):
                        last = nc.tensor.matmul(x_ps[:, D + f * P:D + (f + 1) * P], wq[:, c, f * P:(f + 1) * P], xT[:, u, c, :],
                                                start=c == 0, stop=c == DC - 1)
                last.then_inc(q_done, 1)
                pe.wait_ge(q_evac, DC * (g + 1))
                if reuse1:
                    pe.wait_ge(z_added, g)
                for k, heads in enumerate(BANK_HEADS):
                    for c in range(DC):
                        mine = [h for h in heads if h // half == c]
                        if mine:
                            at0 = (mine[0] - heads[0]) * NCTX
                            last = nc.tensor.matmul(s_ps[:, k, at0:at0 + len(mine) * NCTX], qT[:, u, c, :],
                                                    kbd[:, c, b, (mine[0] % half) * NCTX:(mine[-1] % half + 1) * NCTX],
                                                    start=True, stop=True)
                last.then_inc(scored, 1)

            def back(b, g, u, reuse1):
                pe.wait_ge(exped, g + 1)
                for k in range(4):
                    if reuse1 or k >= 2:
                        pe.wait_ge(p_evac, 4 * g + (k - 1))
                    for h in range(4 * k, 4 * k + 4):
                        last = nc.tensor.transpose(pt_ps[0:NCTX, k % 2, (h % 4) * P:(h % 4 + 1) * P],
                                                   z[:, u, h * NCTX:(h + 1) * NCTX], env.ident[:])
                    last.then_inc(p_turned, 1)
                pe.wait_ge(p_evac, 4 * (g + 1))
                if reuse1:
                    pe.wait_ge(a_evac, g)
                for h in range(H):
                    last = nc.tensor.matmul(o_ps[:, h * HD:(h + 1) * HD], pT[0:NCTX, h * P:(h + 1) * P],
                                            v[0:NCTX, b, h * HD:(h + 1) * HD], start=True, stop=True)
                last.then_inc(pv_done, 1)
                pe.wait_ge(at_ready, g + 1)
                for c in range(DC):
                    last = nc.tensor.transpose(o_ps[:, D + c * P:D + (c + 1) * P], at[:, c * P:(c + 1) * P], env.ident[:])
                last.then_inc(a_turned, 1)
                pe.wait_ge(a_evac, g + 1)
                if reuse1:
                    pe.wait_ge(added, g)
                nc.tensor.matmul(y_ps[:, 0:D], env.ones[0:1, :], bo[:], start=True, stop=False)
                for c in range(DC):
                    last = nc.tensor.matmul(y_ps[:, 0:D], aT[:, c, :], wo[:, c, :], start=False, stop=c == DC - 1)
                last.then_inc(y_done, 1)

            body(pe, front, back)



TOP_P = 0.8


def gated_ffn_stage(nc, env, tag, args, name):
    w = lambda n: args[f"{name}_{n}"]
    with ExitStack() as ctx:
        st = Stage(nc, ctx, tag)
        xnT = st.sb("xnT", [P, DC, T])
        gate = st.sb("gate", [P, TILES, E])
        layernorm_stage(nc, env, tag + "l", env.x, dst_T=xnT)
        with ExitStack() as inner:
            token_gates(nc, env, Stage(nc, inner, tag + "g"), inner, w, xnT, gate)
        with ExitStack() as inner:
            gated_experts(nc, env, Stage(nc, inner, tag + "e"), inner, w, xnT, gate)


def token_gates(nc, env, st, ctx, w, xnT, gate):
    wr, br = st.sb("wr", [P, DC, E]), st.sb("br", [P, E])
    b2 = st.sb("b2", [E, D])
    lower = st.sb("lower", [P, E, E])
    lg, pr, cum, rank = (st.sb(n, [P, TILES, E]) for n in ("lg", "pr", "cum", "rank"))
    above, same = st.sb("above", [P, TILES, E, E]), st.sb("same", [P, TILES, E, E])
    col = st.sb("col", [P, TILES])
    gT = st.sb("gT", [E, T])
    lg_ps, g_ps, y_ps = st.ps("lg_ps", [P, 512]), st.ps("g_ps", [P, 4, 512]), st.ps("y_ps", [P, 2, 512])
    loaded, ones_set, lower_made, lg_done, shifted, exped, linked, gate_ready, g_turned, gT_ready, y_done, added = (
        st.sem(n) for n in ("loaded", "ones_set", "lower_made", "lg_done", "shifted", "exped", "linked", "gate_ready",
                            "g_turned", "gT_ready", "y_done", "added"))
    block = ctx.enter_context(nc.Block())
    over_e = lambda buf: buf[:].unsqueeze(2).to_broadcast([P, TILES, E])
    mine = lambda buf: buf[:].unsqueeze(3).to_broadcast([P, TILES, E, E])
    others = lambda buf: buf[:].unsqueeze(2).to_broadcast([P, TILES, E, E])

    @block.sync
    def _(sp):
        sp.dma_start(wr[:], w("Wr").rearrange("(c p) e -> p c e", p=P)).then_inc(loaded, 16)
        sp.dma_start(br[:], w("br").partition_broadcast(P)).then_inc(loaded, 16)
        sp.dma_start(b2[:], w("b2")).then_inc(loaded, 16)

    @block.gpsimd
    def _(pool):
        nc.gpsimd.memset(lower[:], 1.0).then_inc(ones_set, 1)
        pool.wait_ge(ones_set, 1)
        nc.gpsimd.affine_select(out=lower[:], in_=lower[:], compare_op=ALU.is_ge, fill=0.0, base=0,
                                pattern=[[1, E], [-1, E]], channel_multiplier=0).then_inc(lower_made, 1)

    @block.tensor
    def _(pe):
        pe.wait_ge(loaded, 48)
        for t in range(TILES):
            for c in range(DC):
                last = nc.tensor.matmul(lg_ps[:, t * E:(t + 1) * E], xnT[:, c, t * P:(t + 1) * P], wr[:, c, :],
                                        start=c == 0, stop=c == DC - 1)
        last.then_inc(lg_done, 1)
        pe.wait_ge(gate_ready, 1)
        for t in range(TILES):
            last = nc.tensor.transpose(g_ps[0:E, t // 4, (t % 4) * P:(t % 4 + 1) * P], gate[:, t, :], env.ident[:])
        last.then_inc(g_turned, 1)
        pe.wait_ge(gT_ready, 4)
        for t in range(TILES):
            if t >= 2:
                pe.wait_ge(added, t - 1)
            nc.tensor.matmul(y_ps[:, t % 2, 0:D], gT[:, t * P:(t + 1) * P], b2[:], start=True, stop=True).then_inc(y_done, 1)

    @block.scalar
    def _(act):
        act.wait_ge(shifted, 1)
        nc.scalar.activation(pr[:], lg[:], ACT.Exp).then_inc(exped, 1)
        act.wait_ge(g_turned, 1)
        for k in range(4):
            nc.scalar.copy(gT[:, k * 512:(k + 1) * 512], g_ps[0:E, k, :]).then_inc(gT_ready, 1)

    @block.vector
    def _(dve):
        step = chain(dve, linked)
        tt = lambda o, a, b, op: step(nc.vector.tensor_tensor(o, a, b, op))
        dve.wait_ge(lg_done, 1)
        dve.wait_ge(loaded, 48)
        tt(lg[:], lg_ps[:, 0:TILES * E].rearrange("p (t e) -> p t e", e=E), br[:].unsqueeze(1).to_broadcast([P, TILES, E]), ALU.add)
        step(nc.vector.tensor_reduce(col[:], lg[:], AX_X, ALU.max))
        nc.vector.tensor_tensor(lg[:], lg[:], over_e(col), ALU.subtract).then_inc(shifted, 1)
        dve.wait_ge(exped, 1)
        step(nc.vector.tensor_reduce(col[:], pr[:], AX_X, ALU.add))
        step(nc.vector.reciprocal(col[:], col[:]))
        tt(pr[:], pr[:], over_e(col), ALU.mult)
        dve.wait_ge(lower_made, 1)
        tt(above[:], others(pr), mine(pr), ALU.is_gt)
        tt(same[:], others(pr), mine(pr), ALU.is_equal)
        tt(same[:], same[:], lower[:].unsqueeze(1).to_broadcast([P, TILES, E, E]), ALU.mult)
        tt(above[:], above[:], same[:], ALU.add)
        step(nc.vector.tensor_reduce(rank[:], above[:], AX_X, ALU.add))
        tt(above[:], above[:], others(pr), ALU.mult)
        step(nc.vector.tensor_reduce(cum[:], above[:], AX_X, ALU.add))
        step(nc.vector.tensor_scalar(cum[:], cum[:], TOP_P, None, ALU.is_lt))
        step(nc.vector.scalar_tensor_tensor(cum[:], rank[:], 1.0, cum[:], ALU.is_le, ALU.max))
        nc.vector.tensor_tensor(gate[:], pr[:], cum[:], ALU.mult).then_inc(gate_ready, 1)
        for t in range(TILES):
            dve.wait_ge(y_done, t + 1)
            nc.vector.tensor_tensor(env.x[:, t, :], env.x[:, t, :], y_ps[:, t % 2, 0:D], ALU.add).then_inc(added, 1)


def gated_experts(nc, env, st, ctx, w, xnT, gate):
    CHUNK = 512
    CHUNKS = T // CHUNK
    CT = CHUNK // P
    STEPS = 2 * CHUNKS
    w1, w2 = st.sb("w1", [P, 2, DC, F]), st.sb("w2", [P, 2, FC, D])
    b1 = st.sb("b1", [P, 2, FC])
    hT = st.sb("hT", [P, 2, FC, CHUNK])
    h_ps, y_ps = st.ps("h_ps", [P, 4, 512]), st.ps("y_ps", [P, 4, 512])
    w_loaded = [st.sem(f"w_loaded{v}") for v in range(2)]
    h_done, h_evac, y_done, y_added, table_loaded = (
        st.sem(n) for n in ("h_done", "h_evac", "y_done", "y_added", "table_loaded"))
    block = ctx.enter_context(nc.Block())

    @block.sync
    def _(sp):
        def load(e, v):
            sp.dma_start(b1[:, v], w("b1")[bass.ds(e, 1)].rearrange("a (c p) -> p (a c)", p=P),
                         allow_slow_non_contiguous=True).then_inc(w_loaded[v], 16)
            sp.dma_start(w1[:, v], w("W1")[bass.ds(e, 1)].rearrange("a (c p) f -> p (a c) f", p=P)).then_inc(w_loaded[v], 16)
            sp.dma_start(w2[:, v], w("W2")[bass.ds(e, 1)].rearrange("a (c p) d -> p (a c) d", p=P)).then_inc(w_loaded[v], 16)

        for v in range(2):
            load(v, v)
        with sp.Fori(1, E // 2) as i:
            for v in range(2):
                sp.wait_ge(y_done, CT * CHUNKS * (2 * i + (v - 1)))
                load(2 * i + v, v)

    @block.tensor
    def _(pe):
        def hidden(i, k):
            v, n, s = k // CHUNKS, k % CHUNKS, STEPS * i + k
            if n == 0:
                pe.wait_ge(w_loaded[v], 48 * i + 48)
            for f in range(FC):
                if k or f >= 4:
                    pe.wait_ge(h_evac, FC * s + (f - 3))
                for c in range(DC):
                    last = nc.tensor.matmul(h_ps[:, f % 4, :], w1[:, v, c, f * P:(f + 1) * P],
                                            xnT[:, c, n * CHUNK:(n + 1) * CHUNK], start=c == 0, stop=c == DC - 1)
                last.then_inc(h_done, 1)

        def reduce(i, k):
            v, n, s = k // CHUNKS, k % CHUNKS, STEPS * i + k
            pe.wait_ge(h_evac, FC * s + FC)
            for q in range(CT):
                if k == 0:
                    pe.wait_ge(y_added, CT * s)
                else:
                    pe.wait_ge(y_added, CT * s + (q - 3))
                for f in range(FC):
                    last = nc.tensor.matmul(y_ps[:, q, 0:D], hT[:, k % 2, f, q * P:(q + 1) * P], w2[:, v, f, :],
                                            start=f == 0, stop=f == FC - 1)
                last.then_inc(y_done, 1)

        with pe.Fori(0, E // 2) as i:
            hidden(i, 0)
            for k in range(STEPS):
                if k + 1 < STEPS:
                    hidden(i, k + 1)
                reduce(i, k)

    @block.scalar
    def _(act):
        nc.scalar.activation(hT[:, 0, 0, 0:1], env.eps[:], ACT.Relu).then_inc(table_loaded, 1)
        act.wait_ge(table_loaded, 1)
        with act.Fori(0, E // 2) as i:
            for k in range(STEPS):
                v, s = k // CHUNKS, STEPS * i + k
                if k % CHUNKS == 0:
                    act.wait_ge(w_loaded[v], 48 * i + 48)
                for f in range(FC):
                    if f == 0:
                        act.wait_ge(y_done, CT * s if k == 0 else CT * s - CT)
                    act.wait_ge(h_done, FC * s + (f + 1))
                    nc.scalar.activation(hT[:, k % 2, f, :], h_ps[:, f % 4, :], ACT.Relu,
                                         bias=b1[:, v, f:f + 1]).then_inc(h_evac, 1)

    @block.vector
    def _(dve):
        with dve.Fori(0, E // 2) as i:
            for k in range(STEPS):
                v, n, s = k // CHUNKS, k % CHUNKS, STEPS * i + k
                dve.wait_ge(y_added, CT * s)
                for q in range(CT):
                    xt = env.x[:, n * CT + q, :]
                    dve.wait_ge(y_done, CT * s + (q + 1))
                    nc.vector.scalar_tensor_tensor(xt, y_ps[:, q, 0:D], gate[:, n * CT + q, bass.ds(2 * i + v, 1)], xt,
                                                   ALU.mult, ALU.add).then_inc(y_added, 1)




def build(nc, args, out):
    kern_dram = nc.dram_tensor("conv_kernels", [B, KW], F32).ap()
    rows = lambda m: m.rearrange("b o s j -> b (o s) j")
    with ExitStack() as ctx:
        env = Env(nc, ctx)
        setup_stage(nc, env, args)
        conv_kernels_stage(nc, env, "hs", args, "L0_xattn", kern_dram)
        conv_attention_stage(nc, env, "c0", args, "L0_xattn", kern_dram, args["mask_SxS_bc0"])
        quant_ffn_stage(nc, env, "qf", args, "L0_ffn")
        latent_attention_stage(nc, env, "lt", args, "L1_xattn")
        routed_ffn_stage(nc, env, "m1", args, "L1_ffn", ACT.Relu, False, 320)
        cross_attention_stage(nc, env, "c2", args, "L2_xattn", rows(args["mask_Bx1xSxS2_bk1"]), None, 1)
        gated_ffn_stage(nc, env, "m2", args, "L2_ffn")
        cross_attention_stage(nc, env, "c3", args, "L3_xattn", rows(args["mask_Bx1xSxS2_ik1"]), args["fside_Bx16xSxS2_0"], 0)
        routed_ffn_stage(nc, env, "m3", args, "L3_ffn", ACT.Gelu, True, None)
        store_stage(nc, env, out)


def kernel(**inputs):
    import numpy as _np
    import concourse.bacc as _bacc
    from concourse import mybir as _mybir
    from concourse.bass_utils import run_bass_kernel_spmd as _run

    nc = _bacc.Bacc("TRN2", target_bir_lowering=False, num_devices=1)
    arrays, args = {}, {}
    for name, value in inputs.items():
        a = _np.ascontiguousarray(value)
        arrays[f"in_{name}_dram"] = a
        args[name] = nc.dram_tensor(f"in_{name}_dram", a.shape, _mybir.dt.from_np(a.dtype), kind="ExternalInput").ap()
    out = nc.dram_tensor("out_0_dram", (B, S, D), F32, kind="ExternalOutput").ap()
    build(nc, args, out)
    return _run(nc, [arrays], core_ids=[0]).results[0]["out_0_dram"]
```

```python
from contextlib import ExitStack

import concourse.bass as bass
from concourse import mybir

ALU = mybir.AluOpType
ACT = mybir.ActivationFunctionType
F32 = mybir.dt.float32
BF16 = mybir.dt.bfloat16
U8 = mybir.dt.uint8
I32 = mybir.dt.int32
U32 = mybir.dt.uint32
AX_X = mybir.AxisListType.X
RMAX = bass.bass_isa.ReduceOp.max

P = 128
B, S, D = 2, 1024, 256
NCTX = 77
H = 16
HD = D // H
T = B * S
TILES = T // P
TPB = S // P
DC = D // P
LN_EPS = 1e-5
NEG = -1e30


def chain(eng, sem, base=0):
    done = [0]

    def step(ins):
        done[0] += 1
        ins.then_inc(sem, 1)
        eng.wait_ge(sem, base + done[0])
        return ins

    step.done = done
    return step


class Stage:

    def __init__(self, nc, ctx, tag):
        self.nc, self.ctx, self.tag, self.sems = nc, ctx, tag, []
        ctx.callback(self.clear)

    def sb(self, name, shape, dt=F32):
        return self.ctx.enter_context(self.nc.sbuf_tensor(f"{self.tag}_{name}", shape, dt))

    def ps(self, name, shape, dt=F32):
        return self.ctx.enter_context(self.nc.psum_tensor(f"{self.tag}_{name}", shape, dt))

    def sem(self, name):
        made = self.ctx.enter_context(self.nc.semaphore(f"{self.tag}_{name}"))
        self.sems.append(made)
        return made

    def clear(self):
        with self.nc.Block() as block:
            @block.gpsimd
            def _(pool):
                runs = []
                for num in sorted(s.num for s in self.sems):
                    if runs and runs[-1].stop == num:
                        runs[-1] = range(runs[-1].start, num + 1)
                    else:
                        runs.append(range(num, num + 1))
                for run in runs:
                    pool.sem_clear(run)


def tile_of(buf, t):
    return buf[:, bass.ds(t, 1), :].rearrange("p a n -> p (a n)")


def setup_stage(nc, env, args):
    with ExitStack() as ctx:
        st = Stage(nc, ctx, "set")
        x_loaded, ctx_loaded = st.sem("x_loaded"), st.sem("ctx_loaded")
        zeroed, made = st.sem("zeroed"), st.sem("made")
        block = ctx.enter_context(nc.Block())

        @block.sync
        def _(sp):
            sp.dma_start(env.x[:], args["x"].rearrange("b (t p) d -> p (b t) d", p=P)).then_inc(x_loaded, 16)
            sp.dma_start(env.ctx_tok[0:NCTX], args["ctx_1024"].rearrange("b t d -> t b d")).then_inc(ctx_loaded, 16)
            sp.wait_ge(x_loaded, 16)
            sp.wait_ge(ctx_loaded, 16)

        @block.gpsimd
        def _(pool):
            nc.gpsimd.memset(env.ident[:], 0.0).then_inc(zeroed, 1)
            nc.gpsimd.memset(env.ones[:], 1.0).then_inc(made, 1)
            nc.gpsimd.memset(env.eps[:], LN_EPS).then_inc(made, 1)
            pool.wait_ge(zeroed, 1)
            nc.gpsimd.affine_select(out=env.ident[:], in_=env.ident[:], compare_op=ALU.not_equal, fill=1.0, base=0,
                                    pattern=[[-1, P]], channel_multiplier=1).then_inc(made, 1)


def row_stats(nc, dve, st, step, src, n, mean, var, stats):
    counted = st.sem("counted")
    with dve.Fori(0, n) as t:
        nc.vector.bn_stats(stats[:, bass.ds(t, 1), :].rearrange("p a n -> p (a n)"), tile_of(src, t)).then_inc(counted, 1)
    dve.wait_ge(counted, n)
    merge_stats(nc, step, mean, var, stats, D)


def merge_stats(nc, step, mean, var, stats, width):
    even, odd = stats[:, :, 1], stats[:, :, 4]
    step(nc.vector.tensor_tensor(mean, even, odd, ALU.add))
    step(nc.vector.tensor_tensor(var, even, odd, ALU.subtract))
    step(nc.vector.tensor_scalar(mean, mean, 0.5, None, ALU.mult))
    step(nc.vector.scalar_tensor_tensor(var, var, 0.25, var, ALU.mult, ALU.mult))
    step(nc.vector.scalar_tensor_tensor(var, stats[:, :, 2], 1.0 / width, var, ALU.mult, ALU.add))
    step(nc.vector.scalar_tensor_tensor(var, stats[:, :, 5], 1.0 / width, var, ALU.mult, ALU.add))


def layernorm_stage(nc, env, tag, src, dst_tok=None, dst_T=None):
    with ExitStack() as ctx:
        st = Stage(nc, ctx, tag)
        stats = st.sb("stats", [P, TILES, 6])
        mean, var, rstd = (st.sb(n, [P, TILES]) for n in ("mean", "var", "rstd"))
        turn = st.sb("turn", [P, 2, D])
        turned = st.ps("turned", [P, 2, 512])
        linked, var_ready, std_ready = st.sem("linked"), st.sem("var_ready"), st.sem("std_ready")
        normed, transposed, evacuated = st.sem("normed"), st.sem("transposed"), st.sem("evacuated")
        kept = st.sem("kept")
        both = dst_tok is not None and dst_T is not None
        block = ctx.enter_context(nc.Block())

        @block.vector
        def _(dve):
            step = chain(dve, linked)
            row_stats(nc, dve, st, step, src, TILES, mean[:], var[:], stats)
            nc.vector.tensor_scalar(var[:], var[:], LN_EPS, None, ALU.add).then_inc(var_ready, 1)
            dve.wait_ge(std_ready, 1)
            step(nc.vector.reciprocal(rstd[:], rstd[:]))

            def tile(t, u, reuse):
                if dst_T is not None and reuse:
                    dve.wait_ge(transposed, t - 1)
                if both and reuse:
                    dve.wait_ge(kept, t - 1)
                out = tile_of(dst_tok, t) if dst_T is None else turn[:, u, :]
                nc.vector.tensor_scalar(out, tile_of(src, t), mean[:, bass.ds(t, 1)], rstd[:, bass.ds(t, 1)],
                                        ALU.subtract, ALU.mult).then_inc(normed, 1)

            for u in range(2):
                tile(u, u, False)
            with dve.Fori(1, TILES // 2) as i:
                for u in range(2):
                    tile(2 * i + u, u, True)
            dve.wait_ge(normed, TILES)

        if both:
            @block.gpsimd
            def _(pool):
                with pool.Fori(0, TILES // 2) as i:
                    for u in range(2):
                        pool.wait_ge(normed, 2 * i + (u + 1))
                        nc.gpsimd.tensor_copy(tile_of(dst_tok, 2 * i + u), turn[:, u, :]).then_inc(kept, 1)
                pool.wait_ge(kept, TILES)

        @block.scalar
        def _(act):
            act.wait_ge(var_ready, 1)
            nc.scalar.activation(rstd[:], var[:], ACT.Sqrt).then_inc(std_ready, 1)
            if dst_T is not None:
                with act.Fori(0, TILES // 2) as i:
                    for u in range(2):
                        t = 2 * i + u
                        act.wait_ge(transposed, t + 1)
                        nc.scalar.copy(dst_T[:, :, bass.ds(t * P, P)],
                                       turned[:, u, 0:D].rearrange("p (c t) -> p c t", c=DC)).then_inc(evacuated, 1)
                act.wait_ge(evacuated, TILES)

        if dst_T is not None:
            @block.tensor
            def _(pe):
                def tile(t, u, reuse):
                    pe.wait_ge(normed, t + 1)
                    if reuse:
                        pe.wait_ge(evacuated, t - 1)
                    for c in range(DC):
                        last = nc.tensor.transpose(turned[:, u, c * P:(c + 1) * P], turn[:, u, c * P:(c + 1) * P],
                                                   env.ident[:])
                    last.then_inc(transposed, 1)

                for u in range(2):
                    tile(u, u, False)
                with pe.Fori(1, TILES // 2) as i:
                    for u in range(2):
                        tile(2 * i + u, u, True)


def add_projection_stage(nc, env, tag, rows, weight, bias):
    with ExitStack() as ctx:
        st = Stage(nc, ctx, tag)
        wo, bo = st.sb("wo", [P, DC, D]), st.sb("bo", [1, D])
        rT = st.sb("rT", [P, 2, DC, P])
        t_ps, y_ps = st.ps("t_ps", [P, 2, 512]), st.ps("y_ps", [P, 2, 512])
        loaded, turned, evacuated, y_done, added = (st.sem(n) for n in ("loaded", "turned", "evacuated", "y_done", "added"))
        block = ctx.enter_context(nc.Block())

        @block.sync
        def _(sp):
            sp.dma_start(wo[:], weight.rearrange("(c p) n -> p c n", p=P)).then_inc(loaded, 16)
            sp.dma_start(bo[:], bias.rearrange("(a n) -> a n", a=1)).then_inc(loaded, 16)

        @block.tensor
        def _(pe):
            def turn(t):
                if t >= 2:
                    pe.wait_ge(evacuated, t - 1)
                for c in range(DC):
                    last = nc.tensor.transpose(t_ps[:, t % 2, c * P:(c + 1) * P], rows[:, t, c * P:(c + 1) * P], env.ident[:])
                last.then_inc(turned, 1)

            turn(0)
            pe.wait_ge(loaded, 32)
            for t in range(TILES):
                if t + 1 < TILES:
                    turn(t + 1)
                pe.wait_ge(evacuated, t + 1)
                if t >= 2:
                    pe.wait_ge(added, t - 1)
                nc.tensor.matmul(y_ps[:, t % 2, 0:D], env.ones[0:1, :], bo[:], start=True, stop=False)
                for c in range(DC):
                    last = nc.tensor.matmul(y_ps[:, t % 2, 0:D], rT[:, t % 2, c, :], wo[:, c, :], start=False, stop=c == DC - 1)
                last.then_inc(y_done, 1)

        @block.scalar
        def _(act):
            for t in range(TILES):
                act.wait_ge(turned, t + 1)
                if t >= 2:
                    act.wait_ge(y_done, t - 1)
                nc.scalar.copy(rT[:, t % 2], t_ps[:, t % 2, 0:D].rearrange("p (c t) -> p c t", c=DC)).then_inc(evacuated, 1)

        @block.vector
        def _(dve):
            for t in range(TILES):
                dve.wait_ge(y_done, t + 1)
                nc.vector.tensor_tensor(env.x[:, t, :], env.x[:, t, :], y_ps[:, t % 2, 0:D], ALU.add).then_inc(added, 1)


def store_stage(nc, env, out):
    with ExitStack() as ctx:
        st = Stage(nc, ctx, "fin")
        stored = st.sem("stored")
        block = ctx.enter_context(nc.Block())

        @block.sync
        def _(sp):
            sp.dma_start(out.rearrange("b (t p) d -> p (b t) d", p=P), env.x[:]).then_inc(stored, 16)
            sp.wait_ge(stored, 16)


class Env:

    def __init__(self, nc, ctx):
        sb = lambda name, shape, dt=F32: ctx.enter_context(nc.sbuf_tensor(name, shape, dt))
        self.x = sb("x_res", [P, TILES, D])
        self.ctx_tok = sb("ctx_tok", [P, B, D])
        self.ident = sb("ident", [P, P])
        self.ones = sb("ones", [P, P])
        self.eps = sb("eps", [P, 1])
        sems = lambda name, n: [[ctx.enter_context(nc.semaphore(f"{name}{k}_{i}")) for i in range(n)] for k in range(2)]
        self.scattered = sems("rows_scattered", 1)
        self.stored = sems("expert_rows_stored", 2)
        self.gathered = sems("expert_rows_gathered", TILES)



C = 2 * D
CC = C // P
CQ = C // 4
TAPS = 9
KW = H * TAPS


def conv_kernels_stage(nc, env, tag, args, name, kern_dram):
    w = lambda n: args[f"{name}_{n}"]
    with ExitStack() as ctx:
        st = Stage(nc, ctx, tag)
        sb, ps, sem = st.sb, st.ps, st.sem
        hw, w1, w2 = sb("hw", [P, DC, C]), sb("w1", [P, CC, CQ]), sb("w2", [P, 1])
        kw1, kw2 = sb("kw1", [P, CC, D]), sb("kw2", [P, DC, KW])
        hb, hg, hs = (sb(n, [P, C]) for n in ("hb", "hg", "hs"))
        b1, b2 = sb("b1", [P, 1]), sb("b2", [1, 1])
        kb, kg, ks, kb2 = sb("kb", [B, D]), sb("kg", [B, D]), sb("ks", [B, D]), sb("kb2", [B, KW])
        ctxT = sb("ctxT", [P, DC, B * NCTX])
        eh = sb("eh", [P, B, C])
        ehT = sb("ehT", [P, CC, B * NCTX])
        stats, mean, var, rstd = sb("stats", [P, B, 6]), sb("mean", [P, B]), sb("var", [P, B]), sb("rstd", [P, B])
        kstats, kmean, kvar, krstd = (sb(n, s) for n, s in (("kstats", [B, 1, 6]), ("kmean", [B, 1]), ("kvar", [B, 1]), ("krstd", [B, 1])))
        a1 = sb("a1", [P, B * NCTX])
        aw, one = sb("aw", [1, B, NCTX]), sb("one", [1, B])
        awc = sb("awc", [P, B])
        ccT = sb("ccT", [P, CC, B])
        kh = sb("kh", [B, D])
        khT = sb("khT", [P, DC, B])
        kern, kcol = sb("kern", [B, KW]), sb("kcol", [B, H])
        ps_a, ps_b = ps("ps_a", [P, 512]), ps("ps_b", [P, B, 512])
        loaded, on_pe, on_act, linked, ready, stored = (sem(n) for n in ("loaded", "on_pe", "on_act", "linked", "ready", "stored"))
        block = ctx.enter_context(nc.Block())
        tokens = slice(0, NCTX)
        LOADED, HIST, NORMED, SHIFTED, WEIGHTS, WCOL, POOLED, KHID, KNORMED, KVEC, KSHIFTED, KERNELS = range(1, 13)

        @block.sync
        def _(sp):
            mat = lambda n: w(n).rearrange("(c p) n -> p c n", p=P)
            wide = lambda n, rows: w(n).partition_broadcast(rows)
            loads = [(hw, mat("hist_W")), (w1, mat("ctx_W1")), (w2, w("ctx_W2")), (kw1, mat("kg_W1")), (kw2, mat("kg_W2")),
                     (hb, wide("hist_b", P)), (hg, wide("hist_ln_g", P)), (hs, wide("hist_ln_b", P)),
                     (b1, w("ctx_b1").rearrange("(p a) -> p a", a=1)), (b2, w("ctx_b2").rearrange("(p a) -> p a", a=1)),
                     (kb, wide("kg_b1", B)), (kg, wide("kg_ln_g", B)), (ks, wide("kg_ln_b", B)), (kb2, wide("kg_b2", B))]
            for dst, src in loads:
                sp.dma_start(dst[:], src).then_inc(loaded, 16)
            sp.wait_ge(loaded, 16 * len(loads))
            sp.sem_inc(ready, 1)
            sp.wait_ge(ready, KERNELS)
            sp.dma_start(kern_dram, kern[:]).then_inc(stored, 16)
            sp.wait_ge(stored, 16)

        @block.tensor
        def _(pe):
            for b in range(B):
                for c in range(DC):
                    last = nc.tensor.transpose(ps_a[:, (c * B + b) * NCTX:(c * B + b + 1) * NCTX],
                                               env.ctx_tok[tokens, b, c * P:(c + 1) * P], env.ident[tokens, tokens])
            last.then_inc(on_pe, 1)
            pe.wait_ge(on_act, 1)
            pe.wait_ge(ready, LOADED)
            for b in range(B):
                for c in range(DC):
                    last = nc.tensor.matmul(ps_b[tokens, b, :], ctxT[:, c, b * NCTX:(b + 1) * NCTX], hw[:, c, :], start=c == 0,
                                            stop=c == DC - 1)
            last.then_inc(on_pe, 1)
            pe.wait_ge(on_act, 3)
            for b in range(B):
                for c in range(CC):
                    last = nc.tensor.transpose(ps_b[:, b, c * NCTX:(c + 1) * NCTX], eh[tokens, b, c * P:(c + 1) * P],
                                               env.ident[tokens, tokens])
            last.then_inc(on_pe, 1)
            pe.wait_ge(on_act, 5)
            for c in range(CC):
                last = nc.tensor.matmul(ps_a[:, 0:B * NCTX], w1[:, c, :], ehT[:, c, :], start=c == 0, stop=c == CC - 1)
            last.then_inc(on_pe, 1)
            pe.wait_ge(on_act, 6)
            nc.tensor.matmul(ps_a[0:1, 0:B * NCTX], w2[:], a1[:], start=True, stop=True).then_inc(on_pe, 1)
            pe.wait_ge(ready, WEIGHTS)
            for b in range(B):
                last = nc.tensor.matmul(ps_a[tokens, b:b + 1], aw[0:1, b, :], env.ones[0:1, 0:1], start=True, stop=True)
            last.then_inc(on_pe, 1)
            pe.wait_ge(ready, WCOL)
            for c in range(CC):
                for b in range(B):
                    last = nc.tensor.matmul(ps_a[:, c * B + b:c * B + b + 1], eh[tokens, b, c * P:(c + 1) * P], awc[tokens, b:b + 1],
                                            start=True, stop=True)
            last.then_inc(on_pe, 1)
            pe.wait_ge(ready, POOLED)
            for c in range(CC):
                last = nc.tensor.matmul(ps_a[0:B, 0:D], ccT[:, c, :], kw1[:, c, :], start=c == 0, stop=c == CC - 1)
            last.then_inc(on_pe, 1)
            pe.wait_ge(on_act, 9)
            for c in range(DC):
                last = nc.tensor.transpose(ps_a[:, c * B:(c + 1) * B], kh[:, c * P:(c + 1) * P], env.ident[0:B, 0:B])
            last.then_inc(on_pe, 1)
            pe.wait_ge(ready, KVEC)
            for c in range(DC):
                last = nc.tensor.matmul(ps_a[0:B, 0:KW], khT[:, c, :], kw2[:, c, :], start=c == 0, stop=c == DC - 1)
            last.then_inc(on_pe, 1)

        @block.scalar
        def _(act):
            act.wait_ge(on_pe, 1)
            nc.scalar.copy(ctxT[:], ps_a[:, 0:DC * B * NCTX].rearrange("p (c t) -> p c t", c=DC)).then_inc(on_act, 1)
            act.wait_ge(ready, HIST)
            nc.scalar.activation(rstd[tokens], var[tokens], ACT.Sqrt).then_inc(on_act, 1)
            act.wait_ge(ready, NORMED)
            nc.scalar.activation(eh[tokens], eh[tokens], ACT.Gelu).then_inc(on_act, 1)
            act.wait_ge(on_pe, 3)
            for b in range(B):
                nc.scalar.copy(ehT[:, :, b * NCTX:(b + 1) * NCTX],
                               ps_b[:, b, 0:CC * NCTX].rearrange("p (c t) -> p c t", c=CC)).then_inc(on_act, 1)
            act.wait_ge(on_pe, 4)
            nc.scalar.activation(a1[:], ps_a[:, 0:B * NCTX], ACT.Gelu, bias=b1[:, 0:1]).then_inc(on_act, 1)
            act.wait_ge(ready, SHIFTED)
            nc.scalar.activation(aw[:], aw[:], ACT.Exp).then_inc(on_act, 1)
            act.wait_ge(ready, KHID)
            nc.scalar.activation(krstd[:], kvar[:], ACT.Sqrt).then_inc(on_act, 1)
            act.wait_ge(ready, KNORMED)
            nc.scalar.activation(kh[:], kh[:], ACT.Gelu).then_inc(on_act, 1)
            act.wait_ge(ready, KSHIFTED)
            nc.scalar.activation(kern[:], kern[:], ACT.Exp).then_inc(on_act, 1)

        @block.vector
        def _(dve):
            step = chain(dve, linked)
            tt = lambda o, a, b_, op: step(nc.vector.tensor_tensor(o, a, b_, op))

            def finish(ins):
                ins.then_inc(ready, 1)

            dve.wait_ge(ready, LOADED)
            dve.wait_ge(on_pe, 2)
            for b in range(B):
                tt(eh[tokens, b, :], ps_b[tokens, b, :], hb[tokens, :], ALU.add)
            for b in range(B):
                step(nc.vector.bn_stats(stats[tokens, b, :], eh[tokens, b, :]))
            merge_stats(nc, step, mean[tokens], var[tokens], stats[tokens], C)
            finish(nc.vector.tensor_scalar(var[tokens], var[tokens], LN_EPS, None, ALU.add))
            dve.wait_ge(on_act, 2)
            step(nc.vector.reciprocal(rstd[tokens], rstd[tokens]))
            for b in range(B):
                e = eh[tokens, b, :]
                step(nc.vector.tensor_scalar(e, e, mean[tokens, b:b + 1], rstd[tokens, b:b + 1], ALU.subtract, ALU.mult))
                tt(e, e, hg[tokens, :], ALU.mult)
                if b == 0:
                    tt(e, e, hs[tokens, :], ALU.add)
                else:
                    finish(nc.vector.tensor_tensor(e, e, hs[tokens, :], ALU.add))
            dve.wait_ge(on_pe, 5)
            step(nc.vector.tensor_scalar(aw[:].rearrange("p b t -> p (b t)"), ps_a[0:1, 0:B * NCTX], b2[:, 0:1], None, ALU.add))
            step(nc.vector.tensor_reduce(one[:], aw[:], AX_X, ALU.max))
            finish(nc.vector.tensor_tensor(aw[:], aw[:], one[:].unsqueeze(2).to_broadcast([1, B, NCTX]), ALU.subtract))
            dve.wait_ge(on_act, 7)
            step(nc.vector.tensor_reduce(one[:], aw[:], AX_X, ALU.add))
            step(nc.vector.reciprocal(one[:], one[:]))
            finish(nc.vector.tensor_tensor(aw[:], aw[:], one[:].unsqueeze(2).to_broadcast([1, B, NCTX]), ALU.mult))
            dve.wait_ge(on_pe, 6)
            finish(nc.vector.tensor_copy(awc[tokens], ps_a[tokens, 0:B]))
            dve.wait_ge(on_pe, 7)
            finish(nc.vector.tensor_copy(ccT[:].rearrange("p c b -> p (c b)"), ps_a[:, 0:CC * B]))
            dve.wait_ge(on_pe, 8)
            tt(kh[:], ps_a[0:B, 0:D], kb[:], ALU.add)
            step(nc.vector.bn_stats(kstats[:, 0, :], kh[:]))
            merge_stats(nc, step, kmean[:], kvar[:], kstats[:], D)
            finish(nc.vector.tensor_scalar(kvar[:], kvar[:], LN_EPS, None, ALU.add))
            dve.wait_ge(on_act, 8)
            step(nc.vector.reciprocal(krstd[:], krstd[:]))
            step(nc.vector.tensor_scalar(kh[:], kh[:], kmean[:, 0:1], krstd[:, 0:1], ALU.subtract, ALU.mult))
            tt(kh[:], kh[:], kg[:], ALU.mult)
            finish(nc.vector.tensor_tensor(kh[:], kh[:], ks[:], ALU.add))
            dve.wait_ge(on_pe, 9)
            finish(nc.vector.tensor_copy(khT[:].rearrange("p c b -> p (c b)"), ps_a[:, 0:DC * B]))
            dve.wait_ge(on_pe, 10)
            taps = kern[:].rearrange("p (h k) -> p h k", k=TAPS)
            over = kcol[:].unsqueeze(2).to_broadcast([B, H, TAPS])
            tt(kern[:], ps_a[0:B, 0:KW], kb2[:], ALU.add)
            step(nc.vector.tensor_reduce(kcol[:], taps, AX_X, ALU.max))
            finish(nc.vector.tensor_tensor(taps, taps, over, ALU.subtract))
            dve.wait_ge(on_act, 10)
            step(nc.vector.tensor_reduce(kcol[:], taps, AX_X, ALU.add))
            step(nc.vector.reciprocal(kcol[:], kcol[:]))
            finish(nc.vector.tensor_tensor(taps, taps, over, ALU.mult))



TAP = 3
ROWS = P - TAP + 1
WINDOWS = -(-S // ROWS)
PAD = ROWS * WINDOWS + TAP - 1
HEADS = B * H


def conv_attention_stage(nc, env, tag, args, name, kern_dram, mask):
    w = lambda n: args[f"{name}_{n}"]
    dram = lambda n, shape: nc.dram_tensor(f"{tag}_{n}", shape, F32).ap()
    q_dram, k_dram = dram("q", [B, D, PAD]), dram("k", [B, D, PAD])
    mixed_dram = dram("mixed", [B, TAP, D, S])
    with ExitStack() as outer:
        sto = Stage(nc, outer, tag)
        v = sto.sb("v", [P, HEADS, TPB, HD])
        spill = sto.sb("spill", [P, 2, HEADS, TPB])
        other = sto.sb("other", [1, 1], I32)
        with ExitStack() as ctx:
            project_qkv(nc, env, Stage(nc, ctx, tag + "p"), ctx, w, kern_dram, q_dram, k_dram, mixed_dram, v, spill)
        with ExitStack() as ctx:
            compare_mask(nc, env, Stage(nc, ctx, tag + "f"), ctx, mask, other)
        o_tok = sto.sb("o_tok", [P, HEADS, TPB, HD])
        with ExitStack() as ctx:
            st = Stage(nc, ctx, tag + "a")
            banks = st.ps("banks", [P, 8, 512])
            causal = causal_mask(nc, env, st, banks, q_dram, mixed_dram, v, spill, o_tok)
            general = any_mask(nc, env, st, tag, banks, kern_dram, mask, q_dram, k_dram, v, o_tok)
            block = ctx.enter_context(nc.Block())

            def choose(eng, way):
                is_other = eng.value_load(other[0:1, 0:1], min_val=0, max_val=1)
                with eng.If(is_other < 1):
                    causal[way](eng)
                with eng.Else():
                    general[way](eng)

            @block.sync
            def _(sp):
                choose(sp, "sync")

            @block.gpsimd
            def _(pool):
                choose(pool, "gpsimd")

            @block.tensor
            def _(pe):
                choose(pe, "tensor")

            @block.vector
            def _(dve):
                choose(dve, "vector")

            @block.scalar
            def _(act):
                choose(act, "scalar")
        with ExitStack() as ctx:
            project_out(nc, env, Stage(nc, ctx, tag + "o"), ctx, w, o_tok)


def compare_mask(nc, env, st, ctx, mask, other):
    given = st.sb("given", [P, TPB, S], U8)
    after = st.sb("after", [P, TPB, S])
    worst = st.sb("worst", [P, 1])
    sum_ps = st.ps("sum_ps", [P, 512])
    loaded, ones_set, after_made, differs, found, summed, told = (
        st.sem(n) for n in ("loaded", "ones_set", "after_made", "differs", "found", "summed", "told"))
    block = ctx.enter_context(nc.Block())

    @block.sync
    def _(sp):
        sp.dma_start(given[:], mask.rearrange("(t p) j -> p t j", p=P)).then_inc(loaded, 16)
        sp.wait_ge(loaded, 16)

    @block.gpsimd
    def _(pool):
        nc.gpsimd.memset(after[:], 1.0).then_inc(ones_set, 1)
        pool.wait_ge(ones_set, 1)
        nc.gpsimd.affine_select(out=after[:], in_=after[:], compare_op=ALU.is_gt, fill=0.0, base=0,
                                pattern=[[-P, TPB], [1, S]], channel_multiplier=-1).then_inc(after_made, 1)

    @block.vector
    def _(dve):
        dve.wait_ge(loaded, 16)
        dve.wait_ge(after_made, 1)
        nc.vector.tensor_tensor(after[:], given[:], after[:], ALU.not_equal).then_inc(differs, 1)
        dve.wait_ge(differs, 1)
        nc.vector.tensor_reduce(worst[:], after[:].rearrange("p t j -> p (t j)"), AX_X, ALU.max).then_inc(found, 1)
        dve.wait_ge(summed, 1)
        nc.vector.tensor_scalar(other[:], sum_ps[0:1, 0:1], 1.0, None, ALU.min).then_inc(told, 1)
        dve.wait_ge(told, 1)

    @block.tensor
    def _(pe):
        pe.wait_ge(found, 1)
        nc.tensor.matmul(sum_ps[0:1, 0:1], worst[:], env.ones[:, 0:1], start=True, stop=True).then_inc(summed, 1)


def project_qkv(nc, env, st, ctx, w, kern_dram, q_dram, k_dram, mixed_dram, v, spill):
    xT = st.sb("xT", [P, DC, T])
    layernorm_stage(nc, env, st.tag + "l", env.x, dst_T=xT)
    wq, wk, wv = (st.sb(n, [P, DC, D]) for n in ("wq", "wk", "wv"))
    qk = st.sb("qk", [P, 2, B, DC, PAD])
    half = H // DC
    coef = st.sb("coef", [P, B, DC, TAP * TAP])
    ind = st.sb("ind", [P, half])
    mix = st.sb("mix", [P, 2, S])
    near, diag, before = (st.sb(n, [P, S]) for n in ("near", "diag", "before"))
    y_ps, v_ps, d_ps = st.ps("y_ps", [P, 4, 512]), st.ps("v_ps", [P, 2, 512]), st.ps("d_ps", [P, 512])
    loaded, zeroed, y_done, y_evac, v_done, v_evac, stored, coef_loaded, ones_set, ind_lower, ind_made = (
        st.sem(n) for n in ("loaded", "zeroed", "y_done", "y_evac", "v_done", "v_evac", "stored", "coef_loaded", "ones_set",
                            "ind_lower", "ind_made"))
    begun, mixed, mix_parts, crossed, spills, spill_done, spill_evac = (
        st.sem(n) for n in ("begun", "mixed", "mix_parts", "crossed", "spills", "spill_done", "spill_evac"))
    mix_stored = [st.sem(f"mix_stored{u}") for u in range(2)]
    parts = [(b, c) for b in range(B) for c in range(DC)]
    mixes = [(b, c, a) for b, c in parts for a in range(TAP)]
    block = ctx.enter_context(nc.Block())
    HALF = S // 512
    jobs = [(k, b, c, n) for k in range(2) for b in range(B) for c in range(DC) for n in range(HALF)]

    @block.sync
    def _(sp):
        for dst, src in ((wq, "Wq"), (wk, "Wk"), (wv, "Wv")):
            sp.dma_start(dst[:], w(src).rearrange("(c p) n -> p c n", p=P)).then_inc(loaded, 16)
        kern = kern_dram.rearrange("b (c h k) -> h b c k", c=DC, h=half)
        for h in range(half):
            for b in range(B):
                sp.dma_start(coef[h * HD:(h + 1) * HD, b], kern[h, b].partition_broadcast(HD)).then_inc(coef_loaded, 16)
        sp.wait_ge(zeroed, 2)
        for k, dram in enumerate((q_dram, k_dram)):
            sp.wait_ge(y_evac, (k + 1) * len(jobs) // 2)
            sp.dma_start(dram.rearrange("b (c p) t -> p b c t", p=P), qk[:, k]).then_inc(stored, 16)
        for i, (b, c, a) in enumerate(mixes):
            sp.wait_ge(mixed, i + 1)
            sp.dma_start(mixed_dram[b, a, c * P:(c + 1) * P, :], mix[:, i % 2, :]).then_inc(mix_stored[i % 2], 16)
        for u in range(2):
            sp.wait_ge(mix_stored[u], 8 * len(mixes))
        sp.wait_ge(stored, 32)

    @block.gpsimd
    def _(pool):
        nc.gpsimd.memset(qk[:, :, :, :, 0:1], 0.0).then_inc(zeroed, 1)
        nc.gpsimd.memset(qk[:, :, :, :, S + 1:PAD], 0.0).then_inc(zeroed, 1)
        nc.gpsimd.memset(ind[:], 1.0).then_inc(ones_set, 1)
        pool.wait_ge(ones_set, 1)
        nc.gpsimd.affine_select(out=ind[:], in_=ind[:], compare_op=ALU.is_ge, fill=0.0, base=0,
                                pattern=[[-HD, half]], channel_multiplier=1).then_inc(ind_lower, 1)
        pool.wait_ge(ind_lower, 1)
        nc.gpsimd.affine_select(out=ind[:], in_=ind[:], compare_op=ALU.is_ge, fill=0.0, base=HD - 1,
                                pattern=[[HD, half]], channel_multiplier=-1).then_inc(ind_made, 1)

    @block.tensor
    def _(pe):
        pe.wait_ge(loaded, 48)
        for i, (k, b, c, n) in enumerate(jobs):
            if i >= 4:
                pe.wait_ge(y_evac, i - 3)
            for d in range(DC):
                last = nc.tensor.matmul(y_ps[:, i % 4, :], (wq, wk)[k][:, d, c * P:(c + 1) * P],
                                        xT[:, d, b * S + n * 512:b * S + (n + 1) * 512], start=d == 0, stop=d == DC - 1)
            last.then_inc(y_done, 1)
        for t in range(TILES):
            if t >= 2:
                pe.wait_ge(v_evac, t - 1)
            for d in range(DC):
                last = nc.tensor.matmul(v_ps[:, t % 2, 0:D], xT[:, d, t * P:(t + 1) * P], wv[:, d, :], start=d == 0,
                                        stop=d == DC - 1)
            last.then_inc(v_done, 1)
        pe.wait_ge(ind_made, 1)
        for i, (b, c) in enumerate(parts):
            pe.wait_ge(spills, 2 * i + 2)
            for k, feats in enumerate((diag, before)):
                for n in range(TPB):
                    at = ((k * B * DC + i) * TPB + n) * half
                    last = nc.tensor.matmul(d_ps[:, at:at + half], feats[:, n * P:(n + 1) * P], ind[:], start=True, stop=True)
            last.then_inc(spill_done, 1)

    @block.scalar
    def _(act):
        for i, (k, b, c, n) in enumerate(jobs):
            act.wait_ge(y_done, i + 1)
            nc.scalar.mul(qk[:, k, b, c, 1 + n * 512:1 + (n + 1) * 512], y_ps[:, i % 4, :],
                          HD ** -0.5 if k == 0 else 1.0).then_inc(y_evac, 1)
        act.wait_ge(y_evac, len(jobs))
        act.wait_ge(coef_loaded, 16 * half * B)
        act.wait_ge(zeroed, 2)
        for i, (b, c, a) in enumerate(mixes):
            if i >= 2:
                act.wait_ge(mix_stored[i % 2], 16 * (i // 2))
            nc.scalar.activation(mix[:, i % 2, :], qk[:, 1, b, c, 0:S], ACT.Identity,
                                 scale=coef[:, b, c, a * TAP:a * TAP + 1]).then_inc(begun, 1)

    @block.vector
    def _(dve):
        for t in range(TILES):
            dve.wait_ge(v_done, t + 1)
            b, n = divmod(t, TPB)
            nc.vector.tensor_copy(v[:, b * H:(b + 1) * H, n, :],
                                  v_ps[:, t % 2, 0:D].rearrange("p (h d) -> p h d", h=H)).then_inc(v_evac, 1)
        dve.wait_ge(y_evac, len(jobs))
        dve.wait_ge(coef_loaded, 16 * half * B)
        dve.wait_ge(zeroed, 2)
        for i, (b, c, a) in enumerate(mixes):
            row, keys = mix[:, i % 2, :], qk[:, 1, b, c]
            dve.wait_ge(begun, i + 1)
            nc.vector.scalar_tensor_tensor(row, keys[:, 1:S + 1], coef[:, b, c, a * TAP + 1:a * TAP + 2], row, ALU.mult,
                                           ALU.add).then_inc(mix_parts, 1)
            dve.wait_ge(mix_parts, i + 1)
            nc.vector.scalar_tensor_tensor(row, keys[:, 2:S + 2], coef[:, b, c, a * TAP + 2:a * TAP + 3], row, ALU.mult,
                                           ALU.add).then_inc(mixed, 1)
        step = chain(dve, crossed)
        for i, (b, c) in enumerate(parts):
            q, k, tap = qk[:, 0, b, c], qk[:, 1, b, c], lambda n: coef[:, b, c, n:n + 1]
            if i:
                dve.wait_ge(spill_done, i)
            step(nc.vector.tensor_tensor(near[:], q[:, 0:S], k[:, 1:S + 1], ALU.mult))
            step(nc.vector.tensor_scalar(diag[:], q[:, 0:S], tap(2), None, ALU.mult))
            step(nc.vector.scalar_tensor_tensor(diag[:], q[:, 1:S + 1], tap(TAP + 2), diag[:], ALU.mult, ALU.add))
            step(nc.vector.tensor_tensor(diag[:], diag[:], k[:, 2:S + 2], ALU.mult))
            nc.vector.scalar_tensor_tensor(diag[:], near[:], tap(1), diag[:], ALU.mult, ALU.add).then_inc(spills, 1)
            nc.vector.tensor_scalar(before[:], near[:], tap(2), None, ALU.mult).then_inc(spills, 1)
        dve.wait_ge(spill_done, len(parts))
        for k in range(2):
            for i in range(len(parts)):
                at = (k * len(parts) + i) * TPB * half
                nc.vector.tensor_copy(spill[:, k, i * half:(i + 1) * half, :].rearrange("p h t -> p t h"),
                                      d_ps[:, at:at + TPB * half].rearrange("p (t h) -> p t h", t=TPB)).then_inc(spill_evac, 1)
        dve.wait_ge(spill_evac, 2 * len(parts))


def causal_mask(nc, env, st, banks, q_dram, mixed_dram, v, spill, o_tok):
    sb, sem = lambda n, *a: st.sb("tri_" + n, *a), lambda n: st.sem("tri_" + n)
    FEATS = TAP * HD
    PAIRS_IN = 2
    ROUNDS = HEADS // (2 * PAIRS_IN)
    order = [(2 * r + u, (TPB - 1 - m, m)[u]) for r in range(PAIRS_IN) for m in range(TPB) for u in range(2)]
    STEPS = len(order)
    groups = [[range(a, min(a + 4, n + 1)) for a in range(0, n + 1, 4)] for _, n in order]
    first = [sum(len(g) for g in groups[:k]) for k in range(STEPS + 1)]
    GROUPS = first[-1]
    AHEAD = 2
    WIN = P + 1
    qs, ks = sb("qs", [FEATS, 2 * PAIRS_IN, S]), sb("ks", [FEATS, 2 * PAIRS_IN, S])
    own, prev, later = sb("own", [P, WIN]), sb("prev", [P, WIN]), sb("later", [P, WIN])
    off = sb("off", [P, 2 * PAIRS_IN, 2, TPB])
    edge, part = sb("edge", [P, 2, WIN]), sb("part", [P, WIN])
    pr = sb("pr", [P, 2, S])
    pT = sb("pT", [P, 2, S])
    ntop, total, inv = (sb(n, [P, 2]) for n in ("ntop", "total", "inv"))
    s_ps = lambda k: banks[:, 2 * (k % 2):2 * (k % 2) + 2, :].rearrange("p a n -> p (a n)")
    t_ps = lambda g: banks[:, 4 + g % 2, :]
    o_ps = lambda k: banks[:, 6 + k % 2, 0:HD]
    staged = [sem(f"staged{r}") for r in range(PAIRS_IN)]
    t_evac = [sem(f"t_evac{u}") for u in range(2)]
    shapes_zero, shapes, off_ready, edge_part, edge_made, scored, edged, top_ready, exped = (
        sem(n) for n in ("shapes_zero", "shapes", "off_ready", "edge_part", "edge_made", "scored", "edged", "top_ready", "exped"))
    turned, inv_ready, o_done, o_evac, tables = (sem(n) for n in ("turned", "inv_ready", "o_done", "o_evac", "tables"))

    def rounds(eng, body):
        with eng.Fori(0, ROUNDS - 1) as i:
            body(i, False)
        body(ROUNDS - 1, True)

    def on_sync(sp):
        q = q_dram.rearrange("b (h f) t -> (b h) f t", h=H)
        m = mixed_dram.rearrange("b a (h f) t -> a b h f t", h=H)
        per_batch = ROUNDS // B

        def stage(b, i, r):
            for u in range(2 * r, 2 * r + 2):
                h = (i - b * per_batch) * (2 * PAIRS_IN) + u
                for a in range(TAP):
                    rows = slice(a * HD, (a + 1) * HD)
                    sp.dma_start(qs[rows, u, :], q[bass.ds(h + b * H, 1), :, a:a + S].rearrange("x f t -> (x f) t")).then_inc(staged[r], 16)
                    sp.dma_start(ks[rows, u, :], m[a, b, bass.ds(h, 1)].rearrange("x f t -> (x f) t")).then_inc(staged[r], 16)

        for r in range(PAIRS_IN):
            stage(0, 0, r)
        for b in range(B):
            with sp.Fori(max(1, b * per_batch), (b + 1) * per_batch) as i:
                for r in range(PAIRS_IN):
                    sp.wait_ge(scored, STEPS * i + (STEPS // PAIRS_IN * (r + 1) - STEPS))
                    stage(b, i, r)

    def on_gpsimd(pool):
        nc.gpsimd.memset(own[:], 0.0).then_inc(shapes_zero, 1)
        nc.gpsimd.memset(prev[:], 0.0).then_inc(shapes_zero, 1)
        nc.gpsimd.memset(later[:], 0.0).then_inc(shapes_zero, 1)
        pool.wait_ge(shapes_zero, 3)
        nc.gpsimd.affine_select(out=own[:], in_=own[:], compare_op=ALU.not_equal, fill=-1.0, base=1, pattern=[[-1, WIN]],
                                channel_multiplier=1).then_inc(shapes, 1)
        nc.gpsimd.affine_select(out=prev[:], in_=prev[:], compare_op=ALU.not_equal, fill=-1.0, base=0, pattern=[[-1, WIN]],
                                channel_multiplier=1).then_inc(shapes, 1)
        nc.gpsimd.affine_select(out=later[:], in_=later[:], compare_op=ALU.is_ge, fill=NEG, base=1, pattern=[[-1, WIN]],
                                channel_multiplier=1).then_inc(shapes, 1)
        pool.wait_ge(shapes, 3)

        def body(i, last):
            pool.wait_ge(edge_made, STEPS * i)
            for u in range(2 * PAIRS_IN):
                head = bass.ds(i * (2 * PAIRS_IN) + u, 1)
                nc.gpsimd.tensor_copy(off[:, u], spill[:, :, head, :].rearrange("p k a t -> p k (a t)")).then_inc(off_ready, 1)
            pool.wait_ge(off_ready, 2 * PAIRS_IN * i + 2 * PAIRS_IN)
            for k, (u, n) in enumerate(order):
                s = STEPS * i + k
                win = edge[:, k % 2, :]
                pool.wait_ge(edge_made, s)
                pool.wait_ge(edged, s + 1)
                nc.gpsimd.tensor_tensor(win, own[:], off[:, u, 0, n:n + 1].to_broadcast([P, WIN]), ALU.mult).then_inc(edge_part, 1)
                nc.gpsimd.tensor_tensor(part[:], prev[:], off[:, u, 1, n:n + 1].to_broadcast([P, WIN]), ALU.mult).then_inc(edge_part, 1)
                pool.wait_ge(edge_part, 3 * s + 2)
                nc.gpsimd.tensor_tensor(win, win, part[:], ALU.add).then_inc(edge_part, 1)
                pool.wait_ge(edge_part, 3 * s + 3)
                nc.gpsimd.tensor_tensor(win, win, later[:], ALU.add).then_inc(edge_made, 1)

        rounds(pool, body)

    def on_tensor(pe):
        def score(i, k):
            u, n = order[k % STEPS]
            if k % STEPS % (STEPS // PAIRS_IN) == 0:
                r = u // 2
                pe.wait_ge(staged[r], (i + k // STEPS) * (16 * 4 * TAP) + 16 * 4 * TAP)
            pe.wait_ge(exped, STEPS * i + (k + 1))
            keys = (n + 1) * P
            for a in range(0, keys, 512):
                z = min(a + 512, keys)
                last = nc.tensor.matmul(s_ps(k)[:, a:z], qs[:, u, n * P:(n + 1) * P], ks[:, u, a:z], start=True, stop=True)
            last.then_inc(scored, 1)

        def turn(i, k):
            pe.wait_ge(exped, STEPS * i + (k + 1 + AHEAD))
            for g, tiles in enumerate(groups[k]):
                at = first[k] + g
                pe.wait_ge(t_evac[at % 2], GROUPS // 2 * i + at // 2)
                for j in tiles:
                    last = nc.tensor.transpose(t_ps(at)[:, (j - tiles[0]) * P:(j - tiles[0] + 1) * P], pr[:, k % 2, j * P:(j + 1) * P],
                                               env.ident[:])
                    if j == tiles[-1]:
                        last.then_inc(turned, 1)
                    yield

        def weigh(i, k):
            u, n = order[k]
            for at in range(first[k], first[k + 1]):
                pe.wait_ge(t_evac[at % 2], GROUPS // 2 * i + (at // 2 + 1))
            pe.wait_ge(o_evac, STEPS * i + (k + 1))
            head = bass.ds(i * (2 * PAIRS_IN) + u, 1)
            for j in range(n + 1):
                last = nc.tensor.matmul(o_ps(k), pT[:, k % 2, j * P:(j + 1) * P], v[:, head, j, :].rearrange("p a d -> p (a d)"),
                                        start=j == 0, stop=j == n)
                if j == n:
                    last.then_inc(o_done, 1)
                yield

        def by_turns(*works):
            works = list(works)
            while works:
                for work in list(works):
                    if next(work, works) is works:
                        works.remove(work)

        pe.sem_inc(turned, AHEAD)
        pe.sem_inc(o_done, AHEAD)
        score(0, 0)

        def body(i, last):
            for k in range(STEPS):
                if k + 1 < STEPS or not last:
                    score(i, k + 1)
                by_turns(*[weigh(i, k - 1)] * (k > 0), turn(i, k))
            by_turns(weigh(i, STEPS - 1))

        rounds(pe, body)

    def copy_turned(eng, copy, i, k, which):
        for g, tiles in enumerate(groups[k]):
            at = first[k] + g
            if at % 2 == which:
                eng.wait_ge(turned, GROUPS * i + (at + 1 + AHEAD))
                eng.wait_ge(o_done, STEPS * i + (k + 1))
                n = len(tiles) * P
                copy(pT[:, k % 2, tiles[0] * P:tiles[0] * P + n], t_ps(at)[:, 0:n]).then_inc(t_evac[which], 1)

    def on_vector(dve):
        def top(i, k):
            u, n = order[k % STEPS]
            s = STEPS * i + k
            dve.wait_ge(scored, s + 1)
            dve.wait_ge(edge_made, s + 1)
            skip = 1 if n == 0 else 0
            win = s_ps(k)[:, n * P - 1 + skip:(n + 1) * P]
            nc.vector.tensor_tensor(win, win, edge[:, k % 2, skip:], ALU.add).then_inc(edged, 1)
            dve.wait_ge(edged, s + 1 + AHEAD)
            nc.vector.tensor_reduce(ntop[:, k % 2:k % 2 + 1], s_ps(k)[:, 0:(n + 1) * P], AX_X, ALU.max, negate=True).then_inc(top_ready, 1)

        def norm(i, k):
            u, n = order[k]
            s = STEPS * i + k
            dve.wait_ge(o_done, s + 1 + AHEAD)
            dve.wait_ge(inv_ready, s + 1 + AHEAD)
            head = bass.ds(i * (2 * PAIRS_IN) + u, 1)
            nc.vector.tensor_scalar(o_tok[:, head, n, :].rearrange("p a d -> p (a d)"), o_ps(k), inv[:, k % 2:k % 2 + 1], None,
                                    ALU.mult).then_inc(o_evac, 1)

        dve.sem_inc(edged, AHEAD)
        dve.sem_inc(o_evac, AHEAD)
        dve.sem_inc(inv_ready, AHEAD)
        top(0, 0)

        def body(i, last):
            for k in range(STEPS):
                if k + 1 < STEPS or not last:
                    top(i, k + 1)
                copy_turned(dve, nc.vector.tensor_copy, i, k, 1)
                dve.wait_ge(exped, STEPS * i + (k + 1 + AHEAD))
                dve.wait_ge(o_evac, STEPS * i + (k + 1))
                nc.vector.reciprocal(inv[:, k % 2:k % 2 + 1], total[:, k % 2:k % 2 + 1]).then_inc(inv_ready, 1)
                if k:
                    norm(i, k - 1)
            norm(i, STEPS - 1)

        rounds(dve, body)
        dve.wait_ge(o_evac, STEPS * ROUNDS + AHEAD)

    def on_scalar(act):
        nc.scalar.activation(total[:, 0:1], env.eps[:], ACT.Exp).then_inc(tables, 1)
        act.wait_ge(tables, 1)

        def soften(i, k):
            u, n = order[k % STEPS]
            s = STEPS * i + k
            act.wait_ge(top_ready, s + 1)
            act.wait_ge(turned, GROUPS * i + (first[k - 1] + AHEAD if k else AHEAD - len(groups[STEPS - 1])))
            act.wait_ge(inv_ready, s + 1)
            nc.scalar.activation(pr[:, k % 2, 0:(n + 1) * P], s_ps(k)[:, 0:(n + 1) * P], ACT.Exp, bias=ntop[:, k % 2:k % 2 + 1],
                                 accum_out=total[:, k % 2:k % 2 + 1]).then_inc(exped, 1)

        act.sem_inc(exped, AHEAD)
        soften(0, 0)

        def body(i, last):
            for k in range(STEPS):
                if k + 1 < STEPS or not last:
                    soften(i, k + 1)
                copy_turned(act, nc.scalar.copy, i, k, 0)

        rounds(act, body)

    return dict(sync=on_sync, gpsimd=on_gpsimd, tensor=on_tensor, vector=on_vector, scalar=on_scalar)


def any_mask(nc, env, st, tag, banks, kern_dram, mask, q_dram, k_dram, v, o_tok):
    o_dram = nc.dram_tensor(f"{tag}_o", [HEADS, ROWS * WINDOWS, HD], F32).ap()
    sb, sem = lambda n, *a: st.sb("any_" + n, *a), lambda n: st.sem("any_" + n)
    seen, gone = sb("seen", [P, WINDOWS, S], U8), sb("gone", [P, WINDOWS, S], U8)
    kern = sb("kern", [P, HEADS, TAP * TAP])
    tap = sb("tap", [P, TAP * TAP])
    down = sb("down", [P, TAP, P])
    band = sb("band", [P, TAP, P])
    qh, kh = sb("qh", [HD, PAD]), sb("kh", [HD, PAD])
    sm = sb("sm", [P, S + 2])
    z = sb("z", [P, S])
    pT = sb("pT", [P, TPB, P])
    ntop, total, inv = sb("ntop", [P, 1]), sb("total", [P, 1]), sb("inv", [P, 1])
    o = sb("o", [P, HD])
    s_ps, z_ps, t_ps = (banks[:, i:i + 2, :].rearrange("p a n -> p (a n)") for i in (0, 2, 4))
    o_ps = banks[:, 6, :]
    mask_zero, mask_loaded, kern_loaded, mask_ready, down_made, staged, stored, gathered = (
        sem(n) for n in ("mask_zero", "mask_loaded", "kern_loaded", "mask_ready", "down_made", "staged", "stored",
                         "gathered"))
    band_ready, scored, masked, summed, top_ready, exped, turned, t_evac, o_done, o_ready, padded, tables, taken, banded, band_parts, hidden, inv_ready = (
        sem(n) for n in ("band_ready", "scored", "masked", "summed", "top_ready", "exped", "turned", "t_evac", "o_done",
                         "o_ready", "padded", "tables", "taken", "banded", "band_parts", "hidden", "inv_ready"))

    def on_sync(sp):
        sp.wait_ge(mask_zero, 2)
        m = mask
        loads = []
        for i in range(WINDOWS):
            first, last = max(0, i * ROWS - 1), min(S, i * ROWS - 1 + P)
            loads.append((seen, first - (i * ROWS - 1), i, first, last))
            loads.append((gone, 0, i, i * ROWS, min(S, (i + 1) * ROWS)))
        for dst, at, i, first, last in loads:
            sp.dma_start(dst[at:at + last - first, i, :], m[first:last, :]).then_inc(mask_loaded, 16)
        sp.dma_start(kern[:], kern_dram.rearrange("b (h k) -> (b h) k", h=H).partition_broadcast(P)).then_inc(kern_loaded, 16)
        q_rows, k_rows = (d.rearrange("b (h f) t -> (b h) f t", h=H) for d in (q_dram, k_dram))

        def stage(g):
            sp.dma_start(qh[:], q_rows[bass.ds(g, 1)].rearrange("a f t -> (a f) t")).then_inc(staged, 16)
            sp.dma_start(kh[:], k_rows[bass.ds(g, 1)].rearrange("a f t -> (a f) t")).then_inc(staged, 16)

        with sp.Fori(0, HEADS) as g:
            sp.wait_ge(scored, WINDOWS * g)
            stage(g)
            for i in range(WINDOWS):
                sp.wait_ge(o_ready, WINDOWS * g + (i + 1))
                sp.dma_start(o_dram[bass.ds(g, 1), i * ROWS:(i + 1) * ROWS, :].rearrange("a t d -> (a t) d"),
                             o[0:ROWS]).then_inc(stored, 16)
        sp.wait_ge(stored, 16 * WINDOWS * HEADS)
        for n in range(TPB):
            sp.dma_start(o_tok[:, :, n, :], o_dram[:, n * P:(n + 1) * P, :].rearrange("g p d -> p g d")).then_inc(gathered, 16)
        sp.wait_ge(gathered, 16 * TPB)

    def on_gpsimd(pool):
        nc.gpsimd.memset(seen[:], 0.0).then_inc(mask_zero, 1)
        nc.gpsimd.memset(gone[:], 0.0).then_inc(mask_zero, 1)
        nc.gpsimd.memset(sm[:], 0.0).then_inc(padded, 1)
        nc.gpsimd.memset(down[:], 0.0).then_inc(padded, 1)
        pool.wait_ge(padded, 2)
        for a in range(TAP):
            nc.gpsimd.affine_select(out=down[:, a, :], in_=down[:, a, :], compare_op=ALU.not_equal, fill=1.0, base=-a,
                                    pattern=[[-1, P]], channel_multiplier=1).then_inc(down_made, 1)

    def on_tensor(pe):
        with pe.Fori(0, HEADS) as g:
            pe.wait_ge(staged, 32 * g + 32)
            for i in range(WINDOWS):
                s = WINDOWS * g + i
                pe.wait_ge(masked, s)
                for n in range(S // 512):
                    last = nc.tensor.matmul(s_ps[:, n * 512:(n + 1) * 512], qh[:, i * ROWS:i * ROWS + P],
                                            kh[:, 1 + n * 512:1 + (n + 1) * 512], start=True, stop=True)
                last.then_inc(scored, 1)
                if i == 0:
                    pe.wait_ge(band_ready, g + 1)
                pe.wait_ge(masked, s + 1)
                for n in range(S // 512):
                    for c in range(TAP):
                        last = nc.tensor.matmul(z_ps[:, n * 512:(n + 1) * 512], band[:, c, :], sm[:, c + n * 512:c + (n + 1) * 512],
                                                start=c == 0, stop=c == TAP - 1)
                last.then_inc(summed, 1)
                pe.wait_ge(exped, s + 1)
                for j in range(TPB):
                    last = nc.tensor.transpose(t_ps[:, j * P:(j + 1) * P], z[:, j * P:(j + 1) * P], env.ident[:])
                last.then_inc(turned, 1)
                pe.wait_ge(t_evac, s + 1)
                for j in range(TPB):
                    last = nc.tensor.matmul(o_ps[:, 0:HD], pT[:, j, :],
                                            v[:, bass.ds(g, 1), j, :].rearrange("p a d -> p (a d)"), start=j == 0, stop=j == TPB - 1)
                last.then_inc(o_done, 1)

    def on_vector(dve):
        dve.wait_ge(mask_loaded, 32 * WINDOWS)
        nc.vector.tensor_scalar(seen[:], seen[:], 0.0, None, ALU.is_equal).then_inc(mask_ready, 1)
        dve.wait_ge(mask_ready, 1)
        dve.wait_ge(kern_loaded, 16)
        dve.wait_ge(down_made, TAP)

        with dve.Fori(0, HEADS) as g:
            nc.vector.tensor_copy(tap[:], kern[:, bass.ds(g, 1), :].rearrange("p a k -> p (a k)")).then_inc(taken, 1)
            dve.wait_ge(taken, g + 1)
            dve.wait_ge(summed, WINDOWS * g)
            for c in range(TAP):
                for a in range(TAP):
                    weight = tap[:, a * TAP + c:a * TAP + c + 1]
                    if a == 0:
                        ins = nc.vector.tensor_scalar(band[:, c, :], down[:, a, :], weight, None, ALU.mult)
                    else:
                        dve.wait_ge(banded, 6 * g + (2 * c + a))
                        ins = nc.vector.scalar_tensor_tensor(band[:, c, :], down[:, a, :], weight, band[:, c, :], ALU.mult, ALU.add)
                    if a < TAP - 1:
                        ins.then_inc(banded, 1)
                    elif c < TAP - 1:
                        ins.then_inc(band_parts, 1)
                    else:
                        dve.wait_ge(band_parts, (TAP - 1) * (g + 1))
                        ins.then_inc(band_ready, 1)
            for i in range(WINDOWS):
                s = WINDOWS * g + i
                dve.wait_ge(scored, s + 1)
                dve.wait_ge(summed, s)
                nc.vector.tensor_tensor(sm[:, 1:S + 1], s_ps, seen[:, i, :], ALU.mult).then_inc(masked, 1)
                dve.wait_ge(summed, s + 1)
                dve.wait_ge(turned, s)
                nc.vector.scalar_tensor_tensor(z[:], gone[:, i, :], NEG, z_ps, ALU.mult, ALU.add).then_inc(hidden, 1)
                dve.wait_ge(hidden, s + 1)
                nc.vector.tensor_reduce(ntop[:], z[:], AX_X, ALU.max, negate=True).then_inc(top_ready, 1)
                dve.wait_ge(exped, s + 1)
                nc.vector.reciprocal(inv[:], total[:]).then_inc(inv_ready, 1)
                dve.wait_ge(inv_ready, s + 1)
                dve.wait_ge(o_done, s + 1)
                dve.wait_ge(stored, 16 * s)
                nc.vector.tensor_scalar(o[:], o_ps[:, 0:HD], inv[:, 0:1], None, ALU.mult).then_inc(o_ready, 1)

    def on_scalar(act):
        nc.scalar.activation(total[:], env.eps[:], ACT.Exp).then_inc(tables, 1)
        act.wait_ge(tables, 1)
        with act.Fori(0, HEADS) as g:
            for i in range(WINDOWS):
                s = WINDOWS * g + i
                act.wait_ge(top_ready, s + 1)
                nc.scalar.activation(z[:], z[:], ACT.Exp, bias=ntop[:, 0:1], accum_out=total[:]).then_inc(exped, 1)
                act.wait_ge(turned, s + 1)
                act.wait_ge(o_done, s)
                nc.scalar.copy(pT[:].rearrange("p j t -> p (j t)"), t_ps).then_inc(t_evac, 1)

    return dict(sync=on_sync, gpsimd=on_gpsimd, tensor=on_tensor, vector=on_vector, scalar=on_scalar)


def project_out(nc, env, st, ctx, w, o_tok):
    wo, bo = st.sb("wo", [P, DC, D]), st.sb("bo", [1, D])
    row = st.sb("row", [P, 2, D])
    oT = st.sb("oT", [P, 2, DC, P])
    t_ps, y_ps = st.ps("t_ps", [P, 2, 512]), st.ps("y_ps", [P, 2, 512])
    loaded, lined, turned, evacuated, y_done, added = (
        st.sem(n) for n in ("loaded", "lined", "turned", "evacuated", "y_done", "added"))
    block = ctx.enter_context(nc.Block())

    @block.sync
    def _(sp):
        sp.dma_start(wo[:], w("proj_W").rearrange("(c p) n -> p c n", p=P)).then_inc(loaded, 16)
        sp.dma_start(bo[:], w("proj_b").rearrange("(a n) -> a n", a=1)).then_inc(loaded, 16)

    @block.gpsimd
    def _(pool):
        for t in range(TILES):
            b, n = divmod(t, TPB)
            if t >= 2:
                pool.wait_ge(turned, t - 1)
            nc.gpsimd.tensor_copy(row[:, t % 2, :].rearrange("p (h d) -> p h d", h=H),
                                  o_tok[:, b * H:(b + 1) * H, n, :]).then_inc(lined, 1)

    @block.tensor
    def _(pe):
        def turn(t):
            pe.wait_ge(lined, t + 1)
            if t >= 2:
                pe.wait_ge(evacuated, t - 1)
            for c in range(DC):
                last = nc.tensor.transpose(t_ps[:, t % 2, c * P:(c + 1) * P], row[:, t % 2, c * P:(c + 1) * P], env.ident[:])
            last.then_inc(turned, 1)

        turn(0)
        pe.wait_ge(loaded, 32)
        for t in range(TILES):
            if t + 1 < TILES:
                turn(t + 1)
            pe.wait_ge(evacuated, t + 1)
            if t >= 2:
                pe.wait_ge(added, t - 1)
            nc.tensor.matmul(y_ps[:, t % 2, 0:D], env.ones[0:1, :], bo[:], start=True, stop=False)
            for c in range(DC):
                last = nc.tensor.matmul(y_ps[:, t % 2, 0:D], oT[:, t % 2, c, :], wo[:, c, :], start=False, stop=c == DC - 1)
            last.then_inc(y_done, 1)

    @block.scalar
    def _(act):
        for t in range(TILES):
            act.wait_ge(turned, t + 1)
            if t >= 2:
                act.wait_ge(y_done, t - 1)
            nc.scalar.copy(oT[:, t % 2], t_ps[:, t % 2, 0:D].rearrange("p (c t) -> p c t", c=DC)).then_inc(evacuated, 1)

    @block.vector
    def _(dve):
        for t in range(TILES):
            dve.wait_ge(y_done, t + 1)
            nc.vector.tensor_tensor(env.x[:, t, :], env.x[:, t, :], y_ps[:, t % 2, 0:D], ALU.add).then_inc(added, 1)



I = 768
IC = I // P
BLOCK = 32
QA = 32767.0
QW = 7.0
FLOOR = 1e-12
ROUND = 12582912.0
U16 = 65536.0
CHUNKS = T // 512


def quant_ffn_stage(nc, env, tag, args, name):
    w = lambda n: args[f"{name}_{n}"]
    with ExitStack() as ctx:
        st = Stage(nc, ctx, tag)
        xnT = st.sb("xnT", [P, DC, T])
        wT = st.sb("wT", [P, 2, DC, I])
        wdT = st.sb("wdT", [P, IC, D])
        layernorm_stage(nc, env, tag + "l", env.x, dst_T=xnT)
        with ExitStack() as inner:
            quant_weights(nc, env, Stage(nc, inner, tag + "w"), inner, w, wT, wdT)
        with ExitStack() as inner:
            quant_unit(nc, env, Stage(nc, inner, tag + "u"), inner, xnT, wT, wdT)


def quant_weights(nc, env, st, ctx, w, wT, wdT):
    NB = 3 * I * D // P // BLOCK
    raw = st.sb("raw", [P, 3 * I * D // P])
    scale, inv = st.sb("scale", [P, NB]), st.sb("inv", [P, NB])
    t_ps = st.ps("t_ps", [P, 2, 512])
    loaded, linked, ready, turned, evacuated = (st.sem(n) for n in ("loaded", "linked", "ready", "turned", "evacuated"))
    block = ctx.enter_context(nc.Block())
    part = lambda k: raw[:, k * IC * D:(k + 1) * IC * D]
    blocks = raw[:].rearrange("p (b i) -> p b i", i=BLOCK)
    over = lambda buf: buf[:].unsqueeze(2).to_broadcast([P, NB, BLOCK])
    pieces = []
    for k in range(2):
        rows = part(k).rearrange("p (o i) -> p o i", o=IC)
        for c in range(DC):
            for o in range(IC):
                pieces.append((rows[:, o, c * P:(c + 1) * P], (k, c, o)))
    rows = part(2).rearrange("p (o i) -> p o i", o=DC)
    for c in range(IC):
        for o in range(DC):
            pieces.append((rows[:, o, c * P:(c + 1) * P], (2, c, o)))
    flat = [wT[:, 0].rearrange("p c i -> p (c i)"), wT[:, 1].rearrange("p c i -> p (c i)"), wdT[:].rearrange("p c d -> p (c d)")]

    @block.sync
    def _(sp):
        for k, n in enumerate(("w_up", "w_gate")):
            sp.dma_start(part(k).rearrange("p (o i) -> p o i", o=IC), w(n).rearrange("(o p) i -> p o i", p=P)).then_inc(loaded, 16)
        sp.dma_start(part(2).rearrange("p (o i) -> p o i", o=DC), w("w_down").rearrange("(o p) i -> p o i", p=P)).then_inc(loaded, 16)

    @block.vector
    def _(dve):
        step = chain(dve, linked)
        dve.wait_ge(loaded, 48)
        step(nc.vector.tensor_reduce(scale[:], blocks, AX_X, ALU.max, apply_absolute_value=True))
        step(nc.vector.tensor_scalar(scale[:], scale[:], 1.0 / QW, FLOOR, ALU.mult, ALU.max))
        step(nc.vector.reciprocal(inv[:], scale[:]))
        step(nc.vector.tensor_tensor(blocks, blocks, over(inv), ALU.mult))
        step(nc.vector.tensor_scalar(raw[:], raw[:], ROUND, -ROUND, ALU.add, ALU.add))
        step(nc.vector.tensor_scalar(raw[:], raw[:], -QW - 1.0, QW, ALU.max, ALU.min))
        nc.vector.tensor_tensor(blocks, blocks, over(scale), ALU.mult).then_inc(ready, 1)

    @block.tensor
    def _(pe):
        pe.wait_ge(ready, 1)
        for n in range(len(pieces) // 4):
            if n >= 2:
                pe.wait_ge(evacuated, n - 1)
            for q in range(4):
                last = nc.tensor.transpose(t_ps[:, n % 2, q * P:(q + 1) * P], pieces[4 * n + q][0], env.ident[:])
            last.then_inc(turned, 1)

    @block.scalar
    def _(act):
        for n in range(len(pieces) // 4):
            act.wait_ge(turned, n + 1)
            k = pieces[4 * n][1][0]
            at0 = (4 * n - (0, 12, 24)[k]) * P
            nc.scalar.copy(flat[k][:, at0:at0 + 512], t_ps[:, n % 2, :]).then_inc(evacuated, 1)


def quant_unit(nc, env, st, ctx, xnT, wT, wdT):
    sb, ps, sem = st.sb, st.ps, st.sem
    act2 = [sb("up", [P, IC, T]), sb("gate", [P, IC, T])]
    up, gate = act2
    sig = sb("sig", [P, 2, T])
    tops = sb("tops", [P, 2, IC])
    top, amax, scale, inv = (sb(n, [P, 5]) for n in ("top", "amax", "scale", "inv"))
    both = sb("both", [P, 2])
    rnd = sb("rnd", [P, 1])
    h_ps = [ps("up_ps", [P, T]), ps("gate_ps", [P, T])]
    rnd_set, linked, top_ready, reduced, scale_ready, x_ready = (
        sem(n) for n in ("rnd_set", "linked", "top_ready", "reduced", "scale_ready", "x_ready"))
    h_done, up_evac, gate_evac, topped, g_lifted, g_whole, sig_ready, sig_lifted, sig_whole, gs_ready = (
        sem(n) for n in ("h_done", "up_evac", "gate_evac", "topped", "g_lifted", "g_whole", "sig_ready", "sig_lifted", "sig_whole",
                         "gs_ready"))
    u_lifted, u_whole, gs_lifted, gs_whole, o_ready, o_lifted, o_whole, y_done, added = (
        sem(n) for n in ("u_lifted", "u_whole", "gs_lifted", "gs_whole", "o_ready", "o_lifted", "o_whole", "y_done", "added"))
    gs_topped, o_topped = sem("gs_topped"), sem("o_topped")
    block = ctx.enter_context(nc.Block())
    col = lambda buf, k: buf[:, k:k + 1]
    X, UP, GATE, GS, O = range(5)

    @block.gpsimd
    def _(pool):
        nc.gpsimd.memset(rnd[:], ROUND).then_inc(rnd_set, 1)
        for n, ks in enumerate(((X,), (UP, GATE), (GS,), (O,))):
            if n == 3:
                for o in range(IC):
                    pool.wait_ge(u_lifted, o + 1)
                    nc.gpsimd.tensor_scalar(up[:, o, :], up[:, o, :], -ROUND, QA, ALU.add, ALU.min).then_inc(u_whole, 1)
            pool.wait_ge(top_ready, n + 1)
            nc.gpsimd.partition_all_reduce(amax[:, ks[0]:ks[-1] + 1], top[:, ks[0]:ks[-1] + 1], P, RMAX).then_inc(reduced, 1)

    @block.tensor
    def _(pe):
        pe.wait_ge(x_ready, 1)
        for o in range(IC):
            for k in range(2):
                if o:
                    pe.wait_ge((up_evac, gate_evac)[k], o)
                for n in range(CHUNKS):
                    for c in range(DC):
                        last = nc.tensor.matmul(h_ps[k][:, n * 512:(n + 1) * 512], wT[:, k, c, o * P:(o + 1) * P],
                                                xnT[:, c, n * 512:(n + 1) * 512], start=c == 0, stop=c == DC - 1)
                last.then_inc(h_done, 1)
        for t in range(TILES):
            if t % 4 == 0:
                pe.wait_ge(o_whole, t // 4 + 1)
            if t >= 4:
                pe.wait_ge(added, t - 3)
            y = h_ps[0][:, (t % 4) * 512:(t % 4) * 512 + D]
            for o in range(IC):
                last = nc.tensor.matmul(y, gate[:, o, t * P:(t + 1) * P], wdT[:, o, :], start=o == 0, stop=o == IC - 1)
            last.then_inc(y_done, 1)

    def sigmoid_times(dve, o):
        g, s = gate[:, o, :], sig[:, o % 2, :]
        dve.wait_ge(sig_ready, o + 1)
        nc.vector.tensor_scalar(s, s, U16, ROUND, ALU.mult, ALU.add).then_inc(sig_lifted, 1)
        dve.wait_ge(sig_lifted, o + 1)
        nc.vector.tensor_scalar(s, s, -ROUND, U16 - 1.0, ALU.add, ALU.min).then_inc(sig_whole, 1)
        dve.wait_ge(sig_whole, o + 1)
        nc.vector.scalar_tensor_tensor(g, g, col(both, 0), s, ALU.mult, ALU.mult).then_inc(gs_ready, 1)
        dve.wait_ge(gs_ready, o + 1)
        nc.vector.tensor_reduce(tops[:, 0, o:o + 1], g, AX_X, ALU.max, apply_absolute_value=True).then_inc(gs_topped, 1)

    def residual(dve, n):
        for t in range(4 * n, 4 * n + 4):
            xt = env.x[:, t, :]
            dve.wait_ge(y_done, t + 1)
            nc.vector.scalar_tensor_tensor(xt, h_ps[0][:, (t % 4) * 512:(t % 4) * 512 + D], col(scale, O), xt, ALU.mult,
                                           ALU.add).then_inc(added, 1)

    @block.vector
    def _(dve):
        step = chain(dve, linked)

        def scales(n, ks):
            dve.wait_ge(reduced, n + 1)
            cols = slice(ks[0], ks[-1] + 1)
            step(nc.vector.tensor_scalar(scale[:, cols], amax[:, cols], 1.0 / QA, FLOOR, ALU.mult, ALU.max))
            nc.vector.reciprocal(inv[:, cols], scale[:, cols]).then_inc(scale_ready, 1)
            dve.wait_ge(scale_ready, n + 1)

        flat = xnT[:].rearrange("p c t -> p (c t)")
        nc.vector.tensor_reduce(col(top, X), flat, AX_X, ALU.max, apply_absolute_value=True).then_inc(top_ready, 1)
        scales(0, (X,))
        step(nc.vector.tensor_scalar(flat, flat, col(inv, X), ROUND, ALU.mult, ALU.add))
        step(nc.vector.tensor_scalar(flat, flat, -ROUND, -QA - 1.0, ALU.add, ALU.max))
        nc.vector.tensor_scalar(flat, flat, QA, col(scale, X), ALU.min, ALU.mult).then_inc(x_ready, 1)
        for o in range(IC):
            dve.wait_ge(h_done, 2 * o + 2)
            nc.vector.tensor_copy(gate[:, o, :], h_ps[1][:]).then_inc(gate_evac, 1)
            dve.wait_ge(up_evac, o + 1)
            nc.vector.tensor_reduce(tops[:, 0, o:o + 1], up[:, o, :], AX_X, ALU.max, apply_absolute_value=True).then_inc(topped, 1)
            dve.wait_ge(gate_evac, o + 1)
            nc.vector.tensor_reduce(tops[:, 1, o:o + 1], gate[:, o, :], AX_X, ALU.max, apply_absolute_value=True).then_inc(topped, 1)
        dve.wait_ge(topped, 2 * IC)
        nc.vector.tensor_reduce(top[:, UP:GATE + 1], tops[:], AX_X, ALU.max).then_inc(top_ready, 1)
        scales(1, (UP, GATE))
        step(nc.vector.tensor_scalar(col(both, 0), col(scale, GATE), 1.0 / U16, None, ALU.mult))
        for o in range(IC):
            g, s = gate[:, o, :], sig[:, o % 2, :]
            dve.wait_ge(g_lifted, o + 1)
            nc.vector.tensor_scalar(g, g, -ROUND, QA, ALU.add, ALU.min).then_inc(g_whole, 1)
            if o:
                sigmoid_times(dve, o - 1)
        sigmoid_times(dve, IC - 1)
        dve.wait_ge(gs_topped, IC)
        nc.vector.tensor_reduce(col(top, GS), tops[:, 0, :], AX_X, ALU.max).then_inc(top_ready, 1)
        scales(2, (GS,))
        step(nc.vector.tensor_tensor(col(both, 1), col(scale, GS), col(scale, UP), ALU.mult))
        for o in range(IC):
            g = gate[:, o, :]
            dve.wait_ge(gs_lifted, o + 1)
            nc.vector.tensor_scalar(g, g, -ROUND, QA, ALU.add, ALU.min).then_inc(gs_whole, 1)
            dve.wait_ge(gs_whole, o + 1)
            dve.wait_ge(u_whole, o + 1)
            nc.vector.scalar_tensor_tensor(g, g, col(both, 1), up[:, o, :], ALU.mult, ALU.mult).then_inc(o_ready, 1)
            dve.wait_ge(o_ready, o + 1)
            nc.vector.tensor_reduce(tops[:, 1, o:o + 1], g, AX_X, ALU.max, apply_absolute_value=True).then_inc(o_topped, 1)
        dve.wait_ge(o_topped, IC)
        nc.vector.tensor_reduce(col(top, O), tops[:, 1, :], AX_X, ALU.max).then_inc(top_ready, 1)
        scales(3, (O,))
        for n in range(CHUNKS):
            part = gate[:, :, n * 512:(n + 1) * 512]
            dve.wait_ge(o_lifted, n + 1)
            nc.vector.tensor_scalar(part, part, -ROUND, QA, ALU.add, ALU.min).then_inc(o_whole, 1)
            if n:
                residual(dve, n - 1)
        residual(dve, CHUNKS - 1)

    def sigmoid(act, o):
        act.wait_ge(g_whole, o + 1)
        if o >= 2:
            act.wait_ge(gs_ready, o - 1)
        nc.scalar.activation(sig[:, o % 2, :], gate[:, o, :], ACT.Sigmoid, scale=col(scale, GATE)).then_inc(sig_ready, 1)

    @block.scalar
    def _(act):
        act.wait_ge(rnd_set, 1)

        def lift(buf, k, done):
            nc.scalar.activation(buf, buf, ACT.Identity, bias=rnd[:, 0:1], scale=col(inv, k)).then_inc(done, 1)

        for o in range(IC):
            act.wait_ge(h_done, 2 * o + 1)
            nc.scalar.copy(up[:, o, :], h_ps[0][:]).then_inc(up_evac, 1)
        act.wait_ge(scale_ready, 2)
        act.wait_ge(gate_evac, IC)
        for o in range(IC):
            lift(gate[:, o, :], GATE, g_lifted)
            if o:
                sigmoid(act, o - 1)
        sigmoid(act, IC - 1)
        for o in range(IC):
            lift(up[:, o, :], UP, u_lifted)
        act.wait_ge(scale_ready, 3)
        for o in range(IC):
            lift(gate[:, o, :], GS, gs_lifted)
        act.wait_ge(scale_ready, 4)
        for n in range(CHUNKS):
            lift(gate[:, :, n * 512:(n + 1) * 512], O, o_lifted)



F16 = mybir.dt.float16
DH = 64
INNER = H * DH
PAIRS = INNER // P
KT = TPB + 1
KEYS = S + NCTX
KPAD = KT * P
NEG_MAX = -3.4028234663852886e38


def latent_attention_stage(nc, env, tag, args, name):
    w = lambda n: args[f"{name}_{n}"]
    with ExitStack() as ctx:
        st = Stage(nc, ctx, tag)
        sb = st.sb
        xn = sb("xn", [P, TILES, D])
        layernorm_stage(nc, env, tag + "l", env.x, dst_tok=xn)
        p = {n: sb(n, s) for n, s in (("mean", [P, TILES + B]), ("rstd", [P, TILES + B]), ("gl", [P, DC]), ("bl", [P, DC]),
                                       ("gx", [P, DC]), ("bx", [P, DC]), ("gain", [P, 1]), ("gmax", [P, 1]), ("hide", [P, B, NCTX]),
                                       ("hide_key", [P, B]))}
        latent_norms(nc, env, st, tag, args, w, xn, p)
        for b in range(B):
            with ExitStack() as inner:
                sti = Stage(nc, inner, f"{tag}b{b}")
                qT, kT = sti.sb("qT", [P, 2, PAIRS, S], F16), sti.sb("kT", [P, 2, PAIRS, KEYS], F16)
                v = sti.sb("v", [P, KT, INNER])
                with ExitStack() as deep:
                    latent_project(nc, env, Stage(nc, deep, f"{tag}p{b}"), deep, w, b, xn, p, qT, kT, v)
                oT = sti.sb("oT", [P, PAIRS, S])
                with ExitStack() as deep:
                    latent_attend(nc, env, Stage(nc, deep, f"{tag}a{b}"), deep, b, p, xn, qT, kT, v, oT)
                with ExitStack() as deep:
                    latent_emit(nc, env, Stage(nc, deep, f"{tag}o{b}"), deep, w, b, oT)


def latent_norms(nc, env, outer, tag, args, w, xn, p):
    with ExitStack() as ctx:
        st = Stage(nc, ctx, tag + "n")
        stats = st.sb("stats", [P, TILES + B, 6])
        var = st.sb("var", [P, TILES + B])
        mask_in = st.sb("mask_in", [P, B, NCTX], U8)
        loaded, counted, linked, var_ready, std_ready = (st.sem(n) for n in ("loaded", "counted", "linked", "var_ready", "std_ready"))
        gains, small = st.sb("gains", [P, 2, DH]), st.sb("small", [P, 1])
        hidden_key = st.sb("hidden_key", [P, B], U8)
        key_zero = st.sem("key_zero")
        block = ctx.enter_context(nc.Block())

        @block.sync
        def _(sp):
            for n, k in (("ln_l_g", "gl"), ("ln_l_b", "bl"), ("ln_x_g", "gx"), ("ln_x_b", "bx")):
                sp.dma_start(p[k][:], w(n).rearrange("(c p) -> p c", p=P), allow_slow_non_contiguous=True).then_inc(loaded, 16)
            for i, n in enumerate(("qn_g", "kn_g")):
                sp.dma_start(gains[:, i, :], w(n).partition_broadcast(P)).then_inc(loaded, 16)
            for half in range(2):
                rows = slice(half * DH, (half + 1) * DH)
                sp.dma_start(p["gain"][rows, :], w("qn_g").rearrange("(p a) -> p a", a=1)).then_inc(loaded, 16)
                sp.dma_start(small[rows, :], w("kn_g").rearrange("(p a) -> p a", a=1)).then_inc(loaded, 16)
            sp.dma_start(mask_in[:], args["mask_BxS2_bf1"].partition_broadcast(P)).then_inc(loaded, 16)
            sp.wait_ge(key_zero, 1)
            sp.dma_start(hidden_key[0:NCTX], args["mask_BxS2_bf1"].rearrange("b k -> k b"), allow_slow_non_contiguous=True).then_inc(loaded, 16)
            sp.wait_ge(loaded, 192)

        @block.gpsimd
        def _(pool):
            nc.gpsimd.memset(hidden_key[:], 0.0).then_inc(key_zero, 1)

        @block.vector
        def _(dve):
            step = chain(dve, linked)
            step(nc.vector.memset(stats[:, TILES:, :], 0.0))
            with dve.Fori(0, TILES) as t:
                nc.vector.bn_stats(tile_of(stats, t), tile_of(xn, t)).then_inc(counted, 1)
            for b in range(B):
                nc.vector.bn_stats(stats[0:NCTX, TILES + b, :], env.ctx_tok[0:NCTX, b, :]).then_inc(counted, 1)
            dve.wait_ge(counted, TILES + B)
            merge_stats(nc, step, p["mean"][:], var[:], stats, D)
            nc.vector.tensor_scalar(var[:], var[:], LN_EPS, None, ALU.add).then_inc(var_ready, 1)
            dve.wait_ge(loaded, 192)
            both = gains[:, 0, :]
            step(nc.vector.tensor_tensor(both, both, gains[:, 1, :], ALU.mult))
            step(nc.vector.scalar_tensor_tensor(gains[:, 1, :], both, -1.0, both, ALU.mult, ALU.max))
            step(nc.vector.tensor_reduce(p["gmax"][:], gains[:, 1, :], AX_X, ALU.max))
            step(nc.vector.tensor_scalar(p["gmax"][:], p["gmax"][:], 1e-30, None, ALU.max))
            step(nc.vector.tensor_tensor(p["gain"][:], p["gain"][:], small[:], ALU.mult))
            step(nc.vector.reciprocal(small[:], p["gmax"][:]))
            step(nc.vector.tensor_tensor(p["gain"][:], p["gain"][:], small[:], ALU.mult))
            step(nc.vector.tensor_scalar(p["gmax"][:], p["gmax"][:], DH ** -0.5, None, ALU.mult))
            step(nc.vector.tensor_scalar(p["hide_key"][:], hidden_key[:], 0.0, NEG_MAX, ALU.is_equal, ALU.mult))
            step(nc.vector.tensor_scalar(p["hide"][:], mask_in[:], 0.0, NEG_MAX, ALU.is_equal, ALU.mult))
            dve.wait_ge(std_ready, 1)
            step(nc.vector.reciprocal(p["rstd"][:], p["rstd"][:]))

        @block.scalar
        def _(act):
            act.wait_ge(var_ready, 1)
            nc.scalar.activation(p["rstd"][:], var[:], ACT.Sqrt).then_inc(std_ready, 1)


def latent_project(nc, env, st, ctx, w, b, xn, p, qT, kT, v):
    sb, ps, sem = st.sb, st.ps, st.sem
    wq, wkv = sb("wq", [P, DC, INNER]), sb("wkv", [P, DC, 2 * INNER])
    turn = sb("turn", [P, 2, D])
    lT = sb("lT", [P, 2, DC, P])
    sq = sb("sq", [P, 2, INNER])
    ss, rn = sb("ss", [P, 2, H]), sb("rn", [P, 2, H])
    qk = sb("qk", [P, 2, INNER])
    q_ps, k_ps, t_ps = ps("q_ps", [P, INNER]), ps("k_ps", [P, INNER]), ps("t_ps", [P, INNER])
    v_ps, x_ps = ps("v_ps", [P, 512]), ps("x_ps", [P, 512])
    loaded, normed, x_turned, x_evac, q_done, k_done, v_done, v_evac = (
        sem(n) for n in ("loaded", "normed", "x_turned", "x_evac", "q_done", "k_done", "v_done", "v_evac"))
    squared, summed, rooted, floored, inv_ready, scaled, turned, evacuated, table_loaded, halved = (
        sem(n) for n in ("squared", "summed", "rooted", "floored", "inv_ready", "scaled", "turned", "evacuated", "table_loaded", "halved"))
    block = ctx.enter_context(nc.Block())
    g0 = b * TPB

    LAST = TPB
    rows_of = lambda n: NCTX if isinstance(n, int) and n == LAST else P
    sides_of = lambda n: (1,) if isinstance(n, int) and n == LAST else (0, 1)
    side_at = lambda n, k: 2 * n if isinstance(n, int) and n == LAST else 2 * n + k

    def tiles(eng, work):
        for n in range(2):
            work(n, n)
        with eng.Fori(1, TPB // 2 - 1) as i:
            for u in range(2):
                work(2 * i + u, u)
        for n in range(TPB - 2, LAST + 1):
            work(n, n % 2)

    @block.sync
    def _(sp):
        sp.dma_start(wq[:], w("Wq").rearrange("(c p) n -> p c n", p=P)).then_inc(loaded, 16)
        sp.dma_start(wkv[:], w("Wkv").rearrange("(c p) n -> p c n", p=P)).then_inc(loaded, 16)

    @block.vector
    def _(dve):
        def normalise(n, u, reuse):
            rows = rows_of(n)
            if reuse:
                dve.wait_ge(x_turned, n - 1)
            if rows == P:
                src, col = tile_of(xn, n + g0), bass.ds(n + g0, 1)
            else:
                src, col = env.ctx_tok[0:rows, b, :], slice(TILES + b, TILES + b + 1)
            nc.vector.tensor_scalar(turn[0:rows, u, :], src, p["mean"][0:rows, col], p["rstd"][0:rows, col],
                                    ALU.subtract, ALU.mult).then_inc(normed, 1)

        def work(n, u):
            rows, sides, begun = rows_of(n), sides_of(n), not (isinstance(n, int) and n == 0)
            if begun:
                dve.wait_ge(rooted, n)
            for k in sides:
                dve.wait_ge(squared, side_at(n, k) + 1)
                nc.vector.tensor_reduce(ss[0:rows, k, :], sq[0:rows, k, :].rearrange("p (h d) -> p h d", h=H), AX_X,
                                        ALU.add).then_inc(summed, 1)
            if not (isinstance(n, int) and n > LAST - 2):
                normalise(n + 2, u, True)
            norms = rn[0:rows] if len(sides) == 2 else rn[0:rows, 1, :]
            dve.wait_ge(rooted, n + 1)
            nc.vector.tensor_scalar(norms, norms, 1e-8, None, ALU.max).then_inc(floored, 1)
            dve.wait_ge(floored, n + 1)
            nc.vector.reciprocal(norms, norms).then_inc(inv_ready, 1)
            dve.wait_ge(inv_ready, n + 1)
            for k in sides:
                if begun:
                    dve.wait_ge(turned, 4 * n + (2 * k - 2))
                src = (q_ps, k_ps)[k]
                nc.vector.tensor_tensor(qk[0:rows, k, :].rearrange("p (h d) -> p h d", h=H),
                                        src[0:rows, :].rearrange("p (h d) -> p h d", h=H),
                                        rn[0:rows, k, :].unsqueeze(2).to_broadcast([rows, H, DH]), ALU.mult).then_inc(scaled, 1)
            for k in sides:
                for half in range(2):
                    dve.wait_ge(halved, 2 * side_at(n, k) + (half + 1))
                    src = t_ps[:, half * 512:(half + 1) * 512].rearrange("p (c t) -> p c t", c=4)[:, :, 0:rows]
                    hi, lo = ((qT, kT)[k][:, i, half * 4:(half + 1) * 4, bass.ds(n * P, rows)] for i in range(2))
                    if k == 0:
                        nc.vector.tensor_tensor(lo, src, hi, ALU.subtract).then_inc(evacuated, 1)
                    else:
                        nc.vector.scalar_tensor_tensor(lo, src, p["gain"][:, 0:1], hi, ALU.mult, ALU.subtract).then_inc(evacuated, 1)

        for n in range(2):
            normalise(n, n, False)
        tiles(dve, work)

    @block.scalar
    def _(act):
        nc.scalar.activation(ss[:, 0, 0:1], env.eps[:], ACT.Sqrt).then_inc(table_loaded, 1)
        act.wait_ge(table_loaded, 1)

        def affine(n, u, reuse):
            rows = rows_of(n)
            g, o = (p["gl"], p["bl"]) if rows == P else (p["gx"], p["bx"])
            act.wait_ge(x_turned, n + 1)
            if reuse:
                act.wait_ge(v_done, 2 * n - 2)
            for c in range(DC):
                nc.scalar.activation(lT[:, u, c, 0:rows], x_ps[:, c * P:c * P + rows], ACT.Identity, bias=o[:, c:c + 1],
                                     scale=g[:, c:c + 1]).then_inc(x_evac, 1)

        def work(n, u):
            rows, sides, begun = rows_of(n), sides_of(n), not (isinstance(n, int) and n == 0)
            for k in sides:
                act.wait_ge((q_done, k_done)[k], n + 1)
                if begun:
                    act.wait_ge(summed, 2 * n + (k - 1))
                nc.scalar.activation(sq[0:rows, k, :], (q_ps, k_ps)[k][0:rows, :], ACT.Square).then_inc(squared, 1)
            if not (isinstance(n, int) and n == LAST):
                affine(n + 1, 1 - u, begun)
            for k in range(2):
                act.wait_ge(v_done, 2 * n + (k + 1))
                nc.scalar.copy(v[0:rows, bass.ds(n, 1), k * 512:(k + 1) * 512].rearrange("p a n -> p (a n)"),
                               v_ps[0:rows, :]).then_inc(v_evac, 1)
            act.wait_ge(summed, side_at(n, 1) + 1)
            if begun:
                act.wait_ge(scaled, 2 * n)
            src, dst = (ss[0:rows], rn[0:rows]) if len(sides) == 2 else (ss[0:rows, 1, :], rn[0:rows, 1, :])
            nc.scalar.activation(dst, src, ACT.Sqrt, scale=1.0 / DH).then_inc(rooted, 1)
            for k in sides:
                for half in range(2):
                    act.wait_ge(turned, 2 * side_at(n, k) + (half + 1))
                    dst = (qT, kT)[k][:, 0, half * 4:(half + 1) * 4, bass.ds(n * P, rows)]
                    nc.scalar.activation(dst, t_ps[:, half * 512:(half + 1) * 512].rearrange("p (c t) -> p c t", c=4)[:, :, 0:rows],
                                         ACT.Identity, scale=1.0 if k == 0 else p["gain"][:, 0:1]).then_inc(halved, 1)

        affine(0, 0, False)
        tiles(act, work)

    @block.tensor
    def _(pe):
        pe.wait_ge(loaded, 32)

        def turn_x(n, u, begun):
            rows = rows_of(n)
            pe.wait_ge(normed, n + 1)
            if begun:
                pe.wait_ge(x_evac, DC * n)
            for c in range(DC):
                last = nc.tensor.transpose(x_ps[:, c * P:c * P + rows], turn[0:rows, u, c * P:(c + 1) * P],
                                           env.ident[0:rows, 0:rows])
            last.then_inc(x_turned, 1)

        def queries_or_keys(n, u, k, begun):
            rows = rows_of(n)
            pe.wait_ge(x_evac, DC * n + DC)
            if begun:
                pe.wait_ge(scaled, 2 * n + (k - 1))
            for half in range(2):
                for c in range(DC):
                    wt = (wq, wkv)[k][:, c, half * 512:(half + 1) * 512]
                    last = nc.tensor.matmul((q_ps, k_ps)[k][0:rows, half * 512:(half + 1) * 512], lT[:, u, c, 0:rows], wt,
                                            start=c == 0, stop=c == DC - 1)
            last.then_inc((q_done, k_done)[k], 1)

        def values(n, u, begun):
            rows = rows_of(n)
            for half in range(2):
                if begun or half:
                    pe.wait_ge(v_evac, 2 * n + half)
                for c in range(DC):
                    last = nc.tensor.matmul(v_ps[0:rows, :], lT[:, u, c, 0:rows],
                                            wkv[:, c, INNER + half * 512:INNER + (half + 1) * 512], start=c == 0, stop=c == DC - 1)
                last.then_inc(v_done, 1)

        def turn_side(n, k):
            rows = rows_of(n)
            pe.wait_ge(scaled, side_at(n, k) + 1)
            for half in range(2):
                if not (isinstance(n, int) and n == 0 and k == 0):
                    pe.wait_ge(evacuated, 2 * side_at(n, k) + (half - 1))
                for c in range(4 * half, 4 * half + 4):
                    last = nc.tensor.transpose(t_ps[:, c * P:c * P + rows], qk[0:rows, k, c * P:(c + 1) * P],
                                               env.ident[0:rows, 0:rows])
                last.then_inc(turned, 1)

        def work(n, u):
            more = not (isinstance(n, int) and n == LAST)
            for k in range(2):
                if more and k in sides_of(n + 1):
                    queries_or_keys(n + 1, 1 - u, k, True)
                if k in sides_of(n):
                    turn_side(n, k)
            if not (isinstance(n, int) and n > LAST - 2):
                turn_x(n + 2, u, True)
            if more:
                values(n + 1, 1 - u, True)

        turn_x(0, 0, False)
        for k in range(2):
            queries_or_keys(0, 0, k, False)
        turn_x(1, 1, True)
        values(0, 0, False)
        tiles(pe, work)


def latent_attend(nc, env, st, ctx, b, p, xn, qT, kT, v, oT):
    sb, ps, sem = st.sb, st.ps, st.sem
    TOP = (DH, DH + 32)
    ROWS2 = TOP[1] + 1
    QT = TPB
    EXPS, HEAD_PAIRS, AHEAD = 2 * KT, H // 2, 4
    q11, q2 = sb("q11", [P, 2, S], F16), sb("q2", [ROWS2, 2, S], F16)
    k12, k1 = sb("k12", [P, 2, KEYS], F16), sb("k1", [ROWS2, 2, KEYS], F16)
    vh = sb("vh", [P, 2, KT, P])
    pT = xn[:, b * TPB:(b + 1) * TPB, :].rearrange("p (u c a) d -> p u c (a d)", u=2, c=2)
    ident = sb("ident", [P, P], F16)
    ntop = sb("ntop", [P, QT])
    top_rows = sb("top_rows", [P, QT, ROWS2], F16)
    inv = sb("inv", [DH, 2, 512])
    o = sb("o", [P, 2, 512])
    s_ps, t_ps, o_ps = ps("s_ps", [P, 3 * 512]), ps("t_ps", [P, 2, 512]), ps("o_ps", [P, 2, 512])
    qk_staged, v_staged = ([sem(f"{n}_staged{u}") for u in range(2)] for n in ("qk", "v"))
    filled, scored, hidden, top_ready, split_part, split_ready, top_turned, top_placed = (
        sem(n) for n in ("filled", "scored", "hidden", "top_ready", "split_part", "split_ready", "top_turned", "top_placed"))
    t_done, exped, weighed, inv_ready, o_evac, kept, table_loaded = (
        sem(n) for n in ("t_done", "exped", "weighed", "inv_ready", "o_evac", "kept", "table_loaded"))
    block = ctx.enter_context(nc.Block())

    def pairs(eng, body):
        with eng.Fori(0, HEAD_PAIRS - 1) as i:
            body(i, False)
        body(HEAD_PAIRS - 1, True)

    @block.sync
    def _(sp):
        def stage(i, u, reuse):
            h = 2 * i + u
            half, pair = slice(u * DH, (u + 1) * DH), bass.ds(i, 1)
            flat = lambda ap: ap.rearrange("p a n -> p (a n)")
            if reuse:
                sp.wait_ge(t_done, EXPS * h - EXPS)
            for dst, src in ((q11[0:DH, u], qT[half, 0, pair]), (q11[DH:P, u], qT[half, 0, pair]), (q2[0:DH, u], qT[half, 1, pair]),
                             (k12[0:DH, u], kT[half, 0, pair]), (k12[DH:P, u], kT[half, 1, pair]), (k1[0:DH, u], kT[half, 0, pair])):
                sp.dma_start(dst, flat(src)).then_inc(qk_staged[u], 16)
            if reuse:
                sp.wait_ge(weighed, EXPS * h - EXPS + AHEAD)
            cols = bass.ds(i * P + u * DH, DH)
            sp.dma_start(vh[:, u, 0:TPB, 0:DH], v[:, 0:TPB, cols]).then_inc(v_staged[u], 16)
            sp.dma_start(vh[0:NCTX, u, TPB, 0:DH], v[0:NCTX, TPB, cols]).then_inc(v_staged[u], 16)

        sp.wait_ge(filled, 7)
        for u in range(2):
            stage(0, u, False)
        with sp.Fori(1, HEAD_PAIRS) as i:
            for u in range(2):
                stage(i, u, True)

    @block.gpsimd
    def _(pool):
        step = chain(pool, filled)
        step(nc.gpsimd.memset(q2[DH:ROWS2], 0.0))
        step(nc.gpsimd.memset(k1[DH:ROWS2], 0.0))
        step(nc.gpsimd.memset(vh[:, :, :, DH:P], 1.0))
        step(nc.gpsimd.memset(top_rows[:], 0.0))
        step(nc.gpsimd.tensor_copy(ident[:], env.ident[:]))
        for row in TOP:
            step(nc.gpsimd.memset(k1[row:row + 1], 1.0))

    @block.tensor
    def _(pe):
        def score(h, i, u, n):
            if n == 0:
                pe.wait_ge(qk_staged[u], 96 * i + 96)
                pe.wait_ge(top_placed, h)
            pe.wait_ge(top_ready, QT * h + n)
            rows = slice(n * P, (n + 1) * P)
            for g in range(3):
                cols = slice(g * 512, min((g + 1) * 512, KEYS))
                nc.tensor.matmul(s_ps[:, cols], q11[:, u, rows], k12[:, u, cols], start=True, stop=False)
                last = nc.tensor.matmul(s_ps[:, cols], q2[0:DH, u, rows], k1[0:DH, u, cols], start=False, stop=True)
            last.then_inc(scored, 1)

        def turn_top(h):
            pe.wait_ge(split_ready, h + 1)
            for n in range(QT):
                last = nc.tensor.matmul(s_ps[0:ROWS2, n * P:(n + 1) * P], top_rows[:, n, :], ident[:], start=True, stop=True)
            last.then_inc(top_turned, 1)

        def by_keys(h, u, j, begun):
            rows = P if j < TPB else NCTX
            keys = slice(j * P, j * P + rows)
            if j == 0:
                pe.wait_ge(top_placed, h + 1)
            for c in range(2):
                if begun:
                    pe.wait_ge(exped, EXPS * h + (2 * j + c - 1))
                cols = slice(c * 512, (c + 1) * 512)
                nc.tensor.matmul(t_ps[0:rows, c, :], k12[:, u, keys], q11[:, u, cols], start=True, stop=False)
                nc.tensor.matmul(t_ps[0:rows, c, :], k1[:, u, keys], q2[:, u, cols], start=False, stop=True).then_inc(t_done, 1)

        def weigh(h, i, u, j):
            rows = P if j < TPB else NCTX
            if j == 0:
                pe.wait_ge(v_staged[u], 32 * i + 32)
                pe.wait_ge(o_evac, 2 * h)
            for c in range(2):
                pe.wait_ge(exped, EXPS * h + (2 * j + c + 1))
                nc.tensor.matmul(o_ps[:, c, :], vh[0:rows, u, j, :], pT[0:rows, (u * KT + j) % 2, c, :], start=j == 0,
                                 stop=j == KT - 1).then_inc(weighed, 1)

        pe.sem_inc(weighed, AHEAD)
        pe.wait_ge(filled, 7)
        for n in range(QT):
            score(0, 0, 0, n)
        turn_top(0)
        by_keys(0, 0, 0, False)

        def beside(n):
            return n + 1 if n < QT // 2 else n

        def body(i, last):
            for u in range(2):
                h = 2 * i + u
                more = not (last and u == 1)
                for j in range(KT):
                    tiles = [n for n in range(QT) if beside(n) == j] if more else []
                    for n in tiles[:1]:
                        score(h + 1, i + u, 1 - u, n)
                    if more and j == KT - 1:
                        turn_top(h + 1)
                    if j < KT - 1:
                        by_keys(h, u, j + 1, True)
                    for n in tiles[1:]:
                        score(h + 1, i + u, 1 - u, n)
                    weigh(h, i, u, j)
                    if j == KT - 1 and more:
                        by_keys(h + 1, 1 - u, 0, True)

        pairs(pe, body)

    @block.vector
    def _(dve):
        dve.wait_ge(filled, 7)

        def top(h, n):
            dve.wait_ge(scored, QT * h + (n + 1))
            ctx_keys = s_ps[:, S:KEYS]
            nc.vector.tensor_tensor(ctx_keys, ctx_keys, p["hide"][:, b, :], ALU.add).then_inc(hidden, 1)
            dve.wait_ge(hidden, QT * h + (n + 1))
            if n == 0:
                dve.wait_ge(split_ready, h)
            nc.vector.tensor_reduce(ntop[:, n:n + 1], s_ps[:, 0:KEYS], AX_X, ALU.max, negate=True).then_inc(top_ready, 1)

        def split(h):
            hi, lo = (top_rows[:, :, r] for r in TOP)
            dve.wait_ge(top_ready, QT * h + QT)
            dve.wait_ge(top_turned, h)
            nc.vector.tensor_copy(hi, ntop[:]).then_inc(split_part, 1)
            dve.wait_ge(split_part, h + 1)
            nc.vector.tensor_tensor(lo, ntop[:], hi, ALU.subtract).then_inc(split_ready, 1)

        def keep(h, i, u):
            for c in range(2):
                dve.wait_ge(o_evac, 2 * h + (c + 1))
                dve.wait_ge(kept, 2 * h)
                nc.vector.reciprocal(inv[:, c, :], o[DH:P, c, :]).then_inc(inv_ready, 1)
                dve.wait_ge(inv_ready, 2 * h + (c + 1))
                out = oT[u * DH:(u + 1) * DH, bass.ds(i, 1), c * 512:(c + 1) * 512].rearrange("p a n -> p (a n)")
                nc.vector.tensor_tensor(out, o[0:DH, c, :], inv[:, c, :], ALU.mult).then_inc(kept, 1)

        for n in range(QT):
            top(0, n)
        split(0)

        def body(i, last):
            for u in range(2):
                h = 2 * i + u
                if not (last and u == 1):
                    for n in range(QT):
                        top(h + 1, n)
                    split(h + 1)
                keep(h, i, u)

        pairs(dve, body)
        dve.wait_ge(kept, 2 * H)

    @block.scalar
    def _(act):
        nc.scalar.activation(inv[:, 0, 0:1], env.eps[0:DH], ACT.Exp).then_inc(table_loaded, 1)
        act.wait_ge(table_loaded, 1)
        act.wait_ge(filled, 7)

        def place_top(h, u):
            act.wait_ge(top_turned, h + 1)
            nc.scalar.copy(q2[TOP[0]:ROWS2, u, :], s_ps[TOP[0]:ROWS2, 0:S]).then_inc(top_placed, 1)

        place_top(0, 0)

        def body(i, last):
            for u in range(2):
                h = 2 * i + u
                for j in range(KT):
                    rows = P if j < TPB else NCTX
                    for c in range(2):
                        t = EXPS * h + (2 * j + c + 1)
                        act.wait_ge(t_done, t)
                        act.wait_ge(weighed, t)
                        dst = pT[0:rows, (u * KT + j) % 2, c, :]
                        bias = p["hide_key"][0:rows, b:b + 1] if j == TPB else 0.0
                        nc.scalar.activation(dst, t_ps[0:rows, c, :], ACT.Exp, bias=bias, scale=p["gmax"][0:rows, 0:1]).then_inc(exped, 1)
                if not (last and u == 1):
                    place_top(h + 1, 1 - u)
                for c in range(2):
                    act.wait_ge(weighed, EXPS * h + (EXPS - 1 + c + AHEAD))
                    act.wait_ge(kept, 2 * h)
                    nc.scalar.copy(o[:, c, :], o_ps[:, c, :]).then_inc(o_evac, 1)

        pairs(act, body)


def latent_emit(nc, env, st, ctx, w, b, oT):
    wout, bout = st.sb("wout", [P, PAIRS, D]), st.sb("bout", [1, D])
    y_ps = st.ps("y_ps", [P, 4, 512])
    loaded, y_done, added = st.sem("loaded"), st.sem("y_done"), st.sem("added")
    block = ctx.enter_context(nc.Block())

    @block.sync
    def _(sp):
        sp.dma_start(wout[:], w("Wout").rearrange("(c p) n -> p c n", p=P)).then_inc(loaded, 16)
        sp.dma_start(bout[:], w("bout").rearrange("(a n) -> a n", a=1)).then_inc(loaded, 16)

    @block.tensor
    def _(pe):
        pe.wait_ge(loaded, 32)
        for n in range(TPB):
            if n >= 4:
                pe.wait_ge(added, n - 3)
            nc.tensor.matmul(y_ps[:, n % 4, 0:D], env.ones[0:1, :], bout[:], start=True, stop=False)
            for c in range(PAIRS):
                last = nc.tensor.matmul(y_ps[:, n % 4, 0:D], oT[:, c, n * P:(n + 1) * P], wout[:, c, :], start=False,
                                        stop=c == PAIRS - 1)
            last.then_inc(y_done, 1)

    @block.vector
    def _(dve):
        for n in range(TPB):
            t = b * TPB + n
            dve.wait_ge(y_done, n + 1)
            nc.vector.tensor_tensor(env.x[:, t, :], env.x[:, t, :], y_ps[:, n % 4, 0:D], ALU.add).then_inc(added, 1)



E = 8
F = 1024
FC = F // P
NT = T // P + E - 1


def routed_ffn_stage(nc, env, tag, args, name, func, biased, capacity):
    w = lambda n: args[f"{name}_{n}"]
    sorted_x = nc.dram_tensor(f"{tag}_sorted_x", [NT * P, D], F32).ap()
    sorted_y = nc.dram_tensor(f"{tag}_sorted_y", [NT * P, D], F32).ap()
    with ExitStack() as ctx:
        st = Stage(nc, ctx, tag)
        w1 = st.sb("w1", [P, E, DC, F])
        w2 = st.sb("w2", [P, E, FC, D])
        b1 = st.sb("b1", [P, E, FC]) if biased else None
        b2 = st.sb("b2", [P, E, D]) if biased else None
        slot = st.sb("slot", [P, TILES], U32)
        weight = st.sb("weight", [P, TILES])
        expert_of = st.sb("expert_of", [P, NT], I32)
        weights_loaded = st.sem("weights_loaded")
        with ExitStack() as inner:
            route_tokens(nc, env, Stage(nc, inner, tag + "r"), inner, tag, w, capacity, sorted_x, slot, weight, expert_of,
                  w1, w2, b1, b2, weights_loaded)
        with ExitStack() as inner:
            routed_experts(nc, env, Stage(nc, inner, tag + "e"), inner, func, sorted_x, sorted_y, expert_of, w1, w2, b1, b2,
                    weights_loaded)
        with ExitStack() as inner:
            combine_experts(nc, env, Stage(nc, inner, tag + "c"), inner, sorted_y, slot, weight)


def route_tokens(nc, env, st, ctx, tag, w, capacity, sorted_x, slot, weight, expert_of, w1, w2, b1, b2, weights_loaded):
    xn = st.sb("xn", [P, TILES, D])
    xnT = st.sb("xnT", [P, DC, T])
    layernorm_stage(nc, env, tag + "l", env.x, dst_tok=xn, dst_T=xnT)
    gate = st.sb("gate", [P, DC, E])
    zero = st.sb("zero", [P, D])
    upto = st.sb("upto", [P, P])
    ids = st.sb("ids", [P, E])
    tile_ids = st.sb("tile_ids", [P, NT])
    lg, pr, hot, cand, place = (st.sb(n, [P, TILES, E]) for n in ("lg", "pr", "hot", "cand", "place"))
    off, count = st.sb("off", [P, TILES, E]), st.sb("count", [P, TILES, E])
    col = [st.sb(f"col{i}", [P, TILES]) for i in range(4)]
    per = [st.sb(f"per{i}", [P, E]) for i in range(5)]
    ends = st.sb("ends", [P, NT, E])
    tile_expert = st.sb("tile_expert", [P, NT])
    lg_ps, cum_ps, tot_ps = (st.ps(n, [P, 512]) for n in ("lg_ps", "cum_ps", "tot_ps"))
    gate_loaded, zero_made, zero_stored, upto_ones, consts = (
        st.sem(n) for n in ("gate_loaded", "zero_made", "zero_stored", "upto_ones", "consts"))
    lg_done, shifted, exped, hot_ready, counted, linked, slot_ready = (
        st.sem(n) for n in ("lg_done", "shifted", "exped", "hot_ready", "counted", "linked", "slot_ready"))
    scattered, = env.scattered.pop()
    block = ctx.enter_context(nc.Block())
    te = lambda buf: buf[:, 0:TILES * E].rearrange("p (t e) -> p t e", e=E)
    over_e = lambda buf: buf[:].unsqueeze(2).to_broadcast([P, TILES, E])
    over_t = lambda buf: buf[:].unsqueeze(1).to_broadcast([P, TILES, E])

    @block.sync
    def _(sp):
        sp.dma_start(gate[:], w("gate_w").rearrange("(c p) e -> p c e", p=P)).then_inc(gate_loaded, 16)
        sp.wait_ge(zero_made, 1)
        sp.dma_start(sorted_x.rearrange("(j p) d -> p j d", p=P),
                     zero[:].unsqueeze(1).to_broadcast([P, NT, D])).then_inc(zero_stored, 16)
        sp.dma_start(w1[:], w("w1").rearrange("e (c p) f -> p e c f", p=P)).then_inc(weights_loaded, 16)
        sp.dma_start(w2[:], w("w2").rearrange("e (c p) d -> p e c d", p=P)).then_inc(weights_loaded, 16)
        if b1 is not None:
            sp.dma_start(b1[:], w("b1").rearrange("e (c p) -> p e c", p=P), allow_slow_non_contiguous=True).then_inc(weights_loaded, 16)
            sp.dma_start(b2[:], w("b2").partition_broadcast(P)).then_inc(weights_loaded, 16)

    @block.gpsimd
    def _(pool):
        nc.gpsimd.memset(zero[:], 0.0).then_inc(zero_made, 1)
        nc.gpsimd.memset(upto[:], 1.0).then_inc(upto_ones, 1)
        nc.gpsimd.iota(ids[:], [[1, E]], base=0, channel_multiplier=0, allow_small_or_imprecise_dtypes=True).then_inc(consts, 1)
        nc.gpsimd.iota(tile_ids[:], [[1, NT]], base=0, channel_multiplier=0, allow_small_or_imprecise_dtypes=True).then_inc(consts, 1)
        pool.wait_ge(upto_ones, 1)
        nc.gpsimd.affine_select(out=upto[:], in_=upto[:], compare_op=ALU.is_ge, fill=0.0, base=0, pattern=[[1, P]],
                                channel_multiplier=-1).then_inc(consts, 1)
        pool.wait_ge(slot_ready, 1)
        pool.wait_ge(zero_stored, 16)
        for t in range(TILES):
            nc.gpsimd.indirect_dma_start(sorted_x, bass.IndirectOffsetOnAxis(ap=slot[:, t:t + 1], axis=0),
                                         xn[:, t, :], None).then_inc(scattered, 16)
        pool.wait_ge(scattered, 16 * TILES)

    @block.tensor
    def _(pe):
        pe.wait_ge(gate_loaded, 16)
        for t in range(TILES):
            for c in range(DC):
                last = nc.tensor.matmul(lg_ps[:, t * E:(t + 1) * E], xnT[:, c, t * P:(t + 1) * P], gate[:, c, :],
                                        start=c == 0, stop=c == DC - 1)
        last.then_inc(lg_done, 1)
        pe.wait_ge(hot_ready, 1)
        pe.wait_ge(consts, 3)
        hot2 = hot[:].rearrange("p t e -> p (t e)")
        nc.tensor.matmul(cum_ps[:, 0:TILES * E], upto[:], hot2, start=True, stop=True)
        nc.tensor.matmul(tot_ps[:, 0:TILES * E], env.ones[:], hot2, start=True, stop=True).then_inc(counted, 1)

    @block.scalar
    def _(act):
        act.wait_ge(shifted, 1)
        nc.scalar.activation(pr[:], lg[:], ACT.Exp).then_inc(exped, 1)

    @block.vector
    def _(dve):
        step = chain(dve, linked)
        tt = lambda o, a, b, op: step(nc.vector.tensor_tensor(o, a, b, op))
        ts = lambda o, a, s1, s2, op0, op1=None: step(
            nc.vector.tensor_scalar(o, a, s1, s2, op0) if op1 is None else nc.vector.tensor_scalar(o, a, s1, s2, op0, op1))
        dve.wait_ge(lg_done, 1)
        step(nc.vector.tensor_reduce(col[0][:], te(lg_ps), AX_X, ALU.max))
        nc.vector.tensor_tensor(lg[:], te(lg_ps), over_e(col[0]), ALU.subtract).then_inc(shifted, 1)
        dve.wait_ge(exped, 1)
        step(nc.vector.tensor_reduce(col[1][:], pr[:], AX_X, ALU.add))
        step(nc.vector.reciprocal(col[1][:], col[1][:]))
        tt(pr[:], pr[:], over_e(col[1]), ALU.mult)
        step(nc.vector.tensor_reduce(weight[:], pr[:], AX_X, ALU.max))
        tt(cand[:], pr[:], over_e(weight), ALU.is_lt)
        dve.wait_ge(consts, 3)
        step(nc.vector.scalar_tensor_tensor(cand[:], cand[:], float(E), over_t(ids), ALU.mult, ALU.add))
        step(nc.vector.tensor_reduce(col[2][:], cand[:], AX_X, ALU.min))
        nc.vector.tensor_tensor(hot[:], over_t(ids), over_e(col[2]), ALU.is_equal).then_inc(hot_ready, 1)
        dve.wait_ge(counted, 1)
        step(nc.vector.tensor_copy(count[:], te(tot_ps)))
        step(nc.vector.memset(off[:, 0, :], 0.0))
        for t in range(1, TILES):
            tt(off[:, t, :], off[:, t - 1, :], count[:, t - 1, :], ALU.add)
        tt(per[0][:], off[:, TILES - 1, :], count[:, TILES - 1, :], ALU.add)
        ts(per[1][:], per[0][:], 1.0 / P, (P - 1.0) / P - 0.5 + 0.5 / P, ALU.mult, ALU.add)
        ts(per[1][:], per[1][:], ROUND, -ROUND, ALU.add, ALU.add)
        step(nc.vector.tensor_copy(per[2][:, 0:1], per[1][:, 0:1]))
        for e in range(1, E):
            tt(per[2][:, e:e + 1], per[2][:, e - 1:e], per[1][:, e:e + 1], ALU.add)
        tt(per[3][:], per[2][:], per[1][:], ALU.subtract)
        ts(per[3][:], per[3][:], float(P), -1.0, ALU.mult, ALU.add)
        tt(place[:], off[:], te(cum_ps), ALU.add)
        tt(cand[:], place[:], over_t(per[3]), ALU.add)
        tt(cand[:], cand[:], hot[:], ALU.mult)
        step(nc.vector.tensor_reduce(col[3][:], cand[:], AX_X, ALU.add))
        nc.vector.tensor_copy(slot[:], col[3][:]).then_inc(slot_ready, 1)
        if capacity is not None:
            tt(place[:], place[:], hot[:], ALU.mult)
            step(nc.vector.tensor_reduce(col[0][:], place[:], AX_X, ALU.add))
            ts(col[0][:], col[0][:], float(capacity), None, ALU.is_le)
            tt(weight[:], weight[:], col[0][:], ALU.mult)
        tt(ends[:], per[2][:].unsqueeze(1).to_broadcast([P, NT, E]), tile_ids[:].unsqueeze(2).to_broadcast([P, NT, E]), ALU.is_le)
        step(nc.vector.tensor_reduce(tile_expert[:], ends[:], AX_X, ALU.add))
        ts(tile_expert[:], tile_expert[:], float(E - 1), None, ALU.min)
        step(nc.vector.tensor_copy(expert_of[:], tile_expert[:]))


def routed_experts(nc, env, st, ctx, func, sorted_x, sorted_y, expert_of, w1, w2, b1, b2, weights_loaded):
    xs, ys = st.sb("xs", [P, 2, D]), st.sb("ys", [P, 2, D])
    xT = st.sb("xT", [P, 2, DC, P])
    h = st.sb("h", [P, 2, F])
    hT = st.sb("hT", [P, FC, P])
    x_ps, y_ps = st.ps("x_ps", [P, 512]), st.ps("y_ps", [P, 512])
    h_ps = st.ps("h_ps", [P, 2, F])
    t_ps = st.ps("t_ps", [P, F])
    xs_loaded = [st.sem(f"xs_loaded{u}") for u in range(2)]
    ys_stored = env.stored.pop()
    x_turned, x_evac, h_done, h_evac, h_turned, hT_evac, y_done, y_evac = (
        st.sem(n) for n in ("x_turned", "x_evac", "h_done", "h_evac", "h_turned", "hT_evac", "y_done", "y_evac"))
    table_loaded = st.sem("table_loaded")
    HB = F // 512
    EV = FC if b1 is not None else HB
    block = ctx.enter_context(nc.Block())

    def of_buffer(j, u):
        return 8 * j + (16 - 8 * u)

    def pipeline(eng, front, back):
        front(0, 0)
        with eng.Fori(0, (NT - 1) // 2) as i:
            for v in range(2):
                front(2 * i + (1 + v), 1 - v)
                back(2 * i + v, v)
        back(NT - 1, (NT - 1) % 2)

    @block.sync
    def _(sp):
        def load(j, u):
            if not isinstance(j, int):
                sp.wait_ge(x_turned, j - 1)
            sp.dma_start(xs[:, u, :], sorted_x[bass.ds(j * P, P), :]).then_inc(xs_loaded[u], 16)

        load(0, 0)
        load(1, 1)
        with sp.Fori(1, (NT - 1) // 2) as i:
            for u in range(2):
                load(2 * i + u, u)
        sp.wait_ge(x_turned, NT - 2)
        load(NT - 1, (NT - 1) % 2)

    @block.gpsimd
    def _(pool):
        def store(j, u):
            pool.wait_ge(y_evac, j + 1)
            nc.gpsimd.dma_start(sorted_y[bass.ds(j * P, P), :], ys[:, u, :]).then_inc(ys_stored[u], 16)

        with pool.Fori(0, (NT - 1) // 2) as i:
            for u in range(2):
                store(2 * i + u, u)
        store(NT - 1, (NT - 1) % 2)
        pool.wait_ge(ys_stored[0], 16 * ((NT + 1) // 2))
        pool.wait_ge(ys_stored[1], 16 * (NT // 2))

    @block.tensor
    def _(pe):
        pe.wait_ge(weights_loaded, 32 if b1 is None else 64)

        def turn_x(j, u):
            pe.wait_ge(xs_loaded[u], of_buffer(j, u))
            if not isinstance(j, int):
                pe.wait_ge(x_evac, j)
            for c in range(DC):
                last = nc.tensor.transpose(x_ps[:, c * P:(c + 1) * P], xs[:, u, c * P:(c + 1) * P], env.ident[:])
            last.then_inc(x_turned, 1)

        def expand(j, u):
            e = pe.value_load(expert_of[0:1, bass.ds(j, 1)], min_val=0, max_val=E - 1)
            pe.wait_ge(x_evac, j + 1)
            for k in range(HB):
                for c in range(DC):
                    last = nc.tensor.matmul(h_ps[:, u, k * 512:(k + 1) * 512], xT[:, u, c, :],
                                            w1[:, bass.ds(e, 1), c, k * 512:(k + 1) * 512].rearrange("p a n -> p (a n)"),
                                            start=c == 0, stop=c == DC - 1)
            last.then_inc(h_done, 1)

        def turn_h(j, u, reuse):
            pe.wait_ge(h_evac, HB * (j + 1))
            if reuse:
                pe.wait_ge(hT_evac, EV * j)
            for f in range(FC):
                last = nc.tensor.transpose(t_ps[:, f * P:(f + 1) * P], h[:, u, f * P:(f + 1) * P], env.ident[:])
            last.then_inc(h_turned, 1)

        def reduce(j, u, reuse):
            e = pe.value_load(expert_of[0:1, bass.ds(j, 1)], min_val=0, max_val=E - 1)
            pe.wait_ge(hT_evac, EV * (j + 1))
            if reuse:
                pe.wait_ge(y_evac, j)
            for f in range(FC):
                last = nc.tensor.matmul(y_ps[:, 0:D], hT[:, f, :], w2[:, bass.ds(e, 1), f, :].rearrange("p a n -> p (a n)"),
                                        start=f == 0, stop=f == FC - 1)
            last.then_inc(y_done, 1)

        turn_x(0, 0)
        expand(0, 0)
        with pe.Fori(0, (NT - 1) // 2) as i:
            for v in range(2):
                j, u = 2 * i + v, v
                turn_x(j + 1, 1 - u)
                turn_h(j, u, True)
                expand(j + 1, 1 - u)
                reduce(j, u, True)
        turn_h(NT - 1, (NT - 1) % 2, True)
        reduce(NT - 1, (NT - 1) % 2, True)

    @block.scalar
    def _(act):
        def front(j, u):
            act.wait_ge(x_turned, j + 1)
            nc.scalar.copy(xT[:, u], x_ps[:, 0:D].rearrange("p (c t) -> p c t", c=DC)).then_inc(x_evac, 1)

        def back(j, u):
            e = act.value_load(expert_of[0:1, bass.ds(j, 1)], min_val=0, max_val=E - 1) if b1 is not None else None
            act.wait_ge(h_turned, j + 1)
            for k in range(EV):
                n = F // EV // P
                fs = slice(k * n, (k + 1) * n)
                bias = b1[:, bass.ds(e, 1), k] if b1 is not None else 0.0
                nc.scalar.activation(hT[:, fs, :], t_ps[:, k * n * P:(k + 1) * n * P].rearrange("p (f t) -> p f t", f=n),
                                     func, bias=bias).then_inc(hT_evac, 1)

        nc.scalar.activation(hT[:, 0, 0:1], env.eps[:], func).then_inc(table_loaded, 1)
        act.wait_ge(table_loaded, 1)
        pipeline(act, front, back)

    @block.vector
    def _(dve):
        def front(j, u):
            dve.wait_ge(h_done, j + 1)
            for k in range(HB):
                nc.vector.tensor_copy(h[:, u, k * 512:(k + 1) * 512], h_ps[:, u, k * 512:(k + 1) * 512]).then_inc(h_evac, 1)

        def back(j, u):
            e = dve.value_load(expert_of[0:1, bass.ds(j, 1)], min_val=0, max_val=E - 1) if b2 is not None else None
            dve.wait_ge(y_done, j + 1)
            if not isinstance(j, int):
                dve.wait_ge(ys_stored[u], of_buffer(j, u) - 16)
            elif j >= 2:
                dve.wait_ge(ys_stored[u], 16 * (j // 2))
            if b2 is None:
                nc.vector.tensor_copy(ys[:, u, :], y_ps[:, 0:D]).then_inc(y_evac, 1)
            else:
                nc.vector.tensor_tensor(ys[:, u, :], y_ps[:, 0:D], b2[:, bass.ds(e, 1), :].rearrange("p a n -> p (a n)"),
                                        ALU.add).then_inc(y_evac, 1)

        pipeline(dve, front, back)


def combine_experts(nc, env, st, ctx, sorted_y, slot, weight):
    yg = st.sb("yg", [P, TILES, D])
    gathered = env.gathered.pop()
    added = st.sem("added")
    block = ctx.enter_context(nc.Block())

    @block.gpsimd
    def _(pool):
        for t in range(TILES):
            nc.gpsimd.indirect_dma_start(yg[:, t, :], None, sorted_y, bass.IndirectOffsetOnAxis(ap=slot[:, t:t + 1], axis=0)
                                         ).then_inc(gathered[t], 16)

    @block.vector
    def _(dve):
        for t in range(TILES):
            dve.wait_ge(gathered[t], 16)
            nc.vector.scalar_tensor_tensor(env.x[:, t, :], yg[:, t, :], weight[:, t:t + 1], env.x[:, t, :], ALU.mult,
                                           ALU.add).then_inc(added, 1)
        dve.wait_ge(added, TILES)



WIDE = H * NCTX
BANK_HEADS = (range(0, 6), range(6, 12), range(12, 16))


def spread(ap, shape):
    return ap.to_broadcast(shape)


def cross_attention_stage(nc, env, tag, args, name, mask, side, hides):
    w = lambda n: args[f"{name}_{n}"]
    with ExitStack() as ctx:
        st = Stage(nc, ctx, tag)
        qT, kbd = st.sb("qT", [P, DC, T]), st.sb("kbd", [P, DC, B, H // DC * NCTX])
        v, neg = st.sb("v", [P, B, D]), st.sb("neg", [P, TILES, NCTX])
        with ExitStack() as inner:
            cross_operands(nc, env, Stage(nc, inner, tag + "p"), inner, w, mask, hides, qT, kbd, v, neg)
        out = st.sb("out", [P, TILES, D])
        with ExitStack() as inner:
            cross_attend(nc, env, Stage(nc, inner, tag + "a"), inner, side, qT, kbd, v, neg, out)
        add_projection_stage(nc, env, tag + "o", out, w("Wo"), w("bo"))


def cross_operands(nc, env, st, ctx, w, mask, hides, qT, kbd, v, neg):
    sb, ps, sem = st.sb, st.ps, st.sem
    half = H // DC
    xT = sb("xT", [P, DC, T])
    layernorm_stage(nc, env, st.tag + "l", env.x, dst_T=xT)
    wq, wk, wv = (sb(n, [P, DC, D]) for n in ("wq", "wk", "wv"))
    bq, bqs, bk, bv = sb("bq", [P, DC]), sb("bqs", [P, DC]), sb("bk", [P, DC]), sb("bv", [P, D])
    mask_in = sb("mask_in", [P, TILES, NCTX], mask.dtype)
    ind = sb("ind", [P, half])
    ctxT, kT = sb("ctxT", [P, DC, B * NCTX]), sb("kT", [P, DC, B * NCTX])
    q_ps, c_ps, k_ps, v_ps = ps("q_ps", [P, 4, 512]), ps("c_ps", [P, 512]), ps("k_ps", [P, 512]), ps("v_ps", [P, 512])
    kv_loaded, q_loaded, mask_loaded, ones_set, ind_lower, ind_made, bqs_ready, neg_ready = (
        sem(n) for n in ("kv_loaded", "q_loaded", "mask_loaded", "ones_set", "ind_lower", "ind_made", "bqs_ready", "neg_ready"))
    ctx_turned, ctx_evac, k_done, k_ready, kbd_ready, v_done, v_ready, q_done, q_evac = (
        sem(n) for n in ("ctx_turned", "ctx_evac", "k_done", "k_ready", "kbd_ready", "v_done", "v_ready", "q_done", "q_evac"))
    block = ctx.enter_context(nc.Block())
    jobs = [(f, n) for n in range(T // 512) for f in range(DC)]

    @block.sync
    def _(sp):
        mat = lambda n: w(n).rearrange("(c p) n -> p c n", p=P)
        col = lambda n: w(n).rearrange("(c p) -> p c", p=P)
        sp.dma_start(wk[:], mat("Wk")).then_inc(kv_loaded, 16)
        sp.dma_start(wv[:], mat("Wv")).then_inc(kv_loaded, 16)
        sp.dma_start(bk[:], col("bk"), allow_slow_non_contiguous=True).then_inc(kv_loaded, 16)
        sp.dma_start(bv[:], w("bv").partition_broadcast(P)).then_inc(kv_loaded, 16)
        sp.dma_start(wq[:], mat("Wq")).then_inc(q_loaded, 16)
        sp.dma_start(bq[:], col("bq"), allow_slow_non_contiguous=True).then_inc(q_loaded, 16)
        sp.dma_start(mask_in[:], mask.rearrange("b (t p) j -> p (b t) j", p=P)).then_inc(mask_loaded, 16)

    @block.gpsimd
    def _(pool):
        nc.gpsimd.memset(ind[:], 1.0).then_inc(ones_set, 1)
        pool.wait_ge(ones_set, 1)
        nc.gpsimd.affine_select(out=ind[:], in_=ind[:], compare_op=ALU.is_ge, fill=0.0, base=0,
                                pattern=[[-HD, half]], channel_multiplier=1).then_inc(ind_lower, 1)
        pool.wait_ge(ind_lower, 1)
        nc.gpsimd.affine_select(out=ind[:], in_=ind[:], compare_op=ALU.is_ge, fill=0.0, base=HD - 1,
                                pattern=[[HD, half]], channel_multiplier=-1).then_inc(ind_made, 1)

    @block.tensor
    def _(pe):
        for b in range(B):
            for c in range(DC):
                last = nc.tensor.transpose(c_ps[:, (c * B + b) * NCTX:(c * B + b + 1) * NCTX],
                                           env.ctx_tok[0:NCTX, b, c * P:(c + 1) * P], env.ident[0:NCTX, 0:NCTX])
        last.then_inc(ctx_turned, 1)
        pe.wait_ge(kv_loaded, 64)
        pe.wait_ge(ctx_evac, 1)
        for f in range(DC):
            for c in range(DC):
                last = nc.tensor.matmul(k_ps[:, f * B * NCTX:(f + 1) * B * NCTX], wk[:, c, f * P:(f + 1) * P],
                                        ctxT[:, c, :], start=c == 0, stop=c == DC - 1)
        last.then_inc(k_done, 1)
        for b in range(B):
            for c in range(DC):
                last = nc.tensor.matmul(v_ps[0:NCTX, b * D:(b + 1) * D], ctxT[:, c, b * NCTX:(b + 1) * NCTX], wv[:, c, :],
                                        start=c == 0, stop=c == DC - 1)
        last.then_inc(v_done, 1)
        pe.wait_ge(q_loaded, 32)
        for i, (f, n) in enumerate(jobs):
            if i >= 4:
                pe.wait_ge(q_evac, i - 3)
            for c in range(DC):
                last = nc.tensor.matmul(q_ps[:, i % 4, :], wq[:, c, f * P:(f + 1) * P], xT[:, c, n * 512:(n + 1) * 512],
                                        start=c == 0, stop=c == DC - 1)
            last.then_inc(q_done, 1)

    @block.scalar
    def _(act):
        act.wait_ge(ctx_turned, 1)
        nc.scalar.copy(ctxT[:].rearrange("p c t -> p (c t)"), c_ps[:, 0:DC * B * NCTX]).then_inc(ctx_evac, 1)
        act.wait_ge(bqs_ready, 1)
        for i, (f, n) in enumerate(jobs):
            act.wait_ge(q_done, i + 1)
            nc.scalar.activation(qT[:, f, n * 512:(n + 1) * 512], q_ps[:, i % 4, :], ACT.Identity, bias=bqs[:, f:f + 1],
                                 scale=HD ** -0.5).then_inc(q_evac, 1)

    @block.vector
    def _(dve):
        dve.wait_ge(q_loaded, 32)
        nc.vector.tensor_scalar(bqs[:], bq[:], HD ** -0.5, None, ALU.mult).then_inc(bqs_ready, 1)
        dve.wait_ge(mask_loaded, 16)
        if hides:
            nc.vector.tensor_scalar(neg[:], mask_in[:], -1e15, None, ALU.mult).then_inc(neg_ready, 1)
        else:
            nc.vector.tensor_scalar(neg[:], mask_in[:], 0.0, NEG, ALU.is_equal, ALU.mult).then_inc(neg_ready, 1)
        dve.wait_ge(kv_loaded, 64)
        dve.wait_ge(ind_made, 1)
        dve.wait_ge(k_done, 1)
        for c in range(DC):
            nc.vector.tensor_scalar(kT[:, c, :], k_ps[:, c * B * NCTX:(c + 1) * B * NCTX], bk[:, c:c + 1], None,
                                    ALU.add).then_inc(k_ready, 1)
        dve.wait_ge(k_ready, DC)
        for c in range(DC):
            for b in range(B):
                nc.vector.tensor_tensor(kbd[:, c, b, :].rearrange("p (h j) -> p h j", h=half),
                                        spread(kT[:, c:c + 1, b * NCTX:(b + 1) * NCTX], [P, half, NCTX]),
                                        spread(ind[:, :].unsqueeze(2), [P, half, NCTX]), ALU.mult).then_inc(kbd_ready, 1)
        dve.wait_ge(v_done, 1)
        for b in range(B):
            nc.vector.tensor_tensor(v[0:NCTX, b, :], v_ps[0:NCTX, b * D:(b + 1) * D], bv[0:NCTX, :], ALU.add).then_inc(v_ready, 1)


def cross_attend(nc, env, st, ctx, side, qT, kbd, v, neg, out):
    sb, ps, sem = st.sb, st.ps, st.sem
    half = H // DC
    q = sb("q", [P, 2, DC, P])
    bias = sb("bias", [P, 2, WIDE]) if side is not None else None
    z = sb("z", [P, 2, WIDE])
    top, total, inv = (sb(n, [P, 2, H]) for n in ("top", "total", "inv"))
    pT = sb("pT", [P, 2, H * P])
    s_ps, pt_ps, o_ps = ps("s_ps", [P, 3, 512]), ps("pt_ps", [P, 2, 512]), ps("o_ps", [P, 2, 512])
    side_loaded = [sem(f"side_loaded{u}") for u in range(2)]
    q_placed = [sem(f"q_placed{u}") for u in range(2)]
    scored, biased, z_part, z_added, top_ready, shifted, exped = (
        sem(n) for n in ("scored", "biased", "z_part", "z_added", "top_ready", "shifted", "exped"))
    summed, inv_ready, p_turned, p_evac, weighed, normed, table_loaded = (
        sem(n) for n in ("summed", "inv_ready", "p_turned", "p_evac", "weighed", "normed", "table_loaded"))
    block = ctx.enter_context(nc.Block())
    by_head = lambda ap, n=H: ap.rearrange("p (h j) -> p h j", h=n)
    AHEAD = 2

    def tiles(eng, front, back):
        for b in range(B):
            g0 = b * TPB
            front(b, g0, 0)
            if b:
                back(b - 1, g0 - 1, 1)
            front(b, g0 + 1, 1)
            back(b, g0, 0)
            with eng.Fori(g0 // 2 + 1, g0 // 2 + TPB // 2) as i:
                for u in range(2):
                    front(b, 2 * i + u, u)
                    back(b, 2 * i + u - 1, 1 - u)
        back(B - 1, TILES - 1, 1)

    def of_buffer(g, u):
        return 8 * g + (16 - 8 * u)

    @block.sync
    def _(sp):
        def load(b, g, u):
            if not (isinstance(g, int) and g < 2):
                sp.wait_ge(scored, g - 1)
            sp.dma_start(q[:, u], qT[:, :, bass.ds(g * P, P)]).then_inc(q_placed[u], 16)
            if side is not None:
                sp.wait_ge(z_added, g + 1)
                rows = bass.ds((g - b * TPB) * P, P)
                sp.dma_start(by_head(bias[:, u, :]), side[b, :, rows, :].rearrange("h p j -> p h j")).then_inc(side_loaded[u], 16)

        tiles(sp, load, lambda *a: None)

    @block.gpsimd
    def _(pool):
        def hide(g, u):
            bt = by_head(bias[:, u, :])
            pool.wait_ge(side_loaded[u], of_buffer(g, u))
            nc.gpsimd.tensor_tensor(bt, bt, spread(neg[:, bass.ds(g, 1), :], [P, H, NCTX]), ALU.add).then_inc(biased, 1)

        def shift(g, u):
            zt = by_head(z[:, u, :])
            pool.wait_ge(top_ready, g + 1)
            nc.gpsimd.tensor_tensor(zt, zt, spread(top[:, u, :].unsqueeze(2), [P, H, NCTX]), ALU.subtract).then_inc(shifted, 1)

        if side is not None:
            hide(0, 0)
        with pool.Fori(0, TILES // 2 - 1) as i:
            for u in range(2):
                if side is not None:
                    hide(2 * i + (u + 1), 1 - u)
                shift(2 * i + u, u)
        if side is not None:
            hide(TILES - 1, 1)
        for u in range(2):
            shift(TILES - 2 + u, u)

    @block.tensor
    def _(pe):
        def score(b, g, u):
            pe.wait_ge(q_placed[u], of_buffer(g, u))
            pe.wait_ge(z_added, g + AHEAD)
            for k, heads in enumerate(BANK_HEADS):
                for c in range(DC):
                    mine = [h for h in heads if h // half == c]
                    if mine:
                        at = (mine[0] - heads[0]) * NCTX
                        last = nc.tensor.matmul(s_ps[:, k, at:at + len(mine) * NCTX], q[:, u, c, :],
                                                kbd[:, c, b, (mine[0] % half) * NCTX:(mine[-1] % half + 1) * NCTX],
                                                start=True, stop=True)
            last.then_inc(scored, 1)

        def weigh(b, g, u):
            pe.wait_ge(exped, g + 1)
            pe.wait_ge(normed, g + 1)

            def product(h):
                last = nc.tensor.matmul(o_ps[:, u, h * HD:(h + 1) * HD], pT[0:NCTX, u, h * P:(h + 1) * P],
                                        v[0:NCTX, b, h * HD:(h + 1) * HD], start=True, stop=True)
                if h == H - 1:
                    last.then_inc(weighed, 1)

            for k in range(6):
                pe.wait_ge(p_evac, 4 * g + k)
                for r in range(4):
                    if k < 4:
                        last = nc.tensor.transpose(pt_ps[0:NCTX, k % 2, r * P:(r + 1) * P],
                                                   z[:, u, (4 * k + r) * NCTX:(4 * k + r + 1) * NCTX], env.ident[:])
                        if r == 3:
                            last.then_inc(p_turned, 1)
                    if k >= 2:
                        product(4 * (k - 2) + r)

        pe.sem_inc(p_turned, 4 * AHEAD)
        tiles(pe, score, weigh)

    @block.vector
    def _(dve):
        def attend(b, g, u):
            dve.wait_ge(scored, g + 1)
            dve.wait_ge(p_turned, 4 * g + 4)
            if side is not None:
                dve.wait_ge(biased, g + 1)
            for k, heads in enumerate(BANK_HEADS):
                n, cols = len(heads), slice(heads[0] * NCTX, (heads[-1] + 1) * NCTX)
                add = by_head(bias[:, u, cols], n) if side is not None else spread(neg[:, bass.ds(g, 1), :], [P, n, NCTX])
                nc.vector.tensor_tensor(by_head(z[:, u, cols], n), by_head(s_ps[:, k, 0:n * NCTX], n), add,
                                        ALU.add).then_inc(z_added if k == 2 else z_part, 1)
            dve.wait_ge(z_part, 2 * g + 2)
            dve.wait_ge(z_added, g + 1 + AHEAD)
            nc.vector.tensor_reduce(top[:, u, :], by_head(z[:, u, :]), AX_X, ALU.max).then_inc(top_ready, 1)

        def normalise(b, g, u):
            dve.wait_ge(exped, g + 1)
            nc.vector.tensor_reduce(total[:, u, :], by_head(z[:, u, :]), AX_X, ALU.add).then_inc(summed, 1)
            dve.wait_ge(summed, g + 1)
            dve.wait_ge(normed, g + 1)
            nc.vector.reciprocal(inv[:, u, :], total[:, u, :]).then_inc(inv_ready, 1)
            dve.wait_ge(inv_ready, g + 1)
            dve.wait_ge(weighed, g + 1)
            nc.vector.tensor_tensor(by_head(tile_of(out, g)), by_head(o_ps[:, u, 0:D]),
                                    spread(inv[:, u, :].unsqueeze(2), [P, H, HD]), ALU.mult).then_inc(normed, 1)

        dve.sem_inc(z_added, AHEAD)
        dve.sem_inc(normed, AHEAD)
        tiles(dve, attend, normalise)
        dve.wait_ge(normed, TILES + AHEAD)

    @block.scalar
    def _(act):
        nc.scalar.activation(total[:, 0, :], env.ones[:, 0:H], ACT.Exp).then_inc(table_loaded, 1)
        act.wait_ge(table_loaded, 1)

        def soften(g, u):
            act.wait_ge(shifted, g + 1)
            nc.scalar.activation(z[:, u, :], z[:, u, :], ACT.Exp).then_inc(exped, 1)

        def evacuate(b, g, u):
            if not (isinstance(g, int) and g == 0):
                act.wait_ge(weighed, g - 1)
            for k in range(4):
                act.wait_ge(p_turned, 4 * g + (k + 1 + 4 * AHEAD))
                nc.scalar.copy(pT[0:NCTX, u, k * 512:(k + 1) * 512], pt_ps[0:NCTX, k % 2, :]).then_inc(p_evac, 1)
            if not (isinstance(g, int) and g == TILES - 1):
                soften(g + 1, 1 - u)

        act.sem_inc(p_evac, 1)
        soften(0, 0)
        tiles(act, lambda *a: None, evacuate)



TOP_P = 0.8


def gated_ffn_stage(nc, env, tag, args, name):
    w = lambda n: args[f"{name}_{n}"]
    with ExitStack() as ctx:
        st = Stage(nc, ctx, tag)
        xnT = st.sb("xnT", [P, DC, T])
        gate = st.sb("gate", [P, TILES, E])
        layernorm_stage(nc, env, tag + "l", env.x, dst_T=xnT)
        with ExitStack() as inner:
            token_gates(nc, env, Stage(nc, inner, tag + "g"), inner, w, xnT, gate)
        with ExitStack() as inner:
            gated_experts(nc, env, Stage(nc, inner, tag + "e"), inner, w, xnT, gate)


def token_gates(nc, env, st, ctx, w, xnT, gate):
    wr, br = st.sb("wr", [P, DC, E]), st.sb("br", [P, E])
    b2 = st.sb("b2", [E, D])
    lower = st.sb("lower", [P, E, E])
    lg, pr, cum, rank = (st.sb(n, [P, TILES, E]) for n in ("lg", "pr", "cum", "rank"))
    above, same = st.sb("above", [P, TILES, E, E]), st.sb("same", [P, TILES, E, E])
    col = st.sb("col", [P, TILES])
    gT = st.sb("gT", [E, T])
    lg_ps, g_ps, y_ps = st.ps("lg_ps", [P, 512]), st.ps("g_ps", [P, 4, 512]), st.ps("y_ps", [P, 2, 512])
    loaded, ones_set, lower_made, lg_done, shifted, exped, linked, gate_ready, g_turned, gT_ready, y_done, added = (
        st.sem(n) for n in ("loaded", "ones_set", "lower_made", "lg_done", "shifted", "exped", "linked", "gate_ready",
                            "g_turned", "gT_ready", "y_done", "added"))
    block = ctx.enter_context(nc.Block())
    over_e = lambda buf: buf[:].unsqueeze(2).to_broadcast([P, TILES, E])
    mine = lambda buf: buf[:].unsqueeze(3).to_broadcast([P, TILES, E, E])
    others = lambda buf: buf[:].unsqueeze(2).to_broadcast([P, TILES, E, E])

    @block.sync
    def _(sp):
        sp.dma_start(wr[:], w("Wr").rearrange("(c p) e -> p c e", p=P)).then_inc(loaded, 16)
        sp.dma_start(br[:], w("br").partition_broadcast(P)).then_inc(loaded, 16)
        sp.dma_start(b2[:], w("b2")).then_inc(loaded, 16)

    @block.gpsimd
    def _(pool):
        nc.gpsimd.memset(lower[:], 1.0).then_inc(ones_set, 1)
        pool.wait_ge(ones_set, 1)
        nc.gpsimd.affine_select(out=lower[:], in_=lower[:], compare_op=ALU.is_ge, fill=0.0, base=0,
                                pattern=[[1, E], [-1, E]], channel_multiplier=0).then_inc(lower_made, 1)

    @block.tensor
    def _(pe):
        pe.wait_ge(loaded, 48)
        for t in range(TILES):
            for c in range(DC):
                last = nc.tensor.matmul(lg_ps[:, t * E:(t + 1) * E], xnT[:, c, t * P:(t + 1) * P], wr[:, c, :],
                                        start=c == 0, stop=c == DC - 1)
        last.then_inc(lg_done, 1)
        pe.wait_ge(gate_ready, 1)
        for t in range(TILES):
            last = nc.tensor.transpose(g_ps[0:E, t // 4, (t % 4) * P:(t % 4 + 1) * P], gate[:, t, :], env.ident[:])
        last.then_inc(g_turned, 1)
        pe.wait_ge(gT_ready, 4)
        for t in range(TILES):
            if t >= 2:
                pe.wait_ge(added, t - 1)
            nc.tensor.matmul(y_ps[:, t % 2, 0:D], gT[:, t * P:(t + 1) * P], b2[:], start=True, stop=True).then_inc(y_done, 1)

    @block.scalar
    def _(act):
        act.wait_ge(shifted, 1)
        nc.scalar.activation(pr[:], lg[:], ACT.Exp).then_inc(exped, 1)
        act.wait_ge(g_turned, 1)
        for k in range(4):
            nc.scalar.copy(gT[:, k * 512:(k + 1) * 512], g_ps[0:E, k, :]).then_inc(gT_ready, 1)

    @block.vector
    def _(dve):
        step = chain(dve, linked)
        tt = lambda o, a, b, op: step(nc.vector.tensor_tensor(o, a, b, op))
        dve.wait_ge(lg_done, 1)
        dve.wait_ge(loaded, 48)
        tt(lg[:], lg_ps[:, 0:TILES * E].rearrange("p (t e) -> p t e", e=E), br[:].unsqueeze(1).to_broadcast([P, TILES, E]), ALU.add)
        step(nc.vector.tensor_reduce(col[:], lg[:], AX_X, ALU.max))
        nc.vector.tensor_tensor(lg[:], lg[:], over_e(col), ALU.subtract).then_inc(shifted, 1)
        dve.wait_ge(exped, 1)
        step(nc.vector.tensor_reduce(col[:], pr[:], AX_X, ALU.add))
        step(nc.vector.reciprocal(col[:], col[:]))
        tt(pr[:], pr[:], over_e(col), ALU.mult)
        dve.wait_ge(lower_made, 1)
        tt(above[:], others(pr), mine(pr), ALU.is_gt)
        tt(same[:], others(pr), mine(pr), ALU.is_equal)
        tt(same[:], same[:], lower[:].unsqueeze(1).to_broadcast([P, TILES, E, E]), ALU.mult)
        tt(above[:], above[:], same[:], ALU.add)
        step(nc.vector.tensor_reduce(rank[:], above[:], AX_X, ALU.add))
        tt(above[:], above[:], others(pr), ALU.mult)
        step(nc.vector.tensor_reduce(cum[:], above[:], AX_X, ALU.add))
        step(nc.vector.tensor_scalar(cum[:], cum[:], TOP_P, None, ALU.is_lt))
        step(nc.vector.scalar_tensor_tensor(cum[:], rank[:], 1.0, cum[:], ALU.is_le, ALU.max))
        nc.vector.tensor_tensor(gate[:], pr[:], cum[:], ALU.mult).then_inc(gate_ready, 1)
        for t in range(TILES):
            dve.wait_ge(y_done, t + 1)
            nc.vector.tensor_tensor(env.x[:, t, :], env.x[:, t, :], y_ps[:, t % 2, 0:D], ALU.add).then_inc(added, 1)


def gated_experts(nc, env, st, ctx, w, xnT, gate):
    CHUNK = 512
    CHUNKS = T // CHUNK
    CT = CHUNK // P
    STEPS = 2 * CHUNKS
    w1, w2 = st.sb("w1", [P, 2, DC, F]), st.sb("w2", [P, 2, FC, D])
    b1 = st.sb("b1", [P, 2, FC])
    hT = st.sb("hT", [P, 2, FC, CHUNK])
    h_ps, y_ps = st.ps("h_ps", [P, 4, 512]), st.ps("y_ps", [P, 4, 512])
    w_loaded = [st.sem(f"w_loaded{v}") for v in range(2)]
    h_done, h_evac, y_done, y_added, table_loaded = (
        st.sem(n) for n in ("h_done", "h_evac", "y_done", "y_added", "table_loaded"))
    block = ctx.enter_context(nc.Block())

    @block.sync
    def _(sp):
        def load(e, v):
            sp.dma_start(b1[:, v], w("b1")[bass.ds(e, 1)].rearrange("a (c p) -> p (a c)", p=P),
                         allow_slow_non_contiguous=True).then_inc(w_loaded[v], 16)
            sp.dma_start(w1[:, v], w("W1")[bass.ds(e, 1)].rearrange("a (c p) f -> p (a c) f", p=P)).then_inc(w_loaded[v], 16)
            sp.dma_start(w2[:, v], w("W2")[bass.ds(e, 1)].rearrange("a (c p) d -> p (a c) d", p=P)).then_inc(w_loaded[v], 16)

        for v in range(2):
            load(v, v)
        with sp.Fori(1, E // 2) as i:
            for v in range(2):
                sp.wait_ge(y_done, CT * CHUNKS * (2 * i + (v - 1)))
                load(2 * i + v, v)

    @block.tensor
    def _(pe):
        def hidden(i, k):
            v, n, s = k // CHUNKS, k % CHUNKS, STEPS * i + k
            if n == 0:
                pe.wait_ge(w_loaded[v], 48 * i + 48)
            for f in range(FC):
                if k or f >= 4:
                    pe.wait_ge(h_evac, FC * s + (f - 3))
                for c in range(DC):
                    last = nc.tensor.matmul(h_ps[:, f % 4, :], w1[:, v, c, f * P:(f + 1) * P],
                                            xnT[:, c, n * CHUNK:(n + 1) * CHUNK], start=c == 0, stop=c == DC - 1)
                last.then_inc(h_done, 1)

        def reduce(i, k):
            v, n, s = k // CHUNKS, k % CHUNKS, STEPS * i + k
            pe.wait_ge(h_evac, FC * s + FC)
            for q in range(CT):
                if k == 0:
                    pe.wait_ge(y_added, CT * s)
                else:
                    pe.wait_ge(y_added, CT * s + (q - 3))
                for f in range(FC):
                    last = nc.tensor.matmul(y_ps[:, q, 0:D], hT[:, k % 2, f, q * P:(q + 1) * P], w2[:, v, f, :],
                                            start=f == 0, stop=f == FC - 1)
                last.then_inc(y_done, 1)

        with pe.Fori(0, E // 2) as i:
            hidden(i, 0)
            for k in range(STEPS):
                if k + 1 < STEPS:
                    hidden(i, k + 1)
                reduce(i, k)

    @block.scalar
    def _(act):
        nc.scalar.activation(hT[:, 0, 0, 0:1], env.eps[:], ACT.Relu).then_inc(table_loaded, 1)
        act.wait_ge(table_loaded, 1)
        with act.Fori(0, E // 2) as i:
            for k in range(STEPS):
                v, s = k // CHUNKS, STEPS * i + k
                if k % CHUNKS == 0:
                    act.wait_ge(w_loaded[v], 48 * i + 48)
                for f in range(FC):
                    if f == 0:
                        act.wait_ge(y_done, CT * s if k == 0 else CT * s - CT)
                    act.wait_ge(h_done, FC * s + (f + 1))
                    nc.scalar.activation(hT[:, k % 2, f, :], h_ps[:, f % 4, :], ACT.Relu,
                                         bias=b1[:, v, f:f + 1]).then_inc(h_evac, 1)

    @block.vector
    def _(dve):
        with dve.Fori(0, E // 2) as i:
            for k in range(STEPS):
                v, n, s = k // CHUNKS, k % CHUNKS, STEPS * i + k
                dve.wait_ge(y_added, CT * s)
                for q in range(CT):
                    xt = env.x[:, n * CT + q, :]
                    dve.wait_ge(y_done, CT * s + (q + 1))
                    nc.vector.scalar_tensor_tensor(xt, y_ps[:, q, 0:D], gate[:, n * CT + q, bass.ds(2 * i + v, 1)], xt,
                                                   ALU.mult, ALU.add).then_inc(y_added, 1)




def build(nc, args, out):
    kern_dram = nc.dram_tensor("conv_kernels", [B, KW], F32).ap()
    rows = lambda m: m.rearrange("b o s j -> b (o s) j")
    with ExitStack() as ctx:
        env = Env(nc, ctx)
        setup_stage(nc, env, args)
        conv_kernels_stage(nc, env, "hs", args, "L0_xattn", kern_dram)
        conv_attention_stage(nc, env, "c0", args, "L0_xattn", kern_dram, args["mask_SxS_bc0"])
        quant_ffn_stage(nc, env, "qf", args, "L0_ffn")
        latent_attention_stage(nc, env, "lt", args, "L1_xattn")
        routed_ffn_stage(nc, env, "m1", args, "L1_ffn", ACT.Relu, False, 320)
        cross_attention_stage(nc, env, "c2", args, "L2_xattn", rows(args["mask_Bx1xSxS2_bk1"]), None, 1)
        gated_ffn_stage(nc, env, "m2", args, "L2_ffn")
        cross_attention_stage(nc, env, "c3", args, "L3_xattn", rows(args["mask_Bx1xSxS2_ik1"]), args["fside_Bx16xSxS2_0"], 0)
        routed_ffn_stage(nc, env, "m3", args, "L3_ffn", ACT.Gelu, True, None)
        store_stage(nc, env, out)


def kernel(**inputs):
    import numpy as _np
    import concourse.bacc as _bacc
    from concourse import mybir as _mybir
    from concourse.bass_utils import run_bass_kernel_spmd as _run

    nc = _bacc.Bacc("TRN2", target_bir_lowering=False, num_devices=1)
    arrays, args = {}, {}
    for name, value in inputs.items():
        a = _np.ascontiguousarray(value)
        arrays[f"in_{name}_dram"] = a
        args[name] = nc.dram_tensor(f"in_{name}_dram", a.shape, _mybir.dt.from_np(a.dtype), kind="ExternalInput").ap()
    out = nc.dram_tensor("out_0_dram", (B, S, D), F32, kind="ExternalOutput").ap()
    build(nc, args, out)
    return _run(nc, [arrays], core_ids=[0]).results[0]["out_0_dram"]
```

```python
from contextlib import ExitStack

import concourse.bass as bass
from concourse import mybir

ALU = mybir.AluOpType
ACT = mybir.ActivationFunctionType
F32 = mybir.dt.float32
BF16 = mybir.dt.bfloat16
U8 = mybir.dt.uint8
I32 = mybir.dt.int32
U32 = mybir.dt.uint32
AX_X = mybir.AxisListType.X
RMAX = bass.bass_isa.ReduceOp.max

P = 128
B, S, D = 2, 1024, 256
NCTX = 77
H = 16
HD = D // H
T = B * S
TILES = T // P
TPB = S // P
DC = D // P
LN_EPS = 1e-5
UNROLL = 8
NEG = -1e30


def chain(eng, sem, base=0):
    done = [0]

    def step(ins):
        done[0] += 1
        ins.then_inc(sem, 1)
        eng.wait_ge(sem, base + done[0])
        return ins

    step.done = done
    return step


class Stage:

    def __init__(self, nc, ctx, tag):
        self.nc, self.ctx, self.tag, self.sems = nc, ctx, tag, []
        ctx.push(lambda kind, *_: self.clear() if kind is None else None)

    def sb(self, name, shape, dt=F32):
        return self.ctx.enter_context(self.nc.sbuf_tensor(f"{self.tag}_{name}", shape, dt))

    def ps(self, name, shape, dt=F32):
        return self.ctx.enter_context(self.nc.psum_tensor(f"{self.tag}_{name}", shape, dt))

    def sem(self, name):
        made = self.ctx.enter_context(self.nc.semaphore(f"{self.tag}_{name}"))
        self.sems.append(made)
        return made

    def clear(self):
        with self.nc.Block() as block:
            @block.gpsimd
            def _(pool):
                runs = []
                for num in sorted(s.num for s in self.sems):
                    if runs and runs[-1].stop == num:
                        runs[-1] = range(runs[-1].start, num + 1)
                    else:
                        runs.append(range(num, num + 1))
                for run in runs:
                    pool.sem_clear(run)


def tile_of(buf, t):
    return buf[:, bass.ds(t, 1), :].rearrange("p a n -> p (a n)")


def setup_stage(nc, env, args):
    with ExitStack() as ctx:
        st = Stage(nc, ctx, "set")
        x_loaded, ctx_loaded = st.sem("x_loaded"), st.sem("ctx_loaded")
        zeroed, made = st.sem("zeroed"), st.sem("made")
        block = ctx.enter_context(nc.Block())

        @block.sync
        def _(sp):
            sp.dma_start(env.x[:], args["x"].rearrange("b (t p) d -> p (b t) d", p=P)).then_inc(x_loaded, 16)
            sp.dma_start(env.ctx_tok[0:NCTX], args["ctx_1024"].rearrange("b t d -> t b d")).then_inc(ctx_loaded, 16)
            sp.wait_ge(x_loaded, 16)
            sp.wait_ge(ctx_loaded, 16)

        @block.gpsimd
        def _(pool):
            nc.gpsimd.memset(env.ident[:], 0.0).then_inc(zeroed, 1)
            nc.gpsimd.memset(env.ones[:], 1.0).then_inc(made, 1)
            nc.gpsimd.memset(env.eps[:], LN_EPS).then_inc(made, 1)
            pool.wait_ge(zeroed, 1)
            nc.gpsimd.affine_select(out=env.ident[:], in_=env.ident[:], compare_op=ALU.not_equal, fill=1.0, base=0,
                                    pattern=[[-1, P]], channel_multiplier=1).then_inc(made, 1)


def row_stats(nc, dve, st, step, src, n, mean, var, stats):
    counted = st.sem("counted")
    with dve.Fori(0, n // UNROLL) as i:
        for u in range(UNROLL):
            t = UNROLL * i + u
            nc.vector.bn_stats(tile_of(stats, t), tile_of(src, t)).then_inc(counted, 1)
    dve.wait_ge(counted, n)
    merge_stats(nc, step, mean, var, stats, D)


def merge_stats(nc, step, mean, var, stats, width):
    even, odd = stats[:, :, 1], stats[:, :, 4]
    step(nc.vector.tensor_tensor(mean, even, odd, ALU.add))
    step(nc.vector.tensor_tensor(var, even, odd, ALU.subtract))
    step(nc.vector.tensor_scalar(mean, mean, 0.5, None, ALU.mult))
    step(nc.vector.scalar_tensor_tensor(var, var, 0.25, var, ALU.mult, ALU.mult))
    step(nc.vector.scalar_tensor_tensor(var, stats[:, :, 2], 1.0 / width, var, ALU.mult, ALU.add))
    step(nc.vector.scalar_tensor_tensor(var, stats[:, :, 5], 1.0 / width, var, ALU.mult, ALU.add))


def layernorm_stage(nc, env, tag, src, dst_tok=None, dst_T=None, ahead=None, ahead_pool=None):
    with ExitStack() as ctx:
        st = Stage(nc, ctx, tag)
        stats = st.sb("stats", [P, TILES, 6])
        mean, var, rstd = (st.sb(n, [P, TILES]) for n in ("mean", "var", "rstd"))
        RING = 4
        turn = st.sb("turn", [P, RING, D])
        turned = st.ps("turned", [P, RING, 512])
        linked, var_ready, std_ready = st.sem("linked"), st.sem("var_ready"), st.sem("std_ready")
        normed, transposed, evacuated = st.sem("normed"), st.sem("transposed"), st.sem("evacuated")
        kept = st.sem("kept")
        both = dst_tok is not None and dst_T is not None
        block = ctx.enter_context(nc.Block())

        if ahead is not None:
            @block.sync
            def _(sp):
                ahead(sp)

        if ahead_pool is not None:
            @block.gpsimd
            def _(pool):
                ahead_pool(pool)

        @block.vector
        def _(dve):
            step = chain(dve, linked)
            row_stats(nc, dve, st, step, src, TILES, mean[:], var[:], stats)
            nc.vector.tensor_scalar(var[:], var[:], LN_EPS, None, ALU.add).then_inc(var_ready, 1)
            dve.wait_ge(std_ready, 1)
            step(nc.vector.reciprocal(rstd[:], rstd[:]))

            def tile(t, u, reuse):
                if dst_T is not None and reuse:
                    dve.wait_ge(transposed, t - (RING - 1))
                for out, done in ((turn[:, u, :], normed), (tile_of(dst_tok, t), kept)) if both else (
                        (turn[:, u, :] if dst_tok is None else tile_of(dst_tok, t), normed),):
                    nc.vector.tensor_scalar(out, tile_of(src, t), mean[:, bass.ds(t, 1)], rstd[:, bass.ds(t, 1)],
                                            ALU.subtract, ALU.mult).then_inc(done, 1)

            for u in range(UNROLL):
                tile(u, u % RING, u >= RING)
            with dve.Fori(1, TILES // UNROLL) as i:
                for u in range(UNROLL):
                    tile(UNROLL * i + u, u % RING, True)
            dve.wait_ge(normed, TILES)
            if both:
                dve.wait_ge(kept, TILES)

        @block.scalar
        def _(act):
            act.wait_ge(var_ready, 1)
            nc.scalar.activation(rstd[:], var[:], ACT.Sqrt).then_inc(std_ready, 1)
            if dst_T is not None:
                with act.Fori(0, TILES // UNROLL) as i:
                    for u in range(UNROLL):
                        t = UNROLL * i + u
                        act.wait_ge(transposed, t + 1)
                        nc.scalar.copy(dst_T[:, :, bass.ds(t * P, P)],
                                       turned[:, u % RING, 0:D].rearrange("p (c t) -> p c t", c=DC)).then_inc(evacuated, 1)
                act.wait_ge(evacuated, TILES)

        if dst_T is not None:
            @block.tensor
            def _(pe):
                def tile(t, u, reuse):
                    pe.wait_ge(normed, t + 1)
                    if reuse:
                        pe.wait_ge(evacuated, t - (RING - 1))
                    for c in range(DC):
                        last = nc.tensor.transpose(turned[:, u, c * P:(c + 1) * P], turn[:, u, c * P:(c + 1) * P],
                                                   env.ident[:])
                    last.then_inc(transposed, 1)

                for u in range(UNROLL):
                    tile(u, u % RING, u >= RING)
                with pe.Fori(1, TILES // UNROLL) as i:
                    for u in range(UNROLL):
                        tile(UNROLL * i + u, u % RING, True)


def add_projection_stage(nc, env, tag, rows, weight, bias):
    with ExitStack() as ctx:
        st = Stage(nc, ctx, tag)
        wo, bo = st.sb("wo", [P, DC, D]), st.sb("bo", [1, D])
        rT = st.sb("rT", [P, 2, DC, P])
        t_ps, y_ps = st.ps("t_ps", [P, 2, 512]), st.ps("y_ps", [P, 2, 512])
        loaded, turned, evacuated, y_done, added = (st.sem(n) for n in ("loaded", "turned", "evacuated", "y_done", "added"))
        block = ctx.enter_context(nc.Block())

        @block.sync
        def _(sp):
            sp.dma_start(wo[:], weight.rearrange("(c p) n -> p c n", p=P)).then_inc(loaded, 16)
            sp.dma_start(bo[:], bias.rearrange("(a n) -> a n", a=1)).then_inc(loaded, 16)

        @block.tensor
        def _(pe):
            def turn(t):
                if t >= 2:
                    pe.wait_ge(evacuated, t - 1)
                for c in range(DC):
                    last = nc.tensor.transpose(t_ps[:, t % 2, c * P:(c + 1) * P], rows[:, t, c * P:(c + 1) * P], env.ident[:])
                last.then_inc(turned, 1)

            turn(0)
            pe.wait_ge(loaded, 32)
            for t in range(TILES):
                if t + 1 < TILES:
                    turn(t + 1)
                pe.wait_ge(evacuated, t + 1)
                if t >= 2:
                    pe.wait_ge(added, t - 1)
                nc.tensor.matmul(y_ps[:, t % 2, 0:D], env.ones[0:1, :], bo[:], start=True, stop=False)
                for c in range(DC):
                    last = nc.tensor.matmul(y_ps[:, t % 2, 0:D], rT[:, t % 2, c, :], wo[:, c, :], start=False, stop=c == DC - 1)
                last.then_inc(y_done, 1)

        @block.scalar
        def _(act):
            for t in range(TILES):
                act.wait_ge(turned, t + 1)
                if t >= 2:
                    act.wait_ge(y_done, t - 1)
                nc.scalar.copy(rT[:, t % 2], t_ps[:, t % 2, 0:D].rearrange("p (c t) -> p c t", c=DC)).then_inc(evacuated, 1)

        @block.vector
        def _(dve):
            for t in range(TILES):
                dve.wait_ge(y_done, t + 1)
                nc.vector.tensor_tensor(env.x[:, t, :], env.x[:, t, :], y_ps[:, t % 2, 0:D], ALU.add).then_inc(added, 1)


def store_stage(nc, env, out):
    with ExitStack() as ctx:
        st = Stage(nc, ctx, "fin")
        stored = st.sem("stored")
        block = ctx.enter_context(nc.Block())

        @block.sync
        def _(sp):
            sp.dma_start(out.rearrange("b (t p) d -> p (b t) d", p=P), env.x[:]).then_inc(stored, 16)
            sp.wait_ge(stored, 16)


class Env:

    def __init__(self, nc, ctx):
        sb = lambda name, shape, dt=F32: ctx.enter_context(nc.sbuf_tensor(name, shape, dt))
        self.x = sb("x_res", [P, TILES, D])
        self.ctx_tok = sb("ctx_tok", [P, B, D])
        self.ident = sb("ident", [P, P])
        self.ones = sb("ones", [P, P])
        self.eps = sb("eps", [P, 1])
        sems = lambda name, n: [[ctx.enter_context(nc.semaphore(f"{name}{k}_{i}")) for i in range(n)] for k in range(2)]
        self.scattered = sems("rows_scattered", 1)
        self.stored = sems("expert_rows_stored", 2)
        self.gathered = sems("expert_rows_gathered", TILES)



C = 2 * D
CC = C // P
CQ = C // 4
TAPS = 9
KW = H * TAPS


def conv_kernels_stage(nc, env, tag, args, name, kern_dram):
    w = lambda n: args[f"{name}_{n}"]
    with ExitStack() as ctx:
        st = Stage(nc, ctx, tag)
        sb, ps, sem = st.sb, st.ps, st.sem
        hw, w1, w2 = sb("hw", [P, DC, C]), sb("w1", [P, CC, CQ]), sb("w2", [P, 1])
        kw1, kw2 = sb("kw1", [P, CC, D]), sb("kw2", [P, DC, KW])
        hb, hg, hs = (sb(n, [P, C]) for n in ("hb", "hg", "hs"))
        b1, b2 = sb("b1", [P, 1]), sb("b2", [1, 1])
        kb, kg, ks, kb2 = sb("kb", [B, D]), sb("kg", [B, D]), sb("ks", [B, D]), sb("kb2", [B, KW])
        ctxT = sb("ctxT", [P, DC, B * NCTX])
        eh = sb("eh", [P, B, C])
        ehT = sb("ehT", [P, CC, B * NCTX])
        stats, mean, var, rstd = sb("stats", [P, B, 6]), sb("mean", [P, B]), sb("var", [P, B]), sb("rstd", [P, B])
        kstats, kmean, kvar, krstd = (sb(n, s) for n, s in (("kstats", [B, 1, 6]), ("kmean", [B, 1]), ("kvar", [B, 1]), ("krstd", [B, 1])))
        a1 = sb("a1", [P, B * NCTX])
        aw, one = sb("aw", [1, B, NCTX]), sb("one", [1, B])
        awc = sb("awc", [P, B])
        ccT = sb("ccT", [P, CC, B])
        kh = sb("kh", [B, D])
        khT = sb("khT", [P, DC, B])
        kern, kcol = sb("kern", [B, KW]), sb("kcol", [B, H])
        ps_a, ps_b = ps("ps_a", [P, 512]), ps("ps_b", [P, B, 512])
        loaded, on_pe, on_act, linked, ready, stored = (sem(n) for n in ("loaded", "on_pe", "on_act", "linked", "ready", "stored"))
        block = ctx.enter_context(nc.Block())
        tokens = slice(0, NCTX)
        LOADED, HIST, NORMED, SHIFTED, WEIGHTS, WCOL, POOLED, KHID, KNORMED, KVEC, KSHIFTED, KERNELS = range(1, 13)

        @block.sync
        def _(sp):
            mat = lambda n: w(n).rearrange("(c p) n -> p c n", p=P)
            wide = lambda n, rows: w(n).partition_broadcast(rows)
            loads = [(hw, mat("hist_W")), (w1, mat("ctx_W1")), (w2, w("ctx_W2")), (kw1, mat("kg_W1")), (kw2, mat("kg_W2")),
                     (hb, wide("hist_b", P)), (hg, wide("hist_ln_g", P)), (hs, wide("hist_ln_b", P)),
                     (b1, w("ctx_b1").rearrange("(p a) -> p a", a=1)), (b2, w("ctx_b2").rearrange("(p a) -> p a", a=1)),
                     (kb, wide("kg_b1", B)), (kg, wide("kg_ln_g", B)), (ks, wide("kg_ln_b", B)), (kb2, wide("kg_b2", B))]
            for dst, src in loads:
                sp.dma_start(dst[:], src).then_inc(loaded, 16)
            sp.wait_ge(loaded, 16 * len(loads))
            sp.sem_inc(ready, 1)
            sp.wait_ge(ready, KERNELS)
            sp.dma_start(kern_dram, kern[:]).then_inc(stored, 16)
            sp.wait_ge(stored, 16)

        @block.tensor
        def _(pe):
            for b in range(B):
                for c in range(DC):
                    last = nc.tensor.transpose(ps_a[:, (c * B + b) * NCTX:(c * B + b + 1) * NCTX],
                                               env.ctx_tok[tokens, b, c * P:(c + 1) * P], env.ident[tokens, tokens])
            last.then_inc(on_pe, 1)
            pe.wait_ge(on_act, 1)
            pe.wait_ge(ready, LOADED)
            for b in range(B):
                for c in range(DC):
                    last = nc.tensor.matmul(ps_b[tokens, b, :], ctxT[:, c, b * NCTX:(b + 1) * NCTX], hw[:, c, :], start=c == 0,
                                            stop=c == DC - 1)
            last.then_inc(on_pe, 1)
            pe.wait_ge(on_act, 3)
            for b in range(B):
                for c in range(CC):
                    last = nc.tensor.transpose(ps_b[:, b, c * NCTX:(c + 1) * NCTX], eh[tokens, b, c * P:(c + 1) * P],
                                               env.ident[tokens, tokens])
            last.then_inc(on_pe, 1)
            pe.wait_ge(on_act, 5)
            for c in range(CC):
                last = nc.tensor.matmul(ps_a[:, 0:B * NCTX], w1[:, c, :], ehT[:, c, :], start=c == 0, stop=c == CC - 1)
            last.then_inc(on_pe, 1)
            pe.wait_ge(on_act, 6)
            nc.tensor.matmul(ps_a[0:1, 0:B * NCTX], w2[:], a1[:], start=True, stop=True).then_inc(on_pe, 1)
            pe.wait_ge(ready, WEIGHTS)
            for b in range(B):
                last = nc.tensor.matmul(ps_a[tokens, b:b + 1], aw[0:1, b, :], env.ones[0:1, 0:1], start=True, stop=True)
            last.then_inc(on_pe, 1)
            pe.wait_ge(ready, WCOL)
            for c in range(CC):
                for b in range(B):
                    last = nc.tensor.matmul(ps_a[:, c * B + b:c * B + b + 1], eh[tokens, b, c * P:(c + 1) * P], awc[tokens, b:b + 1],
                                            start=True, stop=True)
            last.then_inc(on_pe, 1)
            pe.wait_ge(ready, POOLED)
            for c in range(CC):
                last = nc.tensor.matmul(ps_a[0:B, 0:D], ccT[:, c, :], kw1[:, c, :], start=c == 0, stop=c == CC - 1)
            last.then_inc(on_pe, 1)
            pe.wait_ge(on_act, 9)
            for c in range(DC):
                last = nc.tensor.transpose(ps_a[:, c * B:(c + 1) * B], kh[:, c * P:(c + 1) * P], env.ident[0:B, 0:B])
            last.then_inc(on_pe, 1)
            pe.wait_ge(ready, KVEC)
            for c in range(DC):
                last = nc.tensor.matmul(ps_a[0:B, 0:KW], khT[:, c, :], kw2[:, c, :], start=c == 0, stop=c == DC - 1)
            last.then_inc(on_pe, 1)

        @block.scalar
        def _(act):
            act.wait_ge(on_pe, 1)
            nc.scalar.copy(ctxT[:], ps_a[:, 0:DC * B * NCTX].rearrange("p (c t) -> p c t", c=DC)).then_inc(on_act, 1)
            act.wait_ge(ready, HIST)
            nc.scalar.activation(rstd[tokens], var[tokens], ACT.Sqrt).then_inc(on_act, 1)
            act.wait_ge(ready, NORMED)
            nc.scalar.activation(eh[tokens], eh[tokens], ACT.Gelu).then_inc(on_act, 1)
            act.wait_ge(on_pe, 3)
            for b in range(B):
                nc.scalar.copy(ehT[:, :, b * NCTX:(b + 1) * NCTX],
                               ps_b[:, b, 0:CC * NCTX].rearrange("p (c t) -> p c t", c=CC)).then_inc(on_act, 1)
            act.wait_ge(on_pe, 4)
            nc.scalar.activation(a1[:], ps_a[:, 0:B * NCTX], ACT.Gelu, bias=b1[:, 0:1]).then_inc(on_act, 1)
            act.wait_ge(ready, SHIFTED)
            nc.scalar.activation(aw[:], aw[:], ACT.Exp).then_inc(on_act, 1)
            act.wait_ge(ready, KHID)
            nc.scalar.activation(krstd[:], kvar[:], ACT.Sqrt).then_inc(on_act, 1)
            act.wait_ge(ready, KNORMED)
            nc.scalar.activation(kh[:], kh[:], ACT.Gelu).then_inc(on_act, 1)
            act.wait_ge(ready, KSHIFTED)
            nc.scalar.activation(kern[:], kern[:], ACT.Exp).then_inc(on_act, 1)

        @block.vector
        def _(dve):
            step = chain(dve, linked)
            tt = lambda o, a, b_, op: step(nc.vector.tensor_tensor(o, a, b_, op))

            def finish(ins):
                ins.then_inc(ready, 1)

            dve.wait_ge(ready, LOADED)
            dve.wait_ge(on_pe, 2)
            for b in range(B):
                tt(eh[tokens, b, :], ps_b[tokens, b, :], hb[tokens, :], ALU.add)
            for b in range(B):
                step(nc.vector.bn_stats(stats[tokens, b, :], eh[tokens, b, :]))
            merge_stats(nc, step, mean[tokens], var[tokens], stats[tokens], C)
            finish(nc.vector.tensor_scalar(var[tokens], var[tokens], LN_EPS, None, ALU.add))
            dve.wait_ge(on_act, 2)
            step(nc.vector.reciprocal(rstd[tokens], rstd[tokens]))
            for b in range(B):
                e = eh[tokens, b, :]
                step(nc.vector.tensor_scalar(e, e, mean[tokens, b:b + 1], rstd[tokens, b:b + 1], ALU.subtract, ALU.mult))
                tt(e, e, hg[tokens, :], ALU.mult)
                if b == 0:
                    tt(e, e, hs[tokens, :], ALU.add)
                else:
                    finish(nc.vector.tensor_tensor(e, e, hs[tokens, :], ALU.add))
            dve.wait_ge(on_pe, 5)
            step(nc.vector.tensor_scalar(aw[:].rearrange("p b t -> p (b t)"), ps_a[0:1, 0:B * NCTX], b2[:, 0:1], None, ALU.add))
            step(nc.vector.tensor_reduce(one[:], aw[:], AX_X, ALU.max))
            finish(nc.vector.tensor_tensor(aw[:], aw[:], one[:].unsqueeze(2).to_broadcast([1, B, NCTX]), ALU.subtract))
            dve.wait_ge(on_act, 7)
            step(nc.vector.tensor_reduce(one[:], aw[:], AX_X, ALU.add))
            step(nc.vector.reciprocal(one[:], one[:]))
            finish(nc.vector.tensor_tensor(aw[:], aw[:], one[:].unsqueeze(2).to_broadcast([1, B, NCTX]), ALU.mult))
            dve.wait_ge(on_pe, 6)
            finish(nc.vector.tensor_copy(awc[tokens], ps_a[tokens, 0:B]))
            dve.wait_ge(on_pe, 7)
            finish(nc.vector.tensor_copy(ccT[:].rearrange("p c b -> p (c b)"), ps_a[:, 0:CC * B]))
            dve.wait_ge(on_pe, 8)
            tt(kh[:], ps_a[0:B, 0:D], kb[:], ALU.add)
            step(nc.vector.bn_stats(kstats[:, 0, :], kh[:]))
            merge_stats(nc, step, kmean[:], kvar[:], kstats[:], D)
            finish(nc.vector.tensor_scalar(kvar[:], kvar[:], LN_EPS, None, ALU.add))
            dve.wait_ge(on_act, 8)
            step(nc.vector.reciprocal(krstd[:], krstd[:]))
            step(nc.vector.tensor_scalar(kh[:], kh[:], kmean[:, 0:1], krstd[:, 0:1], ALU.subtract, ALU.mult))
            tt(kh[:], kh[:], kg[:], ALU.mult)
            finish(nc.vector.tensor_tensor(kh[:], kh[:], ks[:], ALU.add))
            dve.wait_ge(on_pe, 9)
            finish(nc.vector.tensor_copy(khT[:].rearrange("p c b -> p (c b)"), ps_a[:, 0:DC * B]))
            dve.wait_ge(on_pe, 10)
            taps = kern[:].rearrange("p (h k) -> p h k", k=TAPS)
            over = kcol[:].unsqueeze(2).to_broadcast([B, H, TAPS])
            tt(kern[:], ps_a[0:B, 0:KW], kb2[:], ALU.add)
            step(nc.vector.tensor_reduce(kcol[:], taps, AX_X, ALU.max))
            finish(nc.vector.tensor_tensor(taps, taps, over, ALU.subtract))
            dve.wait_ge(on_act, 10)
            step(nc.vector.tensor_reduce(kcol[:], taps, AX_X, ALU.add))
            step(nc.vector.reciprocal(kcol[:], kcol[:]))
            finish(nc.vector.tensor_tensor(taps, taps, over, ALU.mult))



F16 = mybir.dt.float16

TAP = 3
ROWS = P - TAP + 1
WINDOWS = -(-S // ROWS)
PAD = ROWS * WINDOWS + TAP - 1
HEADS = B * H


def conv_attention_stage(nc, env, tag, args, name, kern_dram, mask):
    w = lambda n: args[f"{name}_{n}"]
    dram = lambda n, shape: nc.dram_tensor(f"{tag}_{n}", shape, F32).ap()
    q_dram, k_dram = dram("q", [B, D, PAD]), dram("k", [B, D, PAD])
    halves = lambda n: nc.dram_tensor(f"{tag}_{n}", [2, TAP, B, D, S], F16).ap()
    near_dram, mixed_dram = halves("near"), halves("mixed")
    with ExitStack() as outer:
        sto = Stage(nc, outer, tag)
        v = sto.sb("v", [P, HEADS, TPB, HD])
        spill = sto.sb("spill", [P, 3, HEADS, TPB])
        size = sto.sb("size", [P, 1])
        other = sto.sb("other", [1, 1], I32)
        with ExitStack() as ctx:
            project_qkv(nc, env, Stage(nc, ctx, tag + "p"), ctx, w, kern_dram, q_dram, k_dram, near_dram, mixed_dram, v, spill,
                        size, mask, other)
        oT, sums = sto.sb("oT", [P, B * DC, S]), sto.sb("sums", [P, B * DC, S])
        with ExitStack() as ctx:
            st = Stage(nc, ctx, tag + "a")
            banks = st.ps("banks", [P, 8, 512])
            causal = causal_mask(nc, env, st, banks, near_dram, mixed_dram, v, spill, size, oT, sums)
            general = any_mask(nc, env, st, tag, banks, kern_dram, mask, q_dram, k_dram, v, oT, sums)
            block = ctx.enter_context(nc.Block())

            def choose(eng, way):
                is_other = eng.value_load(other[0:1, 0:1], min_val=0, max_val=1)
                with eng.If(is_other < 1):
                    causal[way](eng)
                with eng.Else():
                    general[way](eng)

            @block.sync
            def _(sp):
                choose(sp, "sync")

            @block.gpsimd
            def _(pool):
                choose(pool, "gpsimd")

            @block.tensor
            def _(pe):
                choose(pe, "tensor")

            @block.vector
            def _(dve):
                choose(dve, "vector")

            @block.scalar
            def _(act):
                choose(act, "scalar")
        with ExitStack() as ctx:
            project_out(nc, env, Stage(nc, ctx, tag + "o"), ctx, w, oT, sums)


def project_qkv(nc, env, st, ctx, w, kern_dram, q_dram, k_dram, near_dram, mixed_dram, v, spill, size, mask, other):
    xT = st.sb("xT", [P, DC, T])
    layernorm_stage(nc, env, st.tag + "l", env.x, dst_T=xT)
    wq, wk, wv = (st.sb(n, [P, DC, D]) for n in ("wq", "wk", "wv"))
    qk = st.sb("qk", [P, 2, B, DC, PAD])
    half = H // DC
    coef = st.sb("coef", [P, B, DC, TAP * TAP])
    ind = st.sb("ind", [P, half])
    mix = st.sb("mix", [P, 2, S])
    near, diag, before = st.sb("near", [P, S]), st.sb("diag", [P, S]), st.sb("before", [P, S + 1])
    q16 = st.sb("q16", [P, 2, B, DC, S + 2], F16)
    mix16 = st.sb("mix16", [P, 2, 2, S], F16)
    amax, top, down = st.sb("amax", [P, 2]), st.sb("top", [P, 2]), st.sb("down", [P, 3])
    y_ps, v_ps, d_ps = st.ps("y_ps", [P, 4, 512]), st.ps("v_ps", [P, 2, 512]), st.ps("d_ps", [P, 2, 512])
    loaded, zeroed, y_done, y_evac, v_done, v_evac, stored, coef_loaded, ones_set, ind_lower, ind_made = (
        st.sem(n) for n in ("loaded", "zeroed", "y_done", "y_evac", "v_done", "v_evac", "stored", "coef_loaded", "ones_set",
                            "ind_lower", "ind_made"))
    begun, mixed, mix_parts, crossed, spills, spill_done, spill_evac = (
        st.sem(n) for n in ("begun", "mixed", "mix_parts", "crossed", "spills", "spill_done", "spill_evac"))
    topped, reduced, scaled, sized, q_halved, q_split, q_stored, halved, split, before_zero = (
        st.sem(n) for n in ("topped", "reduced", "scaled", "sized", "q_halved", "q_split", "q_stored", "halved", "split",
                            "before_zero"))
    mix_stored = [st.sem(f"mix_stored{u}") for u in range(2)]
    given, after, worst = st.sb("given", [P, TPB, S], U8), st.sb("after", [P, TPB, S]), st.sb("worst", [P, 1])
    mask_loaded, after_ones, after_made, differs, found, told_sum, told = (
        st.sem(n) for n in ("mask_loaded", "after_ones", "after_made", "differs", "found", "told_sum", "told"))
    parts = [(b, c) for b in range(B) for c in range(DC)]
    mixes = [(b, c, a) for b, c in parts for a in range(TAP)]
    block = ctx.enter_context(nc.Block())
    HALF = S // 512
    jobs = [(k, b, c, n) for k in range(2) for b in range(B) for c in range(DC) for n in range(HALF)]

    @block.sync
    def _(sp):
        for dst, src in ((wq, "Wq"), (wk, "Wk"), (wv, "Wv")):
            sp.dma_start(dst[:], w(src).rearrange("(c p) n -> p c n", p=P)).then_inc(loaded, 16)
        sp.dma_start(given[:], mask.rearrange("(t p) j -> p t j", p=P)).then_inc(mask_loaded, 16)
        kern = kern_dram.rearrange("b (c h k) -> h b c k", c=DC, h=half)
        for h in range(half):
            for b in range(B):
                sp.dma_start(coef[h * HD:(h + 1) * HD, b], kern[h, b].partition_broadcast(HD)).then_inc(coef_loaded, 16)
        sp.wait_ge(zeroed, 2)
        for k, dram in enumerate((q_dram, k_dram)):
            sp.wait_ge(y_evac, (k + 1) * len(jobs) // 2)
            sp.dma_start(dram.rearrange("b (c p) t -> p b c t", p=P), qk[:, k]).then_inc(stored, 16)
        sp.wait_ge(q_split, len(parts))
        for x in range(2):
            for a in range(TAP):
                sp.dma_start(near_dram[x, a].rearrange("b (c p) t -> p b c t", p=P), q16[:, x, :, :, a:a + S]).then_inc(q_stored, 16)
        for i, (b, c, a) in enumerate(mixes):
            sp.wait_ge(split, i + 1)
            sp.dma_start(mixed_dram[:, a, b, c * P:(c + 1) * P, :].rearrange("x p t -> p x t"), mix16[:, i % 2]).then_inc(mix_stored[i % 2], 16)
        for u in range(2):
            sp.wait_ge(mix_stored[u], 8 * len(mixes))
        sp.wait_ge(q_stored, 32 * TAP)
        sp.wait_ge(stored, 32)

    @block.gpsimd
    def _(pool):
        nc.gpsimd.memset(qk[:, :, :, :, 0:1], 0.0).then_inc(zeroed, 1)
        nc.gpsimd.memset(qk[:, :, :, :, S + 1:PAD], 0.0).then_inc(zeroed, 1)
        nc.gpsimd.memset(after[:], 1.0).then_inc(after_ones, 1)
        pool.wait_ge(after_ones, 1)
        nc.gpsimd.affine_select(out=after[:], in_=after[:], compare_op=ALU.is_gt, fill=0.0, base=0,
                                pattern=[[-P, TPB], [1, S]], channel_multiplier=-1).then_inc(after_made, 1)
        nc.gpsimd.memset(ind[:], 1.0).then_inc(ones_set, 1)
        pool.wait_ge(ones_set, 1)
        nc.gpsimd.affine_select(out=ind[:], in_=ind[:], compare_op=ALU.is_ge, fill=0.0, base=0,
                                pattern=[[-HD, half]], channel_multiplier=1).then_inc(ind_lower, 1)
        pool.wait_ge(ind_lower, 1)
        nc.gpsimd.affine_select(out=ind[:], in_=ind[:], compare_op=ALU.is_ge, fill=0.0, base=HD - 1,
                                pattern=[[HD, half]], channel_multiplier=-1).then_inc(ind_made, 1)
        nc.gpsimd.memset(before[:, S:S + 1], 0.0).then_inc(before_zero, 1)
        pool.wait_ge(topped, 2)
        nc.gpsimd.partition_all_reduce(amax[:], top[:], P, RMAX).then_inc(reduced, 1)

    @block.tensor
    def _(pe):
        pe.wait_ge(loaded, 48)
        for i, (k, b, c, n) in enumerate(jobs):
            if i >= 4:
                pe.wait_ge(y_evac, i - 3)
            for d in range(DC):
                last = nc.tensor.matmul(y_ps[:, i % 4, :], (wq, wk)[k][:, d, c * P:(c + 1) * P],
                                        xT[:, d, b * S + n * 512:b * S + (n + 1) * 512], start=d == 0, stop=d == DC - 1)
            last.then_inc(y_done, 1)
        for t in range(TILES):
            if t >= 2:
                pe.wait_ge(v_evac, t - 1)
            for d in range(DC):
                last = nc.tensor.matmul(v_ps[:, t % 2, 0:D], xT[:, d, t * P:(t + 1) * P], wv[:, d, :], start=d == 0,
                                        stop=d == DC - 1)
            last.then_inc(v_done, 1)
        pe.wait_ge(ind_made, 1)
        for i, (b, c) in enumerate(parts):
            pe.wait_ge(spills, 2 * i + 2)
            for k, (feats, ahead) in enumerate(((diag, 0), (before, 0), (before, 1))):
                for n in range(TPB):
                    at = ((k % 2 * B * DC + i) * TPB + n) * half
                    last = nc.tensor.matmul(d_ps[:, k // 2, at:at + half], feats[:, n * P + ahead:(n + 1) * P + ahead], ind[:],
                                            start=True, stop=True)
            last.then_inc(spill_done, 1)
        pe.wait_ge(found, 1)
        pe.wait_ge(v_evac, TILES)
        nc.tensor.matmul(v_ps[0:1, 0, 0:1], worst[:], env.ones[:, 0:1], start=True, stop=True).then_inc(told_sum, 1)

    @block.scalar
    def _(act):
        for i, (k, b, c, n) in enumerate(jobs):
            act.wait_ge(y_done, i + 1)
            nc.scalar.mul(qk[:, k, b, c, 1 + n * 512:1 + (n + 1) * 512], y_ps[:, i % 4, :],
                          HD ** -0.5 if k == 0 else 1.0).then_inc(y_evac, 1)
        for t in range(TILES):
            act.wait_ge(v_done, t + 1)
            b, n = divmod(t, TPB)
            nc.scalar.copy(v[:, b * H:(b + 1) * H, n, :],
                           v_ps[:, t % 2, 0:D].rearrange("p (h d) -> p h d", h=H)).then_inc(v_evac, 1)
        act.wait_ge(y_evac, len(jobs))
        act.wait_ge(coef_loaded, 16 * half * B)
        act.wait_ge(zeroed, 2)
        act.wait_ge(scaled, 2)
        for i, (b, c) in enumerate(parts):
            nc.scalar.activation(q16[:, 0, b, c, :], qk[:, 0, b, c, 0:S + 2], ACT.Identity, scale=down[:, 0:1]).then_inc(q_halved, 1)

        def first_tap(i):
            b, c, a = mixes[i]
            if i >= 2:
                act.wait_ge(split, i - 1)
            nc.scalar.activation(mix[:, i % 2, :], qk[:, 1, b, c, 0:S], ACT.Identity,
                                 scale=coef[:, b, c, a * TAP:a * TAP + 1]).then_inc(begun, 1)

        first_tap(0)
        for i in range(len(mixes)):
            if i + 1 < len(mixes):
                first_tap(i + 1)
            if i >= 2:
                act.wait_ge(mix_stored[i % 2], 16 * (i // 2))
            act.wait_ge(mixed, i + 1)
            nc.scalar.activation(mix16[:, i % 2, 0, :], mix[:, i % 2, :], ACT.Identity, scale=down[:, 1:2]).then_inc(halved, 1)

    @block.vector
    def _(dve):
        dve.wait_ge(mask_loaded, 16)
        dve.wait_ge(after_made, 1)
        nc.vector.tensor_tensor(after[:], given[:], after[:], ALU.not_equal).then_inc(differs, 1)
        dve.wait_ge(differs, 1)
        nc.vector.tensor_reduce(worst[:], after[:].rearrange("p t j -> p (t j)"), AX_X, ALU.max).then_inc(found, 1)
        dve.wait_ge(y_evac, len(jobs))
        dve.wait_ge(coef_loaded, 16 * half * B)
        dve.wait_ge(zeroed, 2)
        for k in range(2):
            nc.vector.tensor_reduce(top[:, k:k + 1], qk[:, k].rearrange("p b c t -> p (b c t)"), AX_X, ALU.max,
                                    apply_absolute_value=True).then_inc(topped, 1)
        dve.wait_ge(reduced, 1)
        nc.vector.tensor_scalar(amax[:], amax[:], 1e-30, None, ALU.max).then_inc(sized, 1)
        dve.wait_ge(sized, 1)
        nc.vector.reciprocal(down[:, 0:2], amax[:]).then_inc(scaled, 1)
        nc.vector.tensor_tensor(size[:], amax[:, 0:1], amax[:, 1:2], ALU.mult).then_inc(scaled, 1)
        dve.wait_ge(scaled, 2)
        nc.vector.tensor_tensor(down[:, 2:3], down[:, 0:1], down[:, 1:2], ALU.mult).then_inc(sized, 1)
        for i, (b, c) in enumerate(parts):
            dve.wait_ge(q_halved, i + 1)
            nc.vector.scalar_tensor_tensor(q16[:, 1, b, c, :], qk[:, 0, b, c, 0:S + 2], down[:, 0:1], q16[:, 0, b, c, :],
                                           ALU.mult, ALU.subtract).then_inc(q_split, 1)

        def rest(i):
            dve.wait_ge(halved, i + 1)
            nc.vector.scalar_tensor_tensor(mix16[:, i % 2, 1, :], mix[:, i % 2, :], down[:, 1:2], mix16[:, i % 2, 0, :],
                                           ALU.mult, ALU.subtract).then_inc(split, 1)

        step = chain(dve, crossed)

        def spilled(i):
            b, c = parts[i]
            q, k, tap = qk[:, 0, b, c], qk[:, 1, b, c], lambda n: coef[:, b, c, n:n + 1]
            if i:
                dve.wait_ge(spill_done, i)
            step(nc.vector.tensor_tensor(near[:], q[:, 0:S], k[:, 1:S + 1], ALU.mult))
            step(nc.vector.tensor_scalar(diag[:], q[:, 0:S], tap(2), None, ALU.mult))
            step(nc.vector.scalar_tensor_tensor(diag[:], q[:, 1:S + 1], tap(TAP + 2), diag[:], ALU.mult, ALU.add))
            step(nc.vector.tensor_tensor(diag[:], diag[:], k[:, 2:S + 2], ALU.mult))
            nc.vector.scalar_tensor_tensor(diag[:], near[:], tap(1), diag[:], ALU.mult, ALU.add).then_inc(spills, 1)
            nc.vector.tensor_scalar(before[:, 0:S], near[:], tap(2), None, ALU.mult).then_inc(spills, 1)

        dve.wait_ge(before_zero, 1)
        for i, (b, c, a) in enumerate(mixes):
            row, keys = mix[:, i % 2, :], qk[:, 1, b, c]
            if a == 0:
                spilled(i // TAP)
            dve.wait_ge(begun, i + 1)
            nc.vector.scalar_tensor_tensor(row, keys[:, 1:S + 1], coef[:, b, c, a * TAP + 1:a * TAP + 2], row, ALU.mult,
                                           ALU.add).then_inc(mix_parts, 1)
            if i:
                rest(i - 1)
            dve.wait_ge(mix_parts, i + 1)
            nc.vector.scalar_tensor_tensor(row, keys[:, 2:S + 2], coef[:, b, c, a * TAP + 2:a * TAP + 3], row, ALU.mult,
                                           ALU.add).then_inc(mixed, 1)
        rest(len(mixes) - 1)
        dve.wait_ge(spill_done, len(parts))
        dve.wait_ge(sized, 2)
        for k in range(3):
            for i in range(len(parts)):
                at = (k % 2 * len(parts) + i) * TPB * half
                nc.vector.tensor_scalar(spill[:, k, i * half:(i + 1) * half, :].rearrange("p h t -> p t h"),
                                        d_ps[:, k // 2, at:at + TPB * half].rearrange("p (t h) -> p t h", t=TPB),
                                        down[:, 2:3], None, ALU.mult).then_inc(spill_evac, 1)
        dve.wait_ge(told_sum, 1)
        nc.vector.tensor_scalar(other[:], v_ps[0:1, 0, 0:1], 1.0, None, ALU.min).then_inc(told, 1)
        dve.wait_ge(spill_evac, 3 * len(parts))
        dve.wait_ge(told, 1)


def causal_mask(nc, env, st, banks, near_dram, mixed_dram, v, spill, size, oT, sums):
    sb, sem = lambda n, *a: st.sb("tri_" + n, *a), lambda n: st.sem("tri_" + n)
    FEATS = TAP * HD
    TOP = (64, 96)
    ROWS2 = TOP[1] + 1
    BUFS = 4
    GROUP = 4
    PER_ROUND = 2 * GROUP
    ROUNDS = HEADS // PER_ROUND
    SUMS = GROUP * HD
    WIN = P + 1
    order = (1, 2, 3, 5, 7, 6, 4, 0)
    chunks = [[(max(j * P, c * 512), (c + 1) * 512, c, max(j * P - c * 512, 0)) for c in range(2)] if j < 4 else
              [(j * P, S, j % 2, 0)] for j in range(TPB)]
    before = [sum(len(c) for c in chunks[:j]) for j in range(TPB + 1)]
    CHUNKS = before[-1]
    q11, q2 = sb("q11", [2 * FEATS, BUFS, S], F16), sb("q2", [ROWS2, BUFS, S], F16)
    k12, k1 = sb("k12", [2 * FEATS, BUFS, S], F16), sb("k1", [ROWS2, BUFS, S], F16)
    vg = sb("vg", [P, 2, GROUP, TPB, P])
    own, prev = sb("own", [P, WIN]), sb("prev", [P, WIN])
    later, ident_b, ident_h = sb("later", [P, P], BF16), sb("ident_b", [P, P], BF16), sb("ident_h", [P, P], F16)
    off = sb("off", [P, PER_ROUND, 3, TPB])
    edge, part = sb("edge", [P, 2, WIN]), sb("part", [P, WIN])
    pT = sb("pT", [P, 2, 2, 512])
    ntop = sb("ntop", [P, TPB])
    top_rows = sb("top_rows", [P, TPB, ROWS2], F16)
    s_ps = lambda t: banks[:, 2 * (t % 2):2 * (t % 2) + 2, :].rearrange("p a n -> p (a n)")
    m_ps = s_ps(1)
    t_ps, o_ps = banks[:, 4:6, :], banks[:, 6:8, :]
    staged = [sem(f"staged{u}") for u in range(BUFS)]
    v_staged = [sem(f"v_staged{u}") for u in range(2)]
    filled, off_ready, edge_part, edge_made, scored, edged, top_ready, split_part, split_ready = (
        sem(n) for n in ("filled", "off_ready", "edge_part", "edge_made", "scored", "edged", "top_ready", "split_part", "split_ready"))
    top_turned, top_placed, t_done, t_part, t_edged, exped, weighed, o_evac, tables = (
        sem(n) for n in ("top_turned", "top_placed", "t_done", "t_part", "t_edged", "exped", "weighed", "o_evac", "tables"))
    FILLS = 13
    vg_filled = sem("vg_filled")

    def rounds(eng, body):
        with eng.Fori(0, ROUNDS - 1) as i:
            body(i, False)
        body(ROUNDS - 1, True)

    def on_sync(sp):
        rows = lambda dram, half, h: dram.rearrange("x a b (h f) t -> x (b h) a f t", f=HD)[half, bass.ds(h, 1)]

        def stage(h, r, reuse):
            u = r % BUFS
            if reuse:
                sp.wait_ge(t_done, TPB * h - TPB * (BUFS - 1))
            for dst, at, dram, half in ((q11, 0, near_dram, 0), (q11, FEATS, near_dram, 0), (q2, 0, near_dram, 1),
                                        (k12, 0, mixed_dram, 0), (k12, FEATS, mixed_dram, 1), (k1, 0, mixed_dram, 0)):
                sp.dma_start(dst[at:at + FEATS, u, :],
                             rows(dram, half, h).rearrange("z a f t -> (z a) f t")).then_inc(staged[u], 16)
            if r % GROUP == 0:
                sp.wait_ge(vg_filled, 1 + GROUP)
                if reuse:
                    sp.wait_ge(weighed, CHUNKS * h - CHUNKS * GROUP + 2)
                for n in range(GROUP):
                    sp.dma_start(vg[:, r // GROUP, n, :, n * HD:(n + 1) * HD],
                                 v[:, bass.ds(h + n, 1), :, :].rearrange("p z t d -> p (z t) d")).then_inc(v_staged[r // GROUP], 16)

        sp.wait_ge(filled, 2)
        for r in range(PER_ROUND):
            stage(r, r, r >= BUFS)
        with sp.Fori(1, ROUNDS) as i:
            for r in range(PER_ROUND):
                stage(i * PER_ROUND + r, r, True)

    def on_gpsimd(pool):
        step = chain(pool, filled)
        fill = lambda buf, *a: step(nc.gpsimd.memset(buf, *a))
        fill(q2[:], 0.0)
        fill(k1[:], 0.0)
        for row in TOP:
            fill(k1[row:row + 1], 1.0)
        fill(top_rows[:], 0.0)
        step(nc.gpsimd.tensor_copy(ident_h[:], env.ident[:]))
        step(nc.gpsimd.tensor_copy(ident_b[:], env.ident[:]))
        fill(later[:], 0.0)
        step(nc.gpsimd.affine_select(out=later[:], in_=later[:], compare_op=ALU.is_ge, fill=NEG, base=0, pattern=[[-1, P]],
                                     channel_multiplier=1))
        for buf, base in ((own, 1), (prev, 0)):
            fill(buf[:], 0.0)
            step(nc.gpsimd.affine_select(out=buf[:], in_=buf[:], compare_op=ALU.not_equal, fill=-1.0, base=base,
                                         pattern=[[-1, WIN]], channel_multiplier=1))

        def edges(h, spills, t):
            n = order[t]
            s = TPB * h + t
            win = edge[:, t % 2, :]
            pool.wait_ge(edge_made, s)
            pool.wait_ge(edged, s + 1)
            nc.gpsimd.tensor_tensor(win, own[:], spills[:, 0, n:n + 1].to_broadcast([P, WIN]), ALU.mult).then_inc(edge_part, 1)
            nc.gpsimd.tensor_tensor(part[:], prev[:], spills[:, 1, n:n + 1].to_broadcast([P, WIN]), ALU.mult).then_inc(edge_part, 1)
            pool.wait_ge(edge_part, 2 * s + 2)
            nc.gpsimd.tensor_tensor(win, win, part[:], ALU.add).then_inc(edge_made, 1)

        def body(i, last):
            pool.wait_ge(edge_made, TPB * PER_ROUND * i)
            for r in range(PER_ROUND):
                head = bass.ds(i * PER_ROUND + r, 1)
                nc.gpsimd.tensor_copy(off[:, r], spill[:, :, head, :].rearrange("p k z t -> p k (z t)")).then_inc(off_ready, 1)
            pool.wait_ge(off_ready, PER_ROUND * i + PER_ROUND)
            for r in range(PER_ROUND):
                for t in range(TPB):
                    edges(i * PER_ROUND + r, off[:, r], t)

        rounds(pool, body)

    def on_tensor(pe):
        def score(h, r, t):
            u, n, s = r % BUFS, order[t], TPB * h + t
            if t == 0:
                i = h // PER_ROUND if isinstance(h, int) else h_round[0]
                pe.wait_ge(staged[u], (96 * (PER_ROUND // BUFS)) * i + 96 * (r // BUFS + 1))
            if not (isinstance(s, int) and s < 2):
                pe.wait_ge(top_ready, s - 1)
            if t == 1:
                pe.wait_ge(top_placed, h)
            queries = slice(n * P, (n + 1) * P)
            for a in range(0, (n + 1) * P, 512):
                z = min(a + 512, (n + 1) * P)
                nc.tensor.matmul(s_ps(t)[:, a:z], q11[:, u, queries], k12[:, u, a:z], start=True, stop=False)
                last = nc.tensor.matmul(s_ps(t)[:, a:z], q2[0:FEATS, u, queries], k1[0:FEATS, u, a:z], start=False, stop=z <= n * P)
            last = nc.tensor.matmul(s_ps(t)[:, n * P:(n + 1) * P], ident_b[:], later[:], start=False, stop=True)
            last.then_inc(scored, 1)

        def turn_top(h):
            pe.wait_ge(split_ready, h + 1)
            for n in range(TPB):
                last = nc.tensor.matmul(m_ps[0:ROWS2, n * P:(n + 1) * P], top_rows[:, n, :], ident_h[:], start=True, stop=True)
            last.then_inc(top_turned, 1)

        def by_keys(h, r, j):
            u = r % BUFS
            if j == 0:
                pe.wait_ge(top_placed, h + 1)
            keys = slice(j * P, (j + 1) * P)
            for x, (a, z, c, at) in enumerate(chunks[j]):
                pe.wait_ge(exped, CHUNKS * h + (before[j] + x))
                out = t_ps[:, c, at:at + z - a]
                nc.tensor.matmul(out, k12[:, u, keys], q11[:, u, a:z], start=True, stop=False)
                last = nc.tensor.matmul(out, k1[:, u, keys], q2[:, u, a:z], start=False, stop=x > 0)
                if x == 0:
                    last = nc.tensor.matmul(t_ps[:, c, at:at + P], later[:], ident_b[:], start=False, stop=True)
            last.then_inc(t_done, 1)

        def weigh(h, r, j):
            i = h_round[0]
            if r % GROUP == 0 and j == 0:
                pe.wait_ge(v_staged[r // GROUP], 16 * GROUP * i + 16 * GROUP)
                pe.wait_ge(o_evac, 4 * (2 * i + r // GROUP))
            for x, (a, z, c, at) in enumerate(chunks[j]):
                pe.wait_ge(exped, CHUNKS * h + (before[j] + x + 2))
                bank, col = divmod(a, 512)
                first, end = r % GROUP == 0 and j == 0, r % GROUP == GROUP - 1 and j == (3 if bank == 0 else TPB - 1)
                nc.tensor.matmul(o_ps[:, bank, col:col + z - a], vg[:, r // GROUP, r % GROUP, j, :],
                                 pT[:, j % 2, c, at:at + z - a], start=first, stop=end).then_inc(weighed, 1)

        h_round = [0]
        pe.sem_inc(weighed, 2)
        pe.wait_ge(filled, FILLS)
        for t in range(TPB):
            score(0, 0, t)
        turn_top(0)

        def body(i, last):
            for r in range(PER_ROUND):
                h = PER_ROUND * i + r
                more = not (last and r == PER_ROUND - 1)

                def ahead(t):
                    if more:
                        h_round[0] = i + 1 if r == PER_ROUND - 1 else i
                        score(h + 1, (r + 1) % PER_ROUND, t)
                        h_round[0] = i

                h_round[0] = i
                ahead(0)
                by_keys(h, r, 0)
                ahead(1)
                for j in range(TPB):
                    if j + 2 < TPB:
                        ahead(j + 2)
                    if j + 1 < TPB:
                        by_keys(h, r, j + 1)
                    if more and j == TPB - 2:
                        turn_top(h + 1)
                    weigh(h, r, j)

        rounds(pe, body)

    def on_vector(dve):
        nc.vector.memset(vg[:], 0.0).then_inc(vg_filled, 1)
        dve.wait_ge(vg_filled, 1)
        for n in range(GROUP):
            nc.vector.memset(vg[:, :, n, :, SUMS + n * HD:SUMS + (n + 1) * HD], 1.0).then_inc(vg_filled, 1)
        dve.wait_ge(vg_filled, 1 + GROUP)
        dve.wait_ge(filled, FILLS)

        def top(h, t):
            n, s = order[t], TPB * h + t
            dve.wait_ge(scored, s + 1)
            dve.wait_ge(edge_made, s + 1)
            skip = 1 if n == 0 else 0
            win = s_ps(t)[:, n * P - 1 + skip:(n + 1) * P]
            nc.vector.tensor_tensor(win, win, edge[:, t % 2, skip:], ALU.add).then_inc(edged, 1)
            dve.wait_ge(edged, s + 1 + 2)
            if t == 0:
                dve.wait_ge(split_ready, h)
            nc.vector.tensor_reduce(ntop[:, n:n + 1], s_ps(t)[:, 0:(n + 1) * P], AX_X, ALU.max, negate=True).then_inc(top_ready, 1)

        def split(h):
            hi, lo = (top_rows[:, :, row] for row in TOP)
            dve.wait_ge(top_ready, TPB * h + TPB)
            dve.wait_ge(top_turned, h)
            nc.vector.tensor_copy(hi, ntop[:]).then_inc(split_part, 1)
            dve.wait_ge(split_part, h + 1)
            nc.vector.tensor_tensor(lo, ntop[:], hi, ALU.subtract).then_inc(split_ready, 1)

        def take_off(h, r, j):
            s = TPB * h + j
            a, z, c, at = chunks[j][0]
            width = WIN if j + 1 < TPB else P
            flat = t_ps.rearrange("p a n -> p (a n)")
            win = flat[:, c * 512 + at:c * 512 + at + width]
            if j == 0:
                dve.wait_ge(spills_ready, PER_ROUND * h_round[0] + (r + 1))
            dve.wait_ge(t_done, s + 1)
            nc.vector.scalar_tensor_tensor(win, prev[:, 0:width], mine[:, r, 0, j:j + 1], win, ALU.mult, ALU.add).then_inc(t_part, 1)
            dve.wait_ge(t_part, s + 1)
            nc.vector.scalar_tensor_tensor(win, own[:, 0:width], mine[:, r, 1, j:j + 1], win, ALU.mult, ALU.add).then_inc(t_edged, 1)

        spills_ready = sem("spills_ready")
        mine = off_dve
        h_round = [0]
        dve.sem_inc(edged, 2)
        for t in range(TPB):
            top(0, t)
        split(0)

        def body(i, last):
            h_round[0] = i
            dve.wait_ge(t_edged, TPB * PER_ROUND * i)
            for r in range(PER_ROUND):
                head = bass.ds(i * PER_ROUND + r, 1)
                nc.vector.tensor_copy(mine[:, r], spill[:, 0:3:2, head, :].rearrange("p k z t -> p k (z t)")).then_inc(spills_ready, 1)
            for r in range(PER_ROUND):
                h = PER_ROUND * i + r
                more = not (last and r == PER_ROUND - 1)
                if more:
                    top(h + 1, 0)
                take_off(h, r, 0)
                if more:
                    top(h + 1, 1)
                for j in range(TPB):
                    if more and j + 2 < TPB:
                        top(h + 1, j + 2)
                        if j + 3 == TPB:
                            split(h + 1)
                    if j + 1 < TPB:
                        take_off(h, r, j + 1)

        rounds(dve, body)

    def on_scalar(act):
        nc.scalar.activation(ntop_dummy[:], env.eps[:], ACT.Exp).then_inc(tables, 1)
        act.wait_ge(tables, 1)
        act.wait_ge(filled, FILLS)
        act.sem_inc(exped, 1)

        def place_top(h, r):
            act.wait_ge(top_turned, h + 1)
            nc.scalar.copy(q2[TOP[0]:ROWS2, r % BUFS, :], m_ps[TOP[0]:ROWS2, :]).then_inc(top_placed, 1)

        place_top(0, 0)

        def body(i, last):
            for r in range(PER_ROUND):
                h = PER_ROUND * i + r
                for j in range(TPB):
                    if j == TPB - 1 and not (last and r == PER_ROUND - 1):
                        place_top(h + 1, r + 1)
                    act.wait_ge(t_edged, TPB * h + (j + 1))
                    act.wait_ge(weighed, CHUNKS * h + (before[j - 1] + 2 if j else 1))
                    for a, z, c, at in chunks[j]:
                        nc.scalar.activation(pT[:, j % 2, c, at:at + z - a], t_ps[:, c, at:at + z - a], ACT.Exp,
                                             scale=size[:, 0:1]).then_inc(exped, 1)
                if r % GROUP == GROUP - 1:
                    keep(i, r, h)

        def keep(i, r, h):
            act.wait_ge(weighed, CHUNKS * h + (CHUNKS + 2))
            rows = slice(r // GROUP * SUMS, (r // GROUP + 1) * SUMS)
            for c in range(2):
                cols = slice(c * 512, (c + 1) * 512)
                for dst, src in ((oT, o_ps[0:SUMS, c, :]), (sums, o_ps[SUMS:P, c, :])):
                    nc.scalar.copy(dst[rows, bass.ds(i, 1), cols].rearrange("p z t -> p (z t)"), src).then_inc(o_evac, 1)

        rounds(act, body)
        act.wait_ge(o_evac, 4 * 2 * ROUNDS)

    off_dve = sb("off_dve", [P, PER_ROUND, 2, TPB])
    ntop_dummy = sb("warm", [P, 1])
    return dict(sync=on_sync, gpsimd=on_gpsimd, tensor=on_tensor, vector=on_vector, scalar=on_scalar)


def any_mask(nc, env, st, tag, banks, kern_dram, mask, q_dram, k_dram, v, oT, sums):
    o_dram = nc.dram_tensor(f"{tag}_o", [HEADS, HD, ROWS * WINDOWS], F32).ap()
    sb, sem = lambda n, *a: st.sb("any_" + n, *a), lambda n: st.sem("any_" + n)
    seen, gone = sb("seen", [P, WINDOWS, S], U8), sb("gone", [P, WINDOWS, S], U8)
    kern = sb("kern", [P, HEADS, TAP * TAP])
    tap = sb("tap", [P, TAP * TAP])
    down = sb("down", [P, TAP, P])
    band = sb("band", [P, TAP, P])
    qh, kh = sb("qh", [HD, PAD]), sb("kh", [HD, PAD])
    sm = sb("sm", [P, S + 2])
    z = sb("z", [P, S])
    pT = sb("pT", [P, TPB, P])
    ntop, total, inv = sb("ntop", [P, 1]), sb("total", [P, 1]), sb("inv", [P, 1])
    o, vals = sb("o", [HD, ROWS]), sb("vals", [P, TPB, HD])
    s_ps, z_ps, t_ps = (banks[:, i:i + 2, :].rearrange("p a n -> p (a n)") for i in (0, 2, 4))
    o_ps = banks[:, 6, :]
    mask_zero, mask_loaded, kern_loaded, mask_ready, down_made, staged, stored, gathered = (
        sem(n) for n in ("mask_zero", "mask_loaded", "kern_loaded", "mask_ready", "down_made", "staged", "stored",
                         "gathered"))
    band_ready, scored, masked, summed, top_ready, exped, turned, t_evac, o_done, o_ready, padded, tables, taken, banded, band_parts, hidden, inv_ready, normed = (
        sem(n) for n in ("band_ready", "scored", "masked", "summed", "top_ready", "exped", "turned", "t_evac", "o_done",
                         "o_ready", "padded", "tables", "taken", "banded", "band_parts", "hidden", "inv_ready", "normed"))

    def on_sync(sp):
        sp.wait_ge(mask_zero, 2)
        m = mask
        loads = []
        for i in range(WINDOWS):
            first, last = max(0, i * ROWS - 1), min(S, i * ROWS - 1 + P)
            loads.append((seen, first - (i * ROWS - 1), i, first, last))
            loads.append((gone, 0, i, i * ROWS, min(S, (i + 1) * ROWS)))
        for dst, at, i, first, last in loads:
            sp.dma_start(dst[at:at + last - first, i, :], m[first:last, :]).then_inc(mask_loaded, 16)
        sp.dma_start(kern[:], kern_dram.rearrange("b (h k) -> (b h) k", h=H).partition_broadcast(P)).then_inc(kern_loaded, 16)
        q_rows, k_rows = (d.rearrange("b (h f) t -> (b h) f t", h=H) for d in (q_dram, k_dram))

        def stage(g):
            sp.dma_start(qh[:], q_rows[bass.ds(g, 1)].rearrange("a f t -> (a f) t")).then_inc(staged, 16)
            sp.dma_start(kh[:], k_rows[bass.ds(g, 1)].rearrange("a f t -> (a f) t")).then_inc(staged, 16)

        with sp.Fori(0, HEADS) as g:
            sp.wait_ge(scored, WINDOWS * g)
            stage(g)
            for i in range(WINDOWS):
                sp.wait_ge(o_ready, WINDOWS * g + (i + 1))
                sp.dma_start(o_dram[bass.ds(g, 1), :, i * ROWS:(i + 1) * ROWS].rearrange("a d t -> (a d) t"),
                             o[:]).then_inc(stored, 16)
        sp.wait_ge(stored, 16 * WINDOWS * HEADS)
        sp.dma_start(oT[:], o_dram.rearrange("(i h) d t -> (h d) i t", h=H // DC)[:, :, 0:S]).then_inc(gathered, 16)
        sp.wait_ge(gathered, 16)

    def on_gpsimd(pool):
        nc.gpsimd.memset(seen[:], 0.0).then_inc(mask_zero, 1)
        nc.gpsimd.memset(gone[:], 0.0).then_inc(mask_zero, 1)
        nc.gpsimd.memset(sm[:], 0.0).then_inc(padded, 1)
        nc.gpsimd.memset(down[:], 0.0).then_inc(padded, 1)
        nc.gpsimd.memset(sums[:], 1.0).then_inc(padded, 1)
        pool.wait_ge(padded, 3)
        for a in range(TAP):
            nc.gpsimd.affine_select(out=down[:, a, :], in_=down[:, a, :], compare_op=ALU.not_equal, fill=1.0, base=-a,
                                    pattern=[[-1, P]], channel_multiplier=1).then_inc(down_made, 1)

    def on_tensor(pe):
        with pe.Fori(0, HEADS) as g:
            pe.wait_ge(staged, 32 * g + 32)
            for i in range(WINDOWS):
                s = WINDOWS * g + i
                pe.wait_ge(masked, s)
                for n in range(S // 512):
                    last = nc.tensor.matmul(s_ps[:, n * 512:(n + 1) * 512], qh[:, i * ROWS:i * ROWS + P],
                                            kh[:, 1 + n * 512:1 + (n + 1) * 512], start=True, stop=True)
                last.then_inc(scored, 1)
                if i == 0:
                    pe.wait_ge(band_ready, g + 1)
                pe.wait_ge(masked, s + 1)
                for n in range(S // 512):
                    for c in range(TAP):
                        last = nc.tensor.matmul(z_ps[:, n * 512:(n + 1) * 512], band[:, c, :], sm[:, c + n * 512:c + (n + 1) * 512],
                                                start=c == 0, stop=c == TAP - 1)
                last.then_inc(summed, 1)
                pe.wait_ge(normed, s + 1)
                for j in range(TPB):
                    last = nc.tensor.transpose(t_ps[:, j * P:(j + 1) * P], z[:, j * P:(j + 1) * P], env.ident[:])
                last.then_inc(turned, 1)
                pe.wait_ge(t_evac, s + 1)
                for j in range(TPB):
                    last = nc.tensor.matmul(o_ps[0:HD, 0:P], vals[:, j, :], pT[:, j, :], start=j == 0, stop=j == TPB - 1)
                last.then_inc(o_done, 1)

    def on_vector(dve):
        dve.wait_ge(mask_loaded, 32 * WINDOWS)
        nc.vector.tensor_scalar(seen[:], seen[:], 0.0, None, ALU.is_equal).then_inc(mask_ready, 1)
        dve.wait_ge(mask_ready, 1)
        dve.wait_ge(kern_loaded, 16)
        dve.wait_ge(down_made, TAP)

        with dve.Fori(0, HEADS) as g:
            nc.vector.tensor_copy(tap[:], kern[:, bass.ds(g, 1), :].rearrange("p a k -> p (a k)")).then_inc(taken, 1)
            dve.wait_ge(o_done, WINDOWS * g)
            nc.vector.tensor_copy(vals[:], v[:, bass.ds(g, 1)].rearrange("p a t d -> p (a t) d")).then_inc(taken, 1)
            dve.wait_ge(taken, 2 * g + 2)
            dve.wait_ge(summed, WINDOWS * g)
            for c in range(TAP):
                for a in range(TAP):
                    weight = tap[:, a * TAP + c:a * TAP + c + 1]
                    if a == 0:
                        ins = nc.vector.tensor_scalar(band[:, c, :], down[:, a, :], weight, None, ALU.mult)
                    else:
                        dve.wait_ge(banded, 6 * g + (2 * c + a))
                        ins = nc.vector.scalar_tensor_tensor(band[:, c, :], down[:, a, :], weight, band[:, c, :], ALU.mult, ALU.add)
                    if a < TAP - 1:
                        ins.then_inc(banded, 1)
                    elif c < TAP - 1:
                        ins.then_inc(band_parts, 1)
                    else:
                        dve.wait_ge(band_parts, (TAP - 1) * (g + 1))
                        ins.then_inc(band_ready, 1)
            for i in range(WINDOWS):
                s = WINDOWS * g + i
                dve.wait_ge(scored, s + 1)
                dve.wait_ge(summed, s)
                nc.vector.tensor_tensor(sm[:, 1:S + 1], s_ps, seen[:, i, :], ALU.mult).then_inc(masked, 1)
                dve.wait_ge(summed, s + 1)
                dve.wait_ge(turned, s)
                nc.vector.scalar_tensor_tensor(z[:], gone[:, i, :], NEG, z_ps, ALU.mult, ALU.add).then_inc(hidden, 1)
                dve.wait_ge(hidden, s + 1)
                nc.vector.tensor_reduce(ntop[:], z[:], AX_X, ALU.max, negate=True).then_inc(top_ready, 1)
                dve.wait_ge(exped, s + 1)
                nc.vector.reciprocal(inv[:], total[:]).then_inc(inv_ready, 1)
                dve.wait_ge(inv_ready, s + 1)
                nc.vector.tensor_scalar(z[:], z[:], inv[:, 0:1], None, ALU.mult).then_inc(normed, 1)
                dve.wait_ge(o_done, s + 1)
                dve.wait_ge(stored, 16 * s)
                nc.vector.tensor_copy(o[:], o_ps[0:HD, 0:ROWS]).then_inc(o_ready, 1)

    def on_scalar(act):
        nc.scalar.activation(total[:], env.eps[:], ACT.Exp).then_inc(tables, 1)
        act.wait_ge(tables, 1)
        with act.Fori(0, HEADS) as g:
            for i in range(WINDOWS):
                s = WINDOWS * g + i
                act.wait_ge(top_ready, s + 1)
                nc.scalar.activation(z[:], z[:], ACT.Exp, bias=ntop[:, 0:1], accum_out=total[:]).then_inc(exped, 1)
                act.wait_ge(turned, s + 1)
                act.wait_ge(o_done, s)
                nc.scalar.copy(pT[:].rearrange("p j t -> p (j t)"), t_ps).then_inc(t_evac, 1)

    return dict(sync=on_sync, gpsimd=on_gpsimd, tensor=on_tensor, vector=on_vector, scalar=on_scalar)


def project_out(nc, env, st, ctx, w, oT, sums):
    wo, bo = st.sb("wo", [P, DC, D]), st.sb("bo", [1, D])
    y_ps = st.ps("y_ps", [P, 4, 512])
    loaded, inverted, ready, y_done, added = (st.sem(n) for n in ("loaded", "inverted", "ready", "y_done", "added"))
    block = ctx.enter_context(nc.Block())
    HALF = S // 512
    parts = [(b, n) for b in range(B) for n in range(HALF)]
    TILES_IN = TILES // len(parts)

    @block.sync
    def _(sp):
        sp.dma_start(wo[:], w("proj_W").rearrange("(c p) n -> p c n", p=P)).then_inc(loaded, 16)
        sp.dma_start(bo[:], w("proj_b").rearrange("(a n) -> a n", a=1)).then_inc(loaded, 16)

    @block.tensor
    def _(pe):
        pe.wait_ge(loaded, 32)
        for t in range(TILES):
            b, n = divmod(t, TPB)
            pe.wait_ge(ready, t // TILES_IN + 1)
            if t >= 4:
                pe.wait_ge(added, t - 3)
            nc.tensor.matmul(y_ps[:, t % 4, 0:D], env.ones[0:1, :], bo[:], start=True, stop=False)
            for c in range(DC):
                last = nc.tensor.matmul(y_ps[:, t % 4, 0:D], oT[:, b * DC + c, n * P:(n + 1) * P], wo[:, c, :], start=False,
                                        stop=c == DC - 1)
            last.then_inc(y_done, 1)

    @block.vector
    def _(dve):
        def divide(k):
            b, n = parts[k]
            at = (slice(None), slice(b * DC, (b + 1) * DC), slice(n * 512, (n + 1) * 512))
            nc.vector.reciprocal(sums[at], sums[at]).then_inc(inverted, 1)
            dve.wait_ge(inverted, k + 1)
            nc.vector.tensor_tensor(oT[at], oT[at], sums[at], ALU.mult).then_inc(ready, 1)

        divide(0)
        for k in range(len(parts)):
            if k + 1 < len(parts):
                divide(k + 1)
            for t in range(k * TILES_IN, (k + 1) * TILES_IN):
                dve.wait_ge(y_done, t + 1)
                nc.vector.tensor_tensor(env.x[:, t, :], env.x[:, t, :], y_ps[:, t % 4, 0:D], ALU.add).then_inc(added, 1)



I = 768
IC = I // P
BLOCK = 32
QA = 32767.0
QW = 7.0
FLOOR = 1e-12
ROUND = 12582912.0
U16 = 65536.0
CHUNKS = T // 512


def quant_ffn_stage(nc, env, tag, args, name):
    w = lambda n: args[f"{name}_{n}"]
    with ExitStack() as ctx:
        st = Stage(nc, ctx, tag)
        xnT = st.sb("xnT", [P, DC, T])
        wT = st.sb("wT", [P, 2, DC, I])
        wdT = st.sb("wdT", [P, IC, D])
        with ExitStack() as inner:
            stw = Stage(nc, inner, tag + "w")
            raw = stw.sb("raw", [P, 3 * I * D // P])
            raw_loaded = stw.sem("raw_loaded")

            def load_raw(sp):
                for k, n in enumerate(("w_up", "w_gate", "w_down")):
                    sp.dma_start(raw[:, k * IC * D:(k + 1) * IC * D].rearrange("p (o i) -> p o i", o=IC if k < 2 else DC),
                                 w(n).rearrange("(o p) i -> p o i", p=P)).then_inc(raw_loaded, 16)

            layernorm_stage(nc, env, tag + "l", env.x, dst_T=xnT, ahead=load_raw)
            quant_weights(nc, env, stw, inner, raw, raw_loaded, wT, wdT)
        with ExitStack() as inner:
            quant_unit(nc, env, Stage(nc, inner, tag + "u"), inner, xnT, wT, wdT)


def quant_weights(nc, env, st, ctx, raw, raw_loaded, wT, wdT):
    NB = 3 * I * D // P // BLOCK
    scale, inv = st.sb("scale", [P, NB]), st.sb("inv", [P, NB])
    t_ps = st.ps("t_ps", [P, 2, 512])
    linked, ready, turned, evacuated = (st.sem(n) for n in ("linked", "ready", "turned", "evacuated"))
    block = ctx.enter_context(nc.Block())
    part = lambda k: raw[:, k * IC * D:(k + 1) * IC * D]
    blocks = raw[:].rearrange("p (b i) -> p b i", i=BLOCK)
    over = lambda buf: buf[:].unsqueeze(2).to_broadcast([P, NB, BLOCK])
    pieces = []
    for k in range(2):
        rows = part(k).rearrange("p (o i) -> p o i", o=IC)
        for c in range(DC):
            for o in range(IC):
                pieces.append((rows[:, o, c * P:(c + 1) * P], (k, c, o)))
    rows = part(2).rearrange("p (o i) -> p o i", o=DC)
    for c in range(IC):
        for o in range(DC):
            pieces.append((rows[:, o, c * P:(c + 1) * P], (2, c, o)))
    flat = [wT[:, 0].rearrange("p c i -> p (c i)"), wT[:, 1].rearrange("p c i -> p (c i)"), wdT[:].rearrange("p c d -> p (c d)")]

    @block.vector
    def _(dve):
        step = chain(dve, linked)
        dve.wait_ge(raw_loaded, 48)
        step(nc.vector.tensor_reduce(scale[:], blocks, AX_X, ALU.max, apply_absolute_value=True))
        step(nc.vector.tensor_scalar(scale[:], scale[:], 1.0 / QW, FLOOR, ALU.mult, ALU.max))
        step(nc.vector.reciprocal(inv[:], scale[:]))
        step(nc.vector.tensor_tensor(blocks, blocks, over(inv), ALU.mult))
        step(nc.vector.tensor_scalar(raw[:], raw[:], ROUND, -ROUND, ALU.add, ALU.add))
        step(nc.vector.tensor_scalar(raw[:], raw[:], -QW - 1.0, QW, ALU.max, ALU.min))
        nc.vector.tensor_tensor(blocks, blocks, over(scale), ALU.mult).then_inc(ready, 1)

    @block.tensor
    def _(pe):
        pe.wait_ge(ready, 1)
        for n in range(len(pieces) // 4):
            if n >= 2:
                pe.wait_ge(evacuated, n - 1)
            for q in range(4):
                last = nc.tensor.transpose(t_ps[:, n % 2, q * P:(q + 1) * P], pieces[4 * n + q][0], env.ident[:])
            last.then_inc(turned, 1)

    @block.scalar
    def _(act):
        for n in range(len(pieces) // 4):
            act.wait_ge(turned, n + 1)
            k = pieces[4 * n][1][0]
            at0 = (4 * n - (0, 12, 24)[k]) * P
            nc.scalar.copy(flat[k][:, at0:at0 + 512], t_ps[:, n % 2, :]).then_inc(evacuated, 1)


def quant_unit(nc, env, st, ctx, xnT, wT, wdT):
    sb, ps, sem = st.sb, st.ps, st.sem
    act2 = [sb("up", [P, IC, T]), sb("gate", [P, IC, T])]
    up, gate = act2
    sig = sb("sig", [P, 2, T])
    tops = sb("tops", [P, 4, IC])
    top, amax, scale, inv = (sb(n, [P, 5]) for n in ("top", "amax", "scale", "inv"))
    both = sb("both", [P, 2])
    rnd = sb("rnd", [P, 1])
    h_ps = [ps("h_ps0", [P, T]), ps("h_ps1", [P, T])]
    rnd_set, linked, top_ready, reduced, scale_ready, x_ready = (
        sem(n) for n in ("rnd_set", "linked", "top_ready", "reduced", "scale_ready", "x_ready"))
    h_done, up_evac, gate_evac, topped, g_lifted, g_whole, sig_ready, sig_lifted, sig_whole, gs_ready = (
        sem(n) for n in ("h_done", "up_evac", "gate_evac", "topped", "g_lifted", "g_whole", "sig_ready", "sig_lifted", "sig_whole",
                         "gs_ready"))
    u_lifted, u_whole, gs_lifted, gs_whole, o_ready, o_lifted, o_whole, y_done, added = (
        sem(n) for n in ("u_lifted", "u_whole", "gs_lifted", "gs_whole", "o_ready", "o_lifted", "o_whole", "y_done", "added"))
    gs_topped, o_topped = sem("gs_topped"), sem("o_topped")
    block = ctx.enter_context(nc.Block())
    col = lambda buf, k: buf[:, k:k + 1]
    X, GATE, UP, GS, O = range(5)
    jobs = [(k, o) for k in (1, 0) for o in range(IC)]

    @block.gpsimd
    def _(pool):
        nc.gpsimd.memset(rnd[:], ROUND).then_inc(rnd_set, 1)
        for k in range(5):
            pool.wait_ge(top_ready, k + 1)
            nc.gpsimd.partition_all_reduce(col(amax, k), col(top, k), P, RMAX).then_inc(reduced, 1)

    @block.tensor
    def _(pe):
        for j, (k, o) in enumerate(jobs):
            if j >= 2:
                before = j - 2
                pe.wait_ge(*((gate_evac, before + 1) if before < IC else (up_evac, before - IC + 1)))
            for n in range(CHUNKS):
                if j == 0:
                    pe.wait_ge(x_ready, n + 1)
                for c in range(DC):
                    last = nc.tensor.matmul(h_ps[j % 2][:, n * 512:(n + 1) * 512], wT[:, k, c, o * P:(o + 1) * P],
                                            xnT[:, c, n * 512:(n + 1) * 512], start=c == 0, stop=c == DC - 1)
            last.then_inc(h_done, 1)
        for t in range(TILES):
            if t % 4 == 0:
                pe.wait_ge(o_whole, t // 4 + 1)
            if t >= 4:
                pe.wait_ge(added, t - 3)
            y = h_ps[0][:, (t % 4) * 512:(t % 4) * 512 + D]
            for o in range(IC):
                last = nc.tensor.matmul(y, gate[:, o, t * P:(t + 1) * P], wdT[:, o, :], start=o == 0, stop=o == IC - 1)
            last.then_inc(y_done, 1)

    def largest(buf, k, o, done):
        nc.vector.tensor_reduce(tops[:, k - 1, o:o + 1], buf[:, o, :], AX_X, ALU.max, apply_absolute_value=True).then_inc(done, 1)

    def sigmoid_times(dve, o):
        g, s = gate[:, o, :], sig[:, o % 2, :]
        dve.wait_ge(sig_ready, o + 1)
        nc.vector.tensor_scalar(s, s, U16, ROUND, ALU.mult, ALU.add).then_inc(sig_lifted, 1)
        dve.wait_ge(sig_lifted, o + 1)
        nc.vector.tensor_scalar(s, s, -ROUND, U16 - 1.0, ALU.add, ALU.min).then_inc(sig_whole, 1)
        dve.wait_ge(sig_whole, o + 1)
        nc.vector.scalar_tensor_tensor(g, g, col(both, 0), s, ALU.mult, ALU.mult).then_inc(gs_ready, 1)
        dve.wait_ge(gs_ready, o + 1)
        largest(gate, GS, o, gs_topped)

    def residual(dve, n):
        for t in range(4 * n, 4 * n + 4):
            xt = env.x[:, t, :]
            dve.wait_ge(y_done, t + 1)
            nc.vector.scalar_tensor_tensor(xt, h_ps[0][:, (t % 4) * 512:(t % 4) * 512 + D], col(scale, O), xt, ALU.mult,
                                           ALU.add).then_inc(added, 1)

    @block.vector
    def _(dve):
        step = chain(dve, linked)

        def send(k, done, count):
            dve.wait_ge(done, count)
            nc.vector.tensor_reduce(col(top, k), tops[:, k - 1, :], AX_X, ALU.max).then_inc(top_ready, 1)

        def scales(k):
            dve.wait_ge(reduced, k + 1)
            step(nc.vector.tensor_scalar(col(scale, k), col(amax, k), 1.0 / QA, FLOOR, ALU.mult, ALU.max))
            nc.vector.reciprocal(col(inv, k), col(scale, k)).then_inc(scale_ready, 1)
            dve.wait_ge(scale_ready, k + 1)

        nc.vector.tensor_reduce(col(top, X), xnT[:].rearrange("p c t -> p (c t)"), AX_X, ALU.max,
                                apply_absolute_value=True).then_inc(top_ready, 1)
        scales(X)
        for n in range(CHUNKS):
            part = xnT[:, :, n * 512:(n + 1) * 512]
            step(nc.vector.tensor_scalar(part, part, col(inv, X), ROUND, ALU.mult, ALU.add))
            step(nc.vector.tensor_scalar(part, part, -ROUND, -QA - 1.0, ALU.add, ALU.max))
            nc.vector.tensor_scalar(part, part, QA, col(scale, X), ALU.min, ALU.mult).then_inc(x_ready, 1)
        for o in range(IC):
            dve.wait_ge(gate_evac, o + 1)
            largest(gate, GATE, o, topped)
        send(GATE, topped, IC)
        scales(GATE)
        step(nc.vector.tensor_scalar(col(both, 0), col(scale, GATE), 1.0 / U16, None, ALU.mult))
        for o in range(IC):
            g = gate[:, o, :]
            dve.wait_ge(g_lifted, o + 1)
            nc.vector.tensor_scalar(g, g, -ROUND, QA, ALU.add, ALU.min).then_inc(g_whole, 1)
            dve.wait_ge(up_evac, o + 1)
            largest(up, UP, o, topped)
            if o == IC - 1:
                send(UP, topped, 2 * IC)
            if o:
                sigmoid_times(dve, o - 1)
        scales(UP)
        sigmoid_times(dve, IC - 1)
        send(GS, gs_topped, IC)
        for o in range(IC):
            dve.wait_ge(u_lifted, o + 1)
            nc.vector.tensor_scalar(up[:, o, :], up[:, o, :], -ROUND, QA, ALU.add, ALU.min).then_inc(u_whole, 1)
        scales(GS)
        step(nc.vector.tensor_tensor(col(both, 1), col(scale, GS), col(scale, UP), ALU.mult))
        for o in range(IC):
            g = gate[:, o, :]
            dve.wait_ge(gs_lifted, o + 1)
            nc.vector.tensor_scalar(g, g, -ROUND, QA, ALU.add, ALU.min).then_inc(gs_whole, 1)
            dve.wait_ge(gs_whole, o + 1)
            dve.wait_ge(u_whole, o + 1)
            nc.vector.scalar_tensor_tensor(g, g, col(both, 1), up[:, o, :], ALU.mult, ALU.mult).then_inc(o_ready, 1)
            dve.wait_ge(o_ready, o + 1)
            largest(gate, O, o, o_topped)
        send(O, o_topped, IC)
        scales(O)
        for n in range(CHUNKS):
            part = gate[:, :, n * 512:(n + 1) * 512]
            dve.wait_ge(o_lifted, n + 1)
            nc.vector.tensor_scalar(part, part, -ROUND, QA, ALU.add, ALU.min).then_inc(o_whole, 1)
            if n:
                residual(dve, n - 1)
        residual(dve, CHUNKS - 1)

    def sigmoid(act, o):
        act.wait_ge(g_whole, o + 1)
        if o >= 2:
            act.wait_ge(gs_ready, o - 1)
        nc.scalar.activation(sig[:, o % 2, :], gate[:, o, :], ACT.Sigmoid, scale=col(scale, GATE)).then_inc(sig_ready, 1)

    @block.scalar
    def _(act):
        act.wait_ge(rnd_set, 1)

        def lift(buf, k, done):
            nc.scalar.activation(buf, buf, ACT.Identity, bias=rnd[:, 0:1], scale=col(inv, k)).then_inc(done, 1)

        for o in range(IC):
            act.wait_ge(h_done, o + 1)
            nc.scalar.copy(gate[:, o, :], h_ps[o % 2][:]).then_inc(gate_evac, 1)
        for o in range(IC):
            act.wait_ge(h_done, IC + o + 1)
            nc.scalar.copy(up[:, o, :], h_ps[(IC + o) % 2][:]).then_inc(up_evac, 1)
            if o == 0:
                act.wait_ge(scale_ready, GATE + 1)
            lift(gate[:, o, :], GATE, g_lifted)
            if o:
                sigmoid(act, o - 1)
        sigmoid(act, IC - 1)
        act.wait_ge(scale_ready, UP + 1)
        for o in range(IC):
            lift(up[:, o, :], UP, u_lifted)
        act.wait_ge(scale_ready, GS + 1)
        for o in range(IC):
            lift(gate[:, o, :], GS, gs_lifted)
        act.wait_ge(scale_ready, O + 1)
        for n in range(CHUNKS):
            lift(gate[:, :, n * 512:(n + 1) * 512], O, o_lifted)



DH = 64
INNER = H * DH
PAIRS = INNER // P
KT = TPB + 1
KEYS = S + NCTX
KPAD = KT * P
NEG_MAX = -3.4028234663852886e38


def latent_attention_stage(nc, env, tag, args, name):
    w = lambda n: args[f"{name}_{n}"]
    with ExitStack() as ctx:
        st = Stage(nc, ctx, tag)
        sb = st.sb
        xn = sb("xn", [P, TILES, D])
        layernorm_stage(nc, env, tag + "l", env.x, dst_tok=xn)
        p = {n: sb(n, s) for n, s in (("mean", [P, TILES + B]), ("rstd", [P, TILES + B]), ("gl", [P, DC]), ("bl", [P, DC]),
                                       ("gx", [P, DC]), ("bx", [P, DC]), ("gain", [P, 1]), ("gmax", [P, 1]), ("hide", [P, B, NCTX]),
                                       ("hide_key", [P, B]))}
        latent_norms(nc, env, st, tag, args, w, xn, p)
        for b in range(B):
            with ExitStack() as inner:
                sti = Stage(nc, inner, f"{tag}b{b}")
                qT, kT = sti.sb("qT", [P, 2, PAIRS, S], F16), sti.sb("kT", [P, 2, PAIRS, KEYS], F16)
                v = sti.sb("v", [P, KT, INNER])
                with ExitStack() as deep:
                    latent_project(nc, env, Stage(nc, deep, f"{tag}p{b}"), deep, w, b, xn, p, qT, kT, v)
                oT = sti.sb("oT", [P, PAIRS, S])
                with ExitStack() as deep:
                    latent_attend(nc, env, Stage(nc, deep, f"{tag}a{b}"), deep, b, p, xn, qT, kT, v, oT)
                with ExitStack() as deep:
                    latent_emit(nc, env, Stage(nc, deep, f"{tag}o{b}"), deep, w, b, oT)


def latent_norms(nc, env, outer, tag, args, w, xn, p):
    with ExitStack() as ctx:
        st = Stage(nc, ctx, tag + "n")
        stats = st.sb("stats", [P, TILES + B, 6])
        var = st.sb("var", [P, TILES + B])
        mask_in = st.sb("mask_in", [P, B, NCTX], U8)
        loaded, counted, linked, var_ready, std_ready = (st.sem(n) for n in ("loaded", "counted", "linked", "var_ready", "std_ready"))
        gains, small = st.sb("gains", [P, 2, DH]), st.sb("small", [P, 1])
        hidden_key = st.sb("hidden_key", [P, B], U8)
        key_zero = st.sem("key_zero")
        block = ctx.enter_context(nc.Block())

        @block.sync
        def _(sp):
            for n, k in (("ln_l_g", "gl"), ("ln_l_b", "bl"), ("ln_x_g", "gx"), ("ln_x_b", "bx")):
                sp.dma_start(p[k][:], w(n).rearrange("(c p) -> p c", p=P), allow_slow_non_contiguous=True).then_inc(loaded, 16)
            for i, n in enumerate(("qn_g", "kn_g")):
                sp.dma_start(gains[:, i, :], w(n).partition_broadcast(P)).then_inc(loaded, 16)
            for half in range(2):
                rows = slice(half * DH, (half + 1) * DH)
                sp.dma_start(p["gain"][rows, :], w("qn_g").rearrange("(p a) -> p a", a=1)).then_inc(loaded, 16)
                sp.dma_start(small[rows, :], w("kn_g").rearrange("(p a) -> p a", a=1)).then_inc(loaded, 16)
            sp.dma_start(mask_in[:], args["mask_BxS2_bf1"].partition_broadcast(P)).then_inc(loaded, 16)
            sp.wait_ge(key_zero, 1)
            sp.dma_start(hidden_key[0:NCTX], args["mask_BxS2_bf1"].rearrange("b k -> k b"), allow_slow_non_contiguous=True).then_inc(loaded, 16)
            sp.wait_ge(loaded, 192)

        @block.gpsimd
        def _(pool):
            nc.gpsimd.memset(hidden_key[:], 0.0).then_inc(key_zero, 1)

        @block.vector
        def _(dve):
            step = chain(dve, linked)
            step(nc.vector.memset(stats[:, TILES:, :], 0.0))
            with dve.Fori(0, TILES // UNROLL) as i:
                for u in range(UNROLL):
                    t = UNROLL * i + u
                    nc.vector.bn_stats(tile_of(stats, t), tile_of(xn, t)).then_inc(counted, 1)
            for b in range(B):
                nc.vector.bn_stats(stats[0:NCTX, TILES + b, :], env.ctx_tok[0:NCTX, b, :]).then_inc(counted, 1)
            dve.wait_ge(counted, TILES + B)
            merge_stats(nc, step, p["mean"][:], var[:], stats, D)
            nc.vector.tensor_scalar(var[:], var[:], LN_EPS, None, ALU.add).then_inc(var_ready, 1)
            dve.wait_ge(loaded, 192)
            both = gains[:, 0, :]
            step(nc.vector.tensor_tensor(both, both, gains[:, 1, :], ALU.mult))
            step(nc.vector.scalar_tensor_tensor(gains[:, 1, :], both, -1.0, both, ALU.mult, ALU.max))
            step(nc.vector.tensor_reduce(p["gmax"][:], gains[:, 1, :], AX_X, ALU.max))
            step(nc.vector.tensor_scalar(p["gmax"][:], p["gmax"][:], 1e-30, None, ALU.max))
            step(nc.vector.tensor_tensor(p["gain"][:], p["gain"][:], small[:], ALU.mult))
            step(nc.vector.reciprocal(small[:], p["gmax"][:]))
            step(nc.vector.tensor_tensor(p["gain"][:], p["gain"][:], small[:], ALU.mult))
            step(nc.vector.tensor_scalar(p["gmax"][:], p["gmax"][:], DH ** -0.5, None, ALU.mult))
            step(nc.vector.tensor_scalar(p["hide_key"][:], hidden_key[:], 0.0, NEG_MAX, ALU.is_equal, ALU.mult))
            step(nc.vector.tensor_scalar(p["hide"][:], mask_in[:], 0.0, NEG_MAX, ALU.is_equal, ALU.mult))
            dve.wait_ge(std_ready, 1)
            step(nc.vector.reciprocal(p["rstd"][:], p["rstd"][:]))

        @block.scalar
        def _(act):
            act.wait_ge(var_ready, 1)
            nc.scalar.activation(p["rstd"][:], var[:], ACT.Sqrt).then_inc(std_ready, 1)


def latent_project(nc, env, st, ctx, w, b, xn, p, qT, kT, v):
    sb, ps, sem = st.sb, st.ps, st.sem
    wq, wkv = sb("wq", [P, DC, INNER]), sb("wkv", [P, DC, 2 * INNER])
    turn = sb("turn", [P, 2, D])
    lT = sb("lT", [P, 2, DC, P])
    sq = sb("sq", [P, 2, INNER])
    ss, rn = sb("ss", [P, 2, H]), sb("rn", [P, 2, H])
    qk = sb("qk", [P, 2, INNER])
    q_ps, k_ps, t_ps = ps("q_ps", [P, INNER]), ps("k_ps", [P, INNER]), ps("t_ps", [P, INNER])
    v_ps, x_ps = ps("v_ps", [P, 512]), ps("x_ps", [P, 512])
    loaded, normed, x_turned, x_evac, q_done, k_done, v_done, v_evac = (
        sem(n) for n in ("loaded", "normed", "x_turned", "x_evac", "q_done", "k_done", "v_done", "v_evac"))
    squared, summed, rooted, floored, inv_ready, scaled, turned, evacuated, table_loaded, halved = (
        sem(n) for n in ("squared", "summed", "rooted", "floored", "inv_ready", "scaled", "turned", "evacuated", "table_loaded", "halved"))
    block = ctx.enter_context(nc.Block())
    g0 = b * TPB

    LAST = TPB
    rows_of = lambda n: NCTX if isinstance(n, int) and n == LAST else P
    sides_of = lambda n: (1,) if isinstance(n, int) and n == LAST else (0, 1)
    side_at = lambda n, k: 2 * n if isinstance(n, int) and n == LAST else 2 * n + k

    def tiles(eng, work):
        for n in range(2):
            work(n, n)
        with eng.Fori(1, TPB // 2 - 1) as i:
            for u in range(2):
                work(2 * i + u, u)
        for n in range(TPB - 2, LAST + 1):
            work(n, n % 2)

    @block.sync
    def _(sp):
        sp.dma_start(wq[:], w("Wq").rearrange("(c p) n -> p c n", p=P)).then_inc(loaded, 16)
        sp.dma_start(wkv[:], w("Wkv").rearrange("(c p) n -> p c n", p=P)).then_inc(loaded, 16)

    @block.vector
    def _(dve):
        def normalise(n, u, reuse):
            rows = rows_of(n)
            if reuse:
                dve.wait_ge(x_turned, n - 1)
            if rows == P:
                src, col = tile_of(xn, n + g0), bass.ds(n + g0, 1)
            else:
                src, col = env.ctx_tok[0:rows, b, :], slice(TILES + b, TILES + b + 1)
            nc.vector.tensor_scalar(turn[0:rows, u, :], src, p["mean"][0:rows, col], p["rstd"][0:rows, col],
                                    ALU.subtract, ALU.mult).then_inc(normed, 1)

        def sums(n, k):
            rows = rows_of(n)
            if k == sides_of(n)[0] and not (isinstance(n, int) and n == 0):
                dve.wait_ge(rooted, n)
            dve.wait_ge(squared, side_at(n, k) + 1)
            nc.vector.tensor_reduce(ss[0:rows, k, :], sq[0:rows, k, :].rearrange("p (h d) -> p h d", h=H), AX_X,
                                    ALU.add).then_inc(summed, 1)

        def scale(n):
            rows, sides = rows_of(n), sides_of(n)
            norms = rn[0:rows] if len(sides) == 2 else rn[0:rows, 1, :]
            dve.wait_ge(rooted, n + 1)
            nc.vector.tensor_scalar(norms, norms, 1e-8, None, ALU.max).then_inc(floored, 1)
            dve.wait_ge(floored, n + 1)
            nc.vector.reciprocal(norms, norms).then_inc(inv_ready, 1)
            dve.wait_ge(inv_ready, n + 1)
            for k in sides:
                if not (isinstance(n, int) and n == 0):
                    dve.wait_ge(turned, 4 * n + (2 * k - 2))
                src = (q_ps, k_ps)[k]
                nc.vector.tensor_tensor(qk[0:rows, k, :].rearrange("p (h d) -> p h d", h=H),
                                        src[0:rows, :].rearrange("p (h d) -> p h d", h=H),
                                        rn[0:rows, k, :].unsqueeze(2).to_broadcast([rows, H, DH]), ALU.mult).then_inc(scaled, 1)

        def rest(n, k):
            rows = rows_of(n)
            for half in range(2):
                dve.wait_ge(halved, 2 * side_at(n, k) + (half + 1))
                src = t_ps[:, half * 512:(half + 1) * 512].rearrange("p (c t) -> p c t", c=4)[:, :, 0:rows]
                hi, lo = ((qT, kT)[k][:, i, half * 4:(half + 1) * 4, bass.ds(n * P, rows)] for i in range(2))
                if k == 0:
                    nc.vector.tensor_tensor(lo, src, hi, ALU.subtract).then_inc(evacuated, 1)
                else:
                    nc.vector.scalar_tensor_tensor(lo, src, p["gain"][:, 0:1], hi, ALU.mult, ALU.subtract).then_inc(evacuated, 1)

        def work(n, u):
            more = not (isinstance(n, int) and n == LAST)
            if not (isinstance(n, int) and n > LAST - 2):
                normalise(n + 2, u, True)
            for k in range(2):
                if more and k in sides_of(n + 1):
                    sums(n + 1, k)
                if k in sides_of(n):
                    rest(n, k)
            if more:
                scale(n + 1)

        for n in range(2):
            normalise(n, n, False)
        for k in range(2):
            sums(0, k)
        scale(0)
        tiles(dve, work)

    @block.scalar
    def _(act):
        nc.scalar.activation(ss[:, 0, 0:1], env.eps[:], ACT.Sqrt).then_inc(table_loaded, 1)
        act.wait_ge(table_loaded, 1)

        def affine(n, u, reuse):
            rows = rows_of(n)
            g, o = (p["gl"], p["bl"]) if rows == P else (p["gx"], p["bx"])
            act.wait_ge(x_turned, n + 1)
            if reuse:
                act.wait_ge(v_done, 2 * n - 2)
            for c in range(DC):
                nc.scalar.activation(lT[:, u, c, 0:rows], x_ps[:, c * P:c * P + rows], ACT.Identity, bias=o[:, c:c + 1],
                                     scale=g[:, c:c + 1]).then_inc(x_evac, 1)

        def square(n, k):
            rows = rows_of(n)
            act.wait_ge((q_done, k_done)[k], n + 1)
            if not (isinstance(n, int) and n == 0):
                act.wait_ge(summed, 2 * n + (k - 1))
            nc.scalar.activation(sq[0:rows, k, :], (q_ps, k_ps)[k][0:rows, :], ACT.Square).then_inc(squared, 1)

        def root(n):
            rows = rows_of(n)
            act.wait_ge(summed, side_at(n, 1) + 1)
            if not (isinstance(n, int) and n == 0):
                act.wait_ge(scaled, 2 * n)
            src, dst = (ss[0:rows], rn[0:rows]) if len(sides_of(n)) == 2 else (ss[0:rows, 1, :], rn[0:rows, 1, :])
            nc.scalar.activation(dst, src, ACT.Sqrt, scale=1.0 / DH).then_inc(rooted, 1)

        def keep_values(n):
            rows = rows_of(n)
            for k in range(2):
                act.wait_ge(v_done, 2 * n + (k + 1))
                nc.scalar.copy(v[0:rows, bass.ds(n, 1), k * 512:(k + 1) * 512].rearrange("p a n -> p (a n)"),
                               v_ps[0:rows, :]).then_inc(v_evac, 1)

        def halve(n, k):
            rows = rows_of(n)
            for half in range(2):
                act.wait_ge(turned, 2 * side_at(n, k) + (half + 1))
                dst = (qT, kT)[k][:, 0, half * 4:(half + 1) * 4, bass.ds(n * P, rows)]
                nc.scalar.activation(dst, t_ps[:, half * 512:(half + 1) * 512].rearrange("p (c t) -> p c t", c=4)[:, :, 0:rows],
                                     ACT.Identity, scale=1.0 if k == 0 else p["gain"][:, 0:1]).then_inc(halved, 1)

        def work(n, u):
            more = not (isinstance(n, int) and n == LAST)
            for k in range(2):
                if more and k in sides_of(n + 1):
                    square(n + 1, k)
                if k in sides_of(n):
                    halve(n, k)
            if not (isinstance(n, int) and n > LAST - 2):
                affine(n + 2, u, True)
            if more:
                root(n + 1)
                keep_values(n + 1)

        affine(0, 0, False)
        for k in range(2):
            square(0, k)
        affine(1, 1, False)
        root(0)
        keep_values(0)
        tiles(act, work)

    @block.tensor
    def _(pe):
        pe.wait_ge(loaded, 32)

        def turn_x(n, u, begun):
            rows = rows_of(n)
            pe.wait_ge(normed, n + 1)
            if begun:
                pe.wait_ge(x_evac, DC * n)
            for c in range(DC):
                last = nc.tensor.transpose(x_ps[:, c * P:c * P + rows], turn[0:rows, u, c * P:(c + 1) * P],
                                           env.ident[0:rows, 0:rows])
            last.then_inc(x_turned, 1)

        def queries_or_keys(n, u, k, begun):
            rows = rows_of(n)
            pe.wait_ge(x_evac, DC * n + DC)
            if begun:
                pe.wait_ge(scaled, 2 * n + (k - 1))
            for half in range(2):
                for c in range(DC):
                    wt = (wq, wkv)[k][:, c, half * 512:(half + 1) * 512]
                    last = nc.tensor.matmul((q_ps, k_ps)[k][0:rows, half * 512:(half + 1) * 512], lT[:, u, c, 0:rows], wt,
                                            start=c == 0, stop=c == DC - 1)
            last.then_inc((q_done, k_done)[k], 1)

        def values(n, u, begun):
            rows = rows_of(n)
            for half in range(2):
                if begun or half:
                    pe.wait_ge(v_evac, 2 * n + half)
                for c in range(DC):
                    last = nc.tensor.matmul(v_ps[0:rows, :], lT[:, u, c, 0:rows],
                                            wkv[:, c, INNER + half * 512:INNER + (half + 1) * 512], start=c == 0, stop=c == DC - 1)
                last.then_inc(v_done, 1)

        def turn_side(n, k):
            rows = rows_of(n)
            pe.wait_ge(scaled, side_at(n, k) + 1)
            for half in range(2):
                if not (isinstance(n, int) and n == 0 and k == 0):
                    pe.wait_ge(evacuated, 2 * side_at(n, k) + (half - 1))
                for c in range(4 * half, 4 * half + 4):
                    last = nc.tensor.transpose(t_ps[:, c * P:c * P + rows], qk[0:rows, k, c * P:(c + 1) * P],
                                               env.ident[0:rows, 0:rows])
                last.then_inc(turned, 1)

        def work(n, u):
            more = not (isinstance(n, int) and n == LAST)
            for k in range(2):
                if more and k in sides_of(n + 1):
                    queries_or_keys(n + 1, 1 - u, k, True)
                if k in sides_of(n):
                    turn_side(n, k)
            if not (isinstance(n, int) and n > LAST - 2):
                turn_x(n + 2, u, True)
            if more:
                values(n + 1, 1 - u, True)

        turn_x(0, 0, False)
        for k in range(2):
            queries_or_keys(0, 0, k, False)
        turn_x(1, 1, True)
        values(0, 0, False)
        tiles(pe, work)


def latent_attend(nc, env, st, ctx, b, p, xn, qT, kT, v, oT):
    sb, ps, sem = st.sb, st.ps, st.sem
    TOP = (DH, DH + 32)
    ROWS2 = TOP[1] + 1
    QT = TPB
    EXPS, HEAD_PAIRS, AHEAD = 2 * KT, H // 2, 4
    q11, q2 = sb("q11", [P, 2, S], F16), sb("q2", [ROWS2, 2, S], F16)
    k12, k1 = sb("k12", [P, 2, KEYS], F16), sb("k1", [ROWS2, 2, KEYS], F16)
    vh = sb("vh", [P, 2, KT, P])
    pT = xn[:, b * TPB:(b + 1) * TPB, :].rearrange("p (u c a) d -> p u c (a d)", u=2, c=2)
    ident = sb("ident", [P, P], F16)
    ntop = sb("ntop", [P, QT])
    top_rows = sb("top_rows", [P, QT, ROWS2], F16)
    inv = sb("inv", [DH, 2, 512])
    o = sb("o", [P, 2, 512])
    s_ps, banks = ps("s_ps", [P, 3 * 512]), ps("banks", [P, 4, 512])
    t_ps, o_ps = banks[:, 0:2, :], banks[:, 2:4, :]
    scores = lambda h, n: s_ps[:, 0:KEYS] if not (isinstance(h, int) and h == 0 and n % 2) else (
        banks[:, 0:3, :].rearrange("p a n -> p (a n)")[:, 0:KEYS])
    through = lambda h, n: QT * h + n if not (isinstance(h, int) and h == 0) else max(n - 1, 0)
    qk_staged, v_staged = ([sem(f"{n}_staged{u}") for u in range(2)] for n in ("qk", "v"))
    filled, scored, hidden, top_ready, split_part, split_ready, top_turned, top_placed = (
        sem(n) for n in ("filled", "scored", "hidden", "top_ready", "split_part", "split_ready", "top_turned", "top_placed"))
    t_done, exped, weighed, inv_ready, o_evac, kept, table_loaded = (
        sem(n) for n in ("t_done", "exped", "weighed", "inv_ready", "o_evac", "kept", "table_loaded"))
    block = ctx.enter_context(nc.Block())

    def pairs(eng, body):
        with eng.Fori(0, HEAD_PAIRS - 1) as i:
            body(i, False)
        body(HEAD_PAIRS - 1, True)

    @block.sync
    def _(sp):
        def stage(i, u, reuse):
            h = 2 * i + u
            half, pair = slice(u * DH, (u + 1) * DH), bass.ds(i, 1)
            flat = lambda ap: ap.rearrange("p a n -> p (a n)")
            if reuse:
                sp.wait_ge(t_done, EXPS * h - EXPS)
            for dst, src in ((q11[0:DH, u], qT[half, 0, pair]), (q11[DH:P, u], qT[half, 0, pair]), (q2[0:DH, u], qT[half, 1, pair]),
                             (k12[0:DH, u], kT[half, 0, pair]), (k12[DH:P, u], kT[half, 1, pair]), (k1[0:DH, u], kT[half, 0, pair])):
                sp.dma_start(dst, flat(src)).then_inc(qk_staged[u], 16)
            if reuse:
                sp.wait_ge(weighed, EXPS * h - EXPS + AHEAD)
            cols = bass.ds(i * P + u * DH, DH)
            sp.dma_start(vh[:, u, 0:TPB, 0:DH], v[:, 0:TPB, cols]).then_inc(v_staged[u], 16)
            sp.dma_start(vh[0:NCTX, u, TPB, 0:DH], v[0:NCTX, TPB, cols]).then_inc(v_staged[u], 16)

        for u in range(2):
            stage(0, u, False)
        with sp.Fori(1, HEAD_PAIRS) as i:
            for u in range(2):
                stage(i, u, True)

    @block.gpsimd
    def _(pool):
        step = chain(pool, filled)
        step(nc.gpsimd.memset(q2[DH:ROWS2], 0.0))
        step(nc.gpsimd.memset(k1[DH:ROWS2], 0.0))
        step(nc.gpsimd.memset(vh[:, :, :, DH:P], 1.0))
        step(nc.gpsimd.memset(top_rows[:], 0.0))
        step(nc.gpsimd.tensor_copy(ident[:], env.ident[:]))
        for row in TOP:
            step(nc.gpsimd.memset(k1[row:row + 1], 1.0))

    @block.tensor
    def _(pe):
        def score(h, i, u, n):
            if n == 0:
                pe.wait_ge(qk_staged[u], 96 * i + 96)
                pe.wait_ge(top_placed, h)
            pe.wait_ge(top_ready, through(h, n))
            rows = slice(n * P, (n + 1) * P)
            for g in range(3):
                cols = slice(g * 512, min((g + 1) * 512, KEYS))
                nc.tensor.matmul(scores(h, n)[:, cols], q11[:, u, rows], k12[:, u, cols], start=True, stop=False)
                last = nc.tensor.matmul(scores(h, n)[:, cols], q2[0:DH, u, rows], k1[0:DH, u, cols], start=False, stop=True)
            last.then_inc(scored, 1)

        def turn_top(h):
            pe.wait_ge(split_ready, h + 1)
            for n in range(QT):
                last = nc.tensor.matmul(s_ps[0:ROWS2, n * P:(n + 1) * P], top_rows[:, n, :], ident[:], start=True, stop=True)
            last.then_inc(top_turned, 1)

        def by_keys(h, u, j, begun):
            rows = P if j < TPB else NCTX
            keys = slice(j * P, j * P + rows)
            if j == 0:
                pe.wait_ge(top_placed, h + 1)
            for c in range(2):
                if begun:
                    pe.wait_ge(exped, EXPS * h + (2 * j + c - 1))
                cols = slice(c * 512, (c + 1) * 512)
                nc.tensor.matmul(t_ps[0:rows, c, :], k12[:, u, keys], q11[:, u, cols], start=True, stop=False)
                nc.tensor.matmul(t_ps[0:rows, c, :], k1[:, u, keys], q2[:, u, cols], start=False, stop=True).then_inc(t_done, 1)

        def weigh(h, i, u, j, c):
            rows = P if j < TPB else NCTX
            if j == 0:
                pe.wait_ge(v_staged[u], 32 * i + 32)
                pe.wait_ge(o_evac, 2 * h)
            pe.wait_ge(exped, EXPS * h + (2 * j + c + 1))
            nc.tensor.matmul(o_ps[:, c, :], vh[0:rows, u, j, :], pT[0:rows, (u * KT + j) % 2, c, :], start=j == 0,
                             stop=j == KT - 1).then_inc(weighed, 1)

        pe.sem_inc(weighed, AHEAD)
        pe.wait_ge(filled, 7)
        for n in range(QT):
            score(0, 0, 0, n)
        turn_top(0)
        by_keys(0, 0, 0, False)

        beside = {(1, 0): 0, (1, 2): 1, (2, 2): 2, (3, 1): 3, (4, 1): 4, (5, 0): 5, (6, 0): 6, (6, 2): 7}

        def body(i, last):
            for u in range(2):
                h = 2 * i + u
                more = not (last and u == 1)
                for j in range(KT):
                    for part in range(3):
                        if more and (j, part) in beside:
                            score(h + 1, i + u, 1 - u, beside[j, part])
                        if part == 0 and j < KT - 1:
                            by_keys(h, u, j + 1, True)
                        if part:
                            weigh(h, i, u, j, part - 1)
                        elif more and j == KT - 2:
                            turn_top(h + 1)
                    if j == KT - 1 and more:
                        by_keys(h + 1, 1 - u, 0, True)

        pairs(pe, body)

    @block.vector
    def _(dve):
        dve.wait_ge(filled, 7)

        def top(h, n):
            dve.wait_ge(scored, QT * h + (n + 1))
            ctx_keys = scores(h, n)[:, S:KEYS]
            nc.vector.tensor_tensor(ctx_keys, ctx_keys, p["hide"][:, b, :], ALU.add).then_inc(hidden, 1)
            dve.wait_ge(hidden, QT * h + (n + 1))
            if n == 0:
                dve.wait_ge(split_ready, h)
            nc.vector.tensor_reduce(ntop[:, n:n + 1], scores(h, n), AX_X, ALU.max, negate=True).then_inc(top_ready, 1)

        def split(h):
            hi, lo = (top_rows[:, :, r] for r in TOP)
            dve.wait_ge(top_ready, QT * h + QT)
            dve.wait_ge(top_turned, h)
            nc.vector.tensor_copy(hi, ntop[:]).then_inc(split_part, 1)
            dve.wait_ge(split_part, h + 1)
            nc.vector.tensor_tensor(lo, ntop[:], hi, ALU.subtract).then_inc(split_ready, 1)

        PIECES, WIDTH = 4, 256

        def keep(h, i, u, k):
            c, cols = k // 2, slice(k % 2 * WIDTH, (k % 2 + 1) * WIDTH)
            dve.wait_ge(o_evac, 2 * h + (c + 1))
            dve.wait_ge(kept, PIECES * h)
            nc.vector.reciprocal(inv[:, c, cols], o[DH:P, c, cols]).then_inc(inv_ready, 1)
            dve.wait_ge(inv_ready, PIECES * h + (k + 1))
            out = oT[u * DH:(u + 1) * DH, bass.ds(i, 1), k * WIDTH:(k + 1) * WIDTH].rearrange("p a n -> p (a n)")
            nc.vector.tensor_tensor(out, o[0:DH, c, cols], inv[:, c, cols], ALU.mult).then_inc(kept, 1)

        for n in range(QT):
            top(0, n)
        split(0)

        def body(i, first, last):
            for u in range(2):
                h, pieces = 2 * i + u, list(range(PIECES))
                for work in ("piece", 0, "piece", 1, 2, 3, 4, 5, 6, "piece", 7, "split", "piece"):
                    if work == "piece":
                        if not (first and u == 0):
                            keep(h - 1, i + (u - 1), 1 - u, pieces.pop(0))
                    elif not (last and u == 1):
                        if work == "split":
                            split(h + 1)
                        else:
                            top(h + 1, work)

        body(0, True, False)
        with dve.Fori(1, HEAD_PAIRS - 1) as i:
            body(i, False, False)
        body(HEAD_PAIRS - 1, False, True)
        for n in range(PIECES):
            keep(H - 1, HEAD_PAIRS - 1, 1, n)
        dve.wait_ge(kept, PIECES * H)

    @block.scalar
    def _(act):
        nc.scalar.activation(inv[:, 0, 0:1], env.eps[0:DH], ACT.Exp).then_inc(table_loaded, 1)
        act.wait_ge(table_loaded, 1)
        act.wait_ge(filled, 7)

        def place_top(h, u):
            act.wait_ge(top_turned, h + 1)
            nc.scalar.copy(q2[TOP[0]:ROWS2, u, :], s_ps[TOP[0]:ROWS2, 0:S]).then_inc(top_placed, 1)

        place_top(0, 0)

        def body(i, last):
            for u in range(2):
                h = 2 * i + u
                for j in range(KT):
                    rows = P if j < TPB else NCTX
                    if j == KT - 1 and not (last and u == 1):
                        place_top(h + 1, 1 - u)
                    for c in range(2):
                        t = EXPS * h + (2 * j + c + 1)
                        act.wait_ge(t_done, t)
                        act.wait_ge(weighed, t)
                        dst = pT[0:rows, (u * KT + j) % 2, c, :]
                        bias = p["hide_key"][0:rows, b:b + 1] if j == TPB else 0.0
                        nc.scalar.activation(dst, t_ps[0:rows, c, :], ACT.Exp, bias=bias, scale=p["gmax"][0:rows, 0:1]).then_inc(exped, 1)
                for c in range(2):
                    act.wait_ge(weighed, EXPS * h + (EXPS - 1 + c + AHEAD))
                    act.wait_ge(kept, 4 * h)
                    nc.scalar.copy(o[:, c, :], o_ps[:, c, :]).then_inc(o_evac, 1)

        pairs(act, body)


def latent_emit(nc, env, st, ctx, w, b, oT):
    wout, bout = st.sb("wout", [P, PAIRS, D]), st.sb("bout", [1, D])
    y_ps = st.ps("y_ps", [P, 4, 512])
    loaded, y_done, added = st.sem("loaded"), st.sem("y_done"), st.sem("added")
    block = ctx.enter_context(nc.Block())

    @block.sync
    def _(sp):
        sp.dma_start(wout[:], w("Wout").rearrange("(c p) n -> p c n", p=P)).then_inc(loaded, 16)
        sp.dma_start(bout[:], w("bout").rearrange("(a n) -> a n", a=1)).then_inc(loaded, 16)

    @block.tensor
    def _(pe):
        pe.wait_ge(loaded, 32)
        for n in range(TPB):
            if n >= 4:
                pe.wait_ge(added, n - 3)
            nc.tensor.matmul(y_ps[:, n % 4, 0:D], env.ones[0:1, :], bout[:], start=True, stop=False)
            for c in range(PAIRS):
                last = nc.tensor.matmul(y_ps[:, n % 4, 0:D], oT[:, c, n * P:(n + 1) * P], wout[:, c, :], start=False,
                                        stop=c == PAIRS - 1)
            last.then_inc(y_done, 1)

    @block.vector
    def _(dve):
        for n in range(TPB):
            t = b * TPB + n
            dve.wait_ge(y_done, n + 1)
            nc.vector.tensor_tensor(env.x[:, t, :], env.x[:, t, :], y_ps[:, n % 4, 0:D], ALU.add).then_inc(added, 1)



E = 8
F = 1024
FC = F // P
NT = T // P + E - 1


def routed_ffn_stage(nc, env, tag, args, name, func, biased, capacity):
    w = lambda n: args[f"{name}_{n}"]
    sorted_x = nc.dram_tensor(f"{tag}_sorted_x", [NT * P, D], F32).ap()
    sorted_y = nc.dram_tensor(f"{tag}_sorted_y", [NT * P, D], F32).ap()
    with ExitStack() as ctx:
        st = Stage(nc, ctx, tag)
        w1 = st.sb("w1", [P, E, DC, F])
        w2 = st.sb("w2", [P, E, FC, D])
        b1 = st.sb("b1", [P, E, FC]) if biased else None
        b2 = st.sb("b2", [P, E, D]) if biased else None
        slot = st.sb("slot", [P, TILES], U32)
        weight = st.sb("weight", [P, TILES])
        expert_of = st.sb("expert_of", [P, NT], I32)
        weights_loaded = st.sem("weights_loaded")
        with ExitStack() as inner:
            route_tokens(nc, env, Stage(nc, inner, tag + "r"), inner, tag, w, capacity, sorted_x, slot, weight, expert_of,
                  w1, w2, b1, b2, weights_loaded)
        with ExitStack() as inner:
            routed_experts(nc, env, Stage(nc, inner, tag + "e"), inner, func, sorted_x, sorted_y, expert_of, w1, w2, b1, b2,
                    weights_loaded)
        with ExitStack() as inner:
            combine_experts(nc, env, Stage(nc, inner, tag + "c"), inner, sorted_y, slot, weight)


def route_tokens(nc, env, st, ctx, tag, w, capacity, sorted_x, slot, weight, expert_of, w1, w2, b1, b2, weights_loaded):
    xn = st.sb("xn", [P, TILES, D])
    xnT = st.sb("xnT", [P, DC, T])
    gate = st.sb("gate", [P, DC, E])
    zero = st.sb("zero", [P, D])
    gate_loaded, zero_made, zero_stored = (st.sem(n) for n in ("gate_loaded", "zero_made", "zero_stored"))

    def zeros(pool):
        nc.gpsimd.memset(zero[:], 0.0).then_inc(zero_made, 1)

    def load(sp):
        sp.dma_start(gate[:], w("gate_w").rearrange("(c p) e -> p c e", p=P)).then_inc(gate_loaded, 16)
        sp.wait_ge(zero_made, 1)
        sp.dma_start(sorted_x.rearrange("(j p) d -> p j d", p=P),
                     zero[:].unsqueeze(1).to_broadcast([P, NT, D])).then_inc(zero_stored, 16)
        sp.dma_start(w1[:], w("w1").rearrange("e (c p) f -> p e c f", p=P)).then_inc(weights_loaded, 16)
        sp.dma_start(w2[:], w("w2").rearrange("e (c p) d -> p e c d", p=P)).then_inc(weights_loaded, 16)
        if b1 is not None:
            sp.dma_start(b1[:], w("b1").rearrange("e (c p) -> p e c", p=P), allow_slow_non_contiguous=True).then_inc(weights_loaded, 16)
            sp.dma_start(b2[:], w("b2").partition_broadcast(P)).then_inc(weights_loaded, 16)

    layernorm_stage(nc, env, tag + "l", env.x, dst_tok=xn, dst_T=xnT, ahead=load, ahead_pool=zeros)
    upto = st.sb("upto", [P, P])
    ids = st.sb("ids", [P, E])
    tile_ids = st.sb("tile_ids", [P, NT])
    lg, pr, hot, cand, place = (st.sb(n, [P, TILES, E]) for n in ("lg", "pr", "hot", "cand", "place"))
    off, count = st.sb("off", [P, TILES, E]), st.sb("count", [P, TILES, E])
    col = [st.sb(f"col{i}", [P, TILES]) for i in range(4)]
    per = [st.sb(f"per{i}", [P, E]) for i in range(5)]
    ends = st.sb("ends", [P, NT, E])
    tile_expert = st.sb("tile_expert", [P, NT])
    lg_ps, cum_ps, tot_ps = (st.ps(n, [P, 512]) for n in ("lg_ps", "cum_ps", "tot_ps"))
    upto_ones, consts = (st.sem(n) for n in ("upto_ones", "consts"))
    lg_done, shifted, exped, hot_ready, counted, linked, slot_ready = (
        st.sem(n) for n in ("lg_done", "shifted", "exped", "hot_ready", "counted", "linked", "slot_ready"))
    scattered, = env.scattered.pop()
    block = ctx.enter_context(nc.Block())
    te = lambda buf: buf[:, 0:TILES * E].rearrange("p (t e) -> p t e", e=E)
    over_e = lambda buf: buf[:].unsqueeze(2).to_broadcast([P, TILES, E])
    over_t = lambda buf: buf[:].unsqueeze(1).to_broadcast([P, TILES, E])

    @block.gpsimd
    def _(pool):
        nc.gpsimd.memset(upto[:], 1.0).then_inc(upto_ones, 1)
        nc.gpsimd.iota(ids[:], [[1, E]], base=0, channel_multiplier=0, allow_small_or_imprecise_dtypes=True).then_inc(consts, 1)
        nc.gpsimd.iota(tile_ids[:], [[1, NT]], base=0, channel_multiplier=0, allow_small_or_imprecise_dtypes=True).then_inc(consts, 1)
        pool.wait_ge(upto_ones, 1)
        nc.gpsimd.affine_select(out=upto[:], in_=upto[:], compare_op=ALU.is_ge, fill=0.0, base=0, pattern=[[1, P]],
                                channel_multiplier=-1).then_inc(consts, 1)
        pool.wait_ge(slot_ready, 1)
        pool.wait_ge(zero_stored, 16)
        for t in range(TILES):
            nc.gpsimd.indirect_dma_start(sorted_x, bass.IndirectOffsetOnAxis(ap=slot[:, t:t + 1], axis=0),
                                         xn[:, t, :], None).then_inc(scattered, 16)
        pool.wait_ge(scattered, 16 * TILES)

    @block.tensor
    def _(pe):
        pe.wait_ge(gate_loaded, 16)
        for t in range(TILES):
            for c in range(DC):
                last = nc.tensor.matmul(lg_ps[:, t * E:(t + 1) * E], xnT[:, c, t * P:(t + 1) * P], gate[:, c, :],
                                        start=c == 0, stop=c == DC - 1)
        last.then_inc(lg_done, 1)
        pe.wait_ge(hot_ready, 1)
        pe.wait_ge(consts, 3)
        hot2 = hot[:].rearrange("p t e -> p (t e)")
        nc.tensor.matmul(cum_ps[:, 0:TILES * E], upto[:], hot2, start=True, stop=True)
        nc.tensor.matmul(tot_ps[:, 0:TILES * E], env.ones[:], hot2, start=True, stop=True).then_inc(counted, 1)

    @block.scalar
    def _(act):
        act.wait_ge(shifted, 1)
        nc.scalar.activation(pr[:], lg[:], ACT.Exp).then_inc(exped, 1)

    @block.vector
    def _(dve):
        step = chain(dve, linked)
        tt = lambda o, a, b, op: step(nc.vector.tensor_tensor(o, a, b, op))
        ts = lambda o, a, s1, s2, op0, op1=None: step(
            nc.vector.tensor_scalar(o, a, s1, s2, op0) if op1 is None else nc.vector.tensor_scalar(o, a, s1, s2, op0, op1))
        dve.wait_ge(lg_done, 1)
        step(nc.vector.tensor_reduce(col[0][:], te(lg_ps), AX_X, ALU.max))
        nc.vector.tensor_tensor(lg[:], te(lg_ps), over_e(col[0]), ALU.subtract).then_inc(shifted, 1)
        dve.wait_ge(exped, 1)
        step(nc.vector.tensor_reduce(col[1][:], pr[:], AX_X, ALU.add))
        step(nc.vector.reciprocal(col[1][:], col[1][:]))
        tt(pr[:], pr[:], over_e(col[1]), ALU.mult)
        step(nc.vector.tensor_reduce(weight[:], pr[:], AX_X, ALU.max))
        tt(cand[:], pr[:], over_e(weight), ALU.is_lt)
        dve.wait_ge(consts, 3)
        step(nc.vector.scalar_tensor_tensor(cand[:], cand[:], float(E), over_t(ids), ALU.mult, ALU.add))
        step(nc.vector.tensor_reduce(col[2][:], cand[:], AX_X, ALU.min))
        nc.vector.tensor_tensor(hot[:], over_t(ids), over_e(col[2]), ALU.is_equal).then_inc(hot_ready, 1)
        dve.wait_ge(counted, 1)
        step(nc.vector.tensor_copy(count[:], te(tot_ps)))
        step(nc.vector.memset(off[:, 0, :], 0.0))
        for t in range(1, TILES):
            tt(off[:, t, :], off[:, t - 1, :], count[:, t - 1, :], ALU.add)
        tt(per[0][:], off[:, TILES - 1, :], count[:, TILES - 1, :], ALU.add)
        ts(per[1][:], per[0][:], 1.0 / P, (P - 1.0) / P - 0.5 + 0.5 / P, ALU.mult, ALU.add)
        ts(per[1][:], per[1][:], ROUND, -ROUND, ALU.add, ALU.add)
        step(nc.vector.tensor_copy(per[2][:, 0:1], per[1][:, 0:1]))
        for e in range(1, E):
            tt(per[2][:, e:e + 1], per[2][:, e - 1:e], per[1][:, e:e + 1], ALU.add)
        tt(per[3][:], per[2][:], per[1][:], ALU.subtract)
        ts(per[3][:], per[3][:], float(P), -1.0, ALU.mult, ALU.add)
        tt(place[:], off[:], te(cum_ps), ALU.add)
        tt(cand[:], place[:], over_t(per[3]), ALU.add)
        tt(cand[:], cand[:], hot[:], ALU.mult)
        step(nc.vector.tensor_reduce(col[3][:], cand[:], AX_X, ALU.add))
        nc.vector.tensor_copy(slot[:], col[3][:]).then_inc(slot_ready, 1)
        if capacity is not None:
            tt(place[:], place[:], hot[:], ALU.mult)
            step(nc.vector.tensor_reduce(col[0][:], place[:], AX_X, ALU.add))
            ts(col[0][:], col[0][:], float(capacity), None, ALU.is_le)
            tt(weight[:], weight[:], col[0][:], ALU.mult)
        tt(ends[:], per[2][:].unsqueeze(1).to_broadcast([P, NT, E]), tile_ids[:].unsqueeze(2).to_broadcast([P, NT, E]), ALU.is_le)
        step(nc.vector.tensor_reduce(tile_expert[:], ends[:], AX_X, ALU.add))
        ts(tile_expert[:], tile_expert[:], float(E - 1), None, ALU.min)
        step(nc.vector.tensor_copy(expert_of[:], tile_expert[:]))


def routed_experts(nc, env, st, ctx, func, sorted_x, sorted_y, expert_of, w1, w2, b1, b2, weights_loaded):
    xs, ys = st.sb("xs", [P, 2, D]), st.sb("ys", [P, 2, D])
    xT = st.sb("xT", [P, 2, DC, P])
    h = st.sb("h", [P, 2, F])
    hT = st.sb("hT", [P, FC, P])
    x_ps, y_ps = st.ps("x_ps", [P, 512]), st.ps("y_ps", [P, 512])
    h_ps = st.ps("h_ps", [P, 2, F])
    t_ps = st.ps("t_ps", [P, F])
    xs_loaded = [st.sem(f"xs_loaded{u}") for u in range(2)]
    ys_stored = env.stored.pop()
    x_turned, x_evac, h_done, h_evac, h_turned, hT_evac, y_done, y_evac = (
        st.sem(n) for n in ("x_turned", "x_evac", "h_done", "h_evac", "h_turned", "hT_evac", "y_done", "y_evac"))
    table_loaded = st.sem("table_loaded")
    HB = F // 512
    EV = FC if b1 is not None else HB
    block = ctx.enter_context(nc.Block())

    def of_buffer(j, u):
        return 8 * j + (16 - 8 * u)

    def pipeline(eng, front, back):
        front(0, 0)
        with eng.Fori(0, (NT - 1) // 2) as i:
            for v in range(2):
                front(2 * i + (1 + v), 1 - v)
                back(2 * i + v, v)
        back(NT - 1, (NT - 1) % 2)

    @block.sync
    def _(sp):
        def load(j, u):
            if not isinstance(j, int):
                sp.wait_ge(x_turned, j - 1)
            sp.dma_start(xs[:, u, :], sorted_x[bass.ds(j * P, P), :]).then_inc(xs_loaded[u], 16)

        load(0, 0)
        load(1, 1)
        with sp.Fori(1, (NT - 1) // 2) as i:
            for u in range(2):
                load(2 * i + u, u)
        sp.wait_ge(x_turned, NT - 2)
        load(NT - 1, (NT - 1) % 2)

    @block.gpsimd
    def _(pool):
        def store(j, u):
            pool.wait_ge(y_evac, j + 1)
            nc.gpsimd.dma_start(sorted_y[bass.ds(j * P, P), :], ys[:, u, :]).then_inc(ys_stored[u], 16)

        with pool.Fori(0, (NT - 1) // 2) as i:
            for u in range(2):
                store(2 * i + u, u)
        store(NT - 1, (NT - 1) % 2)
        pool.wait_ge(ys_stored[0], 16 * ((NT + 1) // 2))
        pool.wait_ge(ys_stored[1], 16 * (NT // 2))

    @block.tensor
    def _(pe):
        pe.wait_ge(weights_loaded, 32 if b1 is None else 64)

        def turn_x(j, u):
            pe.wait_ge(xs_loaded[u], of_buffer(j, u))
            if not isinstance(j, int):
                pe.wait_ge(x_evac, j)
            for c in range(DC):
                last = nc.tensor.transpose(x_ps[:, c * P:(c + 1) * P], xs[:, u, c * P:(c + 1) * P], env.ident[:])
            last.then_inc(x_turned, 1)

        def expand(j, u):
            e = pe.value_load(expert_of[0:1, bass.ds(j, 1)], min_val=0, max_val=E - 1)
            pe.wait_ge(x_evac, j + 1)
            for k in range(HB):
                for c in range(DC):
                    last = nc.tensor.matmul(h_ps[:, u, k * 512:(k + 1) * 512], xT[:, u, c, :],
                                            w1[:, bass.ds(e, 1), c, k * 512:(k + 1) * 512].rearrange("p a n -> p (a n)"),
                                            start=c == 0, stop=c == DC - 1)
            last.then_inc(h_done, 1)

        def turn_h(j, u, reuse):
            pe.wait_ge(h_evac, HB * (j + 1))
            if reuse:
                pe.wait_ge(hT_evac, EV * j)
            for f in range(FC):
                last = nc.tensor.transpose(t_ps[:, f * P:(f + 1) * P], h[:, u, f * P:(f + 1) * P], env.ident[:])
            last.then_inc(h_turned, 1)

        def reduce(j, u, reuse):
            e = pe.value_load(expert_of[0:1, bass.ds(j, 1)], min_val=0, max_val=E - 1)
            pe.wait_ge(hT_evac, EV * (j + 1))
            if reuse:
                pe.wait_ge(y_evac, j)
            for f in range(FC):
                last = nc.tensor.matmul(y_ps[:, 0:D], hT[:, f, :], w2[:, bass.ds(e, 1), f, :].rearrange("p a n -> p (a n)"),
                                        start=f == 0, stop=f == FC - 1)
            last.then_inc(y_done, 1)

        turn_x(0, 0)
        expand(0, 0)
        with pe.Fori(0, (NT - 1) // 2) as i:
            for v in range(2):
                j, u = 2 * i + v, v
                turn_x(j + 1, 1 - u)
                turn_h(j, u, True)
                expand(j + 1, 1 - u)
                reduce(j, u, True)
        turn_h(NT - 1, (NT - 1) % 2, True)
        reduce(NT - 1, (NT - 1) % 2, True)

    @block.scalar
    def _(act):
        def front(j, u):
            act.wait_ge(x_turned, j + 1)
            nc.scalar.copy(xT[:, u], x_ps[:, 0:D].rearrange("p (c t) -> p c t", c=DC)).then_inc(x_evac, 1)

        def back(j, u):
            e = act.value_load(expert_of[0:1, bass.ds(j, 1)], min_val=0, max_val=E - 1) if b1 is not None else None
            act.wait_ge(h_turned, j + 1)
            for k in range(EV):
                n = F // EV // P
                fs = slice(k * n, (k + 1) * n)
                bias = b1[:, bass.ds(e, 1), k] if b1 is not None else 0.0
                nc.scalar.activation(hT[:, fs, :], t_ps[:, k * n * P:(k + 1) * n * P].rearrange("p (f t) -> p f t", f=n),
                                     func, bias=bias).then_inc(hT_evac, 1)

        nc.scalar.activation(hT[:, 0, 0:1], env.eps[:], func).then_inc(table_loaded, 1)
        act.wait_ge(table_loaded, 1)
        pipeline(act, front, back)

    @block.vector
    def _(dve):
        def front(j, u):
            dve.wait_ge(h_done, j + 1)
            for k in range(HB):
                nc.vector.tensor_copy(h[:, u, k * 512:(k + 1) * 512], h_ps[:, u, k * 512:(k + 1) * 512]).then_inc(h_evac, 1)

        def back(j, u):
            e = dve.value_load(expert_of[0:1, bass.ds(j, 1)], min_val=0, max_val=E - 1) if b2 is not None else None
            dve.wait_ge(y_done, j + 1)
            if not isinstance(j, int):
                dve.wait_ge(ys_stored[u], of_buffer(j, u) - 16)
            elif j >= 2:
                dve.wait_ge(ys_stored[u], 16 * (j // 2))
            if b2 is None:
                nc.vector.tensor_copy(ys[:, u, :], y_ps[:, 0:D]).then_inc(y_evac, 1)
            else:
                nc.vector.tensor_tensor(ys[:, u, :], y_ps[:, 0:D], b2[:, bass.ds(e, 1), :].rearrange("p a n -> p (a n)"),
                                        ALU.add).then_inc(y_evac, 1)

        pipeline(dve, front, back)


def combine_experts(nc, env, st, ctx, sorted_y, slot, weight):
    yg = st.sb("yg", [P, TILES, D])
    gathered = env.gathered.pop()
    added = st.sem("added")
    block = ctx.enter_context(nc.Block())

    @block.gpsimd
    def _(pool):
        for t in range(TILES):
            nc.gpsimd.indirect_dma_start(yg[:, t, :], None, sorted_y, bass.IndirectOffsetOnAxis(ap=slot[:, t:t + 1], axis=0)
                                         ).then_inc(gathered[t], 16)

    @block.vector
    def _(dve):
        for t in range(TILES):
            dve.wait_ge(gathered[t], 16)
            nc.vector.scalar_tensor_tensor(env.x[:, t, :], yg[:, t, :], weight[:, t:t + 1], env.x[:, t, :], ALU.mult,
                                           ALU.add).then_inc(added, 1)
        dve.wait_ge(added, TILES)



WIDE = H * NCTX
BANK_HEADS = (range(0, 6), range(6, 12), range(12, 16))


def spread(ap, shape):
    return ap.to_broadcast(shape)


def cross_attention_stage(nc, env, tag, args, name, mask, side, hides):
    w = lambda n: args[f"{name}_{n}"]
    with ExitStack() as ctx:
        st = Stage(nc, ctx, tag)
        qT, kbd = st.sb("qT", [P, DC, T]), st.sb("kbd", [P, DC, B, H // DC * NCTX])
        v, neg = st.sb("v", [P, B, D]), st.sb("neg", [P, TILES, NCTX])
        with ExitStack() as inner:
            cross_operands(nc, env, Stage(nc, inner, tag + "p"), inner, w, mask, hides, qT, kbd, v, neg)
        out = st.sb("out", [P, TILES, D])
        with ExitStack() as inner:
            cross_attend(nc, env, Stage(nc, inner, tag + "a"), inner, side, qT, kbd, v, neg, out)
        add_projection_stage(nc, env, tag + "o", out, w("Wo"), w("bo"))


def cross_operands(nc, env, st, ctx, w, mask, hides, qT, kbd, v, neg):
    sb, ps, sem = st.sb, st.ps, st.sem
    half = H // DC
    xT = sb("xT", [P, DC, T])
    layernorm_stage(nc, env, st.tag + "l", env.x, dst_T=xT)
    wq, wk, wv = (sb(n, [P, DC, D]) for n in ("wq", "wk", "wv"))
    bq, bqs, bk, bv = sb("bq", [P, DC]), sb("bqs", [P, DC]), sb("bk", [P, DC]), sb("bv", [P, D])
    mask_in = sb("mask_in", [P, TILES, NCTX], mask.dtype)
    ind = sb("ind", [P, half])
    ctxT, kT = sb("ctxT", [P, DC, B * NCTX]), sb("kT", [P, DC, B * NCTX])
    q_ps, c_ps, k_ps, v_ps = ps("q_ps", [P, 4, 512]), ps("c_ps", [P, 512]), ps("k_ps", [P, 512]), ps("v_ps", [P, 512])
    kv_loaded, q_loaded, mask_loaded, ones_set, ind_lower, ind_made, bqs_ready, neg_ready = (
        sem(n) for n in ("kv_loaded", "q_loaded", "mask_loaded", "ones_set", "ind_lower", "ind_made", "bqs_ready", "neg_ready"))
    ctx_turned, ctx_evac, k_done, k_ready, kbd_ready, v_done, v_ready, q_done, q_evac = (
        sem(n) for n in ("ctx_turned", "ctx_evac", "k_done", "k_ready", "kbd_ready", "v_done", "v_ready", "q_done", "q_evac"))
    block = ctx.enter_context(nc.Block())
    jobs = [(f, n) for n in range(T // 512) for f in range(DC)]

    @block.sync
    def _(sp):
        mat = lambda n: w(n).rearrange("(c p) n -> p c n", p=P)
        col = lambda n: w(n).rearrange("(c p) -> p c", p=P)
        sp.dma_start(wk[:], mat("Wk")).then_inc(kv_loaded, 16)
        sp.dma_start(wv[:], mat("Wv")).then_inc(kv_loaded, 16)
        sp.dma_start(bk[:], col("bk"), allow_slow_non_contiguous=True).then_inc(kv_loaded, 16)
        sp.dma_start(bv[:], w("bv").partition_broadcast(P)).then_inc(kv_loaded, 16)
        sp.dma_start(wq[:], mat("Wq")).then_inc(q_loaded, 16)
        sp.dma_start(bq[:], col("bq"), allow_slow_non_contiguous=True).then_inc(q_loaded, 16)
        sp.dma_start(mask_in[:], mask.rearrange("b (t p) j -> p (b t) j", p=P)).then_inc(mask_loaded, 16)

    @block.gpsimd
    def _(pool):
        nc.gpsimd.memset(ind[:], 1.0).then_inc(ones_set, 1)
        pool.wait_ge(ones_set, 1)
        nc.gpsimd.affine_select(out=ind[:], in_=ind[:], compare_op=ALU.is_ge, fill=0.0, base=0,
                                pattern=[[-HD, half]], channel_multiplier=1).then_inc(ind_lower, 1)
        pool.wait_ge(ind_lower, 1)
        nc.gpsimd.affine_select(out=ind[:], in_=ind[:], compare_op=ALU.is_ge, fill=0.0, base=HD - 1,
                                pattern=[[HD, half]], channel_multiplier=-1).then_inc(ind_made, 1)

    @block.tensor
    def _(pe):
        for b in range(B):
            for c in range(DC):
                last = nc.tensor.transpose(c_ps[:, (c * B + b) * NCTX:(c * B + b + 1) * NCTX],
                                           env.ctx_tok[0:NCTX, b, c * P:(c + 1) * P], env.ident[0:NCTX, 0:NCTX])
        last.then_inc(ctx_turned, 1)
        pe.wait_ge(kv_loaded, 64)
        pe.wait_ge(ctx_evac, 1)
        for f in range(DC):
            for c in range(DC):
                last = nc.tensor.matmul(k_ps[:, f * B * NCTX:(f + 1) * B * NCTX], wk[:, c, f * P:(f + 1) * P],
                                        ctxT[:, c, :], start=c == 0, stop=c == DC - 1)
        last.then_inc(k_done, 1)
        for b in range(B):
            for c in range(DC):
                last = nc.tensor.matmul(v_ps[0:NCTX, b * D:(b + 1) * D], ctxT[:, c, b * NCTX:(b + 1) * NCTX], wv[:, c, :],
                                        start=c == 0, stop=c == DC - 1)
        last.then_inc(v_done, 1)
        pe.wait_ge(q_loaded, 32)
        for i, (f, n) in enumerate(jobs):
            if i >= 4:
                pe.wait_ge(q_evac, i - 3)
            for c in range(DC):
                last = nc.tensor.matmul(q_ps[:, i % 4, :], wq[:, c, f * P:(f + 1) * P], xT[:, c, n * 512:(n + 1) * 512],
                                        start=c == 0, stop=c == DC - 1)
            last.then_inc(q_done, 1)

    @block.scalar
    def _(act):
        act.wait_ge(ctx_turned, 1)
        nc.scalar.copy(ctxT[:].rearrange("p c t -> p (c t)"), c_ps[:, 0:DC * B * NCTX]).then_inc(ctx_evac, 1)
        act.wait_ge(bqs_ready, 1)
        for i, (f, n) in enumerate(jobs):
            act.wait_ge(q_done, i + 1)
            nc.scalar.activation(qT[:, f, n * 512:(n + 1) * 512], q_ps[:, i % 4, :], ACT.Identity, bias=bqs[:, f:f + 1],
                                 scale=HD ** -0.5).then_inc(q_evac, 1)

    @block.vector
    def _(dve):
        dve.wait_ge(q_loaded, 32)
        nc.vector.tensor_scalar(bqs[:], bq[:], HD ** -0.5, None, ALU.mult).then_inc(bqs_ready, 1)
        dve.wait_ge(mask_loaded, 16)
        if hides:
            nc.vector.tensor_scalar(neg[:], mask_in[:], -1e15, None, ALU.mult).then_inc(neg_ready, 1)
        else:
            nc.vector.tensor_scalar(neg[:], mask_in[:], 0.0, NEG, ALU.is_equal, ALU.mult).then_inc(neg_ready, 1)
        dve.wait_ge(kv_loaded, 64)
        dve.wait_ge(ind_made, 1)
        dve.wait_ge(k_done, 1)
        for c in range(DC):
            nc.vector.tensor_scalar(kT[:, c, :], k_ps[:, c * B * NCTX:(c + 1) * B * NCTX], bk[:, c:c + 1], None,
                                    ALU.add).then_inc(k_ready, 1)
        dve.wait_ge(k_ready, DC)
        for c in range(DC):
            for b in range(B):
                nc.vector.tensor_tensor(kbd[:, c, b, :].rearrange("p (h j) -> p h j", h=half),
                                        spread(kT[:, c:c + 1, b * NCTX:(b + 1) * NCTX], [P, half, NCTX]),
                                        spread(ind[:, :].unsqueeze(2), [P, half, NCTX]), ALU.mult).then_inc(kbd_ready, 1)
        dve.wait_ge(v_done, 1)
        for b in range(B):
            nc.vector.tensor_tensor(v[0:NCTX, b, :], v_ps[0:NCTX, b * D:(b + 1) * D], bv[0:NCTX, :], ALU.add).then_inc(v_ready, 1)


def cross_attend(nc, env, st, ctx, side, qT, kbd, v, neg, out):
    sb, ps, sem = st.sb, st.ps, st.sem
    half = H // DC
    q = sb("q", [P, 2, DC, P])
    bias = sb("bias", [P, 2, WIDE]) if side is not None else None
    z = sb("z", [P, 2, WIDE])
    top, total, inv = (sb(n, [P, 2, H]) for n in ("top", "total", "inv"))
    pT = sb("pT", [P, 2, H * P])
    s_ps, pt_ps, o_ps = ps("s_ps", [P, 3, 512]), ps("pt_ps", [P, 2, 512]), ps("o_ps", [P, 2, 512])
    side_loaded = [sem(f"side_loaded{u}") for u in range(2)]
    q_placed = [sem(f"q_placed{u}") for u in range(2)]
    scored, biased, z_part, z_added, top_ready, shifted, exped = (
        sem(n) for n in ("scored", "biased", "z_part", "z_added", "top_ready", "shifted", "exped"))
    summed, inv_ready, p_turned, p_evac, weighed, normed, table_loaded = (
        sem(n) for n in ("summed", "inv_ready", "p_turned", "p_evac", "weighed", "normed", "table_loaded"))
    block = ctx.enter_context(nc.Block())
    by_head = lambda ap, n=H: ap.rearrange("p (h j) -> p h j", h=n)
    AHEAD = 2

    def tiles(eng, front, back):
        for b in range(B):
            g0 = b * TPB
            front(b, g0, 0)
            if b:
                back(b - 1, g0 - 1, 1)
            front(b, g0 + 1, 1)
            back(b, g0, 0)
            with eng.Fori(g0 // 2 + 1, g0 // 2 + TPB // 2) as i:
                for u in range(2):
                    front(b, 2 * i + u, u)
                    back(b, 2 * i + u - 1, 1 - u)
        back(B - 1, TILES - 1, 1)

    def of_buffer(g, u):
        return 8 * g + (16 - 8 * u)

    @block.sync
    def _(sp):
        def load(b, g, u):
            if not (isinstance(g, int) and g < 2):
                sp.wait_ge(scored, g - 1)
            sp.dma_start(q[:, u], qT[:, :, bass.ds(g * P, P)]).then_inc(q_placed[u], 16)
            if side is not None:
                sp.wait_ge(z_added, g + 1)
                rows = bass.ds((g - b * TPB) * P, P)
                sp.dma_start(by_head(bias[:, u, :]), side[b, :, rows, :].rearrange("h p j -> p h j")).then_inc(side_loaded[u], 16)

        tiles(sp, load, lambda *a: None)

    @block.gpsimd
    def _(pool):
        def hide(g, u):
            bt = by_head(bias[:, u, :])
            pool.wait_ge(side_loaded[u], of_buffer(g, u))
            nc.gpsimd.tensor_tensor(bt, bt, spread(neg[:, bass.ds(g, 1), :], [P, H, NCTX]), ALU.add).then_inc(biased, 1)

        def shift(g, u):
            zt = by_head(z[:, u, :])
            pool.wait_ge(top_ready, g + 1)
            nc.gpsimd.tensor_tensor(zt, zt, spread(top[:, u, :].unsqueeze(2), [P, H, NCTX]), ALU.subtract).then_inc(shifted, 1)

        if side is not None:
            hide(0, 0)
        with pool.Fori(0, TILES // 2 - 1) as i:
            for u in range(2):
                if side is not None:
                    hide(2 * i + (u + 1), 1 - u)
                shift(2 * i + u, u)
        if side is not None:
            hide(TILES - 1, 1)
        for u in range(2):
            shift(TILES - 2 + u, u)

    @block.tensor
    def _(pe):
        def score(b, g, u):
            pe.wait_ge(q_placed[u], of_buffer(g, u))
            pe.wait_ge(z_added, g + AHEAD)
            for k, heads in enumerate(BANK_HEADS):
                for c in range(DC):
                    mine = [h for h in heads if h // half == c]
                    if mine:
                        at = (mine[0] - heads[0]) * NCTX
                        last = nc.tensor.matmul(s_ps[:, k, at:at + len(mine) * NCTX], q[:, u, c, :],
                                                kbd[:, c, b, (mine[0] % half) * NCTX:(mine[-1] % half + 1) * NCTX],
                                                start=True, stop=True)
            last.then_inc(scored, 1)

        def weigh(b, g, u):
            pe.wait_ge(exped, g + 1)
            pe.wait_ge(normed, g + 1)

            def product(h):
                last = nc.tensor.matmul(o_ps[:, u, h * HD:(h + 1) * HD], pT[0:NCTX, u, h * P:(h + 1) * P],
                                        v[0:NCTX, b, h * HD:(h + 1) * HD], start=True, stop=True)
                if h == H - 1:
                    last.then_inc(weighed, 1)

            for k in range(6):
                pe.wait_ge(p_evac, 4 * g + k)
                for r in range(4):
                    if k < 4:
                        last = nc.tensor.transpose(pt_ps[0:NCTX, k % 2, r * P:(r + 1) * P],
                                                   z[:, u, (4 * k + r) * NCTX:(4 * k + r + 1) * NCTX], env.ident[:])
                        if r == 3:
                            last.then_inc(p_turned, 1)
                    if k >= 2:
                        product(4 * (k - 2) + r)

        pe.sem_inc(p_turned, 4 * AHEAD)
        tiles(pe, score, weigh)

    @block.vector
    def _(dve):
        def attend(b, g, u):
            dve.wait_ge(scored, g + 1)
            dve.wait_ge(p_turned, 4 * g + 4)
            if side is not None:
                dve.wait_ge(biased, g + 1)
            for k, heads in enumerate(BANK_HEADS):
                n, cols = len(heads), slice(heads[0] * NCTX, (heads[-1] + 1) * NCTX)
                add = by_head(bias[:, u, cols], n) if side is not None else spread(neg[:, bass.ds(g, 1), :], [P, n, NCTX])
                nc.vector.tensor_tensor(by_head(z[:, u, cols], n), by_head(s_ps[:, k, 0:n * NCTX], n), add,
                                        ALU.add).then_inc(z_added if k == 2 else z_part, 1)
            dve.wait_ge(z_part, 2 * g + 2)
            dve.wait_ge(z_added, g + 1 + AHEAD)
            nc.vector.tensor_reduce(top[:, u, :], by_head(z[:, u, :]), AX_X, ALU.max).then_inc(top_ready, 1)

        def normalise(b, g, u):
            dve.wait_ge(exped, g + 1)
            nc.vector.tensor_reduce(total[:, u, :], by_head(z[:, u, :]), AX_X, ALU.add).then_inc(summed, 1)
            dve.wait_ge(summed, g + 1)
            dve.wait_ge(normed, g + 1)
            nc.vector.reciprocal(inv[:, u, :], total[:, u, :]).then_inc(inv_ready, 1)
            dve.wait_ge(inv_ready, g + 1)
            dve.wait_ge(weighed, g + 1)
            nc.vector.tensor_tensor(by_head(tile_of(out, g)), by_head(o_ps[:, u, 0:D]),
                                    spread(inv[:, u, :].unsqueeze(2), [P, H, HD]), ALU.mult).then_inc(normed, 1)

        dve.sem_inc(z_added, AHEAD)
        dve.sem_inc(normed, AHEAD)
        tiles(dve, attend, normalise)
        dve.wait_ge(normed, TILES + AHEAD)

    @block.scalar
    def _(act):
        nc.scalar.activation(total[:, 0, :], env.ones[:, 0:H], ACT.Exp).then_inc(table_loaded, 1)
        act.wait_ge(table_loaded, 1)

        def soften(g, u):
            act.wait_ge(shifted, g + 1)
            nc.scalar.activation(z[:, u, :], z[:, u, :], ACT.Exp).then_inc(exped, 1)

        def evacuate(b, g, u):
            if not (isinstance(g, int) and g == 0):
                act.wait_ge(weighed, g - 1)
            for k in range(4):
                act.wait_ge(p_turned, 4 * g + (k + 1 + 4 * AHEAD))
                nc.scalar.copy(pT[0:NCTX, u, k * 512:(k + 1) * 512], pt_ps[0:NCTX, k % 2, :]).then_inc(p_evac, 1)
            if not (isinstance(g, int) and g == TILES - 1):
                soften(g + 1, 1 - u)

        act.sem_inc(p_evac, 1)
        soften(0, 0)
        tiles(act, lambda *a: None, evacuate)



TOP_P = 0.8
HALF_TOP = 2.0 ** 14
TINY = 1e-30
XN_SCALE = HALF_TOP / D ** 0.5


def gated_ffn_stage(nc, env, tag, args, name):
    w = lambda n: args[f"{name}_{n}"]
    with ExitStack() as ctx:
        st = Stage(nc, ctx, tag)
        xnT = st.sb("xnT", [P, DC, T])
        gate = st.sb("gate", [P, TILES, E])
        raw1, raw2, b1 = st.sb("raw1", [P, DC, F]), st.sb("raw2", [P, FC, D]), st.sb("b1", [P, FC])
        raw_loaded = st.sem("raw_loaded")

        def load_raw(sp, e):
            sp.dma_start(raw1[:], w("W1")[bass.ds(e, 1)].rearrange("a (c p) f -> p (a c) f", p=P)).then_inc(raw_loaded, 16)
            sp.dma_start(raw2[:], w("W2")[bass.ds(e, 1)].rearrange("a (c p) d -> p (a c) d", p=P)).then_inc(raw_loaded, 16)
            sp.dma_start(b1[:], w("b1")[bass.ds(e, 1)].rearrange("a (c p) -> p (a c)", p=P),
                         allow_slow_non_contiguous=True).then_inc(raw_loaded, 16)

        layernorm_stage(nc, env, tag + "l", env.x, dst_T=xnT)
        with ExitStack() as inner:
            token_gates(nc, env, Stage(nc, inner, tag + "g"), inner, w, xnT, gate, load_raw)
        with ExitStack() as inner:
            gated_experts(nc, env, Stage(nc, inner, tag + "e"), inner, xnT, gate, load_raw, raw_loaded, raw1, raw2, b1)


def token_gates(nc, env, st, ctx, w, xnT, gate, load_raw):
    wr, br = st.sb("wr", [P, DC, E]), st.sb("br", [P, E])
    b2 = st.sb("b2", [E, D])
    lower = st.sb("lower", [P, E, E])
    lg, pr, cum, rank = (st.sb(n, [P, TILES, E]) for n in ("lg", "pr", "cum", "rank"))
    above, same = st.sb("above", [P, TILES, E, E]), st.sb("same", [P, TILES, E, E])
    col = st.sb("col", [P, TILES])
    gT = st.sb("gT", [E, T])
    lg_ps, g_ps, y_ps = st.ps("lg_ps", [P, 512]), st.ps("g_ps", [P, 4, 512]), st.ps("y_ps", [P, 2, 512])
    loaded, ones_set, lower_made, lg_done, shifted, exped, linked, gate_ready, g_turned, gT_ready, y_done, added = (
        st.sem(n) for n in ("loaded", "ones_set", "lower_made", "lg_done", "shifted", "exped", "linked", "gate_ready",
                            "g_turned", "gT_ready", "y_done", "added"))
    block = ctx.enter_context(nc.Block())
    over_e = lambda buf: buf[:].unsqueeze(2).to_broadcast([P, TILES, E])
    mine = lambda buf: buf[:].unsqueeze(3).to_broadcast([P, TILES, E, E])
    others = lambda buf: buf[:].unsqueeze(2).to_broadcast([P, TILES, E, E])

    @block.sync
    def _(sp):
        sp.dma_start(wr[:], w("Wr").rearrange("(c p) e -> p c e", p=P)).then_inc(loaded, 16)
        sp.dma_start(br[:], w("br").partition_broadcast(P)).then_inc(loaded, 16)
        sp.dma_start(b2[:], w("b2")).then_inc(loaded, 16)
        load_raw(sp, 0)

    @block.gpsimd
    def _(pool):
        nc.gpsimd.memset(lower[:], 1.0).then_inc(ones_set, 1)
        pool.wait_ge(ones_set, 1)
        nc.gpsimd.affine_select(out=lower[:], in_=lower[:], compare_op=ALU.is_ge, fill=0.0, base=0,
                                pattern=[[1, E], [-1, E]], channel_multiplier=0).then_inc(lower_made, 1)

    @block.tensor
    def _(pe):
        pe.wait_ge(loaded, 48)
        for t in range(TILES):
            for c in range(DC):
                last = nc.tensor.matmul(lg_ps[:, t * E:(t + 1) * E], xnT[:, c, t * P:(t + 1) * P], wr[:, c, :],
                                        start=c == 0, stop=c == DC - 1)
        last.then_inc(lg_done, 1)
        pe.wait_ge(gate_ready, 1)
        for t in range(TILES):
            last = nc.tensor.transpose(g_ps[0:E, t // 4, (t % 4) * P:(t % 4 + 1) * P], gate[:, t, :], env.ident[:])
        last.then_inc(g_turned, 1)
        pe.wait_ge(gT_ready, 4)
        for t in range(TILES):
            if t >= 2:
                pe.wait_ge(added, t - 1)
            nc.tensor.matmul(y_ps[:, t % 2, 0:D], gT[:, t * P:(t + 1) * P], b2[:], start=True, stop=True).then_inc(y_done, 1)

    @block.scalar
    def _(act):
        act.wait_ge(shifted, 1)
        nc.scalar.activation(pr[:], lg[:], ACT.Exp).then_inc(exped, 1)
        act.wait_ge(g_turned, 1)
        for k in range(4):
            nc.scalar.copy(gT[:, k * 512:(k + 1) * 512], g_ps[0:E, k, :]).then_inc(gT_ready, 1)

    @block.vector
    def _(dve):
        step = chain(dve, linked)
        tt = lambda o, a, b, op: step(nc.vector.tensor_tensor(o, a, b, op))
        dve.wait_ge(lg_done, 1)
        dve.wait_ge(loaded, 48)
        tt(lg[:], lg_ps[:, 0:TILES * E].rearrange("p (t e) -> p t e", e=E), br[:].unsqueeze(1).to_broadcast([P, TILES, E]), ALU.add)
        step(nc.vector.tensor_reduce(col[:], lg[:], AX_X, ALU.max))
        nc.vector.tensor_tensor(lg[:], lg[:], over_e(col), ALU.subtract).then_inc(shifted, 1)
        dve.wait_ge(exped, 1)
        step(nc.vector.tensor_reduce(col[:], pr[:], AX_X, ALU.add))
        step(nc.vector.reciprocal(col[:], col[:]))
        tt(pr[:], pr[:], over_e(col), ALU.mult)
        dve.wait_ge(lower_made, 1)
        tt(above[:], others(pr), mine(pr), ALU.is_gt)
        tt(same[:], others(pr), mine(pr), ALU.is_equal)
        tt(same[:], same[:], lower[:].unsqueeze(1).to_broadcast([P, TILES, E, E]), ALU.mult)
        tt(above[:], above[:], same[:], ALU.add)
        step(nc.vector.tensor_reduce(rank[:], above[:], AX_X, ALU.add))
        tt(above[:], above[:], others(pr), ALU.mult)
        step(nc.vector.tensor_reduce(cum[:], above[:], AX_X, ALU.add))
        step(nc.vector.tensor_scalar(cum[:], cum[:], TOP_P, None, ALU.is_lt))
        step(nc.vector.scalar_tensor_tensor(cum[:], rank[:], 1.0, cum[:], ALU.is_le, ALU.max))
        nc.vector.tensor_tensor(gate[:], pr[:], cum[:], ALU.mult).then_inc(gate_ready, 1)
        for t in range(TILES):
            dve.wait_ge(y_done, t + 1)
            nc.vector.tensor_tensor(env.x[:, t, :], env.x[:, t, :], y_ps[:, t % 2, 0:D], ALU.add).then_inc(added, 1)


def gated_experts(nc, env, st, ctx, xnT, gate, load_raw, raw_loaded, raw1, raw2, b1):
    CHUNK = 512
    CHUNKS = T // CHUNK
    CT = CHUNK // P
    STEPS = 2 * CHUNKS
    FQ = FC // CT
    RING = 4
    SIZES = 8
    x16 = st.sb("x16", [P, 2, DC, T], F16)
    w1, w2 = st.sb("w1", [P, 2, 2, DC, F], F16), st.sb("w2", [P, 2, 2, FC, D], F16)
    hT = st.sb("hT", [P, 2, 2, FC, CHUNK], F16)
    h32 = st.sb("h32", [P, RING, CHUNK])
    top, amax, inv = (st.sb(n, [P, 3]) for n in ("top", "amax", "inv"))
    down = st.sb("down", [P, 2, 3])
    h_scale, y_scale = st.sb("h_scale", [P, 2]), st.sb("y_scale", [P, 2])
    h_bias, y_gate = st.sb("h_bias", [P, 2, FC]), st.sb("y_gate", [P, 2, TILES])
    h_ps, y_ps = st.ps("h_ps", [P, RING, 512]), st.ps("y_ps", [P, CT, 512])
    x_halved, x_split, topped, reduced, sized, w_halved, w_split = (
        st.sem(n) for n in ("x_halved", "x_split", "topped", "reduced", "sized", "w_halved", "w_split"))
    h_done, h_halved, h_split, y_done, y_added, table_loaded = (
        st.sem(n) for n in ("h_done", "h_halved", "h_split", "y_done", "y_added", "table_loaded"))
    block = ctx.enter_context(nc.Block())
    raws = (raw1[:].rearrange("p c f -> p (c f)"), raw2[:].rearrange("p f d -> p (f d)"))
    halves = lambda k, v, part: (w1[:, v, part].rearrange("p c f -> p (c f)"), w2[:, v, part].rearrange("p f d -> p (f d)"))[k]
    PAIRS_OF_HALVES = ((0, 0), (0, 1), (1, 0))

    def pairs(eng, body):
        with eng.Fori(0, E // 2 - 1) as i:
            body(i, False)
        body(E // 2 - 1, True)

    def after(i, k):
        return (k + 1) // CHUNKS % 2, (k + 1) % CHUNKS, STEPS * i + (k + 1)

    @block.sync
    def _(sp):
        def pair(i, last):
            for v in range(1 if last else 2):
                sp.wait_ge(w_split, 2 * (2 * i + (v + 1)))
                load_raw(sp, 2 * i + (v + 1))

        pairs(sp, pair)

    @block.gpsimd
    def _(pool):
        for e in range(E):
            pool.wait_ge(topped, 3 * e + 3)
            if e:
                pool.wait_ge(sized, SIZES * e)
            nc.gpsimd.partition_all_reduce(amax[:], top[:], P, RMAX).then_inc(reduced, 1)

    @block.tensor
    def _(pe):
        pe.sem_inc(y_done, CT)

        def hidden(v, n, s, f):
            if isinstance(s, int) and s < 1 and f < RING:
                pass
            else:
                pe.wait_ge(h_halved, FC * s + (f + 1 - RING))
            for c in range(DC):
                for k, (a, b) in enumerate(PAIRS_OF_HALVES):
                    last = nc.tensor.matmul(h_ps[:, f % RING, :], w1[:, v, a, c, f * P:(f + 1) * P],
                                            x16[:, b, c, n * CHUNK:(n + 1) * CHUNK], start=c == 0 and k == 0,
                                            stop=c == DC - 1 and k == 2)
            last.then_inc(h_done, 1)

        def reduce(i, k, q):
            v, s = k // CHUNKS, STEPS * i + k
            if q == 0:
                pe.wait_ge(h_split, FC * s + (FC + RING))
            pe.wait_ge(y_added, CT * s + (q + 1))
            for f in range(FC):
                for m, (a, b) in enumerate(PAIRS_OF_HALVES):
                    last = nc.tensor.matmul(y_ps[:, q, 0:D], hT[:, k % 2, a, f, q * P:(q + 1) * P], w2[:, v, b, f, :],
                                            start=f == 0 and m == 0, stop=f == FC - 1 and m == 2)
            last.then_inc(y_done, 1)

        def pair(i, last):
            for k in range(STEPS):
                v, n, s = after(i, k)
                follows = not last or k + 1 < STEPS
                if follows and n == 0:
                    pe.wait_ge(w_split, 2 * (2 * i + (k // CHUNKS + 2)))
                for q in range(CT):
                    if follows:
                        for f in range(FQ * q, FQ * q + FQ):
                            hidden(v, n, s, f)
                    reduce(i, k, q)

        pe.wait_ge(w_split, 2)
        pe.wait_ge(x_split, CHUNKS)
        for f in range(FC):
            hidden(0, 0, 0, f)
        pairs(pe, pair)

    @block.scalar
    def _(act):
        nc.scalar.activation(h32[:, 0, 0:1], env.eps[:], ACT.Relu).then_inc(table_loaded, 1)
        act.wait_ge(table_loaded, 1)
        for n in range(CHUNKS):
            cols = slice(n * CHUNK, (n + 1) * CHUNK)
            nc.scalar.activation(x16[:, 0, :, cols], xnT[:, :, cols], ACT.Identity, scale=XN_SCALE).then_inc(x_halved, 1)

        def halve_weights(e, v, k):
            if k == 0:
                act.wait_ge(sized, SIZES * e + SIZES)
            nc.scalar.activation(halves(k, v, 0), raws[k], ACT.Identity, scale=down[:, v, k:k + 1]).then_inc(w_halved, 1)

        def evacuate(kb, v, s, f):
            if f == 0:
                act.wait_ge(y_done, CT * s)
            act.wait_ge(h_done, FC * s + (f + 1))
            act.wait_ge(h_split, FC * s + (f + 1))
            for out in (h32[:, f % RING, :], hT[:, kb, 0, f, :]):
                made = nc.scalar.activation(out, h_ps[:, f % RING, :], ACT.Relu, bias=h_bias[:, v, f:f + 1],
                                            scale=h_scale[:, v:v + 1])
            made.then_inc(h_halved, 1)

        def pair(i, last):
            for k in range(STEPS):
                v, n, s = after(i, k)
                more = not last or k < CHUNKS
                for q in range(CT):
                    if not last or k + 1 < STEPS:
                        for f in range(FQ * q, FQ * q + FQ):
                            evacuate((k + 1) % 2, v, s, f)
                    if more and k % CHUNKS == 1 and q in (1, 2):
                        halve_weights(2 * i + (k // CHUNKS + 1), 1 - k // CHUNKS, q - 1)

        for k in range(2):
            halve_weights(0, 0, k)
        for f in range(FC):
            evacuate(0, 0, 0, f)
        pairs(act, pair)

    @block.vector
    def _(dve):
        dve.sem_inc(y_added, CT)
        dve.sem_inc(h_split, RING)

        def largest(e, k):
            if k == 0:
                dve.wait_ge(raw_loaded, 48 * e + 48)
                if not isinstance(e, int) or e:
                    dve.wait_ge(reduced, e)
            nc.vector.tensor_reduce(top[:, k:k + 1], (*raws, b1[:])[k], AX_X, ALU.max, apply_absolute_value=True).then_inc(topped, 1)

        def sizes(e, v):
            step = chain(dve, sized, SIZES * e)
            col = lambda buf, k: buf[:, k:k + 1]
            dve.wait_ge(reduced, e + 1)
            step(nc.vector.tensor_scalar(amax[:], amax[:], TINY, None, ALU.max))
            step(nc.vector.scalar_tensor_tensor(col(amax, 2), col(amax, 0), float(D), col(amax, 2), ALU.mult, ALU.add))
            step(nc.vector.reciprocal(inv[:], amax[:]))
            step(nc.vector.tensor_scalar(down[:, v], inv[:], HALF_TOP, None, ALU.mult))
            step(nc.vector.scalar_tensor_tensor(col(h_scale, v), col(amax, 0), 1.0 / (XN_SCALE * HALF_TOP), down[:, v, 2:3],
                                                ALU.mult, ALU.mult))
            step(nc.vector.scalar_tensor_tensor(col(y_scale, v), col(amax, 1), HALF_TOP ** -2, col(amax, 2), ALU.mult, ALU.mult))
            step(nc.vector.tensor_scalar(h_bias[:, v], b1[:], down[:, v, 2:3], None, ALU.mult))
            step(nc.vector.tensor_scalar(y_gate[:, v], gate[:, :, bass.ds(e, 1)].rearrange("p t e -> p (t e)"), col(y_scale, v),
                                         None, ALU.mult))

        def split_weights(e, v, k):
            dve.wait_ge(w_halved, 2 * e + (k + 1))
            nc.vector.scalar_tensor_tensor(halves(k, v, 1), raws[k], down[:, v, k:k + 1], halves(k, v, 0), ALU.mult,
                                           ALU.subtract).then_inc(w_split, 1)

        def split_hidden(kb, s, f):
            dve.wait_ge(h_halved, FC * s + (f + 1))
            nc.vector.tensor_tensor(hT[:, kb, 1, f, :], h32[:, f % RING, :], hT[:, kb, 0, f, :], ALU.subtract).then_inc(h_split, 1)

        def add(i, k, q):
            v, n, s = k // CHUNKS, k % CHUNKS, STEPS * i + k
            xt = env.x[:, n * CT + q, :]
            dve.wait_ge(y_done, CT * s + (q + 1 + CT))
            if q == 0:
                dve.wait_ge(y_added, CT * s + CT)
            nc.vector.scalar_tensor_tensor(xt, y_ps[:, q, 0:D], y_gate[:, v, n * CT + q:n * CT + q + 1], xt, ALU.mult,
                                           ALU.add).then_inc(y_added, 1)

        def pair(i, last):
            for k in range(STEPS):
                v, n, s = after(i, k)
                more = not last or k < CHUNKS
                e, ev = 2 * i + (k // CHUNKS + 1), 1 - k // CHUNKS
                for q in range(CT):
                    if not last or k + 1 < STEPS:
                        for f in range(FQ * q, FQ * q + FQ):
                            split_hidden((k + 1) % 2, s, f)
                    add(i, k, q)
                    if more and k % CHUNKS == 0 and q > 0:
                        largest(e, q - 1)
                    if more and k % CHUNKS == 1 and q == 0:
                        sizes(e, ev)
                    if more and k % CHUNKS == 2 and q < 2:
                        split_weights(e, ev, q)

        for k in range(3):
            largest(0, k)
        for n in range(CHUNKS):
            cols = slice(n * CHUNK, (n + 1) * CHUNK)
            dve.wait_ge(x_halved, n + 1)
            nc.vector.scalar_tensor_tensor(x16[:, 1, :, cols], xnT[:, :, cols], XN_SCALE, x16[:, 0, :, cols], ALU.mult,
                                           ALU.subtract).then_inc(x_split, 1)
        sizes(0, 0)
        for k in range(2):
            split_weights(0, 0, k)
        for f in range(FC):
            split_hidden(0, 0, f)
        pairs(dve, pair)




def build(nc, args, out):
    kern_dram = nc.dram_tensor("conv_kernels", [B, KW], F32).ap()
    rows = lambda m: m.rearrange("b o s j -> b (o s) j")
    with ExitStack() as ctx:
        env = Env(nc, ctx)
        setup_stage(nc, env, args)
        conv_kernels_stage(nc, env, "hs", args, "L0_xattn", kern_dram)
        conv_attention_stage(nc, env, "c0", args, "L0_xattn", kern_dram, args["mask_SxS_bc0"])
        quant_ffn_stage(nc, env, "qf", args, "L0_ffn")
        latent_attention_stage(nc, env, "lt", args, "L1_xattn")
        routed_ffn_stage(nc, env, "m1", args, "L1_ffn", ACT.Relu, False, 320)
        cross_attention_stage(nc, env, "c2", args, "L2_xattn", rows(args["mask_Bx1xSxS2_bk1"]), None, 1)
        gated_ffn_stage(nc, env, "m2", args, "L2_ffn")
        cross_attention_stage(nc, env, "c3", args, "L3_xattn", rows(args["mask_Bx1xSxS2_ik1"]), args["fside_Bx16xSxS2_0"], 0)
        routed_ffn_stage(nc, env, "m3", args, "L3_ffn", ACT.Gelu, True, None)
        store_stage(nc, env, out)


def kernel(**inputs):
    import numpy as _np
    import concourse.bacc as _bacc
    from concourse import mybir as _mybir
    from concourse.bass_utils import run_bass_kernel_spmd as _run

    nc = _bacc.Bacc("TRN2", target_bir_lowering=False, num_devices=1)
    arrays, args = {}, {}
    for name, value in inputs.items():
        a = _np.ascontiguousarray(value)
        arrays[f"in_{name}_dram"] = a
        args[name] = nc.dram_tensor(f"in_{name}_dram", a.shape, _mybir.dt.from_np(a.dtype), kind="ExternalInput").ap()
    out = nc.dram_tensor("out_0_dram", (B, S, D), F32, kind="ExternalOutput").ap()
    build(nc, args, out)
    return _run(nc, [arrays], core_ids=[0]).results[0]["out_0_dram"]
```
